# Optimizing a Trainium2 kernel written in Bass

```python
import numpy as np
import jax
import jax.numpy as jnp

def _softmax(x, axis=-1):
    return jax.nn.softmax(x, axis=axis)

def _gelu(x):
    return jax.nn.gelu(x, approximate=True)

def _silu(x):
    return jax.nn.silu(x)

def _sigmoid(x):
    return jax.nn.sigmoid(x)

def _layernorm(x, axis=-1, eps=1e-05):
    m = jnp.mean(x, axis=axis, keepdims=True)
    v = jnp.var(x, axis=axis, keepdims=True)
    return (x - m) / jnp.sqrt(v + eps)

def _scatter_add(tgt, idx, src, axis=0):
    return tgt.at[idx].add(src)

def _segment_sum(src, seg, n):
    return jax.ops.segment_sum(src, seg, n)
kernel_name = 'mk_flamingo_gated_d4_seqx_r8_58b3f8'

def setup_inputs(seed: int=0):
    np.random.seed(seed)
    _w = jnp.asarray

    def _rec_inputs():
        import jax
        import jax.numpy as jnp
        _rk = jax.random.key(seed)
        x = 7.22e-05 + 1 * jax.random.normal(jax.random.fold_in(_rk, 1), (32, 128, 128), jnp.float32)
        _lenS = 128 - jax.random.randint(jax.random.fold_in(_rk, 7), (32,), 0, max(1, 128 // 4) + 1, jnp.int32)
        _lenS2 = 128 - jax.random.randint(jax.random.fold_in(_rk, 8), (32,), 0, max(1, 128 // 4) + 1, jnp.int32)
        _ctx_768P = jax.random.normal(jax.random.fold_in(_rk, 11), (32, 16, 96), jnp.float32)
        _ctx_768c = jax.random.dirichlet(jax.random.fold_in(_rk, 511), 0.3 * jnp.ones((16,), jnp.float32), (32, 128))
        _ctx_768t = jnp.einsum('bsk,bkd->bsd', _ctx_768c, _ctx_768P)
        _ctx_768t = _ctx_768t * jax.lax.rsqrt(jnp.mean(jnp.square(_ctx_768t)) + 1e-12) * 0.953939
        ctx_768 = -0.000191848 + 0.999787 * (_ctx_768t + 0.3 * jax.random.normal(jax.random.fold_in(_rk, 611), (32, 128, 96), jnp.float32))
        _validS = jnp.arange(128)[None, :] < _lenS[:, None]
        _validS2 = jnp.arange(128)[None, :] < _lenS2[:, None]
        _causal = jnp.tril(jnp.ones((128, 128), dtype=bool))
        mask_BxS_bf1 = jnp.ones((32, 128), dtype=bool)
        mask_BxS2_bf1 = jnp.ones((32, 128), dtype=bool)
        _g = jax.random.normal(jax.random.fold_in(_rk, 9001), (2, 4), jnp.float32)
        _g = jnp.sign(_g) * jnp.maximum(jnp.abs(_g), 1.0) + (_g == 0) * 1.0
        g_xattn = _g[0]
        g_ffn = _g[1]
        return (x, ctx_768, mask_BxS_bf1, mask_BxS2_bf1, g_xattn, g_ffn)
    x, ctx_768, mask_BxS_bf1, mask_BxS2_bf1, g_xattn, g_ffn = _rec_inputs()

    def _L0_xattn_setup():
        import jax, jax.numpy as jnp
        import numpy as np
        Q_DIM = 128
        KV_DIM = 96
        HEADS = 16
        DK = Q_DIM // HEADS
        key = jax.random.key(seed)
        ks = jax.random.split(key, 6)
        B, T_q, T_kv = (4, 256, 256)
        s_q = 1.0 / np.sqrt(Q_DIM)
        s_kv = 1.0 / np.sqrt(KV_DIM)
        return {'q_tokens': jax.random.normal(ks[0], (B, T_q, Q_DIM), jnp.float32), 'kv_tokens': jax.random.normal(ks[1], (B, T_kv, KV_DIM), jnp.float32), 'Wq': jax.random.normal(ks[2], (Q_DIM, Q_DIM), jnp.float32) * s_q, 'Wk': jax.random.normal(ks[3], (Q_DIM, KV_DIM), jnp.float32) * s_kv, 'Wv': jax.random.normal(ks[4], (Q_DIM, KV_DIM), jnp.float32) * s_kv, 'Wo': jax.random.normal(ks[5], (Q_DIM, Q_DIM), jnp.float32) * s_q}
    _L0_xattn_all = _L0_xattn_setup()
    _L0_xattn_in = {k: v for k, v in _L0_xattn_all.items() if k in ('Wq', 'Wk', 'Wv', 'Wo')}
    del _L0_xattn_all

    def _L0_ffn_setup():
        import jax, jax.numpy as jnp
        import numpy as np
        E = 8
        K = 2
        D = 128
        F = 512
        FS = 256
        B, S = (2, 128)
        key = jax.random.key(seed)
        ks = jax.random.split(key, 8)
        scale = jnp.float32(0.02)
        return {'x': jax.random.normal(ks[0], (B, S, D), jnp.float32), 'gate_w': jax.random.normal(ks[1], (E, D), jnp.float32) * scale, 'gate_k': jax.random.normal(ks[2], (E, D, F), jnp.float32) * scale, 'up_k': jax.random.normal(ks[3], (E, D, F), jnp.float32) * scale, 'down_k': jax.random.normal(ks[4], (E, F, D), jnp.float32) * scale, 'sh_gate': jax.random.normal(ks[5], (D, FS), jnp.float32) * scale, 'sh_up': jax.random.normal(ks[6], (D, FS), jnp.float32) * scale, 'sh_down': jax.random.normal(ks[7], (FS, D), jnp.float32) * scale}
    _L0_ffn_all = _L0_ffn_setup()
    _L0_ffn_in = {k: v for k, v in _L0_ffn_all.items() if k in ('gate_w', 'gate_k', 'up_k', 'down_k', 'sh_gate', 'sh_up', 'sh_down')}
    del _L0_ffn_all

    def _L1_xattn_setup():
        import jax, jax.numpy as jnp
        import numpy as np
        NUM_HEADS = 16
        CLAMP = 10000.0
        key = jax.random.key(seed)
        ks = jax.random.split(key, 8)
        B, Nq, Nkv, Cq, Ckv = (4, 256, 256, 128, 96)
        s_q = 1.0 / np.sqrt(Cq)
        s_kv = 1.0 / np.sqrt(Ckv)
        return {'query': jax.random.normal(ks[0], (B, Nq, Cq), jnp.float32), 'key_value': jax.random.normal(ks[1], (B, Nkv, Ckv), jnp.float32), 'Wq': jax.random.normal(ks[2], (Cq, Cq), jnp.float32) * s_q, 'bq': jnp.zeros((Cq,), jnp.float32), 'Wk': jax.random.normal(ks[3], (Ckv, Cq), jnp.float32) * s_kv, 'bk': jnp.zeros((Cq,), jnp.float32), 'Wv': jax.random.normal(ks[4], (Ckv, Cq), jnp.float32) * s_kv, 'bv': jnp.zeros((Cq,), jnp.float32), 'Wo': jax.random.normal(ks[5], (Cq, Cq), jnp.float32) * s_q, 'bo': jnp.zeros((Cq,), jnp.float32)}
    _L1_xattn_all = _L1_xattn_setup()
    _L1_xattn_in = {k: v for k, v in _L1_xattn_all.items() if k in ('Wq', 'bq', 'Wk', 'bk', 'Wv', 'bv', 'Wo', 'bo')}
    del _L1_xattn_all

    def _L1_ffn_setup():
        import jax, jax.numpy as jnp
        import numpy as np
        TOP_K = 2
        key = jax.random.key(seed)
        ks = jax.random.split(key, 8)
        B, S, H, F, E = (1, 128, 128, 128, 8)
        Fs = 2 * F
        s = lambda k, shape, scale: jax.random.normal(k, shape, dtype=jnp.float32) * scale
        return {'x': s(ks[0], (B, S, H), 1.0), 'router_w': s(ks[1], (H, E), 0.02), 'gate_w': s(ks[2], (E, H, F), 0.02), 'up_w': s(ks[3], (E, H, F), 0.02), 'down_w': s(ks[4], (E, F, H), 0.02), 'shared_gate_w': s(ks[5], (H, Fs), 0.02), 'shared_up_w': s(ks[6], (H, Fs), 0.02), 'shared_down_w': s(ks[7], (Fs, H), 0.02)}
    _L1_ffn_all = _L1_ffn_setup()
    _L1_ffn_in = {k: v for k, v in _L1_ffn_all.items() if k in ('router_w', 'gate_w', 'up_w', 'down_w', 'shared_gate_w', 'shared_up_w', 'shared_down_w')}
    del _L1_ffn_all

    def _L2_xattn_setup():
        import jax, jax.numpy as jnp
        import numpy as np
        HEADS = 16
        DIM_HEAD = 64
        RANK = 32
        LORA_W = 1.0
        IPA_SCALE = 1.0
        IPA_TOKENS = 4
        SCALE = DIM_HEAD ** (-0.5)

        def _split_heads(t):
            b, n, _ = t.shape
            return t.reshape(b, n, HEADS, DIM_HEAD).transpose(0, 2, 1, 3)

        def _merge_heads(t):
            b, h, n, d = t.shape
            return t.transpose(0, 2, 1, 3).reshape(b, n, h * d)

        def _attention(q_in, k_in, v_in):
            q = _split_heads(q_in)
            k = _split_heads(k_in)
            v = _split_heads(v_in)
            s = jnp.einsum('bhid,bhjd->bhij', q, k) * SCALE
            p = jax.nn.softmax(s, axis=-1)
            o = jnp.einsum('bhij,bhjd->bhid', p, v)
            return _merge_heads(o)

        def _lora(t, down, up, alpha):
            return t @ down @ up * (LORA_W * alpha[0] / RANK)
        key = jax.random.key(seed)
        ks = jax.random.split(key, 20)
        B, N, QD, CD, ID = (8, 512, 128, 96, HEADS * DIM_HEAD)
        CTX = 77 + IPA_TOKENS
        s = 0.02
        return {'x': jax.random.normal(ks[0], (B, N, QD), jnp.float32), 'context': jax.random.normal(ks[1], (B, CTX, CD), jnp.float32), 'Wq': jax.random.normal(ks[2], (QD, ID), jnp.float32) * s, 'Wk': jax.random.normal(ks[3], (CD, ID), jnp.float32) * s, 'Wv': jax.random.normal(ks[4], (CD, ID), jnp.float32) * s, 'Wo': jax.random.normal(ks[5], (ID, QD), jnp.float32) * s, 'bo': jnp.zeros((QD,), jnp.float32), 'q_down': jax.random.normal(ks[6], (QD, RANK), jnp.float32) * s, 'q_up': jax.random.normal(ks[7], (RANK, ID), jnp.float32) * s, 'q_alpha': jnp.ones((1,), jnp.float32) * RANK, 'k_down': jax.random.normal(ks[8], (CD, RANK), jnp.float32) * s, 'k_up': jax.random.normal(ks[9], (RANK, ID), jnp.float32) * s, 'k_alpha': jnp.ones((1,), jnp.float32) * RANK, 'v_down': jax.random.normal(ks[10], (CD, RANK), jnp.float32) * s, 'v_up': jax.random.normal(ks[11], (RANK, ID), jnp.float32) * s, 'v_alpha': jnp.ones((1,), jnp.float32) * RANK, 'o_down': jax.random.normal(ks[12], (ID, RANK), jnp.float32) * s, 'o_up': jax.random.normal(ks[13], (RANK, QD), jnp.float32) * s, 'o_alpha': jnp.ones((1,), jnp.float32) * RANK, 'Wk_ipa': jax.random.normal(ks[14], (CD, ID), jnp.float32) * s, 'Wv_ipa': jax.random.normal(ks[15], (CD, ID), jnp.float32) * s}
    _L2_xattn_all = _L2_xattn_setup()
    _L2_xattn_in = {k: v for k, v in _L2_xattn_all.items() if k in ('Wq', 'Wk', 'Wv', 'Wo', 'bo', 'q_down', 'q_up', 'q_alpha', 'k_down', 'k_up', 'k_alpha', 'v_down', 'v_up', 'v_alpha', 'o_down', 'o_up', 'o_alpha', 'Wk_ipa', 'Wv_ipa')}
    del _L2_xattn_all

    def _L2_ffn_setup():
        import jax, jax.numpy as jnp
        import numpy as np
        TOP_K = 2
        key = jax.random.key(seed)
        ks = jax.random.split(key, 7)
        B_, S, D, F, E, R = (2, 256, 128, 512, 4, 4)
        x = jax.random.normal(ks[0], (B_, S, D), dtype=jnp.float32)
        Wg = jax.random.normal(ks[1], (E, D), dtype=jnp.float32) * (1.0 / np.sqrt(D))
        bg = jnp.zeros((E,), dtype=jnp.float32)
        Wi = jax.random.normal(ks[2], (F, D), dtype=jnp.float32) * (1.0 / np.sqrt(D))
        Wo = jax.random.normal(ks[3], (D, F), dtype=jnp.float32) * (1.0 / np.sqrt(F))
        A = jax.random.normal(ks[4], (E, R, D), dtype=jnp.float32) * (1.0 / np.sqrt(D))
        Bm = jax.random.normal(ks[5], (E, F, R), dtype=jnp.float32) * 0.01
        return {'x': x, 'Wg': Wg, 'bg': bg, 'Wi': Wi, 'Wo': Wo, 'A': A, 'B': Bm}
    _L2_ffn_all = _L2_ffn_setup()
    _L2_ffn_in = {k: v for k, v in _L2_ffn_all.items() if k in ('Wg', 'bg', 'Wi', 'Wo', 'A', 'B')}
    del _L2_ffn_all

    def _L3_xattn_setup():
        import jax, jax.numpy as jnp
        import numpy as np
        B, T, DT, G, DV = (16, 64, 128, 72, 96)
        H, DH = (4, 32)
        INNER = H * DH
        HID = 4 * DT
        N_STATE = 64
        K_TOP = 32

        def layernorm(x, g, b, eps=1e-05):
            m = x.mean(-1, keepdims=True)
            v = x.var(-1, keepdims=True)
            return (x - m) * jax.lax.rsqrt(v + eps) * g + b

        def s4d(x, log_dt, A_re, A_im, C_re, C_im, D_skip):
            Bb, L, D = x.shape
            dt = jnp.exp(log_dt)
            A = A_re + 1j * A_im
            C = C_re + 1j * C_im
            dtA = dt[:, None] * A
            dC = C * (jnp.exp(dtA) - 1.0) / A
            powers = jnp.exp(dtA[:, :, None] * jnp.arange(L))
            K = 2.0 * jnp.einsum('dn,dnl->dl', dC, powers).real
            n = 2 * L
            Kf = jnp.fft.rfft(K, n=n, axis=-1)
            xf = jnp.fft.rfft(x, n=n, axis=1)
            y = jnp.fft.irfft(xf * Kf.T[None], n=n, axis=1)[:, :L]
            return y + x * D_skip
        key = jax.random.key(seed)
        ks = jax.random.split(key, 16)
        s = 0.02
        inp = {'x_text': jax.random.normal(ks[0], (B, T, DT), jnp.float32), 'x_vision': jax.random.normal(ks[1], (B, G, DV), jnp.float32), 'text_mask': jnp.ones((B, T), bool), 'vision_mask': jnp.ones((B, G), bool), 'Wq': jax.random.normal(ks[2], (DT, INNER), jnp.float32) * s, 'Wk': jax.random.normal(ks[3], (DV, INNER), jnp.float32) * s, 'Wv': jax.random.normal(ks[4], (DV, DT), jnp.float32) * s, 'W_film_in': jax.random.normal(ks[5], (DT, 2 * DT), jnp.float32) * s, 'b_film_in': jnp.zeros((2 * DT,), jnp.float32), 'W_film_out': jax.random.normal(ks[6], (DT, 2 * DT), jnp.float32) * s, 'b_film_out': jnp.zeros((2 * DT,), jnp.float32), 'g_norm_in': jnp.ones((DT,), jnp.float32), 'b_norm_in': jnp.zeros((DT,), jnp.float32), 'g_norm_out': jnp.ones((DT,), jnp.float32), 'b_norm_out': jnp.zeros((DT,), jnp.float32), 'g_ffn': jnp.ones((DT,), jnp.float32), 'b_ffn': jnp.zeros((DT,), jnp.float32), 'W1': jax.random.normal(ks[7], (DT, HID), jnp.float32) * s, 'b1': jnp.zeros((HID,), jnp.float32), 'W2': jax.random.normal(ks[8], (HID, DT), jnp.float32) * s, 'b2': jnp.zeros((DT,), jnp.float32), 'log_dt': jnp.log(0.001) + jax.random.uniform(ks[9], (DT,), jnp.float32) * (jnp.log(0.1) - jnp.log(0.001)), 'A_re': -0.5 * jnp.ones((DT, N_STATE), jnp.float32), 'A_im': jnp.tile(jnp.pi * jnp.arange(N_STATE, dtype=jnp.float32), (DT, 1)), 'C_re': jax.random.normal(ks[10], (DT, N_STATE), jnp.float32) * 0.5 ** 0.5, 'C_im': jax.random.normal(ks[11], (DT, N_STATE), jnp.float32) * 0.5 ** 0.5, 'D_skip': jax.random.normal(ks[12], (DT,), jnp.float32), 'mod_gate': jnp.array(0.5, jnp.float32)}
        return inp
    _L3_xattn_all = _L3_xattn_setup()
    _L3_xattn_in = {k: v for k, v in _L3_xattn_all.items() if k in ('Wq', 'Wk', 'Wv', 'W_film_in', 'b_film_in', 'W_film_out', 'b_film_out', 'g_norm_in', 'b_norm_in', 'g_norm_out', 'b_norm_out', 'g_ffn', 'b_ffn', 'W1', 'b1', 'W2', 'b2', 'log_dt', 'A_re', 'A_im', 'C_re', 'C_im', 'D_skip', 'mod_gate')}
    del _L3_xattn_all

    def _L3_ffn_setup():
        import jax, jax.numpy as jnp
        import numpy as np
        B, S = (4, 256)
        D_MODEL, D_FF, N_EXPERTS, TOP_K = (128, 512, 8, 2)
        T = B * S
        CAPACITY_FACTOR, MIN_CAP = (1.25, 4)
        CAP = max(int(CAPACITY_FACTOR * (T * TOP_K / N_EXPERTS)), MIN_CAP)
        key = jax.random.key(seed)
        ks = jax.random.split(key, 6)

        def w(k, shape, fan):
            return jax.random.normal(k, shape, jnp.float32) * fan ** (-0.5)
        return {'x': jax.random.normal(ks[0], (B, S, D_MODEL), jnp.float32), 'Wr': w(ks[1], (D_MODEL, N_EXPERTS), D_MODEL), 'W1': w(ks[2], (N_EXPERTS, D_MODEL, D_FF), D_MODEL), 'b1': jnp.zeros((N_EXPERTS, D_FF), jnp.float32), 'W2': w(ks[3], (N_EXPERTS, D_FF, D_MODEL), D_FF), 'b2': jnp.zeros((N_EXPERTS, D_MODEL), jnp.float32), 'fw1': w(ks[4], (D_MODEL, D_FF), D_MODEL), 'fb1': jnp.zeros((D_FF,), jnp.float32), 'fw2': w(ks[5], (D_FF, D_MODEL), D_FF), 'fb2': jnp.zeros((D_MODEL,), jnp.float32)}
    _L3_ffn_all = _L3_ffn_setup()
    _L3_ffn_in = {k: v for k, v in _L3_ffn_all.items() if k in ('Wr', 'W1', 'b1', 'W2', 'b2', 'fw1', 'fb1', 'fw2', 'fb2')}
    del _L3_ffn_all
    return {'x': x, 'ctx_768': ctx_768, 'mask_BxS_bf1': mask_BxS_bf1, 'mask_BxS2_bf1': mask_BxS2_bf1, 'g_xattn': g_xattn, 'g_ffn': g_ffn, 'L0_xattn_Wq': _L0_xattn_in['Wq'], 'L0_xattn_Wk': _L0_xattn_in['Wk'], 'L0_xattn_Wv': _L0_xattn_in['Wv'], 'L0_xattn_Wo': _L0_xattn_in['Wo'], 'L0_ffn_gate_w': _L0_ffn_in['gate_w'], 'L0_ffn_gate_k': _L0_ffn_in['gate_k'], 'L0_ffn_up_k': _L0_ffn_in['up_k'], 'L0_ffn_down_k': _L0_ffn_in['down_k'], 'L0_ffn_sh_gate': _L0_ffn_in['sh_gate'], 'L0_ffn_sh_up': _L0_ffn_in['sh_up'], 'L0_ffn_sh_down': _L0_ffn_in['sh_down'], 'L1_xattn_Wq': _L1_xattn_in['Wq'], 'L1_xattn_bq': _L1_xattn_in['bq'], 'L1_xattn_Wk': _L1_xattn_in['Wk'], 'L1_xattn_bk': _L1_xattn_in['bk'], 'L1_xattn_Wv': _L1_xattn_in['Wv'], 'L1_xattn_bv': _L1_xattn_in['bv'], 'L1_xattn_Wo': _L1_xattn_in['Wo'], 'L1_xattn_bo': _L1_xattn_in['bo'], 'L1_ffn_router_w': _L1_ffn_in['router_w'], 'L1_ffn_gate_w': _L1_ffn_in['gate_w'], 'L1_ffn_up_w': _L1_ffn_in['up_w'], 'L1_ffn_down_w': _L1_ffn_in['down_w'], 'L1_ffn_shared_gate_w': _L1_ffn_in['shared_gate_w'], 'L1_ffn_shared_up_w': _L1_ffn_in['shared_up_w'], 'L1_ffn_shared_down_w': _L1_ffn_in['shared_down_w'], 'L2_xattn_Wq': _L2_xattn_in['Wq'], 'L2_xattn_Wk': _L2_xattn_in['Wk'], 'L2_xattn_Wv': _L2_xattn_in['Wv'], 'L2_xattn_Wo': _L2_xattn_in['Wo'], 'L2_xattn_bo': _L2_xattn_in['bo'], 'L2_xattn_q_down': _L2_xattn_in['q_down'], 'L2_xattn_q_up': _L2_xattn_in['q_up'], 'L2_xattn_q_alpha': _L2_xattn_in['q_alpha'], 'L2_xattn_k_down': _L2_xattn_in['k_down'], 'L2_xattn_k_up': _L2_xattn_in['k_up'], 'L2_xattn_k_alpha': _L2_xattn_in['k_alpha'], 'L2_xattn_v_down': _L2_xattn_in['v_down'], 'L2_xattn_v_up': _L2_xattn_in['v_up'], 'L2_xattn_v_alpha': _L2_xattn_in['v_alpha'], 'L2_xattn_o_down': _L2_xattn_in['o_down'], 'L2_xattn_o_up': _L2_xattn_in['o_up'], 'L2_xattn_o_alpha': _L2_xattn_in['o_alpha'], 'L2_xattn_Wk_ipa': _L2_xattn_in['Wk_ipa'], 'L2_xattn_Wv_ipa': _L2_xattn_in['Wv_ipa'], 'L2_ffn_Wg': _L2_ffn_in['Wg'], 'L2_ffn_bg': _L2_ffn_in['bg'], 'L2_ffn_Wi': _L2_ffn_in['Wi'], 'L2_ffn_Wo': _L2_ffn_in['Wo'], 'L2_ffn_A': _L2_ffn_in['A'], 'L2_ffn_B': _L2_ffn_in['B'], 'L3_xattn_Wq': _L3_xattn_in['Wq'], 'L3_xattn_Wk': _L3_xattn_in['Wk'], 'L3_xattn_Wv': _L3_xattn_in['Wv'], 'L3_xattn_W_film_in': _L3_xattn_in['W_film_in'], 'L3_xattn_b_film_in': _L3_xattn_in['b_film_in'], 'L3_xattn_W_film_out': _L3_xattn_in['W_film_out'], 'L3_xattn_b_film_out': _L3_xattn_in['b_film_out'], 'L3_xattn_g_norm_in': _L3_xattn_in['g_norm_in'], 'L3_xattn_b_norm_in': _L3_xattn_in['b_norm_in'], 'L3_xattn_g_norm_out': _L3_xattn_in['g_norm_out'], 'L3_xattn_b_norm_out': _L3_xattn_in['b_norm_out'], 'L3_xattn_g_ffn': _L3_xattn_in['g_ffn'], 'L3_xattn_b_ffn': _L3_xattn_in['b_ffn'], 'L3_xattn_W1': _L3_xattn_in['W1'], 'L3_xattn_b1': _L3_xattn_in['b1'], 'L3_xattn_W2': _L3_xattn_in['W2'], 'L3_xattn_b2': _L3_xattn_in['b2'], 'L3_xattn_log_dt': _L3_xattn_in['log_dt'], 'L3_xattn_A_re': _L3_xattn_in['A_re'], 'L3_xattn_A_im': _L3_xattn_in['A_im'], 'L3_xattn_C_re': _L3_xattn_in['C_re'], 'L3_xattn_C_im': _L3_xattn_in['C_im'], 'L3_xattn_D_skip': _L3_xattn_in['D_skip'], 'L3_xattn_mod_gate': _L3_xattn_in['mod_gate'], 'L3_ffn_Wr': _L3_ffn_in['Wr'], 'L3_ffn_W1': _L3_ffn_in['W1'], 'L3_ffn_b1': _L3_ffn_in['b1'], 'L3_ffn_W2': _L3_ffn_in['W2'], 'L3_ffn_b2': _L3_ffn_in['b2'], 'L3_ffn_fw1': _L3_ffn_in['fw1'], 'L3_ffn_fb1': _L3_ffn_in['fb1'], 'L3_ffn_fw2': _L3_ffn_in['fw2'], 'L3_ffn_fb2': _L3_ffn_in['fb2']}

def reference(x, ctx_768, mask_BxS_bf1, mask_BxS2_bf1, g_xattn, g_ffn, L0_xattn_Wq, L0_xattn_Wk, L0_xattn_Wv, L0_xattn_Wo, L0_ffn_gate_w, L0_ffn_gate_k, L0_ffn_up_k, L0_ffn_down_k, L0_ffn_sh_gate, L0_ffn_sh_up, L0_ffn_sh_down, L1_xattn_Wq, L1_xattn_bq, L1_xattn_Wk, L1_xattn_bk, L1_xattn_Wv, L1_xattn_bv, L1_xattn_Wo, L1_xattn_bo, L1_ffn_router_w, L1_ffn_gate_w, L1_ffn_up_w, L1_ffn_down_w, L1_ffn_shared_gate_w, L1_ffn_shared_up_w, L1_ffn_shared_down_w, L2_xattn_Wq, L2_xattn_Wk, L2_xattn_Wv, L2_xattn_Wo, L2_xattn_bo, L2_xattn_q_down, L2_xattn_q_up, L2_xattn_q_alpha, L2_xattn_k_down, L2_xattn_k_up, L2_xattn_k_alpha, L2_xattn_v_down, L2_xattn_v_up, L2_xattn_v_alpha, L2_xattn_o_down, L2_xattn_o_up, L2_xattn_o_alpha, L2_xattn_Wk_ipa, L2_xattn_Wv_ipa, L2_ffn_Wg, L2_ffn_bg, L2_ffn_Wi, L2_ffn_Wo, L2_ffn_A, L2_ffn_B, L3_xattn_Wq, L3_xattn_Wk, L3_xattn_Wv, L3_xattn_W_film_in, L3_xattn_b_film_in, L3_xattn_W_film_out, L3_xattn_b_film_out, L3_xattn_g_norm_in, L3_xattn_b_norm_in, L3_xattn_g_norm_out, L3_xattn_b_norm_out, L3_xattn_g_ffn, L3_xattn_b_ffn, L3_xattn_W1, L3_xattn_b1, L3_xattn_W2, L3_xattn_b2, L3_xattn_log_dt, L3_xattn_A_re, L3_xattn_A_im, L3_xattn_C_re, L3_xattn_C_im, L3_xattn_D_skip, L3_xattn_mod_gate, L3_ffn_Wr, L3_ffn_W1, L3_ffn_b1, L3_ffn_W2, L3_ffn_b2, L3_ffn_fw1, L3_ffn_fb1, L3_ffn_fw2, L3_ffn_fb2):
    import jax
    import jax.numpy as jnp

    def _L0_xattn_ref(q_tokens, kv_tokens, Wq, Wk, Wv, Wo):
        import jax, jax.numpy as jnp
        import numpy as np
        Q_DIM = 128
        KV_DIM = 96
        HEADS = 16
        DK = Q_DIM // HEADS
        B, T_q, _ = q_tokens.shape
        T_kv = kv_tokens.shape[1]
        q = q_tokens @ Wq.T
        k = kv_tokens @ Wk.T
        v = kv_tokens @ Wv.T
        q = q.reshape(B, T_q, HEADS, DK).transpose(0, 2, 1, 3)
        k = k.reshape(B, T_kv, HEADS, DK).transpose(0, 2, 1, 3)
        v = v.reshape(B, T_kv, HEADS, DK).transpose(0, 2, 1, 3)
        scale = 1.0 / jnp.sqrt(jnp.asarray(DK, q.dtype))
        attn = jnp.einsum('bhqd,bhkd->bhqk', q, k) * scale
        attn = jax.nn.softmax(attn, axis=-1)
        out = jnp.einsum('bhqk,bhkd->bhqd', attn, v)
        out = out.transpose(0, 2, 1, 3).reshape(B, T_q, Q_DIM)
        return out @ Wo.T

    def _L0_ffn_ref(x, gate_w, gate_k, up_k, down_k, sh_gate, sh_up, sh_down):
        import jax, jax.numpy as jnp
        import numpy as np
        E = 8
        K = 2
        D = 128
        F = 512
        FS = 256
        B, S = (2, 128)
        b, s, d = x.shape
        xt = x.reshape(-1, d)
        logits = xt @ gate_w.T
        scores = jax.nn.softmax(logits, axis=-1)
        topk_w, topk_i = jax.lax.top_k(scores, K)
        combine = (jax.nn.one_hot(topk_i, E, dtype=xt.dtype) * topk_w[..., None]).sum(axis=1)
        g = jnp.einsum('nd,edf->enf', xt, gate_k)
        u = jnp.einsum('nd,edf->enf', xt, up_k)
        a = jax.nn.silu(g) * u
        eo = jnp.einsum('enf,efd->end', a, down_k)
        y = jnp.einsum('end,ne->nd', eo, combine)
        shared = jax.nn.silu(xt @ sh_gate) * (xt @ sh_up) @ sh_down
        return (y + shared).reshape(b, s, d)

    def _L1_xattn_ref(query, key_value, Wq, bq, Wk, bk, Wv, bv, Wo, bo):
        import jax, jax.numpy as jnp
        import numpy as np
        NUM_HEADS = 16
        CLAMP = 10000.0
        B, Nq, Cq = query.shape
        Nkv = key_value.shape[1]
        H = NUM_HEADS
        D = Cq // H
        scale = D ** (-0.5)
        q = (query @ Wq + bq).reshape(B, Nq, H, D).transpose(0, 2, 1, 3)
        k = (key_value @ Wk + bk).reshape(B, Nkv, H, D).transpose(0, 2, 1, 3)
        v = (key_value @ Wv + bv).reshape(B, Nkv, H, D).transpose(0, 2, 1, 3)
        attn = jnp.einsum('bhqd,bhkd->bhqk', q, k) * scale
        attn = jnp.clip(attn, -CLAMP, CLAMP)
        attn = jax.nn.softmax(attn, axis=-1)
        attn = jnp.where(jnp.any(jnp.isnan(attn)), jnp.asarray(1.0 / Nkv, attn.dtype), attn)
        x = jnp.einsum('bhqk,bhkd->bqhd', attn, v).reshape(B, Nq, Cq)
        return x @ Wo + bo

    def _L1_ffn_ref(x, router_w, gate_w, up_w, down_w, shared_gate_w, shared_up_w, shared_down_w):
        import jax, jax.numpy as jnp
        import numpy as np
        TOP_K = 2
        B, S, H = x.shape
        N = B * S
        xf = x.reshape(N, H)
        scores = jax.nn.softmax(xf @ router_w, axis=-1)
        topk_scores, topk_idx = jax.lax.top_k(scores, TOP_K)
        E = scores.shape[-1]
        combine = jnp.zeros((N, E), dtype=x.dtype).at[jnp.arange(N)[:, None], topk_idx].add(topk_scores)
        g = jnp.einsum('nh,ehf->enf', xf, gate_w)
        u = jnp.einsum('nh,ehf->enf', xf, up_w)
        y = jnp.einsum('enf,efh->enh', jax.nn.silu(g) * u, down_w)
        routed = jnp.einsum('enh,ne->nh', y, combine)
        shared = jax.nn.silu(xf @ shared_gate_w) * (xf @ shared_up_w) @ shared_down_w
        return (shared + routed).reshape(B, S, H)

    def _L2_xattn_ref(x, context, Wq, Wk, Wv, Wo, bo, q_down, q_up, q_alpha, k_down, k_up, k_alpha, v_down, v_up, v_alpha, o_down, o_up, o_alpha, Wk_ipa, Wv_ipa):
        import jax, jax.numpy as jnp
        import numpy as np
        HEADS = 16
        DIM_HEAD = 64
        RANK = 32
        LORA_W = 1.0
        IPA_SCALE = 1.0
        IPA_TOKENS = 4
        SCALE = DIM_HEAD ** (-0.5)

        def _split_heads(t):
            b, n, _ = t.shape
            return t.reshape(b, n, HEADS, DIM_HEAD).transpose(0, 2, 1, 3)

        def _merge_heads(t):
            b, h, n, d = t.shape
            return t.transpose(0, 2, 1, 3).reshape(b, n, h * d)

        def _attention(q_in, k_in, v_in):
            q = _split_heads(q_in)
            k = _split_heads(k_in)
            v = _split_heads(v_in)
            s = jnp.einsum('bhid,bhjd->bhij', q, k) * SCALE
            p = jax.nn.softmax(s, axis=-1)
            o = jnp.einsum('bhij,bhjd->bhid', p, v)
            return _merge_heads(o)

        def _lora(t, down, up, alpha):
            return t @ down @ up * (LORA_W * alpha[0] / RANK)
        q_in = x @ Wq + _lora(x, q_down, q_up, q_alpha)
        end = context.shape[1] - IPA_TOKENS
        org_ctx = context[:, :end, :]
        ipa_ctx = context[:, end:, :]
        k_in = org_ctx @ Wk + _lora(org_ctx, k_down, k_up, k_alpha)
        v_in = org_ctx @ Wv + _lora(org_ctx, v_down, v_up, v_alpha)
        out = _attention(q_in, k_in, v_in)
        ipa_k = ipa_ctx @ Wk_ipa
        ipa_v = ipa_ctx @ Wv_ipa
        out_ipa = _attention(q_in, ipa_k, ipa_v)
        out = out + IPA_SCALE * out_ipa
        return out @ Wo + bo + _lora(out, o_down, o_up, o_alpha)

    def _L2_ffn_ref(x, Wg, bg, Wi, Wo, A, B):
        import jax, jax.numpy as jnp
        import numpy as np
        TOP_K = 2
        E = Wg.shape[0]
        logits = jnp.einsum('bsd,ed->bse', x, Wg) + bg
        scores = jax.nn.softmax(logits, axis=-1)
        topv, topi = jax.lax.top_k(scores, TOP_K)
        w = jnp.sum(jax.nn.one_hot(topi, E, dtype=x.dtype) * topv[..., None], axis=-2)
        base = jnp.einsum('bsd,fd->bsf', x, Wi)
        lora_low = jnp.einsum('bsd,erd->bser', x, A)
        lora = jnp.einsum('bser,efr->bsef', lora_low, B)
        h = jax.nn.relu(base[:, :, None, :] + lora)
        expert_out = jnp.einsum('bsef,df->bsed', h, Wo)
        out = jnp.einsum('bse,bsed->bsd', w, expert_out)
        return out

    def _L3_xattn_ref(x_text, x_vision, text_mask, vision_mask, Wq, Wk, Wv, W_film_in, b_film_in, W_film_out, b_film_out, g_norm_in, b_norm_in, g_norm_out, b_norm_out, g_ffn, b_ffn, W1, b1, W2, b2, log_dt, A_re, A_im, C_re, C_im, D_skip, mod_gate):
        import jax, jax.numpy as jnp
        import numpy as np
        B, T, DT, G, DV = (16, 64, 128, 72, 96)
        H, DH = (4, 32)
        INNER = H * DH
        HID = 4 * DT
        N_STATE = 64
        K_TOP = 32

        def layernorm(x, g, b, eps=1e-05):
            m = x.mean(-1, keepdims=True)
            v = x.var(-1, keepdims=True)
            return (x - m) * jax.lax.rsqrt(v + eps) * g + b

        def s4d(x, log_dt, A_re, A_im, C_re, C_im, D_skip):
            Bb, L, D = x.shape
            dt = jnp.exp(log_dt)
            A = A_re + 1j * A_im
            C = C_re + 1j * C_im
            dtA = dt[:, None] * A
            dC = C * (jnp.exp(dtA) - 1.0) / A
            powers = jnp.exp(dtA[:, :, None] * jnp.arange(L))
            K = 2.0 * jnp.einsum('dn,dnl->dl', dC, powers).real
            n = 2 * L
            Kf = jnp.fft.rfft(K, n=n, axis=-1)
            xf = jnp.fft.rfft(x, n=n, axis=1)
            y = jnp.fft.irfft(xf * Kf.T[None], n=n, axis=1)[:, :L]
            return y + x * D_skip
        Bb, Tt, D = x_text.shape
        Gg = x_vision.shape[1]
        Q = (x_text @ Wq).reshape(Bb, Tt, H, DH)
        K = (x_vision @ Wk).reshape(Bb, Gg, H, DH)
        scores = jnp.einsum('bthd,bghd->bhtg', Q, K) / np.sqrt(DH).astype(np.float32)
        scores = jnp.where(vision_mask[:, None, None, :], scores, -jnp.inf)
        topv, topi = jax.lax.top_k(scores, K_TOP)
        probs = jax.nn.softmax(topv, axis=-1)
        bi = jnp.arange(Bb)[:, None, None, None]
        hi = jnp.arange(H)[None, :, None, None]
        ti = jnp.arange(Tt)[None, None, :, None]
        attn = jnp.zeros_like(scores).at[bi, hi, ti, topi].set(probs)
        attn_mean = attn.mean(axis=1)
        V = x_vision @ Wv
        c_t = jnp.einsum('btg,bgd->btd', attn_mean, V)
        c_t = c_t * text_mask[..., None]
        x = layernorm(x_text, g_norm_in, b_norm_in)
        scale_in, shift_in = jnp.split(c_t @ W_film_in + b_film_in, 2, axis=-1)
        x = x * (1.0 + mod_gate * scale_in) + mod_gate * shift_in
        y = s4d(x, log_dt, A_re, A_im, C_re, C_im, D_skip)
        scale_out, shift_out = jnp.split(c_t @ W_film_out + b_film_out, 2, axis=-1)
        y = y * (1.0 + mod_gate * scale_out) + mod_gate * shift_out
        xt = x_text + y
        h = layernorm(xt, g_ffn, b_ffn)
        h = jax.nn.gelu(h @ W1 + b1, approximate=False) @ W2 + b2
        xt = xt + h
        return layernorm(xt, g_norm_out, b_norm_out)

    def _L3_ffn_ref(x, Wr, W1, b1, W2, b2, fw1, fb1, fw2, fb2):
        import jax, jax.numpy as jnp
        import numpy as np
        B, S = (4, 256)
        D_MODEL, D_FF, N_EXPERTS, TOP_K = (128, 512, 8, 2)
        T = B * S
        CAPACITY_FACTOR, MIN_CAP = (1.25, 4)
        CAP = max(int(CAPACITY_FACTOR * (T * TOP_K / N_EXPERTS)), MIN_CAP)
        Bx, Sx, D = x.shape
        Tn = Bx * Sx
        xf = x.reshape(Tn, D)
        logits = xf @ Wr
        probs = jax.nn.softmax(logits, axis=-1)
        scores, experts = jax.lax.top_k(probs, TOP_K)
        scores = scores / jnp.maximum(scores.sum(-1, keepdims=True), 1e-09)
        y_fb = jax.nn.gelu(xf @ fw1 + fb1, approximate=False) @ fw2 + fb2
        y = jnp.zeros_like(xf)
        fb_mask = jnp.zeros((Tn,), bool)
        for e in range(N_EXPERTS):
            assign = experts == e
            w_e = jnp.where(assign, scores, 0.0).sum(-1)
            eligible = assign.any(-1) & ~fb_mask
            rank = jnp.cumsum(eligible.astype(jnp.int32)) - 1
            keep = eligible & (rank < CAP)
            overflow = eligible & ~keep
            fb_mask = fb_mask | overflow
            y = jnp.where(overflow[:, None], y_fb, y)
            idx = jnp.nonzero(keep, size=CAP, fill_value=0)[0]
            valid = jnp.arange(CAP) < keep.sum()
            h = jax.nn.gelu(xf[idx] @ W1[e] + b1[e], approximate=False)
            y_e = h @ W2[e] + b2[e]
            y = y.at[idx].add(y_e * (w_e[idx] * valid)[:, None])
        return y.reshape(Bx, Sx, D)
    x = x + jnp.tanh(g_xattn[0]) * _L0_xattn_ref(_layernorm(x, axis=-1), ctx_768, L0_xattn_Wq, L0_xattn_Wk, L0_xattn_Wv, L0_xattn_Wo)
    x = x + jnp.tanh(g_ffn[0]) * _L0_ffn_ref(_layernorm(x, axis=-1), L0_ffn_gate_w, L0_ffn_gate_k, L0_ffn_up_k, L0_ffn_down_k, L0_ffn_sh_gate, L0_ffn_sh_up, L0_ffn_sh_down)
    x = x + jnp.tanh(g_xattn[1]) * _L1_xattn_ref(_layernorm(x, axis=-1), ctx_768, L1_xattn_Wq, L1_xattn_bq, L1_xattn_Wk, L1_xattn_bk, L1_xattn_Wv, L1_xattn_bv, L1_xattn_Wo, L1_xattn_bo)
    x = x + jnp.tanh(g_ffn[1]) * _L1_ffn_ref(_layernorm(x, axis=-1), L1_ffn_router_w, L1_ffn_gate_w, L1_ffn_up_w, L1_ffn_down_w, L1_ffn_shared_gate_w, L1_ffn_shared_up_w, L1_ffn_shared_down_w)
    x = x + jnp.tanh(g_xattn[2]) * _L2_xattn_ref(_layernorm(x, axis=-1), ctx_768, L2_xattn_Wq, L2_xattn_Wk, L2_xattn_Wv, L2_xattn_Wo, L2_xattn_bo, L2_xattn_q_down, L2_xattn_q_up, L2_xattn_q_alpha, L2_xattn_k_down, L2_xattn_k_up, L2_xattn_k_alpha, L2_xattn_v_down, L2_xattn_v_up, L2_xattn_v_alpha, L2_xattn_o_down, L2_xattn_o_up, L2_xattn_o_alpha, L2_xattn_Wk_ipa, L2_xattn_Wv_ipa)
    x = x + jnp.tanh(g_ffn[2]) * _L2_ffn_ref(_layernorm(x, axis=-1), L2_ffn_Wg, L2_ffn_bg, L2_ffn_Wi, L2_ffn_Wo, L2_ffn_A, L2_ffn_B)
    x = x + jnp.tanh(g_xattn[3]) * _L3_xattn_ref(_layernorm(x, axis=-1), ctx_768, mask_BxS_bf1, mask_BxS2_bf1, L3_xattn_Wq, L3_xattn_Wk, L3_xattn_Wv, L3_xattn_W_film_in, L3_xattn_b_film_in, L3_xattn_W_film_out, L3_xattn_b_film_out, L3_xattn_g_norm_in, L3_xattn_b_norm_in, L3_xattn_g_norm_out, L3_xattn_b_norm_out, L3_xattn_g_ffn, L3_xattn_b_ffn, L3_xattn_W1, L3_xattn_b1, L3_xattn_W2, L3_xattn_b2, L3_xattn_log_dt, L3_xattn_A_re, L3_xattn_A_im, L3_xattn_C_re, L3_xattn_C_im, L3_xattn_D_skip, L3_xattn_mod_gate)
    x = x + jnp.tanh(g_ffn[3]) * _L3_ffn_ref(_layernorm(x, axis=-1), L3_ffn_Wr, L3_ffn_W1, L3_ffn_b1, L3_ffn_W2, L3_ffn_b2, L3_ffn_fw1, L3_ffn_fb1, L3_ffn_fw2, L3_ffn_fb2)
    return x

_drawn_inputs = setup_inputs


def setup_inputs(seed=0):
    import zlib

    import numpy as np

    out = dict(_drawn_inputs(seed))
    spreads = {'L1_xattn_bq': (0.0, 0.1),
     'L1_xattn_bk': (0.0, 2.0),
     'L1_xattn_bv': (0.0, 0.1),
     'L1_xattn_bo': (0.0, 0.1),
     'L2_xattn_bo': (0.0, 0.1),
     'L2_ffn_bg': (0.0, 0.1),
     'L3_xattn_b_film_in': (0.0, 0.1),
     'L3_xattn_b_film_out': (0.0, 0.1),
     'L3_xattn_g_norm_in': (1.0, 0.2),
     'L3_xattn_b_norm_in': (0.0, 0.1),
     'L3_xattn_g_norm_out': (1.0, 0.2),
     'L3_xattn_b_norm_out': (0.0, 0.1),
     'L3_xattn_g_ffn': (1.0, 0.563),
     'L3_xattn_b_ffn': (0.0, 0.846),
     'L3_xattn_b1': (0.0, 0.1),
     'L3_xattn_b2': (0.0, 0.1),
     'L3_xattn_A_re': (-0.5, 0.2),
     'L3_ffn_b1': (0.0, 0.407),
     'L3_ffn_b2': (0.0, 0.284),
     'L3_ffn_fb1': (0.0, 0.1),
     'L3_ffn_fb2': (0.0, 0.1)}
    factors = {'g_ffn': 23.192,
     'L0_ffn_gate_w': 6.064,
     'L0_ffn_gate_k': 3.398,
     'L0_ffn_up_k': 3.184,
     'L0_ffn_down_k': 3.053,
     'L0_ffn_sh_gate': 2.752,
     'L0_ffn_sh_down': 3.127,
     'L1_ffn_router_w': 3.465,
     'L1_ffn_gate_w': 3.832,
     'L1_ffn_up_w': 3.213,
     'L1_ffn_down_w': 4.28,
     'L2_xattn_Wq': 5.858,
     'L2_xattn_Wk': 5.883,
     'L2_xattn_q_down': 8.0,
     'L2_xattn_q_up': 6.239,
     'L2_xattn_k_down': 8.0,
     'L2_xattn_k_up': 8.0,
     'L2_xattn_Wk_ipa': 3.459,
     'L2_ffn_B': 2.722,
     'L3_xattn_Wq': 9.94,
     'L3_xattn_Wk': 9.784,
     'L1_ffn_shared_up_w': 2.987}
    for name, (base, spread) in spreads.items():
        noise = np.random.default_rng([zlib.crc32(name.encode()), seed]).standard_normal(out[name].shape)
        drawn = base * np.exp(spread * noise) if base else spread * noise
        out[name] = jnp.asarray(drawn.astype(out[name].dtype))
    for name, factor in factors.items():
        out[name] = (out[name] * factor).astype(out[name].dtype)
    return out
```

```python
from contextlib import ExitStack

import concourse.bass as bass
from concourse import mybir

F32 = mybir.dt.float32
U8 = mybir.dt.uint8
U32 = mybir.dt.uint32
ALU = mybir.AluOpType
ACT = mybir.ActivationFunctionType
AX = mybir.AxisListType

P = 128
NB = 32
KV = 96
BODY = 8
TURNS = NB // BODY
GRP = 4
TOK = GRP * P
EPS = 1e-5


CREDIT = 64


def done(n):
    return n + (CREDIT + 1)


class Steps:

    def __init__(self, sem):
        self.done, self.count = sem, 0

    def one(self):
        self.count += 1
        return 1

    def restart(self):
        self.count = 0


class Alloc:

    def __init__(self, nc, ctx, tag):
        self.nc, self.ctx, self.tag, self.sems = nc, ctx, tag, []
        ctx.callback(self.close)

    def sb(self, name, shape, dt=F32):
        return self.ctx.enter_context(self.nc.sbuf_tensor(f"{self.tag}_{name}", shape, dt))

    def ps(self, name, shape):
        return self.ctx.enter_context(self.nc.psum_tensor(f"{self.tag}_{name}", shape, F32))

    def close(self):
        self.nc.clear_and_free_semaphores(self.sems)
        self.nc.all_engine_barrier()

    def sem(self, name):
        s = self.nc.alloc_semaphore(f"{self.tag}_{name}")
        self.sems.append(s)
        return s


class Core:
    pass


def columns(parts):
    at, out = 0, {}
    for name, n in parts:
        out[name] = (at, n)
        at += n
    return out, at


class Packed:

    def __init__(self, tile, place):
        self.tile, self.place = tile, place

    def __getitem__(self, name):
        at, n = self.place[name]
        return self.tile[:, at:at + n]

    def items(self):
        return [(name, self[name]) for name in self.place]



class Norm:

    def __init__(self, a, tag):
        self.stats = a.sb(f"{tag}_stats", [P, 2, GRP, 6])
        self.mv = a.sb(f"{tag}_mv", [P, 2, GRP, 2])
        self.var = a.sb(f"{tag}_var", [P, 2, GRP])
        self.y0 = a.sb(f"{tag}_y0", [P, 2, GRP])
        self.t = a.sb(f"{tag}_newton", [P, 2, GRP])
        self.rs = a.sb(f"{tag}_rs", [P, 2, GRP])
        self.nm = a.sb(f"{tag}_nm", [P, 2, GRP])
        self.var_ready = a.sem(f"{tag}_var_ready")
        self.root_ready = a.sem(f"{tag}_root_ready")

    def statistics(self, nc, vec, row, u):
        for k in range(GRP):
            nc.vector.bn_stats(self.stats[:, u, k, :], row(k)).then_inc(vec.done, vec.one())
        nc.vector.wait_ge(vec.done, vec.count)
        for k in range(GRP):
            nc.vector.bn_aggr(self.mv[:, u, k, :], self.stats[:, u, k, :]).then_inc(vec.done, vec.one())
        nc.vector.wait_ge(vec.done, vec.count)
        nc.vector.tensor_scalar(self.var[:, u, :], self.mv[:, u, :, 1], EPS, None, ALU.add).then_inc(
            self.var_ready, 1)

    def root(self, nc, pool, C, i, u):
        pool.wait_ge(self.var_ready, done(2 * i + u))
        nc.gpsimd.tensor_tensor(self.y0[:, u, :], self.var[:, u, :], C.minus_half[:, :], ALU.pow).then_inc(
            self.root_ready, 1)

    def affine(self, nc, v, vec, i, u):
        y0, var, t, rs, nm = (x[:, u, :] for x in (self.y0, self.var, self.t, self.rs, self.nm))
        v.wait_ge(self.root_ready, done(2 * i + u))
        nc.vector.tensor_tensor(t, y0, y0, ALU.mult).then_inc(vec.done, vec.one())
        nc.vector.wait_ge(vec.done, vec.count)
        nc.vector.tensor_tensor(t, t, var, ALU.mult).then_inc(vec.done, vec.one())
        nc.vector.wait_ge(vec.done, vec.count)
        nc.vector.tensor_scalar(t, t, -0.5, 1.5, ALU.mult, ALU.add).then_inc(vec.done, vec.one())
        nc.vector.wait_ge(vec.done, vec.count)
        nc.vector.tensor_tensor(rs, t, y0, ALU.mult).then_inc(vec.done, vec.one())
        nc.vector.wait_ge(vec.done, vec.count)
        nc.vector.scalar_tensor_tensor(out=nm, in0=self.mv[:, u, :, 0], scalar=-1.0, in1=rs,
                                               op0=ALU.mult, op1=ALU.mult).then_inc(vec.done, vec.one())
        nc.vector.wait_ge(vec.done, vec.count)

    def apply(self, nc, dst, src, u, k):
        return nc.vector.tensor_scalar(dst, src, self.rs[:, u, k:k + 1], self.nm[:, u, k:k + 1], ALU.mult, ALU.add)


class Front:

    def __init__(self, a):
        self.st = a.sb("st", [P, 2, GRP, P])
        self.xnT = a.sb("xnT", [P, 2, TOK])
        self.N = Norm(a, "x")
        self.root_ready = self.N.root_ready
        self.st_ready = a.sem("st_ready")
        self.turned = a.sem("turned")
        self.xnT_ready = a.sem("xnT_ready")

    def open_vector(self, v):
        v.sem_inc(self.N.var_ready, CREDIT)
        v.sem_inc(self.st_ready, CREDIT)

    def statistics(self, nc, v, vec, C, i, u):
        self.N.statistics(nc, vec, lambda k: C.Xt[:, bass.ds(i, 1), GRP * u + k, :], u)

    def root(self, nc, pool, C, i, u):
        self.N.root(nc, pool, C, i, u)

    def normalise(self, nc, v, vec, C, i, u):
        self.N.affine(nc, v, vec, i, u)
        v.wait_ge(self.turned, done(2 * i + u - 2))
        for k in range(GRP):
            ins = self.N.apply(nc, self.st[:, u, k, :], C.Xt[:, bass.ds(i, 1), GRP * u + k, :], u, k)
        ins.then_inc(self.st_ready, 1)

    def turn(self, nc, pe, C, i, u, bank):
        pe.wait_ge(self.st_ready, done(2 * i + u))
        for k in range(GRP):
            ins = nc.tensor.transpose(bank[:, k * P:(k + 1) * P], self.st[:, u, k, :], C.ident)
        ins.then_inc(self.turned, 1)

    def take(self, nc, act, C, i, u, bank):
        act.wait_ge(self.turned, done(2 * i + u))
        nc.scalar.activation(self.xnT[:, u, :], bank, ACT.Identity).then_inc(self.xnT_ready, 1)



HD = 8
HEADS = 16
QUAD = 4
CLAMP = 10000.0


def attention16(nc, C, tag, W, wqT, wkT, wvT, woT, tg, affine):
    units = BODY * QUAD
    scale = HD ** -0.5
    with ExitStack() as ctx:
        a = Alloc(nc, ctx, tag)
        F = Front(a)
        ctxT = a.sb("ctxT", [KV, 2, TOK])
        qT = a.sb("qT", [P, 2, TOK])
        kT = a.sb("kT", [P, 2, TOK])
        kx = a.sb("kx", [P, 2, HEADS, P])
        V = a.sb("V", [P, 2, GRP * HEADS, HD + 1])
        mx = a.sb("mx", [P, 3, QUAD])
        pr = a.sb("pr", [P, 3, QUAD, P])
        pT = a.sb("pT", [P, 2, QUAD, P])
        rden = a.sb("rden", [P, HEADS])
        on = a.sb("on", [P, 2, P])
        oT = a.sb("oT", [P, 2, P])
        bqs = a.sb("bqs", [P, 1])
        res = a.sb("res", [P, P])
        pj = a.ps("pj", [P, 2, 512])
        S = a.ps("S", [P, 2, 512])
        T = a.ps("T", [P, 2, 512])
        O = a.ps("O", [P, 512])
        tail = a.ps("tail", [P, 512])
        Ov = O[:, 0:HEADS * (HD + 1)].rearrange("p (h e) -> p h e", e=HD + 1)
        oTp, outp = tail[:, 0:P], tail[:, P:2 * P]

        ctx_in = [a.sem(f"ctx_in{u}") for u in range(2)]
        once = a.sem("once")
        projected = a.sem("projected")
        q_ready = a.sem("q_ready")
        k_ready = a.sem("k_ready")
        v_ready = a.sem("v_ready")
        spread = a.sem("spread")
        scored = a.sem("scored")
        shifted = a.sem("shifted")
        exped = a.sem("exped")
        flipped = a.sem("flipped")
        pT_ready = a.sem("pT_ready")
        weighed = a.sem("weighed")
        normed = a.sem("normed")
        oT_done = a.sem("oT_done")
        oT_ready = a.sem("oT_ready")
        out_done = a.sem("out_done")
        added = a.sem("added")
        own = a.sem("own")

        block = ctx.enter_context(nc.Block())

        @block.sync
        def _(sp):
            with sp.Fori(0, TURNS) as i:
                for u in range(2):
                    sp.wait_ge(projected, done(6 * i + 3 * u - 4))
                    sp.dma_start(ctxT[:, u, :], C.ctxT_v[:, bass.ds(i, 1), u, :]).then_inc(ctx_in[u], 16)

        @block.gpsimd
        def _(pool):
            pool.sem_inc(F.root_ready, CREDIT)
            pool.sem_inc(spread, CREDIT)
            nc.gpsimd.memset(V[:, :, :, HD:HD + 1], 1.0).then_inc(once, 1)
            with pool.Fori(0, TURNS) as i:
                for u in range(2):
                    F.root(nc, pool, C, i, u)
                for b in range(BODY):
                    u, k = divmod(b, GRP)
                    pool.wait_ge(k_ready, done(2 * i + u))
                    pool.wait_ge(scored, done(units * i + QUAD * (b - 2) + QUAD - 1))
                    for half in range(2):
                        heads = slice(8 * half, 8 * half + 8)
                        nc.gpsimd.tensor_tensor(
                            kx[:, b % 2, heads, :], kT[:, u, k * P:(k + 1) * P].unsqueeze(1).to_broadcast([P, 8, P]),
                            C.mask16[:, heads].unsqueeze(2).to_broadcast([P, 8, P]), ALU.mult).then_inc(spread, 1)

        @block.vector
        def _(v):
            F.open_vector(v)
            v.sem_inc(shifted, CREDIT)
            v.sem_inc(normed, CREDIT)
            v.sem_inc(added, CREDIT)
            vec = Steps(own)
            if affine:
                v.sem_inc(v_ready, CREDIT)
                nc.vector.tensor_scalar(bqs[:, :], W["L1_bq"], scale, None, ALU.mult).then_inc(once, 1)

            def values(i, u):
                v.wait_ge(projected, done(6 * i + 3 * u + 2))
                nc.vector.tensor_tensor(
                    V[:, u, :, 0:HD].rearrange("p (b h) e -> p b h e", b=GRP),
                    pj[:, u, :].rearrange("p (b h e) -> p b h e", b=GRP, e=HD),
                    C.rows["L1_bv"].rearrange("p (h e) -> p h e", e=HD).unsqueeze(1)
                    .to_broadcast([P, GRP, HEADS, HD]), ALU.add).then_inc(v_ready, 1)

            def normalise(i, b):
                v.wait_ge(weighed, done(units * i + QUAD * b + QUAD - 1))
                nc.vector.reciprocal(rden[:, :], Ov[:, :, HD]).then_inc(vec.done, vec.one())
                v.wait_ge(oT_done, done(BODY * i + b - 2))
                nc.vector.wait_ge(vec.done, vec.count)
                nc.vector.tensor_tensor(
                    on[:, b % 2, :].rearrange("p (h e) -> p h e", e=HD), Ov[:, :, 0:HD],
                    rden[:, :].unsqueeze(2).to_broadcast([P, HEADS, HD]), ALU.mult).then_inc(normed, 1)

            def shift(i, s):
                n = units * i + s
                v.wait_ge(flipped, done(n - 3))
                v.wait_ge(scored, done(n))
                bank = S[:, s % 2, :].rearrange("p (j t) -> p j t", j=QUAD)
                if affine:
                    nc.vector.tensor_scalar(pr[:, s % 3, :, :], bank, CLAMP, -CLAMP, ALU.min, ALU.max).then_inc(vec.done, vec.one())
                    nc.vector.wait_ge(vec.done, vec.count)
                    bank = pr[:, s % 3, :, :]
                nc.vector.tensor_reduce(mx[:, s % 3, :], bank, AX.X, ALU.max).then_inc(vec.done, vec.one())
                nc.vector.wait_ge(vec.done, vec.count)
                nc.vector.tensor_tensor(pr[:, s % 3, :, :], bank,
                                        mx[:, s % 3, :].unsqueeze(2).to_broadcast([P, QUAD, P]),
                                        ALU.subtract).then_inc(shifted, 1)

            def residual(i, b):
                v.wait_ge(out_done, done(BODY * i + b))
                src = outp
                if affine:
                    nc.vector.tensor_tensor(res[:, :], outp, C.rows["L1_bo"], ALU.add).then_inc(vec.done, vec.one())
                    nc.vector.wait_ge(vec.done, vec.count)
                    src = res[:, :]
                x = C.Xt[:, bass.ds(i, 1), b, :]
                nc.vector.scalar_tensor_tensor(out=x, in0=src, scalar=tg, in1=x, op0=ALU.mult,
                                               op1=ALU.add).then_inc(added, 1)

            with v.Fori(0, TURNS) as i:
                for u in range(2):
                    F.statistics(nc, v, vec, C, i, u)
                for u in range(2):
                    F.normalise(nc, v, vec, C, i, u)
                if affine:
                    values(i, 0)
                for s in range(units + 9):
                    if s >= 8 and s % QUAD == 0 and s // QUAD - 2 < BODY:
                        normalise(i, s // QUAD - 2)
                    if s == 10 and affine:
                        values(i, 1)
                    if s < units:
                        shift(i, s)
                    if s >= 12 and s % QUAD == 0:
                        residual(i, s // QUAD - 3)
                v.wait_ge(added, done(BODY * i + BODY - 1))
                nc.vector.memset(C.carrier[:, :], 0.0)
                v.wait_ge(vec.done, vec.count)
                v.sem_clear(vec.done)
                vec.restart()

        @block.scalar
        def _(act):
            act.sem_inc(F.xnT_ready, CREDIT)
            act.sem_inc(q_ready, CREDIT)
            act.sem_inc(k_ready, CREDIT)
            act.sem_inc(exped, CREDIT)
            act.sem_inc(pT_ready, CREDIT)
            act.sem_inc(oT_ready, CREDIT)
            if affine:
                act.wait_ge(once, 2)
            else:
                act.sem_inc(v_ready, CREDIT)
                act.wait_ge(once, 1)

            def project(i, u):
                act.wait_ge(projected, done(6 * i + 3 * u))
                nc.scalar.activation(qT[:, u, :], pj[:, u, :], ACT.Identity, scale=scale,
                                     bias=bqs[:, 0:1] if affine else 0.0).then_inc(q_ready, 1)
                act.wait_ge(spread, done(2 * (BODY * i + GRP * u + 3 - BODY) + 1))
                act.wait_ge(projected, done(6 * i + 3 * u + 1))
                nc.scalar.activation(kT[:, u, :], pj[:, 1 - u, :], ACT.Identity,
                                     bias=W["L1_bk"] if affine else 0.0).then_inc(k_ready, 1)
                if not affine:
                    act.wait_ge(projected, done(6 * i + 3 * u + 2))
                    nc.scalar.activation(V[:, u, :, 0:HD], pj[:, u, :].rearrange("p (n e) -> p n e", e=HD),
                                         ACT.Identity).then_inc(v_ready, 1)

            with act.Fori(0, TURNS) as i:
                for u in range(2):
                    F.take(nc, act, C, i, u, pj[:, u, :])
                project(i, 0)
                for s in range(units + 7):
                    n = units * i + s
                    if s == 10:
                        project(i, 1)
                    if s < units:
                        act.wait_ge(shifted, done(n))
                        nc.scalar.activation(pr[:, s % 3, :, :], pr[:, s % 3, :, :], ACT.Exp).then_inc(exped, 1)
                    if 2 <= s < units + 2:
                        m = s - 2
                        act.wait_ge(weighed, done(n - 4))
                        act.wait_ge(flipped, done(n - 2))
                        nc.scalar.activation(pT[:, m % 2, :, :], T[:, m % 2, :].rearrange("p (j t) -> p j t", j=QUAD),
                                             ACT.Identity).then_inc(pT_ready, 1)
                    if s >= 10 and s % QUAD == 2:
                        b = (s - 10) // QUAD
                        act.wait_ge(out_done, done(BODY * i + b - 2))
                        act.wait_ge(oT_done, done(BODY * i + b))
                        nc.scalar.activation(oT[:, b % 2, :], oTp, ACT.Identity).then_inc(oT_ready, 1)

        @block.tensor
        def _(pe):
            pe.sem_inc(F.turned, CREDIT)
            for x in (projected, scored, flipped, weighed, oT_done, out_done):
                pe.sem_inc(x, CREDIT)
            pe.wait_ge(once, 2 if affine else 1)

            def project(i, u):
                g = 2 * i + u
                pe.wait_ge(F.xnT_ready, done(2 * i + 1))
                if u:
                    pe.wait_ge(k_ready, done(2 * i))
                nc.tensor.matmul(pj[:, u, :], wqT, F.xnT[:, u, :], start=True, stop=True).then_inc(projected, 1)
                pe.wait_ge(ctx_in[u], 16 * i + 16)
                if u:
                    pe.wait_ge(v_ready, done(2 * i))
                nc.tensor.matmul(pj[:, 1 - u, :], wkT, ctxT[:, u, :], start=True, stop=True).then_inc(projected, 1)
                pe.wait_ge(q_ready, done(g))
                for k in range(GRP):
                    ins = nc.tensor.matmul(pj[:, u, k * P:(k + 1) * P], ctxT[:, u, k * P:(k + 1) * P], wvT,
                                           start=True, stop=True)
                ins.then_inc(projected, 1)

            with pe.Fori(0, TURNS) as i:
                pe.wait_ge(k_ready, done(2 * i - 1))
                F.turn(nc, pe, C, i, 0, pj[:, 0, :])
                pe.wait_ge(v_ready, done(2 * i - 1))
                F.turn(nc, pe, C, i, 1, pj[:, 1, :])
                project(i, 0)
                for s in range(units + 8):
                    n = units * i + s
                    if s == 10:
                        project(i, 1)
                    if s < units:
                        b, r = divmod(s, QUAD)
                        u, k = divmod(b, GRP)
                        if r == 0:
                            pe.wait_ge(q_ready, done(2 * i + u))
                        if r % 2 == 0:
                            pe.wait_ge(spread, done(2 * (BODY * i + b) + r // 2))
                        pe.wait_ge(shifted, done(n - 2))
                        nc.tensor.matmul(S[:, s % 2, :], qT[:, u, k * P:(k + 1) * P],
                                         kx[:, b % 2, QUAD * r:QUAD * r + QUAD, :],
                                         start=True, stop=True).then_inc(scored, 1)
                    if 2 <= s < units + 2:
                        m = s - 2
                        pe.wait_ge(pT_ready, done(n - 4))
                        pe.wait_ge(exped, done(n - 2))
                        for j in range(QUAD):
                            ins = nc.tensor.transpose(T[:, m % 2, j * P:(j + 1) * P], pr[:, m % 3, j, :], C.ident)
                        ins.then_inc(flipped, 1)
                    if 4 <= s < units + 4:
                        m = s - 4
                        b, r = divmod(m, QUAD)
                        u, k = divmod(b, GRP)
                        if r == 0:
                            pe.wait_ge(v_ready, done(2 * i + u))
                            pe.wait_ge(normed, done(BODY * i + b - 1))
                        pe.wait_ge(pT_ready, done(n - 4))
                        for j in range(QUAD):
                            h = QUAD * r + j
                            ins = nc.tensor.matmul(Ov[:, h, :], pT[:, m % 2, j, :], V[:, u, k * HEADS + h, :],
                                                   start=True, stop=True)
                        ins.then_inc(weighed, 1)
                    if s >= 9 and s % QUAD == 1 and (s - 9) // QUAD < BODY:
                        b = (s - 9) // QUAD
                        pe.wait_ge(added, done(BODY * i + b - 1))
                        pe.wait_ge(normed, done(BODY * i + b))
                        nc.tensor.transpose(oTp, on[:, b % 2, :], C.ident).then_inc(oT_done, 1)
                    if s >= 11 and s % QUAD == 3:
                        b = (s - 11) // QUAD
                        pe.wait_ge(oT_ready, done(BODY * i + b))
                        nc.tensor.matmul(outp, oT[:, b % 2, :], woT, start=True, stop=True).then_inc(out_done, 1)



E8 = 8


class Router:

    def __init__(self, a, n):
        self.n = n
        self.lg = a.sb("lg", [P, BODY, E8])
        self.top = a.sb("top", [P, BODY, 8])
        self.idx = a.sb("idx", [P, BODY, 8], U32)
        self.idf = a.sb("idf", [P, BODY, 2])
        self.ex = a.sb("ex", [P, BODY, E8])
        self.m0 = a.sb("m0", [P, BODY, E8])
        self.m1 = a.sb("m1", [P, BODY, E8])
        self.sum = a.sb("sum", [P, BODY])
        self.rcp = a.sb("rcp", [P, BODY])
        self.shift_done = a.sem("rt_shift")
        self.exp_done = a.sem("rt_exp")

    def choose(self, nc, v, vec, C, i):
        for b in range(BODY):
            nc.vector.max(self.top[:, b, :], self.lg[:, b, :]).then_inc(vec.done, vec.one())
        nc.vector.wait_ge(vec.done, vec.count)
        for b in range(BODY):
            nc.vector.max_index(self.idx[:, b, :], self.top[:, b, :], self.lg[:, b, :]).then_inc(vec.done, vec.one())
        nc.vector.tensor_tensor(self.ex[:, :, :], self.lg[:, :, :], self.top[:, :, 0:1].to_broadcast([P, BODY, E8]),
                                ALU.subtract).then_inc(self.shift_done, 1)
        nc.vector.wait_ge(vec.done, vec.count)
        nc.vector.tensor_copy(self.idf[:, :, :], self.idx[:, :, 0:2]).then_inc(vec.done, vec.one())
        nc.vector.wait_ge(vec.done, vec.count)
        for m, j in ((self.m0, 0), (self.m1, 1)):
            nc.vector.tensor_tensor(m[:, :, :], C.iota8.unsqueeze(1).to_broadcast([P, BODY, E8]),
                                            self.idf[:, :, j:j + 1].to_broadcast([P, BODY, E8]), ALU.is_equal).then_inc(vec.done, vec.one())
        nc.vector.wait_ge(vec.done, vec.count)
        nc.vector.tensor_tensor(self.m0[:, :, :], self.m0[:, :, :], self.m1[:, :, :], ALU.add).then_inc(vec.done, vec.one())

    def exponentials(self, nc, act, i):
        act.wait_ge(self.shift_done, done(i))
        nc.scalar.activation(self.ex[:, :, :], self.ex[:, :, :], ACT.Exp).then_inc(self.exp_done, 1)

    def probabilities(self, nc, v, vec, i):
        v.wait_ge(self.exp_done, done(i))
        nc.vector.tensor_reduce(self.sum[:, :], self.ex[:, :, :], AX.X, ALU.add).then_inc(vec.done, vec.one())
        nc.vector.wait_ge(vec.done, vec.count)
        nc.vector.reciprocal(self.rcp[:, :], self.sum[:, :]).then_inc(vec.done, vec.one())
        nc.vector.tensor_tensor(self.m1[:, :, :], self.ex[:, :, :], self.m0[:, :, :], ALU.mult).then_inc(vec.done, vec.one())
        nc.vector.wait_ge(vec.done, vec.count)


def gated_experts(nc, C, tag, W, nf, tg):
    with ExitStack() as ctx:
        a = Alloc(nc, ctx, tag)
        F = Front(a)
        R = Router(a, BODY)
        wt = a.sb("wt", [P, BODY, E8 + 1])
        sg = a.sb("sg", [P, 2, TOK])
        aT = a.sb("aT", [P, 2, max(nf, 2), TOK])
        tr = a.ps("tr", [P, 512])
        lgp = a.ps("lgp", [P, 512])
        G = a.ps("G", [P, 2, 512])
        U = a.ps("U", [P, 2, 512])
        Y = a.ps("Y", [P, 2, 512])
        gate = W[f"{tag}_gate"].rearrange("p (e c f) -> p e c f", e=E8, c=nf)
        up = W[f"{tag}_up"].rearrange("p (e c f) -> p e c f", e=E8, c=nf)
        down = W[f"{tag}_down"].rearrange("p (e c d) -> p e c d", e=E8, c=nf)
        sgate, sup, sdown = (W[f"{tag}_s{x}"].rearrange("p (c f) -> p c f", c=2) for x in ("gate", "up", "down"))
        router = W[f"{tag}_router"]

        chunks = [(0, c) for c in range(2)] + [(e + 1, c) for e in range(E8) for c in range(nf)]
        N = len(chunks)
        last = {t: n for n, (t, _) in enumerate(chunks)}
        units = E8 + 1

        logits = a.sem("logits")
        lg_read = a.sem("lg_read")
        opened = a.sem("opened")
        gated = a.sem("gated")
        a_ready = a.sem("a_ready")
        closed = a.sem("closed")
        added = a.sem("added")
        once = a.sem("once")
        own = a.sem("own")
        block = ctx.enter_context(nc.Block())

        @block.gpsimd
        def _(pool):
            pool.sem_inc(F.root_ready, CREDIT)
            with pool.Fori(0, TURNS) as i:
                for u in range(2):
                    F.root(nc, pool, C, i, u)

        @block.vector
        def _(v):
            F.open_vector(v)
            for x in (R.shift_done, lg_read, a_ready, added):
                v.sem_inc(x, CREDIT)
            vec = Steps(own)
            nc.vector.tensor_scalar(wt[:, :, E8], wt_ones(C), tg, None, ALU.mult).then_inc(once, 1)
            v.wait_ge(once, 1)

            def activate(i, u, n):
                t, c = chunks[n]
                m = N * (2 * i + u) + n
                v.wait_ge(closed, done(units * (2 * i + u) + t - 2))
                v.wait_ge(gated, done(m))
                nc.vector.tensor_tensor(aT[:, (t + u) % 2, c, :], sg[:, n % 2, :], U[:, n % 2, :],
                                        ALU.mult).then_inc(a_ready, 1)

            def add(i, u, t):
                v.wait_ge(closed, done(units * (2 * i + u) + t))
                v.wait_ge(added, done(units * (2 * i + u) + t - 1))
                for k in range(GRP):
                    b = GRP * u + k
                    x = C.Xt[:, bass.ds(i, 1), b, :]
                    ins = nc.vector.scalar_tensor_tensor(
                        out=x, in0=Y[:, (t + u) % 2, k * P:(k + 1) * P], scalar=wt[:, b, (t + E8) % 9:(t + E8) % 9 + 1],
                        in1=x, op0=ALU.mult, op1=ALU.add)
                ins.then_inc(added, 1)

            with v.Fori(0, TURNS) as i:
                for u in range(2):
                    F.statistics(nc, v, vec, C, i, u)
                for u in range(2):
                    F.normalise(nc, v, vec, C, i, u)
                for n in range(2):
                    activate(i, 0, n)
                v.wait_ge(logits, done(i))
                nc.vector.tensor_copy(R.lg[:, :, :], lgp[:, 0:BODY * E8].rearrange("p (b e) -> p b e", e=E8)).then_inc(
                    lg_read, 1)
                v.wait_ge(lg_read, done(i))
                nc.vector.memset(C.carrier[:, :], 0.0)
                R.choose(nc, v, vec, C, i)
                R.probabilities(nc, v, vec, i)
                nc.vector.tensor_scalar(R.rcp[:, :], R.rcp[:, :], tg, None, ALU.mult).then_inc(vec.done, vec.one())
                nc.vector.wait_ge(vec.done, vec.count)
                nc.vector.tensor_tensor(wt[:, :, 0:E8], R.m1[:, :, :],
                                                R.rcp[:, :].unsqueeze(2).to_broadcast([P, BODY, E8]), ALU.mult).then_inc(vec.done, vec.one())
                nc.vector.wait_ge(vec.done, vec.count)
                for u in range(2):
                    due = 0
                    for n in range(2 if u == 0 else 0, N):
                        activate(i, u, n)
                        while due < units and last[due] + LAG_ADD <= n:
                            add(i, u, due)
                            due += 1
                    for t in range(due, units):
                        add(i, u, t)
                v.wait_ge(added, done(units * (2 * i + 2) - 1))
                nc.vector.memset(C.carrier[:, :], 0.0)
                v.wait_ge(vec.done, vec.count)
                v.sem_clear(vec.done)
                vec.restart()

        @block.scalar
        def _(act):
            for x in (F.xnT_ready, R.exp_done, gated):
                act.sem_inc(x, CREDIT)

            def silu(i, u, n):
                m = N * (2 * i + u) + n
                act.wait_ge(a_ready, done(m - 2))
                act.wait_ge(opened, done(m))
                nc.scalar.activation(sg[:, n % 2, :], G[:, n % 2, :], ACT.Silu).then_inc(gated, 1)

            with act.Fori(0, TURNS) as i:
                for u in range(2):
                    F.take(nc, act, C, i, u, tr[:, :])
                silu(i, 0, 0)
                silu(i, 0, 1)
                R.exponentials(nc, act, i)
                for u in range(2):
                    for n in range(2 if u == 0 else 0, N):
                        silu(i, u, n)

        @block.tensor
        def _(pe):
            for x in (F.turned, logits, opened, closed):
                pe.sem_inc(x, CREDIT)

            def open_chunk(i, u, n):
                t, c = chunks[n]
                m = N * (2 * i + u) + n
                g_w, u_w = (sgate[:, c, :], sup[:, c, :]) if t == 0 else (gate[:, t - 1, c, :], up[:, t - 1, c, :])
                pe.wait_ge(a_ready, done(m - 2))
                nc.tensor.matmul(G[:, n % 2, :], g_w, F.xnT[:, u, :], start=True, stop=True)
                nc.tensor.matmul(U[:, n % 2, :], u_w, F.xnT[:, u, :], start=True, stop=True).then_inc(opened, 1)

            def close(i, u, t):
                pe.wait_ge(a_ready, done(N * (2 * i + u) + last[t]))
                pe.wait_ge(added, done(units * (2 * i + u) + t - 2))
                nchunk = 2 if t == 0 else nf
                for k in range(GRP):
                    for c in range(nchunk):
                        d_w = sdown[:, c, :] if t == 0 else down[:, t - 1, c, :]
                        ins = nc.tensor.matmul(Y[:, (t + u) % 2, k * P:(k + 1) * P],
                                               aT[:, (t + u) % 2, c, k * P:(k + 1) * P], d_w,
                                               start=(c == 0), stop=(c == nchunk - 1))
                ins.then_inc(closed, 1)

            with pe.Fori(0, TURNS) as i:
                pe.wait_ge(F.xnT_ready, done(2 * i - 1))
                F.turn(nc, pe, C, i, 0, tr)
                pe.wait_ge(F.xnT_ready, done(2 * i))
                F.turn(nc, pe, C, i, 1, tr)
                open_chunk(i, 0, 0)
                open_chunk(i, 0, 1)
                pe.wait_ge(F.xnT_ready, done(2 * i + 1))
                pe.wait_ge(lg_read, done(i - 1))
                for b in range(BODY):
                    u, k = divmod(b, GRP)
                    ins = nc.tensor.matmul(lgp[:, b * E8:(b + 1) * E8], F.xnT[:, u, k * P:(k + 1) * P], router,
                                           start=True, stop=True)
                ins.then_inc(logits, 1)
                for u in range(2):
                    due = 0
                    for n in range(2 if u == 0 else 0, N):
                        open_chunk(i, u, n)
                        while due < units and last[due] + LAG_CLOSE <= n:
                            close(i, u, due)
                            due += 1
                    for t in range(due, units):
                        close(i, u, t)


LAG_CLOSE = 2
LAG_ADD = 3


def wt_ones(C):
    return C.ones8



H2, D2 = 16, 64
INNER = H2 * D2
NCH = INNER // P
RANK = 32
IPA = 4
ORG = P - IPA


def merge_lora(nc, C, x2, w96, x3, dram):
    with ExitStack() as ctx:
        a = Alloc(nc, ctx, "merge")
        w32 = Packed(a.sb("w32", [RANK, N32]), PLACE32)
        w4 = Packed(a.sb("w4", [4, N4]), PLACE4)
        ctx_ipa = a.sb("ctx_ipa", [KV, NB, IPA])
        v_ipa = a.sb("v_ipa", [P, INNER])
        al = a.sb("al", [P, 4])
        bank = a.ps("bank", [P, 2, 512])
        loaded, scaled, done = a.sem("loaded"), a.sem("scaled"), a.sem("done")
        product = a.sem("product")
        kept = a.sem("kept")
        pieces = []
        for half in range(2):
            cols = slice(512 * half, 512 * half + 512)
            pieces.append((w32["q_down"], w32["q_up"][:, cols], 512, ("add", x2["L2_q"][:, cols], 0)))
            pieces.append((w32["k_down"], w32["k_up"][:, cols], 512, ("add", w96["L2_k"][:, cols], 1)))
            pieces.append((w32["v_down"], w32["v_up"][:, cols], 512, ("add", w96["L2_v"][:, cols], 2)))
        for half in range(2):
            cols = slice(512 * half, 512 * half + 512)
            pieces.append((ctx_ipa[:, :, :].rearrange("c b t -> c (b t)"), w96["L2_vi"][:, cols], 512,
                           ("copy", v_ipa[:, cols], 0)))
        for c in range(NCH):
            pieces.append((w32["o_down"][:, c * P:(c + 1) * P], w32["o_up"], P,
                           ("add", x2["L2_o"][:, c * P:(c + 1) * P], 3)))
        for e in range(4):
            pieces.append((w4["A"][:, e * P:(e + 1) * P], w4["B"][:, e * 512:(e + 1) * 512], 512,
                           ("lora", C.f2["We"][:, e * 512:(e + 1) * 512], 0)))
        block = ctx.enter_context(nc.Block())

        @block.sync
        def _(sp):
            sp.dma_start(x3.tile, dram["sec_x3"]).then_inc(C.last_landed, 16)
            sp.dma_start(w32.tile[:, :], dram["w32"]).then_inc(loaded, 16)
            sp.dma_start(w4.tile[:, :], dram["w4"]).then_inc(loaded, 16)
            sp.dma_start(ctx_ipa[:, :, :], dram["ctxT"].rearrange("c (b t) -> c b t", b=NB)[:, :, ORG:P]).then_inc(
                loaded, 16)
            sp.wait_ge(loaded, 48)
            sp.wait_ge(done, 1)
            sp.dma_start(C.v_ipa_dram, v_ipa[:, :]).then_inc(kept, 16)
            sp.wait_ge(kept, 16)

        @block.tensor
        def _(pe):
            pe.wait_ge(loaded, 48)
            for n, (lhsT, rhs, w, _) in enumerate(pieces):
                if n >= 2:
                    pe.wait_ge(scaled, n)
                m = lhsT.shape[1]
                nc.tensor.matmul(bank[0:m, n % 2, 0:w], lhsT, rhs, start=True, stop=True).then_inc(product, 1)

        @block.vector
        def _(v):
            nc.vector.tensor_scalar(al[:, :], C.rows["alpha"], 1.0 / RANK, None, ALU.mult).then_inc(scaled, 1)
            v.wait_ge(scaled, 1)
            v.wait_ge(C.late_landed, 16 * LATE)
            for n, (lhsT, _, w, (what, dst, j)) in enumerate(pieces):
                m = lhsT.shape[1]
                v.wait_ge(product, n + 1)
                src = bank[0:m, n % 2, 0:w]
                if what == "copy":
                    ins = nc.vector.tensor_copy(dst, src)
                elif what == "lora":
                    ins = nc.vector.tensor_tensor(dst, src, C.f2["Wi"], ALU.add)
                else:
                    ins = nc.vector.scalar_tensor_tensor(out=dst, in0=src, scalar=al[0:m, j:j + 1], in1=dst,
                                                         op0=ALU.mult, op1=ALU.add)
                ins.then_inc(scaled, 1)
            v.wait_ge(scaled, len(pieces) + 1)
            nc.vector.tensor_scalar(x2["L2_q"], x2["L2_q"], D2 ** -0.5, None, ALU.mult).then_inc(done, 1)


def attention_ipa(nc, C, x2, w96, tg):
    units = BODY * 4
    U = GRP * 4
    NP = 24
    with ExitStack() as ctx:
        a = Alloc(nc, ctx, "L2")
        F = Front(a)
        ctxT = a.sb("ctxT", [KV, TOK])
        qT = a.sb("qT", [P, NCH, TOK])
        kT = a.sb("kT", [P, NCH, TOK])
        V = a.sb("V", [P, GRP, INNER])
        pr = a.sb("pr", [P, 4, 4, P])
        pT = a.sb("pT", [P, 2, 4, P])
        oT = a.sb("oT", [P, NCH, P])
        mx = a.sb("mx", [P, 4, 2, 4])
        sm = a.sb("sm", [P, 4, 2, 4])
        rc = a.sb("rc", [P, 4, 2, 4])
        res = a.sb("res", [P, P])
        pj = a.ps("pj", [P, 2, 512])
        S = a.ps("S", [P, 2, 512])
        T = a.ps("T", [P, 2, 512])
        O = a.ps("O", [P, 2, 512])
        outp = pj[:, 1, 0:P]

        ctx_in = [a.sem(f"ctx_in{u}") for u in range(2)]
        ipa_in = [a.sem(f"ipa_in{u}") for u in range(2)]
        projected = a.sem("projected")
        kept_a = a.sem("kept_a")
        kept_v = a.sem("kept_v")
        scored = a.sem("scored")
        shifted = a.sem("shifted")
        exped = a.sem("exped")
        summed = a.sem("summed")
        scaled = a.sem("scaled")
        flipped = a.sem("flipped")
        pT_ready = a.sem("pT_ready")
        weighed = a.sem("weighed")
        oT_ready = a.sem("oT_ready")
        out_done = a.sem("out_done")
        added = a.sem("added")
        own = a.sem("own")
        block = ctx.enter_context(nc.Block())
        parts = ((0, slice(0, ORG)), (1, slice(ORG, P)))

        @block.sync
        def _(sp):
            with sp.Fori(0, TURNS) as i:
                for u in range(2):
                    g = 2 * i + u
                    sp.wait_ge(projected, done(NP * g - 1))
                    sp.dma_start(ctxT[:, :], C.ctxT_v[:, bass.ds(i, 1), u, :]).then_inc(ctx_in[u], 16)
                    sp.wait_ge(weighed, done(U * g - 1))
                    sp.dma_start(V[ORG:P, :, :], C.v_ipa_v[:, bass.ds(i, 1), u, :, :]).then_inc(ipa_in[u], 16)

        @block.gpsimd
        def _(pool):
            pool.sem_inc(F.root_ready, CREDIT)
            pool.sem_inc(scaled, CREDIT)
            with pool.Fori(0, TURNS) as i:
                for u in range(2):
                    F.root(nc, pool, C, i, u)
                for s in range(units):
                    n = units * i + s
                    pool.wait_ge(summed, done(n))
                    for j, cols in parts:
                        w = cols.stop - cols.start
                        ins = nc.gpsimd.tensor_tensor(pr[:, s % 4, :, cols], pr[:, s % 4, :, cols],
                                                      rc[:, s % 4, j, :].unsqueeze(2).to_broadcast([P, 4, w]), ALU.mult)
                    ins.then_inc(scaled, 1)

        def destination(n):
            if n < 16:
                return (qT if n < 8 else kT)[:, n % 8, :], P
            k, half = divmod(n - 16, 2)
            return V[0:ORG, k, 512 * half:512 * half + 512], ORG

        @block.vector
        def _(v):
            F.open_vector(v)
            for x in (kept_v, shifted, summed, added):
                v.sem_inc(x, CREDIT)
            vec = Steps(own)

            def shift(i, s):
                n = units * i + s
                v.wait_ge(flipped, done(n - 4))
                v.wait_ge(scored, done(n))
                bank = S[:, s % 2, :].rearrange("p (j t) -> p j t", j=4)
                for j, cols in parts:
                    nc.vector.tensor_reduce(mx[:, s % 4, j, :], bank[:, :, cols], AX.X, ALU.max).then_inc(vec.done, vec.one())
                nc.vector.wait_ge(vec.done, vec.count)
                for j, cols in parts:
                    w = cols.stop - cols.start
                    ins = nc.vector.tensor_tensor(pr[:, s % 4, :, cols], bank[:, :, cols],
                                                  mx[:, s % 4, j, :].unsqueeze(2).to_broadcast([P, 4, w]), ALU.subtract)
                ins.then_inc(shifted, 1)

            def total(i, s):
                v.wait_ge(exped, done(units * i + s))
                for j, cols in parts:
                    nc.vector.tensor_reduce(sm[:, s % 4, j, :], pr[:, s % 4, :, cols], AX.X, ALU.add).then_inc(vec.done, vec.one())
                nc.vector.wait_ge(vec.done, vec.count)
                nc.vector.reciprocal(rc[:, s % 4, :, :], sm[:, s % 4, :, :]).then_inc(summed, 1)

            def residual(i, b):
                v.wait_ge(out_done, done(BODY * i + b))
                nc.vector.tensor_tensor(res[:, :], outp, C.rows["L2_bo"], ALU.add).then_inc(vec.done, vec.one())
                nc.vector.wait_ge(vec.done, vec.count)
                x = C.Xt[:, bass.ds(i, 1), b, :]
                nc.vector.scalar_tensor_tensor(out=x, in0=res[:, :], scalar=tg, in1=x, op0=ALU.mult,
                                               op1=ALU.add).then_inc(added, 1)

            with v.Fori(0, TURNS) as i:
                for u in range(2):
                    F.statistics(nc, v, vec, C, i, u)
                for u in range(2):
                    F.normalise(nc, v, vec, C, i, u)
                for u in range(2):
                    for n in range(1, NP, 2):
                        dst, rows = destination(n)
                        v.wait_ge(projected, done(NP * (2 * i + u) + n))
                        nc.vector.tensor_copy(dst, pj[0:rows, 1, :]).then_inc(kept_v, 1)
                    for s in range(U + 8):
                        if s < U:
                            shift(i, U * u + s)
                        if 1 <= s < U + 1:
                            total(i, U * u + s - 1)
                        if s >= 11 and s % 4 == 3:
                            residual(i, GRP * u + (s - 11) // 4)
                v.wait_ge(added, done(BODY * i + BODY - 1))
                nc.vector.memset(C.carrier[:, :], 0.0)
                v.wait_ge(vec.done, vec.count)
                v.sem_clear(vec.done)
                vec.restart()

        @block.scalar
        def _(act):
            for x in (F.xnT_ready, kept_a, exped, pT_ready, oT_ready):
                act.sem_inc(x, CREDIT)

            with act.Fori(0, TURNS) as i:
                for u in range(2):
                    F.take(nc, act, C, i, u, pj[:, 0, :])
                for u in range(2):
                    for n in range(0, NP, 2):
                        dst, rows = destination(n)
                        act.wait_ge(projected, done(NP * (2 * i + u) + n))
                        nc.scalar.activation(dst, pj[0:rows, 0, :], ACT.Identity).then_inc(kept_a, 1)
                    for s in range(U + 7):
                        n = units * i + U * u + s
                        if s < U:
                            act.wait_ge(shifted, done(n))
                            nc.scalar.activation(pr[:, s % 4, :, :], pr[:, s % 4, :, :], ACT.Exp).then_inc(exped, 1)
                        if 3 <= s < U + 3:
                            m = s - 3
                            act.wait_ge(weighed, done(n - 5))
                            act.wait_ge(flipped, done(n - 3))
                            nc.scalar.activation(pT[:, m % 2, :, :],
                                                 T[:, m % 2, :].rearrange("p (j t) -> p j t", j=4),
                                                 ACT.Identity).then_inc(pT_ready, 1)
                        if s >= 6 and s % 2 == 0:
                            m = s - 5
                            b, half = divmod(m // 2, 2)
                            if b < GRP:
                                act.wait_ge(out_done, done(BODY * i + GRP * u + b - 1))
                                act.wait_ge(weighed, done(units * i + U * u + m))
                                nc.scalar.activation(oT[:, 4 * half:4 * half + 4, :],
                                                     O[:, half, :].rearrange("p (c t) -> p c t", c=4),
                                                     ACT.Identity).then_inc(oT_ready, 1)

        @block.tensor
        def _(pe):
            for x in (F.turned, projected, scored, flipped, weighed, out_done):
                pe.sem_inc(x, CREDIT)

            def project(i, u, n):
                g = 2 * i + u
                if n % 2 == 0:
                    pe.wait_ge(kept_a, done(12 * g + n // 2 - 1))
                else:
                    pe.wait_ge(kept_v, done(12 * g + n // 2 - 1))
                bank = pj[:, n % 2, :]
                c = n % 8
                if n < 8:
                    ins = nc.tensor.matmul(bank, x2["L2_q"][:, c * P:(c + 1) * P], F.xnT[:, u, :], start=True, stop=True)
                elif n < 16:
                    bt = bank.rearrange("p (b t) -> p b t", b=GRP)
                    ct = ctxT[:, :].rearrange("c (b t) -> c b t", b=GRP)
                    for w, (_, cols) in (("L2_k", parts[0]), ("L2_ki", parts[1])):
                        ins = nc.tensor.matmul(bt[:, :, cols], w96[w][:, c * P:(c + 1) * P], ct[:, :, cols],
                                               start=True, stop=True)
                else:
                    k, half = divmod(n - 16, 2)
                    ins = nc.tensor.matmul(bank, ctxT[:, k * P:(k + 1) * P],
                                           w96["L2_v"][:, 512 * half:512 * half + 512], start=True, stop=True)
                ins.then_inc(projected, 1)

            with pe.Fori(0, TURNS) as i:
                pe.wait_ge(kept_a, done(24 * i - 1))
                F.turn(nc, pe, C, i, 0, pj[:, 0, :])
                pe.wait_ge(F.xnT_ready, done(2 * i))
                F.turn(nc, pe, C, i, 1, pj[:, 0, :])
                for u in range(2):
                    pe.wait_ge(F.xnT_ready, done(2 * i + 1))
                    pe.wait_ge(added, done(BODY * i + GRP * u - 1))
                    for n in range(NP):
                        if n == 8:
                            pe.wait_ge(ctx_in[u], 16 * i + 16)
                        project(i, u, n)
                    pe.wait_ge(kept_a, done(12 * (2 * i + u) + 11))
                    pe.wait_ge(kept_v, done(12 * (2 * i + u) + 11))
                    for s in range(U + 8):
                        n = units * i + U * u + s
                        if s < U:
                            k, q = divmod(s, 4)
                            p, half = q % 2, q // 2
                            rows = slice(64 * p, 64 * p + 64)
                            pe.wait_ge(shifted, done(n - 2))
                            for j in range(4):
                                c = 4 * half + j
                                ins = nc.tensor.matmul(S[:, s % 2, j * P:(j + 1) * P], qT[rows, c, k * P:(k + 1) * P],
                                                       kT[rows, c, k * P:(k + 1) * P], start=True, stop=True)
                            ins.then_inc(scored, 1)
                        if 3 <= s < U + 3:
                            m = s - 3
                            pe.wait_ge(pT_ready, done(n - 5))
                            pe.wait_ge(scaled, done(n - 3))
                            for j in range(4):
                                ins = nc.tensor.transpose(T[:, m % 2, j * P:(j + 1) * P], pr[:, m % 4, j, :], C.ident)
                            ins.then_inc(flipped, 1)
                        if 5 <= s < U + 5:
                            m = s - 5
                            k, q = divmod(m, 4)
                            p, half = q % 2, q // 2
                            if m == 0:
                                pe.wait_ge(ipa_in[u], 16 * i + 16)
                            pe.wait_ge(oT_ready, done(2 * (BODY * i + GRP * u + k - 1) + half))
                            pe.wait_ge(pT_ready, done(n - 5))
                            for j in range(4):
                                h = 8 * half + 2 * j + p
                                ins = nc.tensor.matmul(O[64 * p:64 * p + 64, half, j * P:(j + 1) * P],
                                                       V[:, k, D2 * h:D2 * h + D2], pT[:, m % 2, j, :],
                                                       start=True, stop=True)
                            ins.then_inc(weighed, 1)
                        if s >= 10 and s % 4 == 2:
                            b = (s - 10) // 4
                            pe.wait_ge(added, done(BODY * i + GRP * u + b - 1))
                            pe.wait_ge(oT_ready, done(2 * (BODY * i + GRP * u + b) + 1))
                            for c in range(NCH):
                                ins = nc.tensor.matmul(outp, oT[:, c, :], x2["L2_o"][:, c * P:(c + 1) * P],
                                                       start=(c == 0), stop=(c == NCH - 1))
                            ins.then_inc(out_done, 1)



def shared_experts(nc, C, tg):
    with ExitStack() as ctx:
        a = Alloc(nc, ctx, "L2f")
        F = Front(a)
        R = Router(a, BODY)
        wt = a.sb("wt", [P, BODY, E8])
        r = a.sb("r", [P, 2, 4, 512])
        half = a.sb("half", [P, 2, 512])
        c = a.sb("c", [P, 2, 512])
        cT = a.sb("cT", [P, 2, 4, P])
        H = a.ps("H", [P, 4, 512])
        T = a.ps("T", [P, 512])
        Y = a.ps("Y", [P, 512])
        tr = a.ps("tr", [P, 512])
        lgp = a.ps("lgp", [P, 512])
        We, Wo, Wg = C.f2["We"], C.f2["Wo"], C.f2["Wg"]
        logits = a.sem("logits")
        lg_read = a.sem("lg_read")
        weights = a.sem("weights")
        opened = a.sem("opened")
        relued = a.sem("relued")
        summed = a.sem("summed")
        flipped = a.sem("flipped")
        cT_ready = a.sem("cT_ready")
        closed = a.sem("closed")
        added = a.sem("added")
        own = a.sem("own")
        block = ctx.enter_context(nc.Block())

        @block.gpsimd
        def _(pool):
            pool.sem_inc(F.root_ready, CREDIT)
            with pool.Fori(0, TURNS) as i:
                for u in range(2):
                    F.root(nc, pool, C, i, u)

        @block.vector
        def _(v):
            F.open_vector(v)
            for x in (R.shift_done, lg_read, weights, summed, added):
                v.sem_inc(x, CREDIT)
            vec = Steps(own)
            nc.vector.memset(R.lg[:, :, :], -1e30).then_inc(vec.done, vec.one())
            v.wait_ge(vec.done, vec.count)
            v.sem_clear(vec.done)
            vec.restart()
            with v.Fori(0, TURNS) as i:
                for u in range(2):
                    F.statistics(nc, v, vec, C, i, u)
                for u in range(2):
                    F.normalise(nc, v, vec, C, i, u)
                v.wait_ge(logits, done(i))
                nc.vector.tensor_tensor(R.lg[:, :, 0:4], lgp[:, 0:BODY * 4].rearrange("p (b e) -> p b e", e=4),
                                        C.rows["L2f_bg"].unsqueeze(1).to_broadcast([P, BODY, 4]),
                                        ALU.add).then_inc(lg_read, 1)
                v.wait_ge(lg_read, done(i))
                nc.vector.memset(C.carrier[:, :], 0.0)
                R.choose(nc, v, vec, C, i)
                R.probabilities(nc, v, vec, i)
                nc.vector.tensor_tensor(wt[:, :, :], R.m1[:, :, :], R.rcp[:, :].unsqueeze(2).to_broadcast([P, BODY, E8]),
                                        ALU.mult).then_inc(weights, 1)
                for s in range(BODY + 2):
                    if s < BODY:
                        n = BODY * i + s
                        v.wait_ge(relued, done(4 * n + 3))
                        v.wait_ge(flipped, done(n - 2))
                        for j, dst in ((0, c), (2, half)):
                            nc.vector.tensor_tensor(dst[:, s % 2, :], r[:, s % 2, j, :], r[:, s % 2, j + 1, :], ALU.add).then_inc(vec.done, vec.one())
                        nc.vector.wait_ge(vec.done, vec.count)
                        nc.vector.tensor_tensor(c[:, s % 2, :], c[:, s % 2, :], half[:, s % 2, :],
                                                ALU.add).then_inc(summed, 1)
                    if s >= 2:
                        b = s - 2
                        v.wait_ge(closed, done(BODY * i + b))
                        x = C.Xt[:, bass.ds(i, 1), b, :]
                        nc.vector.scalar_tensor_tensor(out=x, in0=Y[:, 0:P], scalar=tg, in1=x, op0=ALU.mult,
                                                       op1=ALU.add).then_inc(added, 1)
                v.wait_ge(added, done(BODY * i + BODY - 1))
                nc.vector.memset(C.carrier[:, :], 0.0)
                v.wait_ge(vec.done, vec.count)
                v.sem_clear(vec.done)
                vec.restart()

        @block.scalar
        def _(act):
            for x in (F.xnT_ready, R.exp_done, relued, cT_ready):
                act.sem_inc(x, CREDIT)
            with act.Fori(0, TURNS) as i:
                for u in range(2):
                    F.take(nc, act, C, i, u, tr[:, :])
                R.exponentials(nc, act, i)
                act.wait_ge(weights, done(i))
                for s in range(BODY + 1):
                    n = BODY * i + s
                    if s < BODY:
                        act.wait_ge(summed, done(n - 2))
                        for e in range(4):
                            act.wait_ge(opened, done(4 * n + e))
                            nc.scalar.activation(r[:, s % 2, e, :], H[:, e, :], ACT.Relu,
                                                 scale=wt[:, s, e:e + 1]).then_inc(relued, 1)
                    if s >= 1:
                        act.wait_ge(closed, done(n - 3))
                        act.wait_ge(flipped, done(n - 1))
                        nc.scalar.activation(cT[:, (s - 1) % 2, :, :], T[:, :].rearrange("p (c t) -> p c t", c=4),
                                             ACT.Identity).then_inc(cT_ready, 1)

        @block.tensor
        def _(pe):
            for x in (F.turned, logits, opened, flipped, closed):
                pe.sem_inc(x, CREDIT)
            with pe.Fori(0, TURNS) as i:
                pe.wait_ge(F.xnT_ready, done(2 * i - 1))
                F.turn(nc, pe, C, i, 0, tr)
                pe.wait_ge(F.xnT_ready, done(2 * i))
                F.turn(nc, pe, C, i, 1, tr)
                pe.wait_ge(F.xnT_ready, done(2 * i + 1))
                pe.wait_ge(lg_read, done(i - 1))
                for b in range(BODY):
                    u, k = divmod(b, GRP)
                    ins = nc.tensor.matmul(lgp[:, b * 4:(b + 1) * 4], F.xnT[:, u, k * P:(k + 1) * P], Wg,
                                           start=True, stop=True)
                ins.then_inc(logits, 1)
                for s in range(BODY + 2):
                    n = BODY * i + s
                    if s < BODY:
                        u, k = divmod(s, GRP)
                        for e in range(4):
                            pe.wait_ge(relued, done(4 * (n - 1) + e))
                            nc.tensor.matmul(H[:, e, :], F.xnT[:, u, k * P:(k + 1) * P], We[:, 512 * e:512 * e + 512],
                                             start=True, stop=True).then_inc(opened, 1)
                    if 1 <= s < BODY + 1:
                        pe.wait_ge(cT_ready, done(n - 2))
                        pe.wait_ge(summed, done(n - 1))
                        for j in range(4):
                            ins = nc.tensor.transpose(T[:, j * P:(j + 1) * P], c[:, (s - 1) % 2, j * P:(j + 1) * P], C.ident)
                        ins.then_inc(flipped, 1)
                    if s >= 2:
                        pe.wait_ge(added, done(n - 3))
                        pe.wait_ge(cT_ready, done(n - 2))
                        for j in range(4):
                            ins = nc.tensor.matmul(Y[:, 0:P], cT[:, s % 2, j, :], Wo[:, j * P:(j + 1) * P],
                                                   start=(j == 0), stop=(j == 3))
                        ins.then_inc(closed, 1)



NS = 64
SC = 32
TWO_PI = (6.28125, 0.0019350051879882812, 3.019915981956753e-07)
ROUND = 1.5 * 2.0 ** 23
HALF_TURN = 3.1415925


def convolution_kernel(nc, C, x3, w_rows):
    with ExitStack() as ctx:
        a = Alloc(nc, ctx, "s4d")
        dt = a.sb("dt", [P, 1])
        names = "th q f sh cos sin ar er zr zi z2r z2i wr nr ni den cr ci t0 t1".split()
        B = {n: a.sb(n, [P, NS])[:, :] for n in names}
        Pr = a.sb("Pr", [P, SC, P])
        Pi = a.sb("Pi", [P, SC, P // 2])
        u0 = a.sb("u0", [P, SC, P // 2])
        u1 = a.sb("u1", [P, SC, P // 2])
        K = a.sb("K", [P, P])
        K2 = a.sb("K2", [P, P])
        pad = a.sb("pad", [P, 2 * P])
        dt_done, angle, sines = a.sem("dt_done"), a.sem("angle"), a.sem("sines")
        own, ready, stored = a.sem("own"), a.sem("ready"), a.sem("stored")
        block = ctx.enter_context(nc.Block())

        @block.scalar
        def _(act):
            act.wait_ge(C.last_landed, 16)
            nc.scalar.activation(dt[:, :], x3["log_dt"], ACT.Exp).then_inc(dt_done, 1)
            act.wait_ge(angle, 1)
            nc.scalar.activation(B["er"], B["ar"], ACT.Exp).then_inc(sines, 1)
            nc.scalar.activation(B["sin"], B["f"], ACT.Sin).then_inc(sines, 1)
            nc.scalar.activation(B["sh"], B["f"], ACT.Sin, scale=0.5).then_inc(sines, 1)

        @block.vector
        def _(v):
            vec = Steps(own)

            def tt(out, x, y, op):
                nc.vector.tensor_tensor(out, x, y, op).then_inc(vec.done, vec.one())
                nc.vector.wait_ge(vec.done, vec.count)

            def ts(out, x, s1, s2, op0, op1=ALU.bypass):
                ins = (nc.vector.tensor_scalar(out, x, s1, s2, op0, op1) if s2 is not None
                       else nc.vector.tensor_scalar(out, x, s1, None, op0))
                ins.then_inc(vec.done, vec.one())
                nc.vector.wait_ge(vec.done, vec.count)

            def product(outr, outi, xr, xi, yr, yi, t0, t1):
                tt(t0, xr, yr, ALU.mult)
                tt(t1, xi, yi, ALU.mult)
                tt(outr, t0, t1, ALU.subtract)
                if outi is not None:
                    tt(t0, xr, yi, ALU.mult)
                    tt(t1, xi, yr, ALU.mult)
                    tt(outi, t0, t1, ALU.add)

            v.wait_ge(dt_done, 1)
            ts(B["ar"], x3["A_re"], dt[:, 0:1], None, ALU.mult)
            ts(B["th"], x3["A_im"], dt[:, 0:1], None, ALU.mult)
            ts(B["q"], B["th"], 1.0 / (2.0 * 3.141592653589793), ROUND, ALU.mult, ALU.add)
            ts(B["q"], B["q"], ROUND, None, ALU.subtract)
            src = B["th"]
            for part in TWO_PI:
                nc.vector.scalar_tensor_tensor(out=B["f"], in0=B["q"], scalar=-part, in1=src,
                                                       op0=ALU.mult, op1=ALU.add).then_inc(vec.done, vec.one())
                nc.vector.wait_ge(vec.done, vec.count)
                src = B["f"]
            nc.vector.tensor_scalar(B["f"], B["f"], HALF_TURN, -HALF_TURN, ALU.min, ALU.max).then_inc(angle, 1)
            v.wait_ge(sines, 3)
            tt(B["cos"], B["sh"], B["sh"], ALU.mult)
            ts(B["cos"], B["cos"], -2.0, 1.0, ALU.mult, ALU.add)
            tt(B["zr"], B["er"], B["cos"], ALU.mult)
            tt(B["zi"], B["er"], B["sin"], ALU.mult)
            ts(B["wr"], B["zr"], 1.0, None, ALU.subtract)
            product(B["nr"], B["ni"], x3["C_re"], x3["C_im"], B["wr"], B["zi"], B["t0"], B["t1"])
            tt(B["t0"], x3["A_re"], x3["A_re"], ALU.mult)
            tt(B["t1"], x3["A_im"], x3["A_im"], ALU.mult)
            tt(B["den"], B["t0"], B["t1"], ALU.add)
            nc.vector.reciprocal(B["den"], B["den"]).then_inc(vec.done, vec.one())
            nc.vector.wait_ge(vec.done, vec.count)
            ts(B["den"], B["den"], 2.0, None, ALU.mult)
            ts(B["z2i"], x3["A_im"], -1.0, None, ALU.mult)
            product(B["cr"], B["ci"], B["nr"], B["ni"], x3["A_re"], B["z2i"], B["t0"], B["t1"])
            tt(B["cr"], B["cr"], B["den"], ALU.mult)
            tt(B["ci"], B["ci"], B["den"], ALU.mult)
            for part in range(NS // SC):
                n = slice(SC * part, SC * part + SC)
                nc.vector.tensor_copy(Pr[:, :, 0:1], B["cr"][:, n].unsqueeze(2)).then_inc(vec.done, vec.one())
                nc.vector.tensor_copy(Pi[:, :, 0:1], B["ci"][:, n].unsqueeze(2)).then_inc(vec.done, vec.one())
                nc.vector.wait_ge(vec.done, vec.count)
                L, z = 1, ("zr", "zi")
                while L < P:
                    wide = lambda x: B[x][:, n].unsqueeze(2).to_broadcast([P, SC, L])
                    product(Pr[:, :, L:2 * L], Pi[:, :, L:2 * L] if 2 * L < P else None, Pr[:, :, 0:L], Pi[:, :, 0:L],
                            wide(z[0]), wide(z[1]), u0[:, :, 0:L], u1[:, :, 0:L])
                    if 2 * L < P:
                        new = ("z2r", "z2i") if z[0] in ("zr", "nr") else ("nr", "ni")
                        product(B[new[0]][:, n], B[new[1]][:, n], B[z[0]][:, n], B[z[1]][:, n],
                                B[z[0]][:, n], B[z[1]][:, n], B["t0"][:, n], B["t1"][:, n])
                        z = new
                    L *= 2
                nc.vector.tensor_reduce((K2 if part else K)[:, :], Pr[:, :, :].rearrange("p n l -> p l n"),
                                                AX.X, ALU.add).then_inc(vec.done, vec.one())
                nc.vector.wait_ge(vec.done, vec.count)
            nc.vector.memset(pad[:, :], 0.0).then_inc(vec.done, vec.one())
            nc.vector.wait_ge(vec.done, vec.count)
            tt(pad[:, P - 1:2 * P - 1], K[:, :], K2[:, :], ALU.add)
            tt(pad[:, P - 1:P], pad[:, P - 1:P], x3["D_skip"], ALU.add)
            mg = C.rows["mod_gate"]
            ts(x3["film"], x3["film"], mg, None, ALU.mult)
            ts(C.rows["L3_film"], C.rows["L3_film"], mg, None, ALU.mult)
            for at in (0, 256):
                fb = C.rows["L3_film"][:, at:at + P]
                ts(fb, fb, 1.0, None, ALU.add)
            nc.vector.memset(C.carrier[:, :], 0.0).then_inc(ready, 1)

        @block.sync
        def _(sp):
            sp.wait_ge(ready, 1)
            sp.dma_start(C.kpad_dram, pad[:, :]).then_inc(stored, 16)
            sp.wait_ge(stored, 16)



KTOP = 32
H3, D3 = 4, 32
MASKED = -1e30
TAKEN = -3e38


def attention_top32(nc, C, x3, w96, xin):
    with ExitStack() as ctx:
        a = Alloc(nc, ctx, "L3")
        F = Front(a)
        N2 = Norm(a, "n2")
        ctxT = a.sb("ctxT", [KV, 2, TOK])
        qT = a.sb("qT", [P, 2, TOK])
        kT = a.sb("kT", [P, 2, TOK])
        kx = a.sb("kx", [P, 2, H3, P])
        V = a.sb("V", [P, 2, GRP, P])
        x1 = a.sb("x1", [P, 2, GRP, P])
        A = a.sb("A", [P, 2, H3, P])
        Wk = a.sb("Wk", [P, 2, H3, P])
        E = a.sb("E", [P, 2, H3, P])
        neg = a.sb("neg", [P, P])
        top = a.sb("top", [P, 2, H3, 8])
        top2 = a.sb("top2", [P, H3, 8])
        nmax = a.sb("nmax", [P, 2, H3])
        sm = a.sb("sm", [P, H3])
        rc = a.sb("rc", [P, 2, H3])
        am = a.sb("am", [P, 2, P])
        aT = a.sb("aT", [P, 2, P])
        ctT = a.sb("ctT", [P, 2, TOK])
        film = a.sb("film", [P, 2 * P])
        t = a.sb("t", [P, P])
        pj = a.ps("pj", [P, 2, 512])
        S = a.ps("S", [P, 2, 512])
        tb = a.ps("tb", [P, 512])
        cb = a.ps("cb", [P, 512])
        fb = a.ps("fb", [P, 512])

        ctx_in = [a.sem(f"ctx_in{u}") for u in range(2)]
        ct_out = [a.sem(f"ct_out{u}") for u in range(2)]
        ct_stored = a.sem("ct_stored")
        projected = a.sem("projected")
        q_ready = a.sem("q_ready")
        k_ready = a.sem("k_ready")
        v_ready = a.sem("v_ready")
        spread = a.sem("spread")
        x1_ready = a.sem("x1_ready")
        x1_scaled = a.sem("x1_scaled")
        x1_done = a.sem("x1_done")
        scored = a.sem("scored")
        masked = a.sem("masked")
        chosen = a.sem("chosen")
        exped = a.sem("exped")
        kept = a.sem("kept")
        weights = a.sem("weights")
        weighted = a.sem("weighted")
        meaned = a.sem("meaned")
        am_flipped = a.sem("am_flipped")
        aT_ready = a.sem("aT_ready")
        ct_done = a.sem("ct_done")
        ctT_ready = a.sem("ctT_ready")
        film_done = a.sem("film_done")
        film_read = a.sem("film_read")
        own = a.sem("own")
        block = ctx.enter_context(nc.Block())
        xt = xin[:, :].rearrange("p (i b d) -> p i b d", i=TURNS, b=BODY)
        STEPS = BODY + 7

        @block.sync
        def _(sp):
            sp.sem_inc(ct_stored, CREDIT)
            with sp.Fori(0, TURNS) as i:
                for u in range(2):
                    sp.wait_ge(projected, done(6 * i + 3 * u - 4))
                    sp.dma_start(ctxT[:, u, :], C.ctxT_v[:, bass.ds(i, 1), u, :]).then_inc(ctx_in[u], 16)
                for u in range(2):
                    sp.wait_ge(ctT_ready, done(BODY * i + GRP * u + GRP - 1))
                    sp.dma_start(C.ctT_v[:, bass.ds(i, 1), u, :], ctT[:, u, :]).then_inc(ct_out[u], 16)
                for u in range(2):
                    sp.wait_ge(ct_out[u], 16 * i + 16)
                    sp.sem_inc(ct_stored, 1)

        @block.gpsimd
        def _(pool):
            for x in (F.root_ready, N2.root_ready, spread, x1_done, kept, weighted):
                pool.sem_inc(x, CREDIT)
            with pool.Fori(0, TURNS) as i:
                for u in range(2):
                    F.root(nc, pool, C, i, u)

                def keys(b):
                    u, k = divmod(b, GRP)
                    pool.wait_ge(k_ready, done(2 * i + u))
                    pool.wait_ge(scored, done(BODY * i + b - 2))
                    nc.gpsimd.tensor_tensor(
                        kx[:, b % 2, :, :], kT[:, u, k * P:(k + 1) * P].unsqueeze(1).to_broadcast([P, H3, P]),
                        C.head_mask.unsqueeze(2).to_broadcast([P, H3, P]), ALU.mult).then_inc(spread, 1)

                keys(0)
                keys(1)
                for u in range(2):
                    N2.root(nc, pool, C, i, u)
                for u in range(2):
                    pool.wait_ge(x1_ready, done(2 * i + u))
                    g_row = C.rows["L3_g_in"].unsqueeze(1).to_broadcast([P, GRP, P])
                    b_row = C.rows["L3_b_in"].unsqueeze(1).to_broadcast([P, GRP, P])
                    nc.gpsimd.tensor_tensor(x1[:, u, :, :], x1[:, u, :, :], g_row, ALU.mult).then_inc(x1_scaled, 1)
                    pool.wait_ge(x1_scaled, 2 * i + u + 1)
                    nc.gpsimd.tensor_tensor(x1[:, u, :, :], x1[:, u, :, :], b_row, ALU.add).then_inc(x1_done, 1)
                for s in range(BODY + 1):
                    n = BODY * i + s
                    if s < BODY:
                        pool.wait_ge(exped, done(n))
                        nc.gpsimd.tensor_tensor(E[:, s % 2, :, :], E[:, s % 2, :, :], Wk[:, s % 2, :, :],
                                                ALU.mult).then_inc(kept, 1)
                        if s + 2 < BODY:
                            keys(s + 2)
                    if s >= 1:
                        pool.wait_ge(weights, done(n - 1))
                        e = E[:, (s - 1) % 2, :, :]
                        nc.gpsimd.tensor_tensor(e, e, rc[:, (s - 1) % 2, :].unsqueeze(2).to_broadcast([P, H3, P]),
                                                ALU.mult).then_inc(weighted, 1)

        @block.vector
        def _(v):
            F.open_vector(v)
            for x in (N2.var_ready, x1_ready, masked, chosen, weights, meaned, film_read):
                v.sem_inc(x, CREDIT)
            vec = Steps(own)

            def choose(i, s):
                n = BODY * i + s
                nc.vector.tensor_scalar(neg[:, :], C.kv_mask_v[:, bass.ds(i, 1), s, :], 1.0, -MASKED,
                                                ALU.subtract, ALU.mult).then_inc(vec.done, vec.one())
                v.wait_ge(exped, done(n - 2))
                v.wait_ge(kept, done(n - 2))
                v.wait_ge(scored, done(n))
                nc.vector.wait_ge(vec.done, vec.count)
                nc.vector.tensor_tensor(A[:, s % 2, :, :], S[:, s % 2, :].rearrange("p (h t) -> p h t", h=H3),
                                        neg[:, :].unsqueeze(1).to_broadcast([P, H3, P]), ALU.add).then_inc(masked, 1)
                v.wait_ge(masked, done(n))
                nc.vector.memset(C.carrier[:, :], 0.0)
                for r in range(KTOP // 8):
                    src = A if r == 0 else Wk
                    t8 = top[:, s % 2, :, :] if r == 0 else top2[:, :, :]
                    for h in range(H3):
                        nc.vector.max(t8[:, h, :], src[:, s % 2, h, :]).then_inc(vec.done, vec.one())
                    nc.vector.wait_ge(vec.done, vec.count)
                    for h in range(H3):
                        nc.vector.match_replace(Wk[:, s % 2, h, :], t8[:, h, :], src[:, s % 2, h, :], TAKEN).then_inc(vec.done, vec.one())
                    nc.vector.wait_ge(vec.done, vec.count)
                nc.vector.tensor_scalar(nmax[:, s % 2, :], top[:, s % 2, :, 0], -1.0, None, ALU.mult).then_inc(vec.done, vec.one())
                nc.vector.tensor_tensor(Wk[:, s % 2, :, :], Wk[:, s % 2, :, :], A[:, s % 2, :, :],
                                        ALU.not_equal).then_inc(chosen, 1)

            def total(i, b):
                v.wait_ge(kept, done(BODY * i + b))
                nc.vector.tensor_reduce(sm[:, :], E[:, b % 2, :, :], AX.X, ALU.add).then_inc(vec.done, vec.one())
                nc.vector.wait_ge(vec.done, vec.count)
                nc.vector.reciprocal(sm[:, :], sm[:, :]).then_inc(vec.done, vec.one())
                nc.vector.wait_ge(vec.done, vec.count)
                nc.vector.tensor_scalar(rc[:, b % 2, :], sm[:, :], C.q_mask_v[:, bass.ds(i, 1), b], 1.0 / H3,
                                        ALU.mult, ALU.mult).then_inc(weights, 1)

            def mean(i, b):
                n = BODY * i + b
                v.wait_ge(am_flipped, done(n - 2))
                v.wait_ge(weighted, done(n))
                nc.vector.tensor_reduce(am[:, b % 2, :], E[:, b % 2, :, :].rearrange("p h t -> p t h"), AX.X,
                                        ALU.add).then_inc(meaned, 1)

            def modulate(i, b):
                u, k = divmod(b, GRP)
                n = BODY * i + b
                v.wait_ge(x1_done, done(2 * i + u))
                v.wait_ge(film_done, done(n))
                nc.vector.wait_ge(vec.done, vec.count)
                nc.vector.tensor_tensor(film[:, :], fb[:, 0:2 * P], C.rows["L3_film"][:, 0:2 * P],
                                        ALU.add).then_inc(film_read, 1)
                v.wait_ge(film_read, done(n))
                nc.vector.tensor_tensor(t[:, :], x1[:, u, k, :], film[:, 0:P], ALU.mult).then_inc(vec.done, vec.one())
                nc.vector.wait_ge(vec.done, vec.count)
                nc.vector.tensor_tensor(xt[:, bass.ds(i, 1), b, :], t[:, :], film[:, P:2 * P], ALU.add).then_inc(vec.done, vec.one())

            with v.Fori(0, TURNS) as i:
                for u in range(2):
                    F.statistics(nc, v, vec, C, i, u)
                for u in range(2):
                    F.normalise(nc, v, vec, C, i, u)
                v.wait_ge(F.st_ready, done(2 * i + 1))
                nc.vector.memset(C.carrier[:, :], 0.0)
                for u in range(2):
                    N2.statistics(nc, vec, lambda k: F.st[:, u, k, :], u)
                for u in range(2):
                    N2.affine(nc, v, vec, i, u)
                    for k in range(GRP):
                        ins = N2.apply(nc, x1[:, u, k, :], F.st[:, u, k, :], u, k)
                    ins.then_inc(x1_ready, 1)
                for s in range(STEPS):
                    if s < BODY:
                        choose(i, s)
                    if 1 <= s < BODY + 1:
                        total(i, s - 1)
                    if 2 <= s < BODY + 2:
                        mean(i, s - 2)
                    if 6 <= s < BODY + 6:
                        modulate(i, s - 6)
                v.wait_ge(vec.done, vec.count)
                v.sem_clear(vec.done)
                vec.restart()

        @block.scalar
        def _(act):
            for x in (F.xnT_ready, q_ready, k_ready, v_ready, exped, aT_ready, ctT_ready):
                act.sem_inc(x, CREDIT)
            with act.Fori(0, TURNS) as i:
                for u in range(2):
                    F.take(nc, act, C, i, u, pj[:, u, :])
                for u in range(2):
                    act.wait_ge(projected, done(6 * i + 3 * u))
                    nc.scalar.activation(qT[:, u, :], pj[:, u, :], ACT.Identity,
                                         scale=D3 ** -0.5).then_inc(q_ready, 1)
                    act.wait_ge(spread, done(BODY * i + GRP * u + 3 - BODY))
                    act.wait_ge(projected, done(6 * i + 3 * u + 1))
                    nc.scalar.activation(kT[:, u, :], pj[:, 1 - u, :], ACT.Identity).then_inc(k_ready, 1)
                    act.wait_ge(projected, done(6 * i + 3 * u + 2))
                    nc.scalar.activation(V[:, u, :, :], pj[:, u, :].rearrange("p (b d) -> p b d", b=GRP),
                                         ACT.Identity).then_inc(v_ready, 1)
                for s in range(BODY + 5):
                    n = BODY * i + s
                    if s < BODY:
                        act.wait_ge(weighted, done(n - 2))
                        act.wait_ge(meaned, done(n - 2))
                        act.wait_ge(chosen, done(n))
                        for h in range(H3):
                            ins = nc.scalar.activation(E[:, s % 2, h, :], A[:, s % 2, h, :], ACT.Exp,
                                                       bias=nmax[:, s % 2, h:h + 1])
                        ins.then_inc(exped, 1)
                    if 3 <= s < BODY + 3:
                        act.wait_ge(ct_done, done(n - 5))
                        act.wait_ge(am_flipped, done(n - 3))
                        nc.scalar.activation(aT[:, (s - 3) % 2, :], tb[:, 0:P], ACT.Identity).then_inc(aT_ready, 1)
                    if 4 <= s < BODY + 4:
                        b = s - 4
                        if b % GRP == 0:
                            act.wait_ge(ct_stored, done(2 * (i - 1) + b // GRP))
                        act.wait_ge(ct_done, done(BODY * i + b))
                        nc.scalar.activation(ctT[:, b // GRP, b % GRP * P:(b % GRP + 1) * P], cb[:, 0:P],
                                             ACT.Identity).then_inc(ctT_ready, 1)

        @block.tensor
        def _(pe):
            for x in (F.turned, projected, scored, am_flipped, ct_done, film_done):
                pe.sem_inc(x, CREDIT)

            with pe.Fori(0, TURNS) as i:
                pe.wait_ge(k_ready, done(2 * i - 1))
                F.turn(nc, pe, C, i, 0, pj[:, 0, :])
                pe.wait_ge(v_ready, done(2 * i - 1))
                F.turn(nc, pe, C, i, 1, pj[:, 1, :])
                for u in range(2):
                    g = 2 * i + u
                    pe.wait_ge(F.xnT_ready, done(2 * i + 1))
                    if u:
                        pe.wait_ge(k_ready, done(2 * i))
                    nc.tensor.matmul(pj[:, u, :], x3["q"], F.xnT[:, u, :], start=True, stop=True).then_inc(
                        projected, 1)
                    pe.wait_ge(ctx_in[u], 16 * i + 16)
                    if u:
                        pe.wait_ge(v_ready, done(2 * i))
                    nc.tensor.matmul(pj[:, 1 - u, :], w96["L3_k"], ctxT[:, u, :], start=True, stop=True).then_inc(
                        projected, 1)
                    pe.wait_ge(q_ready, done(g))
                    for k in range(GRP):
                        ins = nc.tensor.matmul(pj[:, u, k * P:(k + 1) * P], ctxT[:, u, k * P:(k + 1) * P],
                                               w96["L3_v"], start=True, stop=True)
                    ins.then_inc(projected, 1)
                for s in range(BODY + 5):
                    n = BODY * i + s
                    if s < BODY:
                        u, k = divmod(s, GRP)
                        pe.wait_ge(q_ready, done(2 * i + u))
                        pe.wait_ge(masked, done(n - 2))
                        pe.wait_ge(spread, done(n))
                        nc.tensor.matmul(S[:, s % 2, :], qT[:, u, k * P:(k + 1) * P], kx[:, s % 2, :, :],
                                         start=True, stop=True).then_inc(scored, 1)
                    if 3 <= s < BODY + 3:
                        pe.wait_ge(aT_ready, done(n - 4))
                        pe.wait_ge(meaned, done(n - 3))
                        nc.tensor.transpose(tb[:, 0:P], am[:, (s - 3) % 2, :], C.ident).then_inc(am_flipped, 1)
                    if 4 <= s < BODY + 4:
                        b = s - 4
                        u, k = divmod(b, GRP)
                        pe.wait_ge(v_ready, done(2 * i + u))
                        pe.wait_ge(ctT_ready, done(n - 5))
                        pe.wait_ge(aT_ready, done(n - 4))
                        nc.tensor.matmul(cb[:, 0:P], V[:, u, k, :], aT[:, b % 2, :], start=True, stop=True).then_inc(
                            ct_done, 1)
                    if 5 <= s:
                        b = s - 5
                        pe.wait_ge(film_read, done(n - 6))
                        pe.wait_ge(ctT_ready, done(n - 5))
                        nc.tensor.matmul(fb[:, 0:2 * P], ctT[:, b // GRP, b % GRP * P:(b % GRP + 1) * P],
                                         x3["film"][:, 0:2 * P], start=True, stop=True).then_inc(film_done, 1)



CD = 16
CHUNKS = P // CD
RING = 3


def convolve(nc, C, xin):
    with ExitStack() as ctx:
        a = Alloc(nc, ctx, "conv")
        xr = a.sb("xr", [P, NB * P])
        Tz = a.sb("Tz", [P, RING, CD, P])
        rev = a.ps("rev", [P, 2, 512])
        Y = a.ps("Y", [P, 2, 512])
        fetched = [a.sem(f"fetched{k}") for k in range(RING)]
        reversed_, kept_a, kept_v = a.sem("reversed"), a.sem("kept_a"), a.sem("kept_v")
        summed, y_a, y_v = a.sem("summed"), a.sem("y_a"), a.sem("y_v")
        xr3 = xr[:, :].rearrange("p (b d) -> p b d", b=NB)
        y3 = xin[:, :].rearrange("p (b d) -> p d b", b=NB)
        kpad = C.kpad_dram
        block = ctx.enter_context(nc.Block())

        @block.sync
        def _(sp):
            for c in range(CHUNKS):
                if c >= RING:
                    sp.wait_ge(summed, c - RING + 1)
                src = bass.AP(tensor=kpad.tensor, offset=kpad.offset + c * CD * 2 * P,
                              ap=[[1, P], [2 * P, CD], [1, P]])
                sp.dma_start(Tz[:, c % RING, :, :], src).then_inc(fetched[c % RING], 16)

        @block.tensor
        def _(pe):
            for c in range(8):
                if c >= 2:
                    pe.wait_ge(kept_v if c % 2 else kept_a, c // 2)
                nc.tensor.matmul(rev[:, c % 2, :], C.reverse, xin[:, 512 * c:512 * c + 512],
                                 start=True, stop=True).then_inc(reversed_, 1)
            pe.wait_ge(kept_a, 4)
            pe.wait_ge(kept_v, 4)
            for c in range(CHUNKS):
                pe.wait_ge(fetched[c % RING], 16 * (c // RING + 1))
                if c >= 2:
                    pe.wait_ge(y_v if c % 2 else y_a, c // 2)
                for d in range(CD):
                    ins = nc.tensor.matmul(Y[:, c % 2, d * NB:(d + 1) * NB], Tz[:, c % RING, d, :],
                                           xr3[:, :, c * CD + d], start=True, stop=True)
                ins.then_inc(summed, 1)

        @block.scalar
        def _(act):
            for c in range(0, 8, 2):
                act.wait_ge(reversed_, c + 1)
                nc.scalar.activation(xr[:, 512 * c:512 * c + 512], rev[:, 0, :], ACT.Identity).then_inc(kept_a, 1)
            for c in range(0, CHUNKS, 2):
                act.wait_ge(summed, c + 1)
                nc.scalar.activation(y3[:, c * CD:(c + 1) * CD, :], Y[:, 0, :].rearrange("p (d b) -> p d b", d=CD),
                                     ACT.Identity).then_inc(y_a, 1)

        @block.vector
        def _(v):
            for c in range(1, 8, 2):
                v.wait_ge(reversed_, c + 1)
                nc.vector.tensor_copy(xr[:, 512 * c:512 * c + 512], rev[:, 1, :]).then_inc(kept_v, 1)
            for c in range(1, CHUNKS, 2):
                v.wait_ge(summed, c + 1)
                nc.vector.tensor_copy(y3[:, c * CD:(c + 1) * CD, :],
                                      Y[:, 1, :].rearrange("p (d b) -> p d b", d=CD)).then_inc(y_v, 1)



def film_feed_forward(nc, C, x3, y, tg):
    NC = 4
    with ExitStack() as ctx:
        a = Alloc(nc, ctx, "L3b")
        F = Front(a)
        NF, NO = Norm(a, "nf"), Norm(a, "no")
        ctT = a.sb("ctT", [P, 2, TOK])
        film = a.sb("film", [P, 2, 2 * P])
        y2 = a.sb("y2", [P, 2, P])
        hn = a.sb("hn", [P, 2, GRP, P])
        hT = a.sb("hT", [P, 2, TOK])
        aT = a.sb("aT", [P, 2, NC, TOK])
        fb = a.ps("fb", [P, 2, 512])
        tr = a.ps("tr", [P, 512])
        U = a.ps("U", [P, 3, 512])
        Y = a.ps("Y", [P, 2, 512])
        ct_in = [a.sem(f"ct_in{u}") for u in range(2)]
        film_done = a.sem("film_done")
        film_read = a.sem("film_read")
        hn_ready = a.sem("hn_ready")
        turned = a.sem("turned2")
        hT_ready = a.sem("hT_ready")
        opened = a.sem("opened")
        a_ready = a.sem("a_ready")
        closed = a.sem("closed")
        y_read = a.sem("y_read")
        own = a.sem("own")
        block = ctx.enter_context(nc.Block())
        yt = y[:, :].rearrange("p (i b d) -> p i b d", i=TURNS, b=BODY)

        @block.sync
        def _(sp):
            with sp.Fori(0, TURNS) as i:
                for u in range(2):
                    sp.wait_ge(film_done, done(BODY * (i - 1) + GRP * u + GRP - 1))
                    sp.dma_start(ctT[:, u, :], C.ctT_v[:, bass.ds(i, 1), u, :]).then_inc(ct_in[u], 16)

        @block.gpsimd
        def _(pool):
            for x in (F.N, NF, NO):
                pool.sem_inc(x.root_ready, CREDIT)
            with pool.Fori(0, TURNS) as i:
                for x in (F.N, NF, NO):
                    for u in range(2):
                        x.root(nc, pool, C, i, u)

        @block.vector
        def _(v):
            for x in (F.N.var_ready, NF.var_ready, NO.var_ready, film_read, hn_ready, y_read):
                v.sem_inc(x, CREDIT)
            vec = Steps(own)
            b2_row = C.rows["L3_b2"].unsqueeze(1).to_broadcast([P, GRP, P])
            g_row = C.rows["L3_g_out"].unsqueeze(1).to_broadcast([P, GRP, P])
            b_row = C.rows["L3_b_out"].unsqueeze(1).to_broadcast([P, GRP, P])
            with v.Fori(0, TURNS) as i:
                for u in range(2):
                    F.statistics(nc, v, vec, C, i, u)
                for u in range(2):
                    F.N.affine(nc, v, vec, i, u)
                    for k in range(GRP):
                        F.N.apply(nc, F.st[:, u, k, :], C.Xt[:, bass.ds(i, 1), GRP * u + k, :], u, k).then_inc(vec.done, vec.one())
                for b in range(BODY):
                    u, k = divmod(b, GRP)
                    v.wait_ge(film_done, done(BODY * i + b))
                    nc.vector.tensor_tensor(film[:, b % 2, :], fb[:, b % 2, 0:2 * P], C.rows["L3_film"][:, 2 * P:4 * P],
                                            ALU.add).then_inc(film_read, 1)
                    v.wait_ge(film_read, done(BODY * i + b))
                    nc.vector.tensor_tensor(y2[:, b % 2, :], yt[:, bass.ds(i, 1), b, :], film[:, b % 2, 0:P],
                                                    ALU.mult).then_inc(vec.done, vec.one())
                    nc.vector.wait_ge(vec.done, vec.count)
                    nc.vector.tensor_tensor(y2[:, b % 2, :], y2[:, b % 2, :], film[:, b % 2, P:2 * P], ALU.add).then_inc(vec.done, vec.one())
                    nc.vector.wait_ge(vec.done, vec.count)
                    nc.vector.tensor_tensor(F.st[:, u, k, :], F.st[:, u, k, :], y2[:, b % 2, :], ALU.add).then_inc(vec.done, vec.one())
                nc.vector.wait_ge(vec.done, vec.count)
                for u in range(2):
                    NF.statistics(nc, vec, lambda k: F.st[:, u, k, :], u)
                for u in range(2):
                    NF.affine(nc, v, vec, i, u)
                    v.wait_ge(turned, done(2 * (i - 1) + u))
                    for k in range(GRP):
                        ins = NF.apply(nc, hn[:, u, k, :], F.st[:, u, k, :], u, k)
                    ins.then_inc(hn_ready, 1)
                    v.wait_ge(hn_ready, done(2 * i + u))
                    nc.vector.tensor_tensor(F.st[:, u, :, :], F.st[:, u, :, :], b2_row, ALU.add).then_inc(vec.done, vec.one())
                nc.vector.wait_ge(vec.done, vec.count)
                for u in range(2):
                    v.wait_ge(closed, done(2 * i + u))
                    nc.vector.tensor_tensor(F.st[:, u, :, :], F.st[:, u, :, :],
                                            Y[:, u, :].rearrange("p (k d) -> p k d", k=GRP), ALU.add).then_inc(y_read, 1)
                    v.wait_ge(y_read, done(2 * i + u))
                    nc.vector.memset(C.carrier[:, :], 0.0)
                    NO.statistics(nc, vec, lambda k: F.st[:, u, k, :], u)
                for u in range(2):
                    NO.affine(nc, v, vec, i, u)
                    for k in range(GRP):
                        NO.apply(nc, F.st[:, u, k, :], F.st[:, u, k, :], u, k).then_inc(vec.done, vec.one())
                    nc.vector.wait_ge(vec.done, vec.count)
                    nc.vector.tensor_tensor(F.st[:, u, :, :], F.st[:, u, :, :], g_row, ALU.mult).then_inc(vec.done, vec.one())
                    nc.vector.wait_ge(vec.done, vec.count)
                    nc.vector.tensor_tensor(F.st[:, u, :, :], F.st[:, u, :, :], b_row, ALU.add).then_inc(vec.done, vec.one())
                    nc.vector.wait_ge(vec.done, vec.count)
                    x = C.Xt[:, bass.ds(i, 1), GRP * u:GRP * u + GRP, :].rearrange("p o k d -> p (o k d)")
                    nc.vector.scalar_tensor_tensor(out=x, in0=F.st[:, u, :, :].rearrange("p k d -> p (k d)"),
                                                           scalar=tg, in1=x, op0=ALU.mult, op1=ALU.add).then_inc(vec.done, vec.one())
                v.wait_ge(vec.done, vec.count)
                v.sem_clear(vec.done)
                vec.restart()

        @block.scalar
        def _(act):
            for x in (hT_ready, a_ready):
                act.sem_inc(x, CREDIT)
            with act.Fori(0, TURNS) as i:
                for u in range(2):
                    act.wait_ge(turned, done(2 * i + u))
                    nc.scalar.activation(hT[:, u, :], tr[:, :], ACT.Identity, scale=x3["g_ffn"],
                                         bias=x3["b_ffn"]).then_inc(hT_ready, 1)
                for u in range(2):
                    for c in range(NC):
                        n = NC * (2 * i + u) + c
                        act.wait_ge(opened, done(n))
                        nc.scalar.activation(aT[:, u, c, :], U[:, (NC * u + c) % 2, :], ACT.Gelu,
                                             bias=x3["b1"][:, c:c + 1]).then_inc(a_ready, 1)

        @block.tensor
        def _(pe):
            for x in (film_done, turned, opened, closed):
                pe.sem_inc(x, CREDIT)
            w2 = x3["W2"].rearrange("p (c d) -> p c d", c=NC)
            with pe.Fori(0, TURNS) as i:
                for b in range(BODY):
                    u, k = divmod(b, GRP)
                    if k == 0:
                        pe.wait_ge(ct_in[u], 16 * i + 16)
                    pe.wait_ge(film_read, done(BODY * i + b - 2))
                    nc.tensor.matmul(fb[:, b % 2, 0:2 * P], ctT[:, u, k * P:(k + 1) * P], x3["film"][:, 2 * P:4 * P],
                                     start=True, stop=True).then_inc(film_done, 1)
                for u in range(2):
                    pe.wait_ge(hT_ready, done(2 * i + u - 1))
                    pe.wait_ge(hn_ready, done(2 * i + u))
                    for k in range(GRP):
                        ins = nc.tensor.transpose(tr[:, k * P:(k + 1) * P], hn[:, u, k, :], C.ident)
                    ins.then_inc(turned, 1)
                for u in range(2):
                    pe.wait_ge(hT_ready, done(2 * i + u))
                    for c in range(NC):
                        n = NC * (2 * i + u) + c
                        pe.wait_ge(a_ready, done(n - 2))
                        nc.tensor.matmul(U[:, (NC * u + c) % 2, :], x3["W1"][:, c * P:(c + 1) * P], hT[:, u, :],
                                         start=True, stop=True).then_inc(opened, 1)
                for u in range(2):
                    pe.wait_ge(a_ready, done(NC * (2 * i + u) + NC - 1))
                    pe.wait_ge(y_read, done(2 * (i - 1) + u))
                    for k in range(GRP):
                        for c in range(NC):
                            ins = nc.tensor.matmul(Y[:, u, k * P:(k + 1) * P], aT[:, u, c, k * P:(k + 1) * P], w2[:, c, :],
                                                   start=(c == 0), stop=(c == NC - 1))
                    ins.then_inc(closed, 1)



NTOK = NB * P
EXPERTS = 8
CAPACITY = 320


EXPERT_ROWS = E8 * CAPACITY
NOWHERE = 4095


def route_with_capacity(nc, C, W, tg, wt, slot, xn, xnT):
    with ExitStack() as ctx:
        a = Alloc(nc, ctx, "rt")
        F = Front(a)
        R = Router(a, BODY)
        share = a.sb("share", [P, NB, E8])
        second = a.sb("second", [P, NB, E8])
        place = a.sb("place", [P, NB, E8])
        picked = a.sb("picked", [P, NB, E8])
        where = a.sb("where", [P, NB])
        zeros = a.sb("zeros", [P, P])
        chosen = a.sb("chosen", [P, NB, E8])
        keep = a.sb("keep", [P, E8, NB])
        free = a.sb("free", [P, NB])
        eligible = a.sb("eligible", [P, NB])
        before = a.sb("before", [P, NB])
        zero = a.sb("zero", [P, NB])
        tr = a.ps("tr", [P, 512])
        lgp = a.ps("lgp", [P, 512])
        rank = a.ps("rank", [P, 512])
        logits = a.sem("logits")
        lg_read = a.sem("lg_read")
        xn_kept, xnT_kept = a.sem("xn_kept"), a.sem("xnT_kept")
        zeroed, cleared = a.sem("zeroed"), a.sem("cleared")
        own, counted, offered, settled = a.sem("own"), a.sem("counted"), a.sem("offered"), a.sem("settled")
        block = ctx.enter_context(nc.Block())
        share_t = share[:, :, :].rearrange("p (i b) e -> p i b e", i=TURNS)
        chosen_t = chosen[:, :, :].rearrange("p (i b) e -> p i b e", i=TURNS)

        second_t = second[:, :, :].rearrange("p (i b) e -> p i b e", i=TURNS)
        xn_t = xn[:, :].rearrange("p (i u t) -> p i u t", i=TURNS, u=2)
        xnT_t = xnT[:, :].rearrange("p (i u t) -> p i u t", i=TURNS, u=2)

        @block.sync
        def _(sp):
            sp.wait_ge(zeroed, 1)
            sp.dma_start(C.expert_in.rearrange("(k p) d -> p k d", p=P),
                         zeros[:, :].unsqueeze(1).to_broadcast([P, EXPERT_ROWS // P, P])).then_inc(cleared, 16)
            sp.wait_ge(cleared, 16)

        @block.gpsimd
        def _(pool):
            nc.gpsimd.memset(zeros[:, :], 0.0).then_inc(zeroed, 1)
            pool.sem_inc(F.root_ready, CREDIT)
            with pool.Fori(0, TURNS) as i:
                for u in range(2):
                    F.root(nc, pool, C, i, u)

        @block.vector
        def _(v):
            F.open_vector(v)
            for x in (R.shift_done, lg_read, xn_kept, xnT_kept):
                v.sem_inc(x, CREDIT)
            vec = Steps(own)
            with v.Fori(0, TURNS) as i:
                for u in range(2):
                    F.statistics(nc, v, vec, C, i, u)
                for u in range(2):
                    F.normalise(nc, v, vec, C, i, u)
                for u in range(2):
                    v.wait_ge(F.st_ready, done(2 * i + u))
                    nc.vector.tensor_scalar(xn_t[:, bass.ds(i, 1), u, :], F.st[:, u, :, :].rearrange("p k d -> p (k d)"),
                                            1.0, None, ALU.mult).then_inc(xn_kept, 1)
                    v.wait_ge(F.xnT_ready, done(2 * i + u))
                    nc.vector.tensor_scalar(xnT_t[:, bass.ds(i, 1), u, :], F.xnT[:, u, :], 1.0, None,
                                            ALU.mult).then_inc(xnT_kept, 1)
                v.wait_ge(logits, done(i))
                nc.vector.tensor_copy(R.lg[:, :, :], lgp[:, 0:BODY * E8].rearrange("p (b e) -> p b e", e=E8)).then_inc(
                    lg_read, 1)
                v.wait_ge(lg_read, done(i))
                nc.vector.memset(C.carrier[:, :], 0.0)
                R.choose(nc, v, vec, C, i)
                nc.vector.tensor_scalar(second_t[:, bass.ds(i, 1), :, :], R.m1[:, :, :].unsqueeze(1), 1.0, None,
                                        ALU.mult).then_inc(vec.done, vec.one())
                nc.vector.wait_ge(vec.done, vec.count)
                R.probabilities(nc, v, vec, i)
                wide = lambda x: x[:, :].unsqueeze(2).to_broadcast([P, BODY, E8])
                nc.vector.tensor_tensor(R.m1[:, :, :], R.m1[:, :, :], wide(R.rcp), ALU.mult).then_inc(vec.done, vec.one())
                nc.vector.wait_ge(vec.done, vec.count)
                nc.vector.tensor_reduce(R.sum[:, :], R.m1[:, :, :], AX.X, ALU.add).then_inc(vec.done, vec.one())
                nc.vector.wait_ge(vec.done, vec.count)
                nc.vector.tensor_scalar(R.sum[:, :], R.sum[:, :], 1e-9, None, ALU.max).then_inc(vec.done, vec.one())
                nc.vector.wait_ge(vec.done, vec.count)
                nc.vector.reciprocal(R.rcp[:, :], R.sum[:, :]).then_inc(vec.done, vec.one())
                nc.vector.wait_ge(vec.done, vec.count)
                one_turn = [P, 1, BODY, E8]
                nc.vector.tensor_tensor(share_t[:, bass.ds(i, 1), :, :], R.m1[:, :, :].unsqueeze(1),
                                                R.rcp[:, :].unsqueeze(1).unsqueeze(3).to_broadcast(one_turn), ALU.mult).then_inc(vec.done, vec.one())
                nc.vector.tensor_scalar(chosen_t[:, bass.ds(i, 1), :, :], R.m0[:, :, :].unsqueeze(1), 1.0, None,
                                                ALU.mult).then_inc(vec.done, vec.one())
                v.wait_ge(xn_kept, done(2 * i + 1))
                nc.vector.memset(C.carrier[:, :], 0.0)
                v.wait_ge(vec.done, vec.count)
                v.sem_clear(vec.done)
                vec.restart()

            def op(out, x, y, f):
                nc.vector.tensor_tensor(out, x, y, f).then_inc(vec.done, vec.one())
                nc.vector.wait_ge(vec.done, vec.count)

            nc.vector.memset(zero[:, :], 0.0).then_inc(vec.done, vec.one())
            nc.vector.memset(free[:, :], 1.0).then_inc(vec.done, vec.one())
            nc.vector.wait_ge(vec.done, vec.count)
            for e in range(EXPERTS):
                op(eligible[:, :], chosen[:, :, e], free[:, :], ALU.mult)
                nc.vector.tensor_tensor_scan(before[:, :], eligible[:, :], zero[:, :], 0.0, ALU.add, ALU.add).then_inc(vec.done, vec.one())
                nc.vector.wait_ge(vec.done, vec.count)
                nc.vector.tensor_tensor(before[:, :], before[:, :], eligible[:, :], ALU.subtract).then_inc(offered, 1)
                v.wait_ge(counted, e + 1)
                nc.vector.scalar_tensor_tensor(out=keep[:, e, :], in0=rank[:, 0:NB], scalar=float(CAPACITY),
                                                       in1=eligible[:, :], op0=ALU.is_le, op1=ALU.mult).then_inc(vec.done, vec.one())
                nc.vector.tensor_scalar(place[:, :, e], rank[:, 0:NB], float(e * CAPACITY - 1 - NOWHERE), None,
                                        ALU.add).then_inc(vec.done, vec.one())
                nc.vector.wait_ge(vec.done, vec.count)
                op(eligible[:, :], eligible[:, :], keep[:, e, :], ALU.subtract)
                op(free[:, :], free[:, :], eligible[:, :], ALU.subtract)
            kept = keep[:, :, :].rearrange("p e b -> p b e")
            op(place[:, :, :], place[:, :, :], kept, ALU.mult)
            op(share[:, :, :], share[:, :, :], kept, ALU.mult)
            op(share[:, :, :], share[:, :, :], free[:, :].unsqueeze(2).to_broadcast([P, NB, E8]), ALU.mult)
            op(chosen[:, :, :], chosen[:, :, :], second[:, :, :], ALU.subtract)
            for j, choice in ((0, chosen), (1, second)):
                op(picked[:, :, :], place[:, :, :], choice[:, :, :], ALU.mult)
                nc.vector.tensor_reduce(where[:, :], picked[:, :, :], AX.X, ALU.add).then_inc(vec.done, vec.one())
                nc.vector.wait_ge(vec.done, vec.count)
                nc.vector.tensor_scalar(where[:, :], where[:, :], float(NOWHERE), None, ALU.add).then_inc(
                    vec.done, vec.one())
                nc.vector.wait_ge(vec.done, vec.count)
                nc.vector.tensor_copy(slot[:, j, :], where[:, :]).then_inc(vec.done, vec.one())
                op(picked[:, :, :], share[:, :, :], choice[:, :, :], ALU.mult)
                nc.vector.tensor_reduce(wt[:, j, :], picked[:, :, :], AX.X, ALU.add).then_inc(vec.done, vec.one())
                nc.vector.wait_ge(vec.done, vec.count)
            nc.vector.tensor_scalar(wt[:, 2, :], free[:, :], -1.0, 1.0, ALU.mult, ALU.add).then_inc(vec.done, vec.one())
            nc.vector.wait_ge(vec.done, vec.count)
            nc.vector.tensor_scalar(wt[:, :, :], wt[:, :, :], tg, None, ALU.mult).then_inc(settled, 1)
            v.wait_ge(settled, 1)

        @block.scalar
        def _(act):
            for x in (F.xnT_ready, R.exp_done):
                act.sem_inc(x, CREDIT)
            with act.Fori(0, TURNS) as i:
                for u in range(2):
                    act.wait_ge(xnT_kept, done(2 * i + u - 2))
                    F.take(nc, act, C, i, u, tr[:, :])
                R.exponentials(nc, act, i)

        @block.tensor
        def _(pe):
            for x in (F.turned, logits):
                pe.sem_inc(x, CREDIT)
            with pe.Fori(0, TURNS) as i:
                pe.wait_ge(F.xnT_ready, done(2 * i - 1))
                F.turn(nc, pe, C, i, 0, tr)
                pe.wait_ge(F.xnT_ready, done(2 * i))
                F.turn(nc, pe, C, i, 1, tr)
                pe.wait_ge(F.xnT_ready, done(2 * i + 1))
                pe.wait_ge(lg_read, done(i - 1))
                for b in range(BODY):
                    u, k = divmod(b, GRP)
                    ins = nc.tensor.matmul(lgp[:, b * E8:(b + 1) * E8], F.xnT[:, u, k * P:(k + 1) * P], W["router"],
                                           start=True, stop=True)
                ins.then_inc(logits, 1)
            for e in range(EXPERTS):
                pe.wait_ge(offered, e + 1)
                nc.tensor.matmul(rank[:, 0:NB], C.upto, eligible[:, :], start=True, stop=False)
                nc.tensor.matmul(rank[:, 0:NB], C.ones, before[:, :], start=False, stop=True).then_inc(counted, 1)


def capacity_experts(nc, C, W, wt, slot, xn, xnT):
    NC = 4
    tiles = [(k, min(P, CAPACITY - k)) for k in range(0, CAPACITY, P)]
    BACK = 4
    with ExitStack() as ctx:
        a = Alloc(nc, ctx, "L3f")
        aT = a.sb("aT", [P, 2, NC, TOK])
        yb = a.sb("yb", [P, 2, GRP, P])
        xg = a.sb("xg", [P, 3, len(tiles), P])
        xgT = a.sb("xgT", [P, 2, CAPACITY])
        yg = a.sb("yg", [P, 2, len(tiles), P])
        tr = a.ps("tr", [P, 512])
        U = a.ps("U", [P, 4, 512])
        Y = a.ps("Y", [P, 2, 512])
        opened, a_ready, closed, y_read, added = (
            a.sem("opened"), a.sem("a_ready"), a.sem("closed"), a.sem("y_read"), a.sem("added"))
        sent = a.sem("sent")
        fetched = [a.sem(f"fetched{q}") for q in range(3)]
        turned = a.sem("turned")
        xgT_ready = a.sem("xgT_ready")
        e_opened, e_active, e_closed = a.sem("e_opened"), a.sem("e_active"), a.sem("e_closed")
        yg_ready = a.sem("yg_ready")
        put = [a.sem(f"put{q}") for q in range(2)]
        back = [a.sem(f"back{q}") for q in range(NB // BACK)]
        summed = a.sem("summed")
        block = ctx.enter_context(nc.Block())
        units = E8 + 1
        w1 = W["W1"].rearrange("p (e c f) -> p e c f", e=units, c=NC)
        w2 = W["W2"].rearrange("p (e c d) -> p e c d", e=units, c=NC)
        b1 = W["b1"].rearrange("p (e c) -> p e c", e=units)
        b2 = C.rows["L3f_b2"].rearrange("p (e d) -> p e d", e=units)
        wt_t = wt[:, :, :].rearrange("p j (i b) -> p j i b", i=TURNS)
        xnT_t = xnT[:, :].rearrange("p (i u t) -> p i u t", i=TURNS, u=2)
        GROUPS = 2 * TURNS
        full = CAPACITY // P
        rest = CAPACITY - full * P

        def rows(dram, e):
            own = dram[e * CAPACITY:(e + 1) * CAPACITY, :]
            return own[0:full * P, :].rearrange("(k p) d -> p k d", p=P), own[full * P:, :]

        @block.gpsimd
        def _(pool):
            for b in range(NB):
                for j in range(2):
                    nc.gpsimd.indirect_dma_start(
                        C.expert_in, bass.IndirectOffsetOnAxis(slot[:, j, b:b + 1], 0), xn[:, b * P:(b + 1) * P], None,
                        bounds_check=EXPERT_ROWS - 1, oob_is_err=False).then_inc(sent, 16)
            pool.wait_ge(sent, 16 * 2 * NB)
            pool.wait_ge(closed, done(GROUPS - 1))
            for q in range(2):
                pool.wait_ge(put[q], 32 * (E8 // 2))
            for b in range(NB):
                for j, dst in ((0, xn), (1, xnT)):
                    nc.gpsimd.indirect_dma_start(
                        dst[:, b * P:(b + 1) * P], None, C.expert_out,
                        bass.IndirectOffsetOnAxis(slot[:, j, b:b + 1], 0),
                        bounds_check=EXPERT_ROWS - 1, oob_is_err=False).then_inc(back[b // BACK], 16)

        @block.sync
        def _(sp):
            def fetch(e):
                if e >= 3:
                    sp.wait_ge(turned, e - 2)
                whole, last = rows(C.expert_in, e)
                sp.dma_start(xg[:, e % 3, 0:full, :], whole).then_inc(fetched[e % 3], 16)
                sp.dma_start(xg[0:rest, e % 3, full, :], last).then_inc(fetched[e % 3], 16)

            sp.wait_ge(sent, 16 * 2 * NB)
            fetch(0)
            fetch(1)
            for e in range(E8):
                if e + 2 < E8:
                    fetch(e + 2)
                sp.wait_ge(yg_ready, e + 1)
                whole, last = rows(C.expert_out, e)
                sp.dma_start(whole, yg[:, e % 2, 0:full, :]).then_inc(put[e % 2], 16)
                sp.dma_start(last, yg[0:rest, e % 2, full, :]).then_inc(put[e % 2], 16)
            for q in range(2):
                sp.wait_ge(put[q], 32 * (E8 // 2))

        @block.vector
        def _(v):
            for x in (y_read, added):
                v.sem_inc(x, CREDIT)
            with v.Fori(0, TURNS) as i:
                for u in range(2):
                    n = 2 * i + u
                    v.wait_ge(closed, done(n))
                    v.wait_ge(added, done(n - 2))
                    nc.vector.tensor_tensor(yb[:, u, :, :], Y[:, u, :].rearrange("p (k d) -> p k d", k=GRP),
                                            b2[:, 0:1, :].to_broadcast([P, GRP, P]), ALU.add).then_inc(y_read, 1)
                    v.wait_ge(y_read, done(n))
                    for k in range(GRP):
                        b = GRP * u + k
                        x = C.Xt[:, bass.ds(i, 1), b, :]
                        ins = nc.vector.scalar_tensor_tensor(out=x, in0=yb[:, u, k, :],
                                                             scalar=wt_t[:, 2, bass.ds(i, 1), b], in1=x,
                                                             op0=ALU.mult, op1=ALU.add)
                    ins.then_inc(added, 1)
            for e in range(E8):
                if e >= 2:
                    v.wait_ge(put[e % 2], 32 * (e // 2))
                v.wait_ge(e_closed, e + 1)
                y = Y[:, e % 2, 0:len(tiles) * P].rearrange("p (k d) -> p k d", d=P)
                nc.vector.tensor_tensor(yg[:, e % 2, 0:full, :], y[:, 0:full, :],
                                        b2[:, e + 1:e + 2, :].to_broadcast([P, full, P]), ALU.add)
                nc.vector.tensor_tensor(yg[0:rest, e % 2, full, :], y[0:rest, full, :], b2[0:rest, e + 1, :],
                                        ALU.add).then_inc(yg_ready, 1)
            v.wait_ge(added, done(GROUPS - 1))
            for j, src in ((0, xn), (1, xnT)):
                for b in range(NB):
                    if j == 0 and b % BACK == 0:
                        v.wait_ge(back[b // BACK], 16 * 2 * BACK)
                    if j == 1 and b == 0:
                        v.wait_ge(summed, 1)
                    x = C.X[:, b * P:(b + 1) * P]
                    ins = nc.vector.scalar_tensor_tensor(out=x, in0=src[:, b * P:(b + 1) * P], scalar=wt[:, j, b:b + 1],
                                                         in1=x, op0=ALU.mult, op1=ALU.add)
                ins.then_inc(summed, 1)
            v.wait_ge(summed, 2)

        @block.scalar
        def _(act):
            act.sem_inc(a_ready, CREDIT)
            with act.Fori(0, TURNS) as i:
                for u in range(2):
                    act.wait_ge(closed, done(2 * i + u - 2))
                    for c in range(NC):
                        act.wait_ge(opened, done(NC * (2 * i + u) + c))
                        nc.scalar.activation(aT[:, u, c, :], U[:, c, :], ACT.Gelu,
                                             bias=b1[:, 0, c:c + 1]).then_inc(a_ready, 1)
            act.wait_ge(closed, done(GROUPS - 1))

            def take(e):
                act.wait_ge(turned, e + 1)
                nc.scalar.activation(xgT[:, e % 2, :], tr[:, 0:CAPACITY], ACT.Identity).then_inc(xgT_ready, 1)

            take(0)
            for e in range(E8):
                if e + 1 < E8:
                    if e >= 1:
                        act.wait_ge(e_opened, NC * e)
                    take(e + 1)
                if e >= 2:
                    act.wait_ge(e_closed, e - 1)
                for c in range(NC):
                    act.wait_ge(e_opened, NC * e + c + 1)
                    nc.scalar.activation(aT[:, e % 2, c, 0:CAPACITY], U[:, c, 0:CAPACITY], ACT.Gelu,
                                         bias=b1[:, e + 1, c:c + 1]).then_inc(e_active, 1)

        @block.tensor
        def _(pe):
            for x in (opened, closed):
                pe.sem_inc(x, CREDIT)

            def close(i, t):
                pe.wait_ge(y_read, done(2 * i + t - 2))
                pe.wait_ge(a_ready, done(NC * (2 * i + t) + NC - 1))
                for k in range(GRP):
                    for c in range(NC):
                        ins = nc.tensor.matmul(Y[:, t % 2, k * P:(k + 1) * P], aT[:, t % 2, c, k * P:(k + 1) * P],
                                               w2[:, 0, c, :], start=(c == 0), stop=(c == NC - 1))
                ins.then_inc(closed, 1)

            with pe.Fori(0, TURNS) as i:
                for u in range(2):
                    for c in range(NC):
                        pe.wait_ge(a_ready, done(NC * (2 * i + u - 1) + c))
                        nc.tensor.matmul(U[:, c, :], w1[:, 0, c, :], xnT_t[:, bass.ds(i, 1), u, :], start=True,
                                         stop=True).then_inc(opened, 1)
                    if u:
                        close(i, 0)
                close(i, 1)
            pe.wait_ge(y_read, done(GROUPS - 1))

            def turn(e):
                pe.wait_ge(fetched[e % 3], 32 * (e // 3 + 1))
                if e:
                    pe.wait_ge(xgT_ready, e)
                for k, (at, m) in enumerate(tiles):
                    ins = nc.tensor.transpose(tr[:, at:at + m], xg[0:m, e % 3, k, :], C.ident[0:m, 0:m])
                ins.then_inc(turned, 1)

            turn(0)
            for e in range(E8 + 1):
                if e < E8:
                    pe.wait_ge(xgT_ready, e + 1)
                    for c in range(NC):
                        if e >= 1:
                            pe.wait_ge(e_active, NC * (e - 1) + c + 1)
                        nc.tensor.matmul(U[:, c, 0:CAPACITY], w1[:, e + 1, c, :], xgT[:, e % 2, :], start=True,
                                         stop=True).then_inc(e_opened, 1)
                    if e + 1 < E8:
                        turn(e + 1)
                if e >= 1:
                    if e >= 3:
                        pe.wait_ge(yg_ready, e - 2)
                    pe.wait_ge(e_active, NC * e)
                    for k, (at, m) in enumerate(tiles):
                        for c in range(NC):
                            ins = nc.tensor.matmul(Y[0:m, (e - 1) % 2, k * P:(k + 1) * P],
                                                   aT[:, (e - 1) % 2, c, at:at + m], w2[:, e, c, :],
                                                   start=(c == 0), stop=(c == NC - 1))
                    ins.then_inc(e_closed, 1)



ROWS = [("gates", 8), ("alpha", 4), ("L1_bo", P), ("L1_bv", P), ("L2_bo", P), ("L2f_bg", 4),
        ("mod_gate", 1), ("L3_film", 512), ("L3_g_in", P), ("L3_b_in", P), ("L3_g_out", P), ("L3_b_out", P), ("L3_b2", P),
        ("L3f_b2", 9 * P)]
SECTIONS = {
    "const": [("ident", P), ("mask16", HEADS), ("iota8", 8), ("ones8", 8), ("minus_half", 4), ("reverse", P),
              ("head_mask", H3), ("upto", P), ("ones", P)],
    "x0": [("L0_q", P), ("L0_o", P)],
    "x1": [("L1_q", P), ("L1_o", P), ("L1_bq", 1), ("L1_bk", 1)],
    "x2": [("L2_q", INNER), ("L2_o", INNER)],
    "f0": [("L0f_router", 8), ("L0f_sgate", 256), ("L0f_sup", 256), ("L0f_sdown", 256),
           ("L0f_gate", 4096), ("L0f_up", 4096), ("L0f_down", 4096)],
    "f1": [("L1f_router", 8), ("L1f_sgate", 256), ("L1f_sup", 256), ("L1f_sdown", 256),
           ("L1f_gate", 1024), ("L1f_up", 1024), ("L1f_down", 1024)],
}
LATER = {
    "f2": [("Wi", 512), ("Wo", 512), ("Wg", 4)],
    "f3": [("router", 8), ("W1", 9 * 512), ("W2", 9 * 512), ("b1", 9 * 4)],
}
LAST = {
    "x3": [("q", P), ("film", 512), ("g_ffn", 1), ("b_ffn", 1), ("W1", 512), ("b1", 4), ("W2", 512), ("log_dt", 1),
           ("D_skip", 1), ("A_re", NS), ("A_im", NS), ("C_re", NS), ("C_im", NS)],
}
LATE = len(LATER)
SECTION96 = [("L0_k", P), ("L0_v", P), ("L1_k", P), ("L1_v", P),
             ("L2_k", INNER), ("L2_v", INNER), ("L2_ki", INNER), ("L2_vi", INNER), ("L3_k", P), ("L3_v", P)]
SECTION32 = [("q_down", P), ("k_down", KV), ("v_down", KV), ("o_down", INNER),
             ("q_up", INNER), ("k_up", INNER), ("v_up", INNER), ("o_up", P)]
SECTION4 = [("A", 512), ("B", 2048)]
ROW_PLACE, ROW_N = columns(ROWS)
PLACES = {s: columns(parts) for s, parts in SECTIONS.items()}
LATER_PLACES = {s: columns(parts) for s, parts in LATER.items()}
LAST_PLACES = {s: columns(parts) for s, parts in LAST.items()}
PLACE32, N32 = columns(SECTION32)
PLACE4, N4 = columns(SECTION4)
PLACE96, N96 = columns(SECTION96)


def load_later(nc, C, later, dram):
    with nc.Block() as block:
        @block.sync
        def _(sp):
            for s, packed in later.items():
                sp.dma_start(packed.tile, dram[f"sec_{s}"]).then_inc(C.late_landed, 16)


def program(nc, dram, out):
    with ExitStack() as ctx:
        C = Core()
        X = ctx.enter_context(nc.sbuf_tensor("X", [P, NB * P], F32))
        rows = ctx.enter_context(nc.sbuf_tensor("rows", [P, ROW_N], F32))
        w96 = ctx.enter_context(nc.sbuf_tensor("w96", [KV, N96], F32))
        tgs = ctx.enter_context(nc.sbuf_tensor("tgs", [P, 8], F32))
        sec = {}
        for s, (place, n) in PLACES.items():
            sec[s] = Packed(ctx.enter_context(nc.sbuf_tensor(f"sec_{s}", [P, n], F32)), place)
        landed = ctx.enter_context(nc.semaphore("landed"))
        C.last_landed = ctx.enter_context(nc.semaphore("last_landed"))
        C.late_landed = ctx.enter_context(nc.semaphore("late_landed"))
        C.v_ipa_dram = nc.dram_tensor("v_ipa", (P, INNER), F32, kind="Internal").ap()
        C.expert_in = nc.dram_tensor("expert_in", (EXPERT_ROWS, P), F32, kind="Internal").ap()
        C.expert_out = nc.dram_tensor("expert_out", (EXPERT_ROWS, P), F32, kind="Internal").ap()
        C.kpad_dram = nc.dram_tensor("kpad", (P, 2 * P), F32, kind="Internal").ap()
        C.ctT_v = nc.dram_tensor("ctT", (P, NB * P), F32, kind="Internal").ap().rearrange(
            "p (i u t) -> p i u t", i=TURNS, u=2)
        kv_mask = ctx.enter_context(nc.sbuf_tensor("kv_mask", [P, NB * P], U8))
        C.kv_mask_v = kv_mask[:, :].rearrange("p (i b t) -> p i b t", i=TURNS, b=BODY)
        q_mask8 = ctx.enter_context(nc.sbuf_tensor("q_mask8", [P, NB], U8))
        q_mask = ctx.enter_context(nc.sbuf_tensor("q_mask", [P, NB], F32))
        C.q_mask_v = q_mask[:, :].rearrange("p (i b) -> p i b", i=TURNS)
        C.v_ipa_v = C.v_ipa_dram.rearrange("(i u b t) n -> t i u b n", i=TURNS, u=2, b=GRP)
        tanh_done = ctx.enter_context(nc.semaphore("tanh_done"))
        stored = ctx.enter_context(nc.semaphore("stored"))

        C.X = X
        C.carrier = ctx.enter_context(nc.sbuf_tensor("carrier", [P, 1], F32))
        C.Xt = X[:, :].rearrange("p (i b d) -> p i b d", i=TURNS, b=BODY)
        C.ctxT_v = dram["ctxT"].rearrange("c (i u t) -> c i u t", i=TURNS, u=2)
        C.rows = Packed(rows, ROW_PLACE)
        K = sec["const"]
        C.ident, C.mask16, C.iota8, C.ones8, C.minus_half, C.reverse, C.head_mask, C.upto, C.ones = (
            K[n] for n in ("ident", "mask16", "iota8", "ones8", "minus_half", "reverse", "head_mask", "upto", "ones"))
        W96 = Packed(w96, PLACE96)

        at, later = 0, {}
        for s, (place, n) in LATER_PLACES.items():
            later[s] = Packed(sec["f0"].tile[:, at:at + n], place)
            at += n
        place, n = LAST_PLACES["x3"]
        x3 = Packed(sec["f1"].tile[:, 0:n], place)
        C.f2 = dict(later["f2"].items())
        C.f2["We"] = sec["f0"].tile[:, at:at + 4 * 512]

        with nc.Block() as block:
            @block.sync
            def _(sp):
                n = 0
                for dst, src in [(X[:, :], dram["x"]), (rows[:, :], dram["rows"].partition_broadcast(P)),
                                 (kv_mask[:, :], dram["kv_mask"].partition_broadcast(P)), (q_mask8[:, :], dram["q_mask"]),
                                 (w96[:, :], dram["w96"])] + [(sec[s].tile[:, :], dram[f"sec_{s}"]) for s in SECTIONS]:
                    sp.dma_start(dst, src).then_inc(landed, 16)
                    n += 16
                sp.wait_ge(landed, n)

            @block.scalar
            def _(act):
                act.wait_ge(landed, 16 * (5 + len(SECTIONS)))
                nc.scalar.activation(tgs[:, :], C.rows["gates"], ACT.Tanh).then_inc(tanh_done, 1)
                nc.scalar.activation(q_mask[:, :], q_mask8[:, :], ACT.Identity).then_inc(tanh_done, 1)
                act.wait_ge(tanh_done, 2)

        tg = lambda n: tgs[:, n:n + 1]
        if STAGES > 0:
            attention16(nc, C, "L0", sec["x0"], sec["x0"]["L0_q"], W96["L0_k"], W96["L0_v"], sec["x0"]["L0_o"], tg(0), False)
        if STAGES > 1:
            gated_experts(nc, C, "L0f", sec["f0"], 4, tg(4))
        if STAGES > 2:
            load_later(nc, C, later, dram)
            attention16(nc, C, "L1", sec["x1"], sec["x1"]["L1_q"], W96["L1_k"], W96["L1_v"], sec["x1"]["L1_o"], tg(1), True)
        if STAGES > 3:
            gated_experts(nc, C, "L1f", sec["f1"], 1, tg(5))
        if STAGES > 4:
            merge_lora(nc, C, sec["x2"], W96, x3, dram)
            attention_ipa(nc, C, sec["x2"], W96, tg(2))
        if STAGES > 5:
            shared_experts(nc, C, tg(6))
        if STAGES > 6:
            with nc.sbuf_tensor("xin", [P, NB * P], F32) as xin:
                convolution_kernel(nc, C, x3, C.rows)
                attention_top32(nc, C, x3, W96, xin)
                convolve(nc, C, xin)
                film_feed_forward(nc, C, x3, xin, tg(3))
        if STAGES > 7:
            with (nc.sbuf_tensor("wt", [P, 3, NB], F32) as wt, nc.sbuf_tensor("slot", [P, 2, NB], U32) as slot,
                  nc.sbuf_tensor("xn", [P, NB * P], F32) as xn, nc.sbuf_tensor("xnT", [P, NB * P], F32) as xnT):
                route_with_capacity(nc, C, later["f3"], tg(7), wt, slot, xn, xnT)
                capacity_experts(nc, C, later["f3"], wt, slot, xn, xnT)

        with nc.Block() as block:
            @block.sync
            def _(sp):
                sp.dma_start(out, X[:, :]).then_inc(stored, 16)
                sp.wait_ge(stored, 16)


STAGES = 8


def kernel(**inputs):
    import numpy as np
    import concourse.bacc as _bacc
    from concourse.bass_utils import run_bass_kernel_spmd as _run

    I = {k: np.asarray(v) for k, v in inputs.items()}
    f = np.arange(P)

    def chunked(w):
        e = w.reshape(-1, w.shape[-2] // P, P, w.shape[-1])
        return e.transpose(2, 0, 1, 3).reshape(P, -1)

    def stacked(w):
        return w.transpose(1, 0, 2).reshape(w.shape[1], -1)

    part = {
        "ident": np.eye(P, dtype=np.float32),
        "mask16": (f[:, None] // HD == np.arange(HEADS)).astype(np.float32),
        "iota8": np.tile(np.arange(8, dtype=np.float32), (P, 1)),
        "ones8": np.ones((P, 8), np.float32),
        "minus_half": np.full((P, 4), -0.5, np.float32),
        "L0_q": I["L0_xattn_Wq"].T, "L0_o": I["L0_xattn_Wo"].T,
        "L0_k": I["L0_xattn_Wk"].T, "L0_v": I["L0_xattn_Wv"].T,
        "L1_q": I["L1_xattn_Wq"], "L1_o": I["L1_xattn_Wo"], "L1_k": I["L1_xattn_Wk"], "L1_v": I["L1_xattn_Wv"],
        "L1_bq": I["L1_xattn_bq"][:, None], "L1_bk": I["L1_xattn_bk"][:, None],
        "L0f_router": I["L0_ffn_gate_w"].T, "L0f_sgate": I["L0_ffn_sh_gate"], "L0f_sup": I["L0_ffn_sh_up"],
        "L0f_sdown": chunked(I["L0_ffn_sh_down"]), "L0f_gate": stacked(I["L0_ffn_gate_k"]),
        "L0f_up": stacked(I["L0_ffn_up_k"]), "L0f_down": chunked(I["L0_ffn_down_k"]),
        "L1f_router": I["L1_ffn_router_w"], "L1f_sgate": I["L1_ffn_shared_gate_w"],
        "L1f_sup": I["L1_ffn_shared_up_w"], "L1f_sdown": chunked(I["L1_ffn_shared_down_w"]),
        "L1f_gate": stacked(I["L1_ffn_gate_w"]), "L1f_up": stacked(I["L1_ffn_up_w"]),
        "L1f_down": chunked(I["L1_ffn_down_w"]),
        "L2_q": I["L2_xattn_Wq"], "L2_o": chunked(I["L2_xattn_Wo"]),
        "L2_k": I["L2_xattn_Wk"], "L2_v": I["L2_xattn_Wv"],
        "L2_ki": I["L2_xattn_Wk_ipa"], "L2_vi": I["L2_xattn_Wv_ipa"],
        "q_down": I["L2_xattn_q_down"].T, "k_down": I["L2_xattn_k_down"].T, "v_down": I["L2_xattn_v_down"].T,
        "o_down": I["L2_xattn_o_down"].T, "q_up": I["L2_xattn_q_up"], "k_up": I["L2_xattn_k_up"],
        "v_up": I["L2_xattn_v_up"], "o_up": I["L2_xattn_o_up"], "L2_bo": I["L2_xattn_bo"],
        "alpha": np.concatenate([I[f"L2_xattn_{n}_alpha"] for n in "qkvo"]),
        "A": I["L2_ffn_A"].transpose(1, 0, 2).reshape(4, 512),
        "B": I["L2_ffn_B"].transpose(2, 0, 1).reshape(4, 2048),
        "Wi": I["L2_ffn_Wi"].T, "Wo": chunked(I["L2_ffn_Wo"].T), "Wg": I["L2_ffn_Wg"].T, "L2f_bg": I["L2_ffn_bg"],
        "reverse": np.ascontiguousarray(np.eye(P, dtype=np.float32)[::-1]),
        "head_mask": (f[:, None] // D3 == np.arange(H3)).astype(np.float32),
        "q": I["L3_xattn_Wq"], "L3_k": I["L3_xattn_Wk"], "L3_v": I["L3_xattn_Wv"],
        "film": np.concatenate([I["L3_xattn_W_film_in"], I["L3_xattn_W_film_out"]], axis=1),
        "g_ffn": I["L3_xattn_g_ffn"][:, None], "b_ffn": I["L3_xattn_b_ffn"][:, None],
        "W1": I["L3_xattn_W1"], "b1": I["L3_xattn_b1"].reshape(4, P).T, "W2": chunked(I["L3_xattn_W2"]),
        "log_dt": I["L3_xattn_log_dt"][:, None], "D_skip": I["L3_xattn_D_skip"][:, None],
        "A_re": I["L3_xattn_A_re"], "A_im": I["L3_xattn_A_im"], "C_re": I["L3_xattn_C_re"], "C_im": I["L3_xattn_C_im"],
        "mod_gate": I["L3_xattn_mod_gate"].reshape(1),
        "L3_film": np.concatenate([I["L3_xattn_b_film_in"], I["L3_xattn_b_film_out"]]),
        "L3_g_in": I["L3_xattn_g_norm_in"], "L3_b_in": I["L3_xattn_b_norm_in"],
        "L3_g_out": I["L3_xattn_g_norm_out"], "L3_b_out": I["L3_xattn_b_norm_out"], "L3_b2": I["L3_xattn_b2"],
        "upto": np.triu(np.ones((P, P), np.float32)), "ones": np.ones((P, P), np.float32),
        "router": I["L3_ffn_Wr"],
        "gates": np.concatenate([I["g_xattn"], I["g_ffn"]]), "L1_bo": I["L1_xattn_bo"], "L1_bv": I["L1_xattn_bv"],
    }

    last = {
        "W1": np.concatenate([I["L3_ffn_fw1"], stacked(I["L3_ffn_W1"])], axis=1),
        "W2": np.concatenate([chunked(I["L3_ffn_fw2"]), chunked(I["L3_ffn_W2"])], axis=1),
        "b1": np.concatenate([I["L3_ffn_fb1"][None], I["L3_ffn_b1"]]).reshape(9, 4, P).transpose(2, 0, 1).reshape(P, 36),
    }
    part["L3f_b2"] = np.concatenate([I["L3_ffn_fb2"], I["L3_ffn_b2"].reshape(-1)])

    def pack(parts, axis, part=part):
        for name, n in parts:
            assert part[name].shape[axis] == n, (name, part[name].shape)
        return np.ascontiguousarray(np.concatenate([part[name] for name, _ in parts], axis=axis))

    arrays = {
        "x": np.ascontiguousarray(I["x"].transpose(1, 0, 2).reshape(P, NB * P)),
        "ctxT": np.ascontiguousarray(I["ctx_768"].transpose(2, 0, 1).reshape(KV, NB * P)),
        "kv_mask": I["mask_BxS2_bf1"].reshape(-1), "q_mask": np.ascontiguousarray(I["mask_BxS_bf1"].T),
        "rows": pack(ROWS, 0), "w96": pack(SECTION96, 1), "w32": pack(SECTION32, 1), "w4": pack(SECTION4, 1),
    }
    for s, parts in {**SECTIONS, **LATER, **LAST}.items():
        arrays[f"sec_{s}"] = pack(parts, 1, {**part, **last} if s == "f3" else part)

    nc = _bacc.Bacc("TRN2", target_bir_lowering=False, num_devices=1)
    dram = {k: nc.dram_tensor(f"in_{k}", v.shape, mybir.dt.from_np(v.dtype), kind="ExternalInput").ap()
            for k, v in arrays.items()}
    out = nc.dram_tensor("out_0", (P, NB * P), F32, kind="ExternalOutput").ap()
    program(nc, dram, out)
    r = _run(nc, [{f"in_{k}": v for k, v in arrays.items()}], core_ids=[0])
    return np.ascontiguousarray(r.results[0]["out_0"].reshape(P, NB, P).transpose(1, 0, 2))
```

```python
from contextlib import ExitStack

import concourse.bass as bass
from concourse import mybir

F32 = mybir.dt.float32
U8 = mybir.dt.uint8
U32 = mybir.dt.uint32
ALU = mybir.AluOpType
ACT = mybir.ActivationFunctionType
AX = mybir.AxisListType

P = 128
NB = 32
KV = 96
BODY = 8
TURNS = NB // BODY
GRP = 4
TOK = GRP * P
EPS = 1e-5


CREDIT = 64


def done(n):
    return n + (CREDIT + 1)


class Steps:

    def __init__(self, sem):
        self.done, self.count = sem, 0

    def one(self):
        self.count += 1
        return 1

    def restart(self):
        self.count = 0


class Alloc:

    def __init__(self, nc, ctx, tag):
        self.nc, self.ctx, self.tag, self.sems = nc, ctx, tag, []
        ctx.callback(self.close)

    def sb(self, name, shape, dt=F32):
        return self.ctx.enter_context(self.nc.sbuf_tensor(f"{self.tag}_{name}", shape, dt))

    def ps(self, name, shape):
        return self.ctx.enter_context(self.nc.psum_tensor(f"{self.tag}_{name}", shape, F32))

    def close(self):
        self.nc.clear_and_free_semaphores(self.sems)
        self.nc.all_engine_barrier()

    def sem(self, name):
        s = self.nc.alloc_semaphore(f"{self.tag}_{name}")
        self.sems.append(s)
        return s


class Core:
    pass


def columns(parts):
    at, out = 0, {}
    for name, n in parts:
        out[name] = (at, n)
        at += n
    return out, at


class Packed:

    def __init__(self, tile, place):
        self.tile, self.place = tile, place

    def __getitem__(self, name):
        at, n = self.place[name]
        return self.tile[:, at:at + n]

    def items(self):
        return [(name, self[name]) for name in self.place]



class Norm:

    def __init__(self, a, tag):
        self.stats = a.sb(f"{tag}_stats", [P, 2, GRP, 6])
        self.mv = a.sb(f"{tag}_mv", [P, 2, GRP, 2])
        self.var = a.sb(f"{tag}_var", [P, 2, GRP])
        self.y0 = a.sb(f"{tag}_y0", [P, 2, GRP])
        self.t = a.sb(f"{tag}_newton", [P, 2, GRP])
        self.rs = a.sb(f"{tag}_rs", [P, 2, GRP])
        self.nm = a.sb(f"{tag}_nm", [P, 2, GRP])
        self.var_ready = a.sem(f"{tag}_var_ready")
        self.root_ready = a.sem(f"{tag}_root_ready")

    def statistics(self, nc, vec, row, u):
        for k in range(GRP):
            nc.vector.bn_stats(self.stats[:, u, k, :], row(k)).then_inc(vec.done, vec.one())
        nc.vector.wait_ge(vec.done, vec.count)
        for k in range(GRP):
            nc.vector.bn_aggr(self.mv[:, u, k, :], self.stats[:, u, k, :]).then_inc(vec.done, vec.one())
        nc.vector.wait_ge(vec.done, vec.count)
        nc.vector.tensor_scalar(self.var[:, u, :], self.mv[:, u, :, 1], EPS, None, ALU.add).then_inc(
            self.var_ready, 1)

    def root(self, nc, pool, C, i, u):
        pool.wait_ge(self.var_ready, done(2 * i + u))
        nc.gpsimd.tensor_tensor(self.y0[:, u, :], self.var[:, u, :], C.minus_half[:, :], ALU.pow).then_inc(
            self.root_ready, 1)

    def affine(self, nc, v, vec, i, u):
        y0, var, t, rs, nm = (x[:, u, :] for x in (self.y0, self.var, self.t, self.rs, self.nm))
        v.wait_ge(self.root_ready, done(2 * i + u))
        nc.vector.tensor_tensor(t, y0, y0, ALU.mult).then_inc(vec.done, vec.one())
        nc.vector.wait_ge(vec.done, vec.count)
        nc.vector.tensor_tensor(t, t, var, ALU.mult).then_inc(vec.done, vec.one())
        nc.vector.wait_ge(vec.done, vec.count)
        nc.vector.tensor_scalar(t, t, -0.5, 1.5, ALU.mult, ALU.add).then_inc(vec.done, vec.one())
        nc.vector.wait_ge(vec.done, vec.count)
        nc.vector.tensor_tensor(rs, t, y0, ALU.mult).then_inc(vec.done, vec.one())
        nc.vector.wait_ge(vec.done, vec.count)
        nc.vector.scalar_tensor_tensor(out=nm, in0=self.mv[:, u, :, 0], scalar=-1.0, in1=rs,
                                               op0=ALU.mult, op1=ALU.mult).then_inc(vec.done, vec.one())
        nc.vector.wait_ge(vec.done, vec.count)

    def apply(self, nc, dst, src, u, k):
        return nc.vector.tensor_scalar(dst, src, self.rs[:, u, k:k + 1], self.nm[:, u, k:k + 1], ALU.mult, ALU.add)


class Front:

    def __init__(self, a):
        self.st = a.sb("st", [P, 2, GRP, P])
        self.xnT = a.sb("xnT", [P, 2, TOK])
        self.N = Norm(a, "x")
        self.root_ready = self.N.root_ready
        self.st_ready = a.sem("st_ready")
        self.turned = a.sem("turned")
        self.xnT_ready = a.sem("xnT_ready")

    def open_vector(self, v):
        v.sem_inc(self.N.var_ready, CREDIT)
        v.sem_inc(self.st_ready, CREDIT)

    def statistics(self, nc, v, vec, C, i, u):
        self.N.statistics(nc, vec, lambda k: C.Xt[:, bass.ds(i, 1), GRP * u + k, :], u)

    def root(self, nc, pool, C, i, u):
        self.N.root(nc, pool, C, i, u)

    def normalise(self, nc, v, vec, C, i, u):
        self.N.affine(nc, v, vec, i, u)
        v.wait_ge(self.turned, done(2 * i + u - 2))
        for k in range(GRP):
            ins = self.N.apply(nc, self.st[:, u, k, :], C.Xt[:, bass.ds(i, 1), GRP * u + k, :], u, k)
        ins.then_inc(self.st_ready, 1)

    def turn(self, nc, pe, C, i, u, bank):
        pe.wait_ge(self.st_ready, done(2 * i + u))
        for k in range(GRP):
            ins = nc.tensor.transpose(bank[:, k * P:(k + 1) * P], self.st[:, u, k, :], C.ident)
        ins.then_inc(self.turned, 1)

    def take(self, nc, act, C, i, u, bank):
        act.wait_ge(self.turned, done(2 * i + u))
        nc.scalar.activation(self.xnT[:, u, :], bank, ACT.Identity).then_inc(self.xnT_ready, 1)



HD = 8
HEADS = 16
QUAD = 4
CLAMP = 10000.0


def of_turn(i, n, count, each):
    m = n // each
    return (i - 1, m + count) if m < 0 else (i, m)


def attention16(nc, C, tag, W, wqT, wkT, wvT, woT, tg, affine, background=(), background_landed=None):
    units = BODY * QUAD

    def due(n, first):
        return (n >= 0 or not first) and n < units

    scale = HD ** -0.5
    with ExitStack() as ctx:
        a = Alloc(nc, ctx, tag)
        F = Front(a)
        ctxT = a.sb("ctxT", [KV, 2, TOK])
        qT = a.sb("qT", [P, 2, TOK])
        kT = a.sb("kT", [P, 2, TOK])
        kx = a.sb("kx", [P, 2, HEADS, P])
        V = a.sb("V", [P, 2, GRP * HEADS, HD + 1])
        mx = a.sb("mx", [P, 4, QUAD])
        pr = a.sb("pr", [P, 4, QUAD, P])
        pT = a.sb("pT", [P, 2, QUAD, P])
        rden = a.sb("rden", [P, HEADS])
        on = a.sb("on", [P, 2, P])
        oT = a.sb("oT", [P, 2, P])
        bqs = a.sb("bqs", [P, 1])
        res = a.sb("res", [P, P])
        pj = a.ps("pj", [P, 2, 512])
        S = a.ps("S", [P, 2, 512])
        T = a.ps("T", [P, 2, 512])
        O = a.ps("O", [P, 512])
        tail = a.ps("tail", [P, 512])
        Ov = O[:, 0:HEADS * (HD + 1)].rearrange("p (h e) -> p h e", e=HD + 1)
        oTp, outp = tail[:, 0:P], tail[:, P:2 * P]

        ctx_in = [a.sem(f"ctx_in{u}") for u in range(2)]
        once = a.sem("once")
        projected = a.sem("projected")
        q_ready = a.sem("q_ready")
        k_ready = a.sem("k_ready")
        v_ready = a.sem("v_ready")
        spread = a.sem("spread")
        scored = a.sem("scored")
        shifted = a.sem("shifted")
        exped = a.sem("exped")
        flipped = a.sem("flipped")
        pT_ready = a.sem("pT_ready")
        weighed = a.sem("weighed")
        normed = a.sem("normed")
        oT_done = a.sem("oT_done")
        oT_ready = a.sem("oT_ready")
        out_done = a.sem("out_done")
        added = a.sem("added")
        own = a.sem("own")

        block = ctx.enter_context(nc.Block())

        @block.sync
        def _(sp):
            def context(i, u):
                sp.dma_start(ctxT[:, u, :], C.ctxT_v[:, bass.ds(i, 1), u, :]).then_inc(ctx_in[u], 16)

            for u in range(2):
                context(0, u)
            for dst, src in background:
                sp.dma_start(dst, src).then_inc(background_landed, 16)
            with sp.Fori(1, TURNS) as i:
                for u in range(2):
                    sp.wait_ge(projected, done(6 * i + 3 * u - 4))
                    context(i, u)

        @block.gpsimd
        def _(pool):
            pool.sem_inc(F.root_ready, CREDIT)
            pool.sem_inc(spread, CREDIT)
            nc.gpsimd.memset(V[:, :, :, HD:HD + 1], 1.0).then_inc(once, 1)

            def keys(i, b):
                u, k = divmod(b, GRP)
                pool.wait_ge(k_ready, done(2 * i + u))
                pool.wait_ge(scored, done(units * i + QUAD * (b - 2) + QUAD - 1))
                for half in range(2):
                    heads = slice(8 * half, 8 * half + 8)
                    nc.gpsimd.tensor_tensor(
                        kx[:, b % 2, heads, :], kT[:, u, k * P:(k + 1) * P].unsqueeze(1).to_broadcast([P, 8, P]),
                        C.mask16[:, heads].unsqueeze(2).to_broadcast([P, 8, P]), ALU.mult).then_inc(spread, 1)

            def front(i):
                for u in range(2):
                    F.root(nc, pool, C, i, u)

            def turn(i, last):
                for b in range(2, BODY):
                    keys(i, b)
                    if b == 4 and not last:
                        front(i + 1)
                if not last:
                    keys(i + 1, 0)
                    keys(i + 1, 1)

            front(0)
            keys(0, 0)
            keys(0, 1)
            with pool.Fori(0, TURNS - 1) as i:
                turn(i, False)
            turn(TURNS - 1, True)

        @block.vector
        def _(v):
            F.open_vector(v)
            v.sem_inc(shifted, CREDIT)
            v.sem_inc(normed, CREDIT)
            v.sem_inc(added, CREDIT)
            vec = Steps(own)
            if affine:
                v.sem_inc(v_ready, CREDIT)
                nc.vector.tensor_scalar(bqs[:, :], W["L1_bq"], scale, None, ALU.mult).then_inc(once, 1)

            def values(i, u):
                v.wait_ge(projected, done(6 * i + 3 * u + 2))
                nc.vector.tensor_tensor(
                    V[:, u, :, 0:HD].rearrange("p (b h) e -> p b h e", b=GRP),
                    pj[:, u, :].rearrange("p (b h e) -> p b h e", b=GRP, e=HD),
                    C.rows["L1_bv"].rearrange("p (h e) -> p h e", e=HD).unsqueeze(1)
                    .to_broadcast([P, GRP, HEADS, HD]), ALU.add).then_inc(v_ready, 1)

            def normalise(i, b):
                v.wait_ge(weighed, done(units * i + QUAD * b + QUAD - 1))
                nc.vector.reciprocal(rden[:, :], Ov[:, :, HD]).then_inc(vec.done, vec.one())
                v.wait_ge(oT_done, done(BODY * i + b - 2))
                nc.vector.wait_ge(vec.done, vec.count)
                nc.vector.tensor_tensor(
                    on[:, b % 2, :].rearrange("p (h e) -> p h e", e=HD), Ov[:, :, 0:HD],
                    rden[:, :].unsqueeze(2).to_broadcast([P, HEADS, HD]), ALU.mult).then_inc(normed, 1)

            def shift(i, s):
                n = units * i + s
                v.wait_ge(flipped, done(n - 4))
                v.wait_ge(scored, done(n))
                bank = S[:, s % 2, :].rearrange("p (j t) -> p j t", j=QUAD)
                if affine:
                    nc.vector.tensor_scalar(pr[:, s % 4, :, :], bank, CLAMP, -CLAMP, ALU.min, ALU.max).then_inc(vec.done, vec.one())
                    nc.vector.wait_ge(vec.done, vec.count)
                    bank = pr[:, s % 4, :, :]
                nc.vector.tensor_reduce(mx[:, s % 4, :], bank, AX.X, ALU.max).then_inc(vec.done, vec.one())
                nc.vector.wait_ge(vec.done, vec.count)
                nc.vector.tensor_tensor(pr[:, s % 4, :, :], bank,
                                        mx[:, s % 4, :].unsqueeze(2).to_broadcast([P, QUAD, P]),
                                        ALU.subtract).then_inc(shifted, 1)

            def residual(i, b):
                v.wait_ge(out_done, done(BODY * i + b))
                src = outp
                if affine:
                    nc.vector.tensor_tensor(res[:, :], outp, C.rows["L1_bo"], ALU.add).then_inc(vec.done, vec.one())
                    nc.vector.wait_ge(vec.done, vec.count)
                    src = res[:, :]
                x = C.Xt[:, bass.ds(i, 1), b, :]
                nc.vector.scalar_tensor_tensor(out=x, in0=src, scalar=tg, in1=x, op0=ALU.mult,
                                               op1=ALU.add).then_inc(added, 1)

            def turn(i, first, last):
                if affine:
                    values(i, 0)
                for s in range(units + (9 if last else 0)):
                    if s % QUAD == 0 and due(s - 8, first):
                        normalise(*of_turn(i, s - 8, BODY, QUAD))
                    if s == 10 and affine:
                        values(i, 1)
                    if s < units:
                        shift(i, s)
                    if s % QUAD == 0 and due(s - 12, first):
                        residual(*of_turn(i, s - 12, BODY, QUAD))
                    if not last and s in (14, 15):
                        F.statistics(nc, v, vec, C, i + 1, s - 14)
                    if not last and s in (18, 19):
                        F.normalise(nc, v, vec, C, i + 1, s - 18)
                v.wait_ge(vec.done, vec.count)
                v.sem_clear(vec.done)
                vec.restart()

            for u in range(2):
                F.statistics(nc, v, vec, C, 0, u)
            for u in range(2):
                F.normalise(nc, v, vec, C, 0, u)
            v.wait_ge(vec.done, vec.count)
            v.sem_clear(vec.done)
            vec.restart()
            turn(0, True, False)
            with v.Fori(1, TURNS - 1) as i:
                turn(i, False, False)
            turn(TURNS - 1, False, True)
            v.wait_ge(added, done(NB - 1))

        @block.scalar
        def _(act):
            act.sem_inc(F.xnT_ready, CREDIT)
            act.sem_inc(q_ready, CREDIT)
            act.sem_inc(k_ready, CREDIT)
            act.sem_inc(exped, CREDIT)
            act.sem_inc(pT_ready, CREDIT)
            act.sem_inc(oT_ready, CREDIT)
            if affine:
                act.wait_ge(once, 2)
            else:
                act.sem_inc(v_ready, CREDIT)
                act.wait_ge(once, 1)

            def project(i, u):
                act.wait_ge(projected, done(6 * i + 3 * u))
                nc.scalar.activation(qT[:, u, :], pj[:, u, :], ACT.Identity, scale=scale,
                                     bias=bqs[:, 0:1] if affine else 0.0).then_inc(q_ready, 1)
                act.wait_ge(spread, done(2 * (BODY * i + GRP * u + 3 - BODY) + 1))
                act.wait_ge(projected, done(6 * i + 3 * u + 1))
                nc.scalar.activation(kT[:, u, :], pj[:, 1 - u, :], ACT.Identity,
                                     bias=W["L1_bk"] if affine else 0.0).then_inc(k_ready, 1)
                if not affine:
                    act.wait_ge(projected, done(6 * i + 3 * u + 2))
                    nc.scalar.activation(V[:, u, :, 0:HD], pj[:, u, :].rearrange("p (n e) -> p n e", e=HD),
                                         ACT.Identity).then_inc(v_ready, 1)

            def front(i):
                for u in range(2):
                    F.take(nc, act, C, i, u, pj[:, u, :])

            def turn(i, first, last):
                for s in range(units + (7 if last else 0)):
                    n = units * i + s
                    if s == 10:
                        project(i, 1)
                    if s == 24 and not last:
                        front(i + 1)
                    if s == units - 1 and not last:
                        project(i + 1, 0)
                    if s < units:
                        act.wait_ge(shifted, done(n))
                        nc.scalar.activation(pr[:, s % 4, :, :], pr[:, s % 4, :, :], ACT.Exp).then_inc(exped, 1)
                    if due(s - 2, first):
                        m = s - 2
                        act.wait_ge(weighed, done(n - 4))
                        act.wait_ge(flipped, done(n - 2))
                        nc.scalar.activation(pT[:, m % 2, :, :], T[:, m % 2, :].rearrange("p (j t) -> p j t", j=QUAD),
                                             ACT.Identity).then_inc(pT_ready, 1)
                    if s % QUAD == 2 and due(s - 10, first):
                        b = (s - 10) // QUAD
                        act.wait_ge(out_done, done(BODY * i + b - 2))
                        act.wait_ge(oT_done, done(BODY * i + b))
                        nc.scalar.activation(oT[:, b % 2, :], oTp, ACT.Identity).then_inc(oT_ready, 1)

            front(0)
            project(0, 0)
            turn(0, True, False)
            with act.Fori(1, TURNS - 1) as i:
                turn(i, False, False)
            turn(TURNS - 1, False, True)

        @block.tensor
        def _(pe):
            pe.sem_inc(F.turned, CREDIT)
            for x in (projected, scored, flipped, weighed, oT_done, out_done):
                pe.sem_inc(x, CREDIT)
            pe.wait_ge(once, 2 if affine else 1)

            def project(i, u):
                g = 2 * i + u
                pe.wait_ge(F.xnT_ready, done(2 * i + 1))
                if u:
                    pe.wait_ge(k_ready, done(2 * i))
                nc.tensor.matmul(pj[:, u, :], wqT, F.xnT[:, u, :], start=True, stop=True).then_inc(projected, 1)
                pe.wait_ge(ctx_in[u], 16 * i + 16)
                if u:
                    pe.wait_ge(v_ready, done(2 * i))
                nc.tensor.matmul(pj[:, 1 - u, :], wkT, ctxT[:, u, :], start=True, stop=True).then_inc(projected, 1)
                pe.wait_ge(q_ready, done(g))
                for k in range(GRP):
                    ins = nc.tensor.matmul(pj[:, u, k * P:(k + 1) * P], ctxT[:, u, k * P:(k + 1) * P], wvT,
                                           start=True, stop=True)
                ins.then_inc(projected, 1)

            def front(i):
                pe.wait_ge(k_ready, done(2 * i - 1))
                F.turn(nc, pe, C, i, 0, pj[:, 0, :])
                pe.wait_ge(v_ready, done(2 * i - 1))
                F.turn(nc, pe, C, i, 1, pj[:, 1, :])

            def turn(i, first, last):
                for s in range(units + (8 if last else 0)):
                    n = units * i + s
                    if s == 10:
                        project(i, 1)
                    if s == 23 and not last:
                        front(i + 1)
                    if s == units - 1 and not last:
                        project(i + 1, 0)
                    if s < units:
                        b, r = divmod(s, QUAD)
                        u, k = divmod(b, GRP)
                        if r == 0:
                            pe.wait_ge(q_ready, done(2 * i + u))
                        if r % 2 == 0:
                            pe.wait_ge(spread, done(2 * (BODY * i + b) + r // 2))
                        pe.wait_ge(shifted, done(n - 2))
                        nc.tensor.matmul(S[:, s % 2, :], qT[:, u, k * P:(k + 1) * P],
                                         kx[:, b % 2, QUAD * r:QUAD * r + QUAD, :],
                                         start=True, stop=True).then_inc(scored, 1)
                    if due(s - 2, first):
                        m = s - 2
                        pe.wait_ge(pT_ready, done(n - 4))
                        pe.wait_ge(exped, done(n - 2))
                        for j in range(QUAD):
                            ins = nc.tensor.transpose(T[:, m % 2, j * P:(j + 1) * P], pr[:, m % 4, j, :], C.ident)
                        ins.then_inc(flipped, 1)
                    if due(s - 4, first):
                        m = s - 4
                        b, r = divmod(m, QUAD)
                        u, k = divmod(b % BODY, GRP)
                        if r == 0:
                            pe.wait_ge(v_ready, done(2 * i + b // GRP))
                            pe.wait_ge(normed, done(BODY * i + b - 1))
                        pe.wait_ge(pT_ready, done(n - 4))
                        for j in range(QUAD):
                            h = QUAD * r + j
                            ins = nc.tensor.matmul(Ov[:, h, :], pT[:, m % 2, j, :], V[:, u, k * HEADS + h, :],
                                                   start=True, stop=True)
                        ins.then_inc(weighed, 1)
                    if s % QUAD == 1 and due(s - 9, first):
                        b = (s - 9) // QUAD
                        pe.wait_ge(added, done(BODY * i + b - 1))
                        pe.wait_ge(normed, done(BODY * i + b))
                        nc.tensor.transpose(oTp, on[:, b % 2, :], C.ident).then_inc(oT_done, 1)
                    if s % QUAD == 3 and due(s - 11, first):
                        b = (s - 11) // QUAD
                        pe.wait_ge(oT_ready, done(BODY * i + b))
                        nc.tensor.matmul(outp, oT[:, b % 2, :], woT, start=True, stop=True).then_inc(out_done, 1)

            front(0)
            project(0, 0)
            turn(0, True, False)
            with pe.Fori(1, TURNS - 1) as i:
                turn(i, False, False)
            turn(TURNS - 1, False, True)



E8 = 8


class Router:

    def __init__(self, a, n):
        self.n = n
        self.lg = a.sb("lg", [P, BODY, E8])
        self.top = a.sb("top", [P, BODY, 8])
        self.idx = a.sb("idx", [P, BODY, 8], U32)
        self.idf = a.sb("idf", [P, BODY, 2])
        self.ex = a.sb("ex", [P, BODY, E8])
        self.m0 = a.sb("m0", [P, BODY, E8])
        self.m1 = a.sb("m1", [P, BODY, E8])
        self.sum = a.sb("sum", [P, BODY])
        self.rcp = a.sb("rcp", [P, BODY])
        self.shift_done = a.sem("rt_shift")
        self.exp_done = a.sem("rt_exp")

    def choose(self, nc, v, vec, C, i):
        for b in range(BODY):
            nc.vector.max(self.top[:, b, :], self.lg[:, b, :]).then_inc(vec.done, vec.one())
        nc.vector.wait_ge(vec.done, vec.count)
        for b in range(BODY):
            nc.vector.max_index(self.idx[:, b, :], self.top[:, b, :], self.lg[:, b, :]).then_inc(vec.done, vec.one())
        nc.vector.tensor_tensor(self.ex[:, :, :], self.lg[:, :, :], self.top[:, :, 0:1].to_broadcast([P, BODY, E8]),
                                ALU.subtract).then_inc(self.shift_done, 1)
        nc.vector.wait_ge(vec.done, vec.count)
        nc.vector.tensor_copy(self.idf[:, :, :], self.idx[:, :, 0:2]).then_inc(vec.done, vec.one())
        nc.vector.wait_ge(vec.done, vec.count)
        for m, j in ((self.m0, 0), (self.m1, 1)):
            nc.vector.tensor_tensor(m[:, :, :], C.iota8.unsqueeze(1).to_broadcast([P, BODY, E8]),
                                            self.idf[:, :, j:j + 1].to_broadcast([P, BODY, E8]), ALU.is_equal).then_inc(vec.done, vec.one())
        nc.vector.wait_ge(vec.done, vec.count)
        nc.vector.tensor_tensor(self.m0[:, :, :], self.m0[:, :, :], self.m1[:, :, :], ALU.add).then_inc(vec.done, vec.one())

    def exponentials(self, nc, act, i):
        act.wait_ge(self.shift_done, done(i))
        nc.scalar.activation(self.ex[:, :, :], self.ex[:, :, :], ACT.Exp).then_inc(self.exp_done, 1)

    def probabilities(self, nc, v, vec, i):
        v.wait_ge(self.exp_done, done(i))
        nc.vector.tensor_reduce(self.sum[:, :], self.ex[:, :, :], AX.X, ALU.add).then_inc(vec.done, vec.one())
        nc.vector.wait_ge(vec.done, vec.count)
        nc.vector.reciprocal(self.rcp[:, :], self.sum[:, :]).then_inc(vec.done, vec.one())
        nc.vector.tensor_tensor(self.m1[:, :, :], self.ex[:, :, :], self.m0[:, :, :], ALU.mult).then_inc(vec.done, vec.one())
        nc.vector.wait_ge(vec.done, vec.count)


def gated_experts(nc, C, tag, W, nf, tg):
    with ExitStack() as ctx:
        a = Alloc(nc, ctx, tag)
        F = Front(a)
        R = Router(a, BODY)
        wt = a.sb("wt", [P, BODY, E8 + 1])
        sg = a.sb("sg", [P, 2, TOK])
        aT = a.sb("aT", [P, 2, max(nf, 2), TOK])
        tr = a.ps("tr", [P, 512])
        lgp = a.ps("lgp", [P, 512])
        G = a.ps("G", [P, 2, 512])
        U = a.ps("U", [P, 2, 512])
        Y = a.ps("Y", [P, 2, 512])
        gate = W[f"{tag}_gate"].rearrange("p (e c f) -> p e c f", e=E8, c=nf)
        up = W[f"{tag}_up"].rearrange("p (e c f) -> p e c f", e=E8, c=nf)
        down = W[f"{tag}_down"].rearrange("p (e c d) -> p e c d", e=E8, c=nf)
        sgate, sup, sdown = (W[f"{tag}_s{x}"].rearrange("p (c f) -> p c f", c=2) for x in ("gate", "up", "down"))
        router = W[f"{tag}_router"]

        chunks = [(0, c) for c in range(2)] + [(e + 1, c) for e in range(E8) for c in range(nf)]
        N = len(chunks)
        last_of = {t: n for n, (t, _) in enumerate(chunks)}
        units = E8 + 1

        logits = a.sem("logits")
        lg_read = a.sem("lg_read")
        opened = a.sem("opened")
        gated = a.sem("gated")
        a_ready = a.sem("a_ready")
        closed = a.sem("closed")
        added = a.sem("added")
        once = a.sem("once")
        own = a.sem("own")
        block = ctx.enter_context(nc.Block())

        @block.gpsimd
        def _(pool):
            pool.sem_inc(F.root_ready, CREDIT)
            with pool.Fori(0, TURNS) as i:
                for u in range(2):
                    F.root(nc, pool, C, i, u)

        @block.vector
        def _(v):
            F.open_vector(v)
            for x in (R.shift_done, lg_read, a_ready, added):
                v.sem_inc(x, CREDIT)
            vec = Steps(own)
            nc.vector.tensor_scalar(wt[:, :, E8], wt_ones(C), tg, None, ALU.mult).then_inc(once, 1)
            v.wait_ge(once, 1)

            def activate(i, u, n):
                t, c = chunks[n]
                m = N * (2 * i + u) + n
                v.wait_ge(closed, done(units * (2 * i + u) + t - 2))
                v.wait_ge(gated, done(m))
                nc.vector.tensor_tensor(aT[:, (t + u) % 2, c, :], sg[:, n % 2, :], U[:, n % 2, :],
                                        ALU.mult).then_inc(a_ready, 1)

            def add(i, u, t):
                v.wait_ge(closed, done(units * (2 * i + u) + t))
                v.wait_ge(added, done(units * (2 * i + u) + t - 1))
                for k in range(GRP):
                    b = GRP * u + k
                    x = C.Xt[:, bass.ds(i, 1), b, :]
                    ins = nc.vector.scalar_tensor_tensor(
                        out=x, in0=Y[:, (t + u) % 2, k * P:(k + 1) * P], scalar=wt[:, b, (t + E8) % 9:(t + E8) % 9 + 1],
                        in1=x, op0=ALU.mult, op1=ALU.add)
                ins.then_inc(added, 1)

            def turn(i, last):
                for n in range(2):
                    activate(i, 0, n)
                v.wait_ge(logits, done(i))
                nc.vector.tensor_copy(R.lg[:, :, :], lgp[:, 0:BODY * E8].rearrange("p (b e) -> p b e", e=E8)).then_inc(
                    lg_read, 1)
                v.wait_ge(lg_read, done(i))
                nc.vector.memset(C.carrier[:, :], 0.0)
                R.choose(nc, v, vec, C, i)
                R.probabilities(nc, v, vec, i)
                nc.vector.tensor_scalar(R.rcp[:, :], R.rcp[:, :], tg, None, ALU.mult).then_inc(vec.done, vec.one())
                nc.vector.wait_ge(vec.done, vec.count)
                nc.vector.tensor_tensor(wt[:, :, 0:E8], R.m1[:, :, :],
                                                R.rcp[:, :].unsqueeze(2).to_broadcast([P, BODY, E8]), ALU.mult).then_inc(vec.done, vec.one())
                nc.vector.wait_ge(vec.done, vec.count)
                for u in range(2):
                    due = 0
                    for n in range(2 if u == 0 else 0, N):
                        if u == 1 and not last:
                            if n in (N - 7, N - 6):
                                F.statistics(nc, v, vec, C, i + 1, n - N + 7)
                            if n in (N - 4, N - 3):
                                F.normalise(nc, v, vec, C, i + 1, n - N + 4)
                        activate(i, u, n)
                        while due < units and last_of[due] + LAG_ADD <= n:
                            add(i, u, due)
                            due += 1
                    for t in range(due, units):
                        add(i, u, t)
                v.wait_ge(vec.done, vec.count)
                v.sem_clear(vec.done)
                vec.restart()

            for u in range(2):
                F.statistics(nc, v, vec, C, 0, u)
            for u in range(2):
                F.normalise(nc, v, vec, C, 0, u)
            v.wait_ge(vec.done, vec.count)
            v.sem_clear(vec.done)
            vec.restart()
            with v.Fori(0, TURNS - 1) as i:
                turn(i, False)
            turn(TURNS - 1, True)
            v.wait_ge(added, done(units * 2 * TURNS - 1))

        @block.scalar
        def _(act):
            for x in (F.xnT_ready, R.exp_done, gated):
                act.sem_inc(x, CREDIT)

            def silu(i, u, n):
                m = N * (2 * i + u) + n
                act.wait_ge(a_ready, done(m - 2))
                act.wait_ge(opened, done(m))
                nc.scalar.activation(sg[:, n % 2, :], G[:, n % 2, :], ACT.Silu).then_inc(gated, 1)

            def turn(i, last):
                silu(i, 0, 0)
                silu(i, 0, 1)
                R.exponentials(nc, act, i)
                for u in range(2):
                    for n in range(2 if u == 0 else 0, N):
                        silu(i, u, n)
                        if u == 1 and n == N - 2 and not last:
                            F.take(nc, act, C, i + 1, 0, tr[:, :])
                if not last:
                    F.take(nc, act, C, i + 1, 1, tr[:, :])

            for u in range(2):
                F.take(nc, act, C, 0, u, tr[:, :])
            with act.Fori(0, TURNS - 1) as i:
                turn(i, False)
            turn(TURNS - 1, True)

        @block.tensor
        def _(pe):
            for x in (F.turned, logits, opened, closed):
                pe.sem_inc(x, CREDIT)

            def open_chunk(i, u, n):
                t, c = chunks[n]
                m = N * (2 * i + u) + n
                g_w, u_w = (sgate[:, c, :], sup[:, c, :]) if t == 0 else (gate[:, t - 1, c, :], up[:, t - 1, c, :])
                pe.wait_ge(a_ready, done(m - 2))
                nc.tensor.matmul(G[:, n % 2, :], g_w, F.xnT[:, u, :], start=True, stop=True)
                nc.tensor.matmul(U[:, n % 2, :], u_w, F.xnT[:, u, :], start=True, stop=True).then_inc(opened, 1)

            def close(i, u, t):
                pe.wait_ge(a_ready, done(N * (2 * i + u) + last_of[t]))
                pe.wait_ge(added, done(units * (2 * i + u) + t - 2))
                nchunk = 2 if t == 0 else nf
                for k in range(GRP):
                    for c in range(nchunk):
                        d_w = sdown[:, c, :] if t == 0 else down[:, t - 1, c, :]
                        ins = nc.tensor.matmul(Y[:, (t + u) % 2, k * P:(k + 1) * P],
                                               aT[:, (t + u) % 2, c, k * P:(k + 1) * P], d_w,
                                               start=(c == 0), stop=(c == nchunk - 1))
                ins.then_inc(closed, 1)

            def front(i, u):
                pe.wait_ge(F.xnT_ready, done(2 * i + u - 1))
                F.turn(nc, pe, C, i, u, tr)

            def turn(i, last):
                open_chunk(i, 0, 0)
                open_chunk(i, 0, 1)
                pe.wait_ge(F.xnT_ready, done(2 * i + 1))
                pe.wait_ge(lg_read, done(i - 1))
                for b in range(BODY):
                    u, k = divmod(b, GRP)
                    ins = nc.tensor.matmul(lgp[:, b * E8:(b + 1) * E8], F.xnT[:, u, k * P:(k + 1) * P], router,
                                           start=True, stop=True)
                ins.then_inc(logits, 1)
                for u in range(2):
                    due = 0
                    for n in range(2 if u == 0 else 0, N):
                        open_chunk(i, u, n)
                        if u == 1 and n == N - 2 and not last:
                            front(i + 1, 0)
                        if u == 1 and n == N - 1 and not last:
                            front(i + 1, 1)
                        while due < units and last_of[due] + LAG_CLOSE <= n:
                            close(i, u, due)
                            due += 1
                    for t in range(due, units):
                        close(i, u, t)

            front(0, 0)
            front(0, 1)
            with pe.Fori(0, TURNS - 1) as i:
                turn(i, False)
            turn(TURNS - 1, True)


LAG_CLOSE = 2
LAG_ADD = 3


def wt_ones(C):
    return C.ones8



CAPACITY = 320
EXPERT_ROWS = E8 * CAPACITY
NOWHERE = 4095
TILES = 2 * NB + E8
STEP = 4
AHEAD = STEP
BACK = 4


def send_rows(nc, slot, xn, dram, rows, sent):
    for b in range(NB):
        for j in range(2):
            nc.gpsimd.indirect_dma_start(
                dram, bass.IndirectOffsetOnAxis(slot[:, j, b:b + 1], 0), xn[:, b * P:(b + 1) * P], None,
                bounds_check=rows - 1, oob_is_err=False).then_inc(sent, 16)


def bring_rows(nc, slot, dram, rows, first, second, back):
    for b in range(NB):
        for j, dst in ((0, first), (1, second)):
            nc.gpsimd.indirect_dma_start(
                dst[:, b * P:(b + 1) * P], None, dram, bass.IndirectOffsetOnAxis(slot[:, j, b:b + 1], 0),
                bounds_check=rows - 1, oob_is_err=False).then_inc(back[b // BACK], 16)


def combine(nc, C, v, wt, first, second, back, summed):
    for q in range(NB // BACK):
        v.wait_ge(back[q], 16 * 2 * BACK)
        for j, src in ((0, first), (1, second)):
            if j == 1:
                v.wait_ge(summed, 2 * q + 1)
            for b in range(BACK * q, BACK * q + BACK):
                x = C.X[:, b * P:(b + 1) * P]
                ins = nc.vector.scalar_tensor_tensor(out=x, in0=src[:, b * P:(b + 1) * P], scalar=wt[:, j, b:b + 1],
                                                     in1=x, op0=ALU.mult, op1=ALU.add)
            ins.then_inc(summed, 1)
    v.wait_ge(summed, 2 * (NB // BACK))


def route(nc, C, tag, router_w, tg, wt, slot, xn, xnT, dram, dram_rows, tile_expert=None):
    capacity = tile_expert is None
    with ExitStack() as ctx:
        a = Alloc(nc, ctx, tag)
        F = Front(a)
        R = Router(a, BODY)
        share = a.sb("share", [P, NB, E8])
        second = a.sb("second", [P, NB, E8])
        place = a.sb("place", [P, NB, E8])
        picked = a.sb("picked", [P, NB, E8])
        where = a.sb("where", [P, NB])
        zeros = a.sb("zeros", [P, P])
        chosen = a.sb("chosen", [P, NB, E8])
        keep = a.sb("keep", [P, E8, NB])
        free = a.sb("free", [P, NB])
        eligible = a.sb("eligible", [P, NB])
        before = a.sb("before", [P, NB])
        zero = a.sb("zero", [P, NB])
        if not capacity:
            before8 = a.sb("before8", [P, E8, NB])
            full = a.sb("full", [P, E8, NB])
            tokens = a.sb("tokens", [P, E8])
            tiles = a.sb("tiles", [P, E8])
            ends = a.sb("ends", [P, E8])
            ended = a.sb("ended", [P, TILES, E8])
            owner = a.sb("owner", [P, TILES])
        tr = a.ps("tr", [P, 512])
        lgp = a.ps("lgp", [P, 512])
        rank = a.ps("rank", [P, 512])
        logits = a.sem("logits")
        lg_read = a.sem("lg_read")
        xn_kept, xnT_kept = a.sem("xn_kept"), a.sem("xnT_kept")
        zeroed, cleared = a.sem("zeroed"), a.sem("cleared")
        own, counted, offered, settled = a.sem("own"), a.sem("counted"), a.sem("offered"), a.sem("settled")
        block = ctx.enter_context(nc.Block())
        share_t = share[:, :, :].rearrange("p (i b) e -> p i b e", i=TURNS)
        chosen_t = chosen[:, :, :].rearrange("p (i b) e -> p i b e", i=TURNS)

        second_t = second[:, :, :].rearrange("p (i b) e -> p i b e", i=TURNS)
        xn_t = xn[:, :].rearrange("p (i u t) -> p i u t", i=TURNS, u=2)
        xnT_t = xnT[:, :].rearrange("p (i u t) -> p i u t", i=TURNS, u=2)

        @block.sync
        def _(sp):
            sp.wait_ge(zeroed, 1)
            sp.dma_start(dram.rearrange("(k p) d -> p k d", p=P),
                         zeros[:, :].unsqueeze(1).to_broadcast([P, dram_rows // P, P])).then_inc(cleared, 16)
            sp.wait_ge(cleared, 16)

        @block.gpsimd
        def _(pool):
            nc.gpsimd.memset(zeros[:, :], 0.0).then_inc(zeroed, 1)
            pool.sem_inc(F.root_ready, CREDIT)
            with pool.Fori(0, TURNS) as i:
                for u in range(2):
                    F.root(nc, pool, C, i, u)

        @block.vector
        def _(v):
            F.open_vector(v)
            for x in (R.shift_done, lg_read, xn_kept, xnT_kept):
                v.sem_inc(x, CREDIT)
            vec = Steps(own)

            def turn(i, last):
                for u in range(2):
                    v.wait_ge(F.st_ready, done(2 * i + u))
                    nc.vector.tensor_scalar(xn_t[:, bass.ds(i, 1), u, :], F.st[:, u, :, :].rearrange("p k d -> p (k d)"),
                                            1.0, None, ALU.mult).then_inc(xn_kept, 1)
                if not last:
                    v.wait_ge(xn_kept, done(2 * i + 1))
                    nc.vector.memset(C.carrier[:, :], 0.0)
                    for u in range(2):
                        F.statistics(nc, v, vec, C, i + 1, u)
                    for u in range(2):
                        F.normalise(nc, v, vec, C, i + 1, u)
                for u in range(2):
                    v.wait_ge(F.xnT_ready, done(2 * i + u))
                    nc.vector.tensor_scalar(xnT_t[:, bass.ds(i, 1), u, :], F.xnT[:, u, :], 1.0, None,
                                            ALU.mult).then_inc(xnT_kept, 1)
                v.wait_ge(logits, done(i))
                nc.vector.tensor_copy(R.lg[:, :, :], lgp[:, 0:BODY * E8].rearrange("p (b e) -> p b e", e=E8)).then_inc(
                    lg_read, 1)
                v.wait_ge(lg_read, done(i))
                nc.vector.memset(C.carrier[:, :], 0.0)
                R.choose(nc, v, vec, C, i)
                nc.vector.tensor_scalar(second_t[:, bass.ds(i, 1), :, :], R.m1[:, :, :].unsqueeze(1), 1.0, None,
                                        ALU.mult).then_inc(vec.done, vec.one())
                nc.vector.wait_ge(vec.done, vec.count)
                R.probabilities(nc, v, vec, i)
                wide = lambda x: x[:, :].unsqueeze(2).to_broadcast([P, BODY, E8])
                if capacity:
                    nc.vector.tensor_tensor(R.m1[:, :, :], R.m1[:, :, :], wide(R.rcp), ALU.mult).then_inc(
                        vec.done, vec.one())
                if capacity:
                    nc.vector.wait_ge(vec.done, vec.count)
                    nc.vector.tensor_reduce(R.sum[:, :], R.m1[:, :, :], AX.X, ALU.add).then_inc(vec.done, vec.one())
                    nc.vector.wait_ge(vec.done, vec.count)
                    nc.vector.tensor_scalar(R.sum[:, :], R.sum[:, :], 1e-9, None, ALU.max).then_inc(vec.done, vec.one())
                    nc.vector.wait_ge(vec.done, vec.count)
                    nc.vector.reciprocal(R.rcp[:, :], R.sum[:, :]).then_inc(vec.done, vec.one())
                    nc.vector.wait_ge(vec.done, vec.count)
                one_turn = [P, 1, BODY, E8]
                nc.vector.tensor_tensor(share_t[:, bass.ds(i, 1), :, :], R.m1[:, :, :].unsqueeze(1),
                                                R.rcp[:, :].unsqueeze(1).unsqueeze(3).to_broadcast(one_turn), ALU.mult).then_inc(vec.done, vec.one())
                nc.vector.tensor_scalar(chosen_t[:, bass.ds(i, 1), :, :], R.m0[:, :, :].unsqueeze(1), 1.0, None,
                                                ALU.mult).then_inc(vec.done, vec.one())
                v.wait_ge(vec.done, vec.count)
                v.sem_clear(vec.done)
                vec.restart()

            for u in range(2):
                F.statistics(nc, v, vec, C, 0, u)
            for u in range(2):
                F.normalise(nc, v, vec, C, 0, u)
            v.wait_ge(vec.done, vec.count)
            v.sem_clear(vec.done)
            vec.restart()
            with v.Fori(0, TURNS - 1) as i:
                turn(i, False)
            turn(TURNS - 1, True)

            def op(out, x, y, f):
                nc.vector.tensor_tensor(out, x, y, f).then_inc(vec.done, vec.one())
                nc.vector.wait_ge(vec.done, vec.count)

            nc.vector.memset(zero[:, :], 0.0).then_inc(vec.done, vec.one())
            nc.vector.wait_ge(vec.done, vec.count)
            if capacity:
                nc.vector.memset(free[:, :], 1.0).then_inc(vec.done, vec.one())
                nc.vector.wait_ge(vec.done, vec.count)
                for e in range(EXPERTS):
                    op(eligible[:, :], chosen[:, :, e], free[:, :], ALU.mult)
                    nc.vector.tensor_tensor_scan(before[:, :], eligible[:, :], zero[:, :], 0.0, ALU.add, ALU.add).then_inc(vec.done, vec.one())
                    nc.vector.wait_ge(vec.done, vec.count)
                    nc.vector.tensor_tensor(before[:, :], before[:, :], eligible[:, :], ALU.subtract).then_inc(offered, 1)
                    v.wait_ge(counted, e + 1)
                    nc.vector.scalar_tensor_tensor(out=keep[:, e, :], in0=rank[:, 0:NB], scalar=float(CAPACITY),
                                                           in1=eligible[:, :], op0=ALU.is_le, op1=ALU.mult).then_inc(vec.done, vec.one())
                    nc.vector.tensor_scalar(place[:, :, e], rank[:, 0:NB], float(e * CAPACITY - 1 - NOWHERE), None,
                                            ALU.add).then_inc(vec.done, vec.one())
                    nc.vector.wait_ge(vec.done, vec.count)
                    op(eligible[:, :], eligible[:, :], keep[:, e, :], ALU.subtract)
                    op(free[:, :], free[:, :], eligible[:, :], ALU.subtract)
                kept = keep[:, :, :].rearrange("p e b -> p b e")
                op(place[:, :, :], place[:, :, :], kept, ALU.mult)
                op(share[:, :, :], share[:, :, :], kept, ALU.mult)
                op(share[:, :, :], share[:, :, :], free[:, :].unsqueeze(2).to_broadcast([P, NB, E8]), ALU.mult)
            else:
                for e in range(E8):
                    nc.vector.tensor_tensor_scan(before8[:, e, :], chosen[:, :, e], zero[:, :], 0.0, ALU.add,
                                                 ALU.add).then_inc(vec.done, vec.one())
                nc.vector.wait_ge(vec.done, vec.count)
                nc.vector.tensor_scalar(tokens[:, :], before8[:, :, NB - 1], 1.0, None, ALU.mult).then_inc(
                    vec.done, vec.one())
                nc.vector.wait_ge(vec.done, vec.count)
                nc.vector.tensor_tensor(before8[:, :, :], before8[:, :, :], chosen[:, :, :].rearrange("p b e -> p e b"),
                                        ALU.subtract).then_inc(offered, 1)
                v.wait_ge(counted, 1)
                nc.vector.tensor_scalar(tokens[:, :], rank[:, NB * E8:NB * E8 + E8], 1.0 / P, None, ALU.mult).then_inc(
                    vec.done, vec.one())
                nc.vector.wait_ge(vec.done, vec.count)
                op(full[:, :, :], tokens[:, :].unsqueeze(2).to_broadcast([P, E8, NB]),
                   C.tile_no[:, 0:NB].unsqueeze(1).to_broadcast([P, E8, NB]), ALU.is_gt)
                nc.vector.tensor_reduce(tiles[:, :], full[:, :, :], AX.X, ALU.add).then_inc(vec.done, vec.one())
                nc.vector.wait_ge(vec.done, vec.count)
                nc.vector.tensor_tensor_scan(ends[:, :], tiles[:, :], zero[:, 0:E8], 0.0, ALU.add, ALU.add).then_inc(
                    vec.done, vec.one())
                nc.vector.wait_ge(vec.done, vec.count)
                op(tiles[:, :], ends[:, :], tiles[:, :], ALU.subtract)
                nc.vector.tensor_scalar(tiles[:, :], tiles[:, :], float(P), -1.0, ALU.mult, ALU.add).then_inc(
                    vec.done, vec.one())
                nc.vector.wait_ge(vec.done, vec.count)
                nc.vector.tensor_tensor(place[:, :, :], rank[:, 0:NB * E8].rearrange("p (e b) -> p b e", e=E8),
                                        tiles[:, :].unsqueeze(1).to_broadcast([P, NB, E8]), ALU.add).then_inc(
                    vec.done, vec.one())
                nc.vector.tensor_tensor(ended[:, :, :], C.tile_no.unsqueeze(2).to_broadcast([P, TILES, E8]),
                                        ends[:, :].unsqueeze(1).to_broadcast([P, TILES, E8]), ALU.is_ge).then_inc(
                    vec.done, vec.one())
                nc.vector.wait_ge(vec.done, vec.count)
                nc.vector.tensor_reduce(owner[:, :], ended[:, :, :], AX.X, ALU.add).then_inc(vec.done, vec.one())
                nc.vector.wait_ge(vec.done, vec.count)
                nc.vector.tensor_scalar(owner[:, :], owner[:, :], float(E8 - 1), None, ALU.min).then_inc(
                    vec.done, vec.one())
                nc.vector.wait_ge(vec.done, vec.count)
                nc.vector.tensor_copy(tile_expert[:, :], owner[:, :]).then_inc(vec.done, vec.one())
                nc.vector.wait_ge(vec.done, vec.count)
            op(chosen[:, :, :], chosen[:, :, :], second[:, :, :], ALU.subtract)
            for j, choice in ((0, chosen), (1, second)):
                op(picked[:, :, :], place[:, :, :], choice[:, :, :], ALU.mult)
                nc.vector.tensor_reduce(where[:, :], picked[:, :, :], AX.X, ALU.add).then_inc(vec.done, vec.one())
                nc.vector.wait_ge(vec.done, vec.count)
                nc.vector.tensor_scalar(where[:, :], where[:, :], float(NOWHERE) if capacity else 0.0, None, ALU.add).then_inc(
                    vec.done, vec.one())
                nc.vector.wait_ge(vec.done, vec.count)
                nc.vector.tensor_copy(slot[:, j, :], where[:, :]).then_inc(vec.done, vec.one())
                op(picked[:, :, :], share[:, :, :], choice[:, :, :], ALU.mult)
                nc.vector.tensor_reduce(wt[:, j, :], picked[:, :, :], AX.X, ALU.add).then_inc(vec.done, vec.one())
                nc.vector.wait_ge(vec.done, vec.count)
            if capacity:
                nc.vector.tensor_scalar(wt[:, 2, :], free[:, :], -1.0, 1.0, ALU.mult, ALU.add).then_inc(vec.done, vec.one())
                nc.vector.wait_ge(vec.done, vec.count)
            shares = 3 if capacity else 2
            nc.vector.tensor_scalar(wt[:, 0:shares, :], wt[:, 0:shares, :], tg, None, ALU.mult).then_inc(settled, 1)
            v.wait_ge(settled, 1)

        @block.scalar
        def _(act):
            for x in (F.xnT_ready, R.exp_done):
                act.sem_inc(x, CREDIT)

            def front(i):
                for u in range(2):
                    act.wait_ge(xnT_kept, done(2 * i + u - 2))
                    F.take(nc, act, C, i, u, tr[:, :])

            front(0)
            with act.Fori(0, TURNS - 1) as i:
                front(i + 1)
                R.exponentials(nc, act, i)
            R.exponentials(nc, act, TURNS - 1)

        @block.tensor
        def _(pe):
            for x in (F.turned, logits):
                pe.sem_inc(x, CREDIT)

            def front(i):
                for u in range(2):
                    pe.wait_ge(F.xnT_ready, done(2 * i + u - 1))
                    F.turn(nc, pe, C, i, u, tr)

            def turn(i):
                pe.wait_ge(F.xnT_ready, done(2 * i + 1))
                pe.wait_ge(lg_read, done(i - 1))
                for b in range(BODY):
                    u, k = divmod(b, GRP)
                    ins = nc.tensor.matmul(lgp[:, b * E8:(b + 1) * E8], F.xnT[:, u, k * P:(k + 1) * P], router_w,
                                           start=True, stop=True)
                ins.then_inc(logits, 1)

            front(0)
            with pe.Fori(0, TURNS - 1) as i:
                turn(i)
                front(i + 1)
            turn(TURNS - 1)
            if capacity:
                for e in range(EXPERTS):
                    pe.wait_ge(offered, e + 1)
                    nc.tensor.matmul(rank[:, 0:NB], C.upto, eligible[:, :], start=True, stop=False)
                    nc.tensor.matmul(rank[:, 0:NB], C.ones, before[:, :], start=False, stop=True).then_inc(counted, 1)
            else:
                pe.wait_ge(offered, 1)
                nc.tensor.matmul(rank[:, 0:NB * E8], C.upto, chosen[:, :, :].rearrange("p b e -> p e b"), start=True,
                                 stop=False)
                nc.tensor.matmul(rank[:, 0:NB * E8], C.ones, before8[:, :, :], start=False, stop=True)
                nc.tensor.matmul(rank[:, NB * E8:NB * E8 + E8], C.ones, tokens[:, :], start=True, stop=True).then_inc(
                    counted, 1)


def tiled_experts(nc, C, tag, W, tg, wt, slot, xn, xnT, tile_expert):
    NC = 4
    TURNS_T = TILES // STEP
    with ExitStack() as ctx:
        a = Alloc(nc, ctx, tag)
        sg = a.sb("sg", [P, 2, TOK])
        hT = a.sb("hT", [P, 2, 2, TOK])
        xg = a.sb("xg", [P, STEP, P])
        xgT = a.sb("xgT", [P, 2, P])
        h = a.sb("h", [P, 2, TOK])
        aT = a.sb("aT", [P, 2, TOK])
        yg = a.sb("yg", [P, STEP, P])
        tr = a.ps("tr", [P, 512])
        G = a.ps("G", [P, 2, 512])
        U = a.ps("U", [P, 2, 512])
        T = a.ps("T", [P, 2, 512])
        Y = a.ps("Y", [P, 512])
        gate = W[f"{tag}_gate"].rearrange("p (e f) -> p e f", e=E8)
        up = W[f"{tag}_up"].rearrange("p (e f) -> p e f", e=E8)
        down = W[f"{tag}_down"].rearrange("p (e c d) -> p e c d", e=E8, c=NC)
        sgate, sup, sdown = (W[f"{tag}_s{x}"].rearrange("p (c f) -> p c f", c=2) for x in ("gate", "up", "down"))
        s_opened, s_gated, s_active, s_closed, s_added = (
            a.sem("s_opened"), a.sem("s_gated"), a.sem("s_active"), a.sem("s_closed"), a.sem("s_added"))
        sent = a.sem("sent")
        fetched = [a.sem(f"fetched{q}") for q in range(STEP)]
        turned = a.sem("turned")
        xgT_ready = a.sem("xgT_ready")
        opened = a.sem("opened")
        gated = a.sem("gated")
        h_ready = a.sem("h_ready")
        flipped = a.sem("flipped")
        aT_ready = a.sem("aT_ready")
        closed = a.sem("closed")
        yg_ready = a.sem("yg_ready")
        put = [a.sem(f"put{q}") for q in range(STEP)]
        yg_free = a.sem("yg_free")
        back = [a.sem(f"back{q}") for q in range(NB // BACK)]
        summed = a.sem("summed")
        block = ctx.enter_context(nc.Block())
        GROUPS = 2 * TURNS
        xnT_t = xnT[:, :].rearrange("p (i u t) -> p i u t", i=TURNS, u=2)
        X_t = C.X[:, :].rearrange("p (i u t) -> p i u t", i=TURNS, u=2)
        rows_in = C.tile_in.rearrange("(i q p) d -> p i q d", q=STEP, p=P)
        rows_out = C.tile_out.rearrange("(i q p) d -> p i q d", q=STEP, p=P)
        owner = tile_expert[:, :].rearrange("p (i q) -> p i q", q=STEP)

        @block.gpsimd
        def _(pool):
            pool.sem_inc(yg_free, CREDIT)
            send_rows(nc, slot, xn, C.tile_in, TILES * P, sent)
            with pool.Fori(0, TURNS_T) as i:
                for q in range(STEP):
                    pool.wait_ge(put[q], 16 * i + 16)
                    pool.sem_inc(yg_free, 1)
            pool.wait_ge(sent, 16 * 2 * NB)
            pool.wait_ge(s_closed, done(GROUPS - 1))
            bring_rows(nc, slot, C.tile_out, TILES * P, xn, xnT, back)

        @block.sync
        def _(sp):
            sp.wait_ge(sent, 16 * 2 * NB)
            for q in range(STEP):
                sp.dma_start(xg[:, q, :], rows_in[:, 0, q, :]).then_inc(fetched[q], 16)
            with sp.Fori(0, TURNS_T) as i:
                for q in range(STEP):
                    sp.wait_ge(turned, done(STEP * i + q))
                    sp.dma_start(xg[:, q, :], rows_in[:, bass.ds(i + 1, 1), q, :]).then_inc(fetched[q], 16)
                    sp.wait_ge(yg_ready, done(STEP * i + q))
                    sp.dma_start(rows_out[:, bass.ds(i, 1), q, :], yg[:, q, :]).then_inc(put[q], 16)
            for q in range(STEP):
                sp.wait_ge(put[q], 16 * TURNS_T)
                sp.wait_ge(fetched[q], 16 * (TURNS_T + 1))

        @block.vector
        def _(v):
            for x in (s_active, s_added, h_ready, yg_ready):
                v.sem_inc(x, CREDIT)

            def add_shared(i, t):
                v.wait_ge(s_closed, done(2 * i + t))
                x = X_t[:, bass.ds(i, 1), t, :]
                nc.vector.scalar_tensor_tensor(out=x, in0=(Y, tr)[t][:, :], scalar=tg, in1=x, op0=ALU.mult,
                                               op1=ALU.add).then_inc(s_added, 1)

            with v.Fori(0, TURNS) as i:
                for u in range(2):
                    for c in range(2):
                        m = 2 * (2 * i + u) + c
                        v.wait_ge(s_closed, done(2 * i + u - 2))
                        v.wait_ge(s_gated, done(m))
                        nc.vector.tensor_tensor(hT[:, u, c, :], sg[:, c, :], U[:, c, :], ALU.mult).then_inc(s_active, 1)
                    if u:
                        add_shared(i, 0)
                add_shared(i, 1)

            def activate(t, n):
                v.wait_ge(flipped, done(n - 2))
                v.wait_ge(gated, done(n))
                nc.vector.tensor_tensor(h[:, t % 2, :], sg[:, t % 2, :], U[:, t % 2, :], ALU.mult).then_inc(h_ready, 1)

            def keep(t, n):
                v.wait_ge(yg_free, done(n - STEP))
                v.wait_ge(closed, done(n))
                nc.vector.tensor_scalar(yg[:, t % STEP, :], Y[:, 0:P], 1.0, None, ALU.mult).then_inc(yg_ready, 1)

            def turn(i, first):
                for q in range(STEP):
                    n = STEP * i + q
                    activate(q, n)
                    if not first or q >= 2:
                        keep(q - 2, n - 2)

            turn(0, True)
            with v.Fori(1, TURNS_T) as i:
                turn(i, False)
            for t in (TILES - 2, TILES - 1):
                keep(t, t)
            combine(nc, C, v, wt, xn, xnT, back, summed)

        @block.scalar
        def _(act):
            for x in (s_gated, xgT_ready, gated, aT_ready):
                act.sem_inc(x, CREDIT)
            with act.Fori(0, TURNS) as i:
                for u in range(2):
                    for c in range(2):
                        m = 2 * (2 * i + u) + c
                        act.wait_ge(s_active, done(m - 2))
                        act.wait_ge(s_opened, done(m))
                        nc.scalar.activation(sg[:, c, :], G[:, c, :], ACT.Silu).then_inc(s_gated, 1)

            def take(t, n):
                act.wait_ge(opened, done(n - 2))
                act.wait_ge(turned, done(n))
                nc.scalar.activation(xgT[:, t % 2, :], tr[:, 0:P], ACT.Identity).then_inc(xgT_ready, 1)

            def silu(t, n):
                act.wait_ge(h_ready, done(n - 2))
                act.wait_ge(opened, done(n))
                nc.scalar.activation(sg[:, t % 2, :], G[:, t % 2, :], ACT.Silu).then_inc(gated, 1)

            def take_hidden(t, n):
                act.wait_ge(closed, done(n - 2))
                act.wait_ge(flipped, done(n))
                nc.scalar.activation(aT[:, t % 2, :], T[:, t % 2, :], ACT.Identity).then_inc(aT_ready, 1)

            def turn(i, first):
                for q in range(STEP):
                    n = STEP * i + q
                    take(q + 1, n + 1)
                    silu(q, n)
                    if not first or q >= 1:
                        take_hidden(q - 1, n - 1)

            act.wait_ge(s_active, done(2 * GROUPS - 1))
            take(0, 0)
            turn(0, True)
            with act.Fori(1, TURNS_T) as i:
                turn(i, False)
            take_hidden(TILES - 1, TILES - 1)

        @block.tensor
        def _(pe):
            for x in (s_opened, s_closed, turned, opened, flipped, closed):
                pe.sem_inc(x, CREDIT)

            def close_shared(i, t):
                pe.wait_ge(s_active, done(2 * (2 * i + t) + 1))
                pe.wait_ge(s_added, done(2 * i + t - 2))
                for k in range(GRP):
                    for c in range(2):
                        ins = nc.tensor.matmul((Y, tr)[t][:, k * P:(k + 1) * P], hT[:, t, c, k * P:(k + 1) * P],
                                               sdown[:, c, :], start=(c == 0), stop=(c == 1))
                ins.then_inc(s_closed, 1)

            with pe.Fori(0, TURNS) as i:
                for u in range(2):
                    for c in range(2):
                        m = 2 * (2 * i + u) + c
                        x = xnT_t[:, bass.ds(i, 1), u, :]
                        pe.wait_ge(s_active, done(m - 2))
                        nc.tensor.matmul(G[:, c, :], sgate[:, c, :], x, start=True, stop=True)
                        nc.tensor.matmul(U[:, c, :], sup[:, c, :], x, start=True, stop=True).then_inc(s_opened, 1)
                    if u:
                        close_shared(i, 0)
                close_shared(i, 1)
            pe.wait_ge(s_added, done(GROUPS - 1))

            def flip_input(t, n, turns):
                pe.wait_ge(xgT_ready, done(n - 1))
                pe.wait_ge(fetched[t % STEP], 16 * turns)
                nc.tensor.transpose(tr[:, 0:P], xg[:, t % STEP, :], C.ident).then_inc(turned, 1)

            def open_tile(t, n, e):
                pe.wait_ge(h_ready, done(n - 2))
                pe.wait_ge(xgT_ready, done(n))
                nc.tensor.matmul(G[:, t % 2, :], xgT[:, t % 2, :], gate[:, bass.ds(e, 1), :], start=True, stop=True)
                nc.tensor.matmul(U[:, t % 2, :], xgT[:, t % 2, :], up[:, bass.ds(e, 1), :], start=True,
                                 stop=True).then_inc(opened, 1)

            def flip_hidden(t, n):
                pe.wait_ge(aT_ready, done(n - 2))
                pe.wait_ge(h_ready, done(n))
                for c in range(NC):
                    ins = nc.tensor.transpose(T[:, t % 2, c * P:(c + 1) * P], h[:, t % 2, c * P:(c + 1) * P], C.ident)
                ins.then_inc(flipped, 1)

            def close_tile(t, n, e):
                pe.wait_ge(yg_ready, done(n - 1))
                pe.wait_ge(aT_ready, done(n))
                for c in range(NC):
                    ins = nc.tensor.matmul(Y[:, 0:P], aT[:, t % 2, c * P:(c + 1) * P], down[:, bass.ds(e, 1), c, :],
                                           start=(c == 0), stop=(c == NC - 1))
                ins.then_inc(closed, 1)

            def expert_of(i, q):
                return pe.value_load(owner[0:1, bass.ds(i, 1), q], min_val=0, max_val=E8 - 1)

            def turn(i, first):
                experts = {q: expert_of(i, q) for q in range(STEP)}
                if not first:
                    experts.update({q: expert_of(i - 1, q + STEP) for q in (-2, -1)})
                for q in range(STEP):
                    n = STEP * i + q
                    flip_input(q + 1, n + 1, i + 1 + (q + 1) // STEP)
                    open_tile(q, n, experts[q])
                    if not first or q >= 1:
                        flip_hidden(q - 1, n - 1)
                    if not first or q >= 2:
                        close_tile(q - 2, n - 2, experts[q - 2])

            flip_input(0, 0, 1)
            turn(0, True)
            with pe.Fori(1, TURNS_T) as i:
                turn(i, False)
            flip_hidden(TILES - 1, TILES - 1)
            for t in (TILES - 2, TILES - 1):
                close_tile(t, t, expert_of(TURNS_T - 1, t % STEP))



H2, D2 = 16, 64
INNER = H2 * D2
NCH = INNER // P
RANK = 32
IPA = 4
ORG = P - IPA


def merge_lora(nc, C, x2, w96, x3, dram):
    with ExitStack() as ctx:
        a = Alloc(nc, ctx, "merge")
        w32 = Packed(a.sb("w32", [RANK, N32]), PLACE32)
        w4 = Packed(a.sb("w4", [4, N4]), PLACE4)
        ctx_ipa = a.sb("ctx_ipa", [KV, NB, IPA])
        v_ipa = a.sb("v_ipa", [P, INNER])
        al = a.sb("al", [P, 4])
        bank = a.ps("bank", [P, 2, 512])
        loaded, scaled, done = a.sem("loaded"), a.sem("scaled"), a.sem("done")
        product = a.sem("product")
        kept = a.sem("kept")
        pieces = []
        for half in range(2):
            cols = slice(512 * half, 512 * half + 512)
            pieces.append((w32["q_down"], w32["q_up"][:, cols], 512, ("add", x2["L2_q"][:, cols], 0)))
            pieces.append((w32["k_down"], w32["k_up"][:, cols], 512, ("add", w96["L2_k"][:, cols], 1)))
            pieces.append((w32["v_down"], w32["v_up"][:, cols], 512, ("add", w96["L2_v"][:, cols], 2)))
        for half in range(2):
            cols = slice(512 * half, 512 * half + 512)
            pieces.append((ctx_ipa[:, :, :].rearrange("c b t -> c (b t)"), w96["L2_vi"][:, cols], 512,
                           ("copy", v_ipa[:, cols], 0)))
        for c in range(NCH):
            pieces.append((w32["o_down"][:, c * P:(c + 1) * P], w32["o_up"], P,
                           ("add", x2["L2_o"][:, c * P:(c + 1) * P], 3)))
        for e in range(4):
            pieces.append((w4["A"][:, e * P:(e + 1) * P], w4["B"][:, e * 512:(e + 1) * 512], 512,
                           ("lora", C.f2["We"][:, e * 512:(e + 1) * 512], 0)))
        block = ctx.enter_context(nc.Block())

        @block.sync
        def _(sp):
            sp.dma_start(x3.tile, dram["sec_x3"]).then_inc(C.last_landed, 16)
            sp.dma_start(w32.tile[:, :], dram["w32"]).then_inc(loaded, 16)
            sp.dma_start(w4.tile[:, :], dram["w4"]).then_inc(loaded, 16)
            sp.dma_start(ctx_ipa[:, :, :], dram["ctxT"].rearrange("c (b t) -> c b t", b=NB)[:, :, ORG:P]).then_inc(
                loaded, 16)
            sp.wait_ge(loaded, 48)
            sp.wait_ge(done, 1)
            sp.dma_start(C.v_ipa_dram, v_ipa[:, :]).then_inc(kept, 16)
            sp.wait_ge(kept, 16)

        @block.tensor
        def _(pe):
            pe.wait_ge(loaded, 48)
            for n, (lhsT, rhs, w, _) in enumerate(pieces):
                if n >= 2:
                    pe.wait_ge(scaled, n)
                m = lhsT.shape[1]
                nc.tensor.matmul(bank[0:m, n % 2, 0:w], lhsT, rhs, start=True, stop=True).then_inc(product, 1)

        @block.vector
        def _(v):
            nc.vector.tensor_scalar(al[:, :], C.rows["alpha"], 1.0 / RANK, None, ALU.mult).then_inc(scaled, 1)
            v.wait_ge(scaled, 1)
            v.wait_ge(C.late_landed, 16 * LATE)
            for n, (lhsT, _, w, (what, dst, j)) in enumerate(pieces):
                m = lhsT.shape[1]
                v.wait_ge(product, n + 1)
                src = bank[0:m, n % 2, 0:w]
                if what == "copy":
                    ins = nc.vector.tensor_copy(dst, src)
                elif what == "lora":
                    ins = nc.vector.tensor_tensor(dst, src, C.f2["Wi"], ALU.add)
                else:
                    ins = nc.vector.scalar_tensor_tensor(out=dst, in0=src, scalar=al[0:m, j:j + 1], in1=dst,
                                                         op0=ALU.mult, op1=ALU.add)
                ins.then_inc(scaled, 1)
            v.wait_ge(scaled, len(pieces) + 1)
            nc.vector.tensor_scalar(x2["L2_q"], x2["L2_q"], D2 ** -0.5, None, ALU.mult).then_inc(done, 1)


def attention_ipa(nc, C, x2, w96, tg):
    units = BODY * 4
    U = GRP * 4
    NP = 24
    with ExitStack() as ctx:
        a = Alloc(nc, ctx, "L2")
        F = Front(a)
        ctxT = a.sb("ctxT", [KV, TOK])
        qT = a.sb("qT", [P, NCH, TOK])
        kT = a.sb("kT", [P, NCH, TOK])
        V = a.sb("V", [P, GRP, INNER])
        pr = a.sb("pr", [P, 4, 4, P])
        pT = a.sb("pT", [P, 2, 4, P])
        oT = a.sb("oT", [P, NCH, P])
        mx = a.sb("mx", [P, 4, 2, 4])
        sm = a.sb("sm", [P, 4, 2, 4])
        rc = a.sb("rc", [P, 4, 2, 4])
        res = a.sb("res", [P, P])
        pj = a.ps("pj", [P, 2, 512])
        S = a.ps("S", [P, 2, 512])
        T = a.ps("T", [P, 2, 512])
        O = a.ps("O", [P, 2, 512])
        outp = pj[:, 1, 0:P]

        ctx_in = [a.sem(f"ctx_in{u}") for u in range(2)]
        ipa_in = [a.sem(f"ipa_in{u}") for u in range(2)]
        projected = a.sem("projected")
        kept_a = a.sem("kept_a")
        kept_v = a.sem("kept_v")
        scored = a.sem("scored")
        shifted = a.sem("shifted")
        exped = a.sem("exped")
        summed = a.sem("summed")
        scaled = a.sem("scaled")
        flipped = a.sem("flipped")
        pT_ready = a.sem("pT_ready")
        weighed = a.sem("weighed")
        oT_ready = a.sem("oT_ready")
        out_done = a.sem("out_done")
        added = a.sem("added")
        own = a.sem("own")
        block = ctx.enter_context(nc.Block())
        parts = ((0, slice(0, ORG)), (1, slice(ORG, P)))

        @block.sync
        def _(sp):
            with sp.Fori(0, TURNS) as i:
                for u in range(2):
                    g = 2 * i + u
                    sp.wait_ge(projected, done(NP * g - 1))
                    sp.dma_start(ctxT[:, :], C.ctxT_v[:, bass.ds(i, 1), u, :]).then_inc(ctx_in[u], 16)
                    sp.wait_ge(weighed, done(U * g - 1))
                    sp.dma_start(V[ORG:P, :, :], C.v_ipa_v[:, bass.ds(i, 1), u, :, :]).then_inc(ipa_in[u], 16)

        @block.gpsimd
        def _(pool):
            pool.sem_inc(F.root_ready, CREDIT)
            pool.sem_inc(scaled, CREDIT)
            with pool.Fori(0, TURNS) as i:
                for u in range(2):
                    F.root(nc, pool, C, i, u)
                for s in range(units):
                    n = units * i + s
                    pool.wait_ge(summed, done(n))
                    for j, cols in parts:
                        w = cols.stop - cols.start
                        ins = nc.gpsimd.tensor_tensor(pr[:, s % 4, :, cols], pr[:, s % 4, :, cols],
                                                      rc[:, s % 4, j, :].unsqueeze(2).to_broadcast([P, 4, w]), ALU.mult)
                    ins.then_inc(scaled, 1)

        def destination(n):
            if n < 16:
                return (qT if n < 8 else kT)[:, n % 8, :], P
            k, half = divmod(n - 16, 2)
            return V[0:ORG, k, 512 * half:512 * half + 512], ORG

        @block.vector
        def _(v):
            F.open_vector(v)
            for x in (kept_v, shifted, summed, added):
                v.sem_inc(x, CREDIT)
            vec = Steps(own)

            def shift(i, s):
                n = units * i + s
                v.wait_ge(flipped, done(n - 4))
                v.wait_ge(scored, done(n))
                bank = S[:, s % 2, :].rearrange("p (j t) -> p j t", j=4)
                for j, cols in parts:
                    nc.vector.tensor_reduce(mx[:, s % 4, j, :], bank[:, :, cols], AX.X, ALU.max).then_inc(vec.done, vec.one())
                nc.vector.wait_ge(vec.done, vec.count)
                for j, cols in parts:
                    w = cols.stop - cols.start
                    ins = nc.vector.tensor_tensor(pr[:, s % 4, :, cols], bank[:, :, cols],
                                                  mx[:, s % 4, j, :].unsqueeze(2).to_broadcast([P, 4, w]), ALU.subtract)
                ins.then_inc(shifted, 1)

            def total(i, s):
                v.wait_ge(exped, done(units * i + s))
                for j, cols in parts:
                    nc.vector.tensor_reduce(sm[:, s % 4, j, :], pr[:, s % 4, :, cols], AX.X, ALU.add).then_inc(vec.done, vec.one())
                nc.vector.wait_ge(vec.done, vec.count)
                nc.vector.reciprocal(rc[:, s % 4, :, :], sm[:, s % 4, :, :]).then_inc(summed, 1)

            def residual(i, b):
                v.wait_ge(out_done, done(BODY * i + b))
                nc.vector.tensor_tensor(res[:, :], outp, C.rows["L2_bo"], ALU.add).then_inc(vec.done, vec.one())
                nc.vector.wait_ge(vec.done, vec.count)
                x = C.Xt[:, bass.ds(i, 1), b, :]
                nc.vector.scalar_tensor_tensor(out=x, in0=res[:, :], scalar=tg, in1=x, op0=ALU.mult,
                                               op1=ALU.add).then_inc(added, 1)

            with v.Fori(0, TURNS) as i:
                for u in range(2):
                    F.statistics(nc, v, vec, C, i, u)
                for u in range(2):
                    F.normalise(nc, v, vec, C, i, u)
                for u in range(2):
                    for n in range(1, NP, 2):
                        dst, rows = destination(n)
                        v.wait_ge(projected, done(NP * (2 * i + u) + n))
                        nc.vector.tensor_copy(dst, pj[0:rows, 1, :]).then_inc(kept_v, 1)
                    for s in range(U + 8):
                        if s < U:
                            shift(i, U * u + s)
                        if 1 <= s < U + 1:
                            total(i, U * u + s - 1)
                        if s >= 11 and s % 4 == 3:
                            residual(i, GRP * u + (s - 11) // 4)
                v.wait_ge(added, done(BODY * i + BODY - 1))
                nc.vector.memset(C.carrier[:, :], 0.0)
                v.wait_ge(vec.done, vec.count)
                v.sem_clear(vec.done)
                vec.restart()

        @block.scalar
        def _(act):
            for x in (F.xnT_ready, kept_a, exped, pT_ready, oT_ready):
                act.sem_inc(x, CREDIT)

            with act.Fori(0, TURNS) as i:
                for u in range(2):
                    F.take(nc, act, C, i, u, pj[:, 0, :])
                for u in range(2):
                    for n in range(0, NP, 2):
                        dst, rows = destination(n)
                        act.wait_ge(projected, done(NP * (2 * i + u) + n))
                        nc.scalar.activation(dst, pj[0:rows, 0, :], ACT.Identity).then_inc(kept_a, 1)
                    for s in range(U + 7):
                        n = units * i + U * u + s
                        if s < U:
                            act.wait_ge(shifted, done(n))
                            nc.scalar.activation(pr[:, s % 4, :, :], pr[:, s % 4, :, :], ACT.Exp).then_inc(exped, 1)
                        if 3 <= s < U + 3:
                            m = s - 3
                            act.wait_ge(weighed, done(n - 5))
                            act.wait_ge(flipped, done(n - 3))
                            nc.scalar.activation(pT[:, m % 2, :, :],
                                                 T[:, m % 2, :].rearrange("p (j t) -> p j t", j=4),
                                                 ACT.Identity).then_inc(pT_ready, 1)
                        if s >= 6 and s % 2 == 0:
                            m = s - 5
                            b, half = divmod(m // 2, 2)
                            if b < GRP:
                                act.wait_ge(out_done, done(BODY * i + GRP * u + b - 1))
                                act.wait_ge(weighed, done(units * i + U * u + m))
                                nc.scalar.activation(oT[:, 4 * half:4 * half + 4, :],
                                                     O[:, half, :].rearrange("p (c t) -> p c t", c=4),
                                                     ACT.Identity).then_inc(oT_ready, 1)

        @block.tensor
        def _(pe):
            for x in (F.turned, projected, scored, flipped, weighed, out_done):
                pe.sem_inc(x, CREDIT)

            def project(i, u, n):
                g = 2 * i + u
                if n % 2 == 0:
                    pe.wait_ge(kept_a, done(12 * g + n // 2 - 1))
                else:
                    pe.wait_ge(kept_v, done(12 * g + n // 2 - 1))
                bank = pj[:, n % 2, :]
                c = n % 8
                if n < 8:
                    ins = nc.tensor.matmul(bank, x2["L2_q"][:, c * P:(c + 1) * P], F.xnT[:, u, :], start=True, stop=True)
                elif n < 16:
                    bt = bank.rearrange("p (b t) -> p b t", b=GRP)
                    ct = ctxT[:, :].rearrange("c (b t) -> c b t", b=GRP)
                    for w, (_, cols) in (("L2_k", parts[0]), ("L2_ki", parts[1])):
                        ins = nc.tensor.matmul(bt[:, :, cols], w96[w][:, c * P:(c + 1) * P], ct[:, :, cols],
                                               start=True, stop=True)
                else:
                    k, half = divmod(n - 16, 2)
                    ins = nc.tensor.matmul(bank, ctxT[:, k * P:(k + 1) * P],
                                           w96["L2_v"][:, 512 * half:512 * half + 512], start=True, stop=True)
                ins.then_inc(projected, 1)

            with pe.Fori(0, TURNS) as i:
                pe.wait_ge(kept_a, done(24 * i - 1))
                F.turn(nc, pe, C, i, 0, pj[:, 0, :])
                pe.wait_ge(F.xnT_ready, done(2 * i))
                F.turn(nc, pe, C, i, 1, pj[:, 0, :])
                for u in range(2):
                    pe.wait_ge(F.xnT_ready, done(2 * i + 1))
                    pe.wait_ge(added, done(BODY * i + GRP * u - 1))
                    for n in range(NP):
                        if n == 8:
                            pe.wait_ge(ctx_in[u], 16 * i + 16)
                        project(i, u, n)
                    pe.wait_ge(kept_a, done(12 * (2 * i + u) + 11))
                    pe.wait_ge(kept_v, done(12 * (2 * i + u) + 11))
                    for s in range(U + 8):
                        n = units * i + U * u + s
                        if s < U:
                            k, q = divmod(s, 4)
                            p, half = q % 2, q // 2
                            rows = slice(64 * p, 64 * p + 64)
                            pe.wait_ge(shifted, done(n - 2))
                            for j in range(4):
                                c = 4 * half + j
                                ins = nc.tensor.matmul(S[:, s % 2, j * P:(j + 1) * P], qT[rows, c, k * P:(k + 1) * P],
                                                       kT[rows, c, k * P:(k + 1) * P], start=True, stop=True)
                            ins.then_inc(scored, 1)
                        if 3 <= s < U + 3:
                            m = s - 3
                            pe.wait_ge(pT_ready, done(n - 5))
                            pe.wait_ge(scaled, done(n - 3))
                            for j in range(4):
                                ins = nc.tensor.transpose(T[:, m % 2, j * P:(j + 1) * P], pr[:, m % 4, j, :], C.ident)
                            ins.then_inc(flipped, 1)
                        if 5 <= s < U + 5:
                            m = s - 5
                            k, q = divmod(m, 4)
                            p, half = q % 2, q // 2
                            if m == 0:
                                pe.wait_ge(ipa_in[u], 16 * i + 16)
                            pe.wait_ge(oT_ready, done(2 * (BODY * i + GRP * u + k - 1) + half))
                            pe.wait_ge(pT_ready, done(n - 5))
                            for j in range(4):
                                h = 8 * half + 2 * j + p
                                ins = nc.tensor.matmul(O[64 * p:64 * p + 64, half, j * P:(j + 1) * P],
                                                       V[:, k, D2 * h:D2 * h + D2], pT[:, m % 2, j, :],
                                                       start=True, stop=True)
                            ins.then_inc(weighed, 1)
                        if s >= 10 and s % 4 == 2:
                            b = (s - 10) // 4
                            pe.wait_ge(added, done(BODY * i + GRP * u + b - 1))
                            pe.wait_ge(oT_ready, done(2 * (BODY * i + GRP * u + b) + 1))
                            for c in range(NCH):
                                ins = nc.tensor.matmul(outp, oT[:, c, :], x2["L2_o"][:, c * P:(c + 1) * P],
                                                       start=(c == 0), stop=(c == NCH - 1))
                            ins.then_inc(out_done, 1)



def shared_experts(nc, C, tg):
    with ExitStack() as ctx:
        a = Alloc(nc, ctx, "L2f")
        F = Front(a)
        R = Router(a, BODY)
        wt = a.sb("wt", [P, BODY, E8])
        r = a.sb("r", [P, 2, 4, 512])
        half = a.sb("half", [P, 2, 512])
        c = a.sb("c", [P, 2, 512])
        cT = a.sb("cT", [P, 2, 4, P])
        H = a.ps("H", [P, 4, 512])
        T = a.ps("T", [P, 512])
        Y = a.ps("Y", [P, 512])
        tr = a.ps("tr", [P, 512])
        lgp = a.ps("lgp", [P, 512])
        We, Wo, Wg = C.f2["We"], C.f2["Wo"], C.f2["Wg"]
        logits = a.sem("logits")
        lg_read = a.sem("lg_read")
        weights = a.sem("weights")
        opened = a.sem("opened")
        relued = a.sem("relued")
        summed = a.sem("summed")
        flipped = a.sem("flipped")
        cT_ready = a.sem("cT_ready")
        closed = a.sem("closed")
        added = a.sem("added")
        own = a.sem("own")
        block = ctx.enter_context(nc.Block())

        @block.gpsimd
        def _(pool):
            pool.sem_inc(F.root_ready, CREDIT)
            with pool.Fori(0, TURNS) as i:
                for u in range(2):
                    F.root(nc, pool, C, i, u)

        @block.vector
        def _(v):
            F.open_vector(v)
            for x in (R.shift_done, lg_read, weights, summed, added):
                v.sem_inc(x, CREDIT)
            vec = Steps(own)
            nc.vector.memset(R.lg[:, :, :], -1e30).then_inc(vec.done, vec.one())
            v.wait_ge(vec.done, vec.count)
            v.sem_clear(vec.done)
            vec.restart()

            def choose(i):
                v.wait_ge(logits, done(i))
                nc.vector.tensor_tensor(R.lg[:, :, 0:4], lgp[:, 0:BODY * 4].rearrange("p (b e) -> p b e", e=4),
                                        C.rows["L2f_bg"].unsqueeze(1).to_broadcast([P, BODY, 4]),
                                        ALU.add).then_inc(lg_read, 1)
                v.wait_ge(lg_read, done(i))
                nc.vector.memset(C.carrier[:, :], 0.0)
                R.choose(nc, v, vec, C, i)
                R.probabilities(nc, v, vec, i)
                nc.vector.tensor_tensor(wt[:, :, :], R.m1[:, :, :], R.rcp[:, :].unsqueeze(2).to_broadcast([P, BODY, E8]),
                                        ALU.mult).then_inc(weights, 1)

            def turn(i, last):
                for s in range(BODY + 2):
                    if not last:
                        if s in (3, 4):
                            F.statistics(nc, v, vec, C, i + 1, s - 3)
                        if s in (5, 6):
                            F.normalise(nc, v, vec, C, i + 1, s - 5)
                        if s == BODY + 1:
                            choose(i + 1)
                    if s < BODY:
                        n = BODY * i + s
                        v.wait_ge(relued, done(4 * n + 3))
                        v.wait_ge(flipped, done(n - 2))
                        for j, dst in ((0, c), (2, half)):
                            nc.vector.tensor_tensor(dst[:, s % 2, :], r[:, s % 2, j, :], r[:, s % 2, j + 1, :], ALU.add).then_inc(vec.done, vec.one())
                        nc.vector.wait_ge(vec.done, vec.count)
                        nc.vector.tensor_tensor(c[:, s % 2, :], c[:, s % 2, :], half[:, s % 2, :],
                                                ALU.add).then_inc(summed, 1)
                    if s >= 2:
                        b = s - 2
                        v.wait_ge(closed, done(BODY * i + b))
                        x = C.Xt[:, bass.ds(i, 1), b, :]
                        nc.vector.scalar_tensor_tensor(out=x, in0=Y[:, 0:P], scalar=tg, in1=x, op0=ALU.mult,
                                                       op1=ALU.add).then_inc(added, 1)
                v.wait_ge(vec.done, vec.count)
                v.sem_clear(vec.done)
                vec.restart()

            for u in range(2):
                F.statistics(nc, v, vec, C, 0, u)
            for u in range(2):
                F.normalise(nc, v, vec, C, 0, u)
            choose(0)
            v.wait_ge(vec.done, vec.count)
            v.sem_clear(vec.done)
            vec.restart()
            with v.Fori(0, TURNS - 1) as i:
                turn(i, False)
            turn(TURNS - 1, True)
            v.wait_ge(added, done(NB - 1))

        @block.scalar
        def _(act):
            for x in (F.xnT_ready, R.exp_done, relued, cT_ready):
                act.sem_inc(x, CREDIT)
            def turn(i, last):
                act.wait_ge(weights, done(i))
                for s in range(BODY + 1):
                    n = BODY * i + s
                    if s < BODY:
                        act.wait_ge(summed, done(n - 2))
                        for e in range(4):
                            act.wait_ge(opened, done(4 * n + e))
                            nc.scalar.activation(r[:, s % 2, e, :], H[:, e, :], ACT.Relu,
                                                 scale=wt[:, s, e:e + 1]).then_inc(relued, 1)
                    if s >= 1:
                        act.wait_ge(closed, done(n - 3))
                        act.wait_ge(flipped, done(n - 1))
                        nc.scalar.activation(cT[:, (s - 1) % 2, :, :], T[:, :].rearrange("p (c t) -> p c t", c=4),
                                             ACT.Identity).then_inc(cT_ready, 1)
                    if s >= BODY - 1 and not last:
                        F.take(nc, act, C, i + 1, s - BODY + 1, tr[:, :])
                if not last:
                    R.exponentials(nc, act, i + 1)

            for u in range(2):
                F.take(nc, act, C, 0, u, tr[:, :])
            R.exponentials(nc, act, 0)
            with act.Fori(0, TURNS - 1) as i:
                turn(i, False)
            turn(TURNS - 1, True)

        @block.tensor
        def _(pe):
            for x in (F.turned, logits, opened, flipped, closed):
                pe.sem_inc(x, CREDIT)

            def front(i, u):
                pe.wait_ge(F.xnT_ready, done(2 * i + u - 1))
                F.turn(nc, pe, C, i, u, tr)

            def route_turn(i):
                pe.wait_ge(F.xnT_ready, done(2 * i + 1))
                pe.wait_ge(lg_read, done(i - 1))
                for b in range(BODY):
                    u, k = divmod(b, GRP)
                    ins = nc.tensor.matmul(lgp[:, b * 4:(b + 1) * 4], F.xnT[:, u, k * P:(k + 1) * P], Wg,
                                           start=True, stop=True)
                ins.then_inc(logits, 1)

            def turn(i, last):
                for s in range(BODY + 2):
                    n = BODY * i + s
                    if s < BODY:
                        u, k = divmod(s, GRP)
                        for e in range(4):
                            pe.wait_ge(relued, done(4 * (n - 1) + e))
                            nc.tensor.matmul(H[:, e, :], F.xnT[:, u, k * P:(k + 1) * P], We[:, 512 * e:512 * e + 512],
                                             start=True, stop=True).then_inc(opened, 1)
                    if s in (BODY - 1, BODY) and not last:
                        front(i + 1, s - BODY + 1)
                    if s == BODY + 1 and not last:
                        route_turn(i + 1)
                    if 1 <= s < BODY + 1:
                        pe.wait_ge(cT_ready, done(n - 2))
                        pe.wait_ge(summed, done(n - 1))
                        for j in range(4):
                            ins = nc.tensor.transpose(T[:, j * P:(j + 1) * P], c[:, (s - 1) % 2, j * P:(j + 1) * P], C.ident)
                        ins.then_inc(flipped, 1)
                    if s >= 2:
                        pe.wait_ge(added, done(n - 3))
                        pe.wait_ge(cT_ready, done(n - 2))
                        for j in range(4):
                            ins = nc.tensor.matmul(Y[:, 0:P], cT[:, s % 2, j, :], Wo[:, j * P:(j + 1) * P],
                                                   start=(j == 0), stop=(j == 3))
                        ins.then_inc(closed, 1)

            front(0, 0)
            front(0, 1)
            route_turn(0)
            with pe.Fori(0, TURNS - 1) as i:
                turn(i, False)
            turn(TURNS - 1, True)



NS = 64
SC = 32
TWO_PI = (6.28125, 0.0019350051879882812, 3.019915981956753e-07)
ROUND = 1.5 * 2.0 ** 23
HALF_TURN = 3.1415925


def convolution_kernel(nc, C, x3, w_rows):
    with ExitStack() as ctx:
        a = Alloc(nc, ctx, "s4d")
        dt = a.sb("dt", [P, 1])
        names = "th q f sh cos sin ar er zr zi z2r z2i wr nr ni den cr ci t0 t1".split()
        B = {n: a.sb(n, [P, NS])[:, :] for n in names}
        Pr = a.sb("Pr", [P, SC, P])
        Pi = a.sb("Pi", [P, SC, P // 2])
        u0 = a.sb("u0", [P, SC, P // 2])
        u1 = a.sb("u1", [P, SC, P // 2])
        K = a.sb("K", [P, P])
        K2 = a.sb("K2", [P, P])
        pad = a.sb("pad", [P, 2 * P])
        dt_done, angle, sines = a.sem("dt_done"), a.sem("angle"), a.sem("sines")
        own, ready, stored = a.sem("own"), a.sem("ready"), a.sem("stored")
        block = ctx.enter_context(nc.Block())

        @block.scalar
        def _(act):
            act.wait_ge(C.last_landed, 16)
            nc.scalar.activation(dt[:, :], x3["log_dt"], ACT.Exp).then_inc(dt_done, 1)
            act.wait_ge(angle, 1)
            nc.scalar.activation(B["er"], B["ar"], ACT.Exp).then_inc(sines, 1)
            nc.scalar.activation(B["sin"], B["f"], ACT.Sin).then_inc(sines, 1)
            nc.scalar.activation(B["sh"], B["f"], ACT.Sin, scale=0.5).then_inc(sines, 1)

        @block.vector
        def _(v):
            vec = Steps(own)

            def tt(out, x, y, op):
                nc.vector.tensor_tensor(out, x, y, op).then_inc(vec.done, vec.one())
                nc.vector.wait_ge(vec.done, vec.count)

            def ts(out, x, s1, s2, op0, op1=ALU.bypass):
                ins = (nc.vector.tensor_scalar(out, x, s1, s2, op0, op1) if s2 is not None
                       else nc.vector.tensor_scalar(out, x, s1, None, op0))
                ins.then_inc(vec.done, vec.one())
                nc.vector.wait_ge(vec.done, vec.count)

            def product(outr, outi, xr, xi, yr, yi, t0, t1):
                tt(t0, xr, yr, ALU.mult)
                tt(t1, xi, yi, ALU.mult)
                tt(outr, t0, t1, ALU.subtract)
                if outi is not None:
                    tt(t0, xr, yi, ALU.mult)
                    tt(t1, xi, yr, ALU.mult)
                    tt(outi, t0, t1, ALU.add)

            v.wait_ge(dt_done, 1)
            ts(B["ar"], x3["A_re"], dt[:, 0:1], None, ALU.mult)
            ts(B["th"], x3["A_im"], dt[:, 0:1], None, ALU.mult)
            ts(B["q"], B["th"], 1.0 / (2.0 * 3.141592653589793), ROUND, ALU.mult, ALU.add)
            ts(B["q"], B["q"], ROUND, None, ALU.subtract)
            src = B["th"]
            for part in TWO_PI:
                nc.vector.scalar_tensor_tensor(out=B["f"], in0=B["q"], scalar=-part, in1=src,
                                                       op0=ALU.mult, op1=ALU.add).then_inc(vec.done, vec.one())
                nc.vector.wait_ge(vec.done, vec.count)
                src = B["f"]
            nc.vector.tensor_scalar(B["f"], B["f"], HALF_TURN, -HALF_TURN, ALU.min, ALU.max).then_inc(angle, 1)
            v.wait_ge(sines, 3)
            tt(B["cos"], B["sh"], B["sh"], ALU.mult)
            ts(B["cos"], B["cos"], -2.0, 1.0, ALU.mult, ALU.add)
            tt(B["zr"], B["er"], B["cos"], ALU.mult)
            tt(B["zi"], B["er"], B["sin"], ALU.mult)
            ts(B["wr"], B["zr"], 1.0, None, ALU.subtract)
            product(B["nr"], B["ni"], x3["C_re"], x3["C_im"], B["wr"], B["zi"], B["t0"], B["t1"])
            tt(B["t0"], x3["A_re"], x3["A_re"], ALU.mult)
            tt(B["t1"], x3["A_im"], x3["A_im"], ALU.mult)
            tt(B["den"], B["t0"], B["t1"], ALU.add)
            nc.vector.reciprocal(B["den"], B["den"]).then_inc(vec.done, vec.one())
            nc.vector.wait_ge(vec.done, vec.count)
            ts(B["den"], B["den"], 2.0, None, ALU.mult)
            ts(B["z2i"], x3["A_im"], -1.0, None, ALU.mult)
            product(B["cr"], B["ci"], B["nr"], B["ni"], x3["A_re"], B["z2i"], B["t0"], B["t1"])
            tt(B["cr"], B["cr"], B["den"], ALU.mult)
            tt(B["ci"], B["ci"], B["den"], ALU.mult)
            for part in range(NS // SC):
                n = slice(SC * part, SC * part + SC)
                nc.vector.tensor_copy(Pr[:, :, 0:1], B["cr"][:, n].unsqueeze(2)).then_inc(vec.done, vec.one())
                nc.vector.tensor_copy(Pi[:, :, 0:1], B["ci"][:, n].unsqueeze(2)).then_inc(vec.done, vec.one())
                nc.vector.wait_ge(vec.done, vec.count)
                L, z = 1, ("zr", "zi")
                while L < P:
                    wide = lambda x: B[x][:, n].unsqueeze(2).to_broadcast([P, SC, L])
                    product(Pr[:, :, L:2 * L], Pi[:, :, L:2 * L] if 2 * L < P else None, Pr[:, :, 0:L], Pi[:, :, 0:L],
                            wide(z[0]), wide(z[1]), u0[:, :, 0:L], u1[:, :, 0:L])
                    if 2 * L < P:
                        new = ("z2r", "z2i") if z[0] in ("zr", "nr") else ("nr", "ni")
                        product(B[new[0]][:, n], B[new[1]][:, n], B[z[0]][:, n], B[z[1]][:, n],
                                B[z[0]][:, n], B[z[1]][:, n], B["t0"][:, n], B["t1"][:, n])
                        z = new
                    L *= 2
                nc.vector.tensor_reduce((K2 if part else K)[:, :], Pr[:, :, :].rearrange("p n l -> p l n"),
                                                AX.X, ALU.add).then_inc(vec.done, vec.one())
                nc.vector.wait_ge(vec.done, vec.count)
            nc.vector.memset(pad[:, :], 0.0).then_inc(vec.done, vec.one())
            nc.vector.wait_ge(vec.done, vec.count)
            tt(pad[:, P - 1:2 * P - 1], K[:, :], K2[:, :], ALU.add)
            tt(pad[:, P - 1:P], pad[:, P - 1:P], x3["D_skip"], ALU.add)
            mg = C.rows["mod_gate"]
            ts(x3["film"], x3["film"], mg, None, ALU.mult)
            ts(C.rows["L3_film"], C.rows["L3_film"], mg, None, ALU.mult)
            for at in (0, 256):
                fb = C.rows["L3_film"][:, at:at + P]
                ts(fb, fb, 1.0, None, ALU.add)
            nc.vector.memset(C.carrier[:, :], 0.0).then_inc(ready, 1)

        @block.sync
        def _(sp):
            sp.wait_ge(ready, 1)
            sp.dma_start(C.kpad_dram, pad[:, :]).then_inc(stored, 16)
            sp.wait_ge(stored, 16)



KTOP = 32
H3, D3 = 4, 32
MASKED = -1e30
TAKEN = -3e38


def attention_top32(nc, C, x3, w96, xin):
    with ExitStack() as ctx:
        a = Alloc(nc, ctx, "L3")
        F = Front(a)
        N2 = Norm(a, "n2")
        ctxT = a.sb("ctxT", [KV, 2, TOK])
        qT = a.sb("qT", [P, 2, TOK])
        kT = a.sb("kT", [P, 2, TOK])
        kx = a.sb("kx", [P, 2, H3, P])
        V = a.sb("V", [P, 2, GRP, P])
        x1 = a.sb("x1", [P, 2, GRP, P])
        A = a.sb("A", [P, 2, H3, P])
        Wk = a.sb("Wk", [P, 2, H3, P])
        E = a.sb("E", [P, 2, H3, P])
        D = a.sb("D", [P, 2, H3, P])
        neg = a.sb("neg", [P, P])
        top = a.sb("top", [P, 2, H3, 8])
        top2 = a.sb("top2", [P, H3, 8])
        nmax = a.sb("nmax", [P, 2, H3])
        sm = a.sb("sm", [P, H3])
        rc = a.sb("rc", [P, 2, H3])
        aT = a.sb("aT", [P, 2, P])
        ctT = a.sb("ctT", [P, 2, TOK])
        t = a.sb("t", [P, P])
        pj = a.ps("pj", [P, 2, 512])
        S = a.ps("S", [P, 2, 512])
        tb = a.ps("tb", [P, 512])
        cb = a.ps("cb", [P, 512])
        fb = a.ps("fb", [P, 512])

        ctx_in = [a.sem(f"ctx_in{u}") for u in range(2)]
        ct_out = [a.sem(f"ct_out{u}") for u in range(2)]
        ct_stored = a.sem("ct_stored")
        projected = a.sem("projected")
        q_ready = a.sem("q_ready")
        k_ready = a.sem("k_ready")
        v_ready = a.sem("v_ready")
        spread = a.sem("spread")
        x1_ready = a.sem("x1_ready")
        x1_scaled = a.sem("x1_scaled")
        x1_done = a.sem("x1_done")
        scored = a.sem("scored")
        masked = a.sem("masked")
        chosen = a.sem("chosen")
        exped = a.sem("exped")
        kept = a.sem("kept")
        weights = a.sem("weights")
        weighted = a.sem("weighted")
        averaged = a.sem("averaged")
        aT_ready = a.sem("aT_ready")
        ct_done = a.sem("ct_done")
        ctT_ready = a.sem("ctT_ready")
        film_done = a.sem("film_done")
        film_read = a.sem("film_read")
        own = a.sem("own")
        block = ctx.enter_context(nc.Block())
        xt = xin[:, :].rearrange("p (i b d) -> p i b d", i=TURNS, b=BODY)
        STEPS = BODY + 5

        @block.sync
        def _(sp):
            sp.sem_inc(ct_stored, CREDIT)
            with sp.Fori(0, TURNS) as i:
                for u in range(2):
                    sp.wait_ge(projected, done(6 * i + 3 * u - 4))
                    sp.dma_start(ctxT[:, u, :], C.ctxT_v[:, bass.ds(i, 1), u, :]).then_inc(ctx_in[u], 16)
                for u in range(2):
                    sp.wait_ge(ctT_ready, done(BODY * i + GRP * u + GRP - 1))
                    sp.dma_start(C.ctT_v[:, bass.ds(i, 1), u, :], ctT[:, u, :]).then_inc(ct_out[u], 16)
                for u in range(2):
                    sp.wait_ge(ct_out[u], 16 * i + 16)
                    sp.sem_inc(ct_stored, 1)

        @block.gpsimd
        def _(pool):
            for x in (F.root_ready, N2.root_ready, spread, x1_done, kept, weighted):
                pool.sem_inc(x, CREDIT)
            with pool.Fori(0, TURNS) as i:
                for u in range(2):
                    F.root(nc, pool, C, i, u)

                def keys(b):
                    u, k = divmod(b, GRP)
                    pool.wait_ge(k_ready, done(2 * i + u))
                    pool.wait_ge(scored, done(BODY * i + b - 2))
                    nc.gpsimd.tensor_tensor(
                        kx[:, b % 2, :, :], kT[:, u, k * P:(k + 1) * P].unsqueeze(1).to_broadcast([P, H3, P]),
                        C.head_mask.unsqueeze(2).to_broadcast([P, H3, P]), ALU.mult).then_inc(spread, 1)

                keys(0)
                keys(1)
                for u in range(2):
                    N2.root(nc, pool, C, i, u)
                for u in range(2):
                    pool.wait_ge(x1_ready, done(2 * i + u))
                    g_row = C.rows["L3_g_in"].unsqueeze(1).to_broadcast([P, GRP, P])
                    b_row = C.rows["L3_b_in"].unsqueeze(1).to_broadcast([P, GRP, P])
                    nc.gpsimd.tensor_tensor(x1[:, u, :, :], x1[:, u, :, :], g_row, ALU.mult).then_inc(x1_scaled, 1)
                    pool.wait_ge(x1_scaled, 2 * i + u + 1)
                    nc.gpsimd.tensor_tensor(x1[:, u, :, :], x1[:, u, :, :], b_row, ALU.add).then_inc(x1_done, 1)
                for s in range(BODY + 1):
                    n = BODY * i + s
                    if s < BODY:
                        pool.wait_ge(exped, done(n))
                        nc.gpsimd.tensor_tensor(E[:, s % 2, :, :], E[:, s % 2, :, :], Wk[:, s % 2, :, :],
                                                ALU.subtract).then_inc(kept, 1)
                        if s + 2 < BODY:
                            keys(s + 2)
                    if s >= 1:
                        pool.wait_ge(weights, done(n - 1))
                        pool.wait_ge(averaged, done(n - 3))
                        nc.gpsimd.tensor_tensor(D[:, (s - 1) % 2, :, :], C.ident.unsqueeze(1).to_broadcast([P, H3, P]),
                                                rc[:, (s - 1) % 2, :].unsqueeze(2).to_broadcast([P, H3, P]),
                                                ALU.mult).then_inc(weighted, 1)

        @block.vector
        def _(v):
            F.open_vector(v)
            for x in (N2.var_ready, x1_ready, masked, chosen, weights, film_read):
                v.sem_inc(x, CREDIT)
            vec = Steps(own)

            def choose(i, s):
                n = BODY * i + s
                nc.vector.tensor_scalar(neg[:, :], C.kv_mask_v[:, bass.ds(i, 1), s, :], 1.0, -MASKED,
                                                ALU.subtract, ALU.mult).then_inc(vec.done, vec.one())
                v.wait_ge(exped, done(n - 2))
                v.wait_ge(kept, done(n - 2))
                v.wait_ge(scored, done(n))
                nc.vector.wait_ge(vec.done, vec.count)
                nc.vector.tensor_tensor(A[:, s % 2, :, :], S[:, s % 2, :].rearrange("p (h t) -> p h t", h=H3),
                                        neg[:, :].unsqueeze(1).to_broadcast([P, H3, P]), ALU.add).then_inc(masked, 1)
                v.wait_ge(masked, done(n))
                nc.vector.memset(C.carrier[:, :], 0.0)
                replaced = [vec.count] * H3
                for r in range(KTOP // 8):
                    src = A if r == 0 else Wk
                    t8 = top[:, s % 2, :, :] if r == 0 else top2[:, :, :]
                    found = []
                    for h in range(H3):
                        nc.vector.wait_ge(vec.done, replaced[h])
                        nc.vector.max(t8[:, h, :], src[:, s % 2, h, :]).then_inc(vec.done, vec.one())
                        found.append(vec.count)
                    for h in range(H3):
                        nc.vector.wait_ge(vec.done, found[h])
                        nc.vector.match_replace(Wk[:, s % 2, h, :], t8[:, h, :], src[:, s % 2, h, :],
                                                TAKEN).then_inc(vec.done, vec.one())
                        replaced[h] = vec.count
                nc.vector.wait_ge(vec.done, vec.count)
                nc.vector.tensor_scalar(nmax[:, s % 2, :], top[:, s % 2, :, 0], -1.0, None, ALU.mult).then_inc(chosen, 1)

            def total(i, b):
                v.wait_ge(kept, done(BODY * i + b))
                nc.vector.tensor_reduce(sm[:, :], E[:, b % 2, :, :], AX.X, ALU.add).then_inc(vec.done, vec.one())
                nc.vector.wait_ge(vec.done, vec.count)
                nc.vector.reciprocal(sm[:, :], sm[:, :]).then_inc(vec.done, vec.one())
                nc.vector.wait_ge(vec.done, vec.count)
                nc.vector.tensor_scalar(rc[:, b % 2, :], sm[:, :], C.q_mask_v[:, bass.ds(i, 1), b], 1.0 / H3,
                                        ALU.mult, ALU.mult).then_inc(weights, 1)

            def modulate(i, b):
                u, k = divmod(b, GRP)
                n = BODY * i + b
                v.wait_ge(x1_done, done(2 * i + u))
                v.wait_ge(film_done, done(n))
                nc.vector.wait_ge(vec.done, vec.count)
                nc.vector.tensor_tensor(t[:, :], x1[:, u, k, :], fb[:, 0:P], ALU.mult).then_inc(vec.done, vec.one())
                nc.vector.wait_ge(vec.done, vec.count)
                nc.vector.tensor_tensor(xt[:, bass.ds(i, 1), b, :], t[:, :], fb[:, P:2 * P], ALU.add).then_inc(
                    film_read, 1)

            with v.Fori(0, TURNS) as i:
                for u in range(2):
                    F.statistics(nc, v, vec, C, i, u)
                for u in range(2):
                    F.normalise(nc, v, vec, C, i, u)
                v.wait_ge(F.st_ready, done(2 * i + 1))
                nc.vector.memset(C.carrier[:, :], 0.0)
                for u in range(2):
                    N2.statistics(nc, vec, lambda k: F.st[:, u, k, :], u)
                for u in range(2):
                    N2.affine(nc, v, vec, i, u)
                    for k in range(GRP):
                        ins = N2.apply(nc, x1[:, u, k, :], F.st[:, u, k, :], u, k)
                    ins.then_inc(x1_ready, 1)
                for s in range(STEPS):
                    if s < BODY:
                        choose(i, s)
                    if 1 <= s < BODY + 1:
                        total(i, s - 1)
                    if 5 <= s < BODY + 5:
                        modulate(i, s - 5)
                v.wait_ge(film_read, done(BODY * i + BODY - 1))
                nc.vector.memset(C.carrier[:, :], 0.0)
                v.wait_ge(vec.done, vec.count)
                v.sem_clear(vec.done)
                vec.restart()

        @block.scalar
        def _(act):
            for x in (F.xnT_ready, q_ready, k_ready, v_ready, exped, aT_ready, ctT_ready):
                act.sem_inc(x, CREDIT)
            with act.Fori(0, TURNS) as i:
                for u in range(2):
                    F.take(nc, act, C, i, u, pj[:, u, :])
                for u in range(2):
                    act.wait_ge(projected, done(6 * i + 3 * u))
                    nc.scalar.activation(qT[:, u, :], pj[:, u, :], ACT.Identity,
                                         scale=D3 ** -0.5).then_inc(q_ready, 1)
                    act.wait_ge(spread, done(BODY * i + GRP * u + 3 - BODY))
                    act.wait_ge(projected, done(6 * i + 3 * u + 1))
                    nc.scalar.activation(kT[:, u, :], pj[:, 1 - u, :], ACT.Identity).then_inc(k_ready, 1)
                    act.wait_ge(projected, done(6 * i + 3 * u + 2))
                    nc.scalar.activation(V[:, u, :, :], pj[:, u, :].rearrange("p (b d) -> p b d", b=GRP),
                                         ACT.Identity).then_inc(v_ready, 1)
                for s in range(BODY + 4):
                    n = BODY * i + s
                    if 2 <= s < BODY + 2:
                        act.wait_ge(ct_done, done(n - 4))
                        act.wait_ge(averaged, done(n - 2))
                        nc.scalar.activation(aT[:, (s - 2) % 2, :], tb[:, 0:P], ACT.Identity).then_inc(aT_ready, 1)
                    if 3 <= s < BODY + 3:
                        b = s - 3
                        if b % GRP == 0:
                            act.wait_ge(ct_stored, done(2 * (i - 1) + b // GRP))
                        act.wait_ge(ct_done, done(BODY * i + b))
                        nc.scalar.activation(ctT[:, b // GRP, b % GRP * P:(b % GRP + 1) * P], cb[:, 0:P],
                                             ACT.Identity).then_inc(ctT_ready, 1)
                    if s < BODY:
                        act.wait_ge(averaged, done(n - 2))
                        act.wait_ge(chosen, done(n))
                        for x in (E, Wk):
                            src = A if x is E else Wk
                            for h in range(H3):
                                ins = nc.scalar.activation(x[:, s % 2, h, :], src[:, s % 2, h, :], ACT.Exp,
                                                           bias=nmax[:, s % 2, h:h + 1])
                        ins.then_inc(exped, 1)

        @block.tensor
        def _(pe):
            for x in (F.turned, projected, scored, averaged, ct_done, film_done):
                pe.sem_inc(x, CREDIT)

            with pe.Fori(0, TURNS) as i:
                pe.wait_ge(k_ready, done(2 * i - 1))
                F.turn(nc, pe, C, i, 0, pj[:, 0, :])
                pe.wait_ge(v_ready, done(2 * i - 1))
                F.turn(nc, pe, C, i, 1, pj[:, 1, :])
                for u in range(2):
                    g = 2 * i + u
                    pe.wait_ge(F.xnT_ready, done(2 * i + 1))
                    if u:
                        pe.wait_ge(k_ready, done(2 * i))
                    nc.tensor.matmul(pj[:, u, :], x3["q"], F.xnT[:, u, :], start=True, stop=True).then_inc(
                        projected, 1)
                    pe.wait_ge(ctx_in[u], 16 * i + 16)
                    if u:
                        pe.wait_ge(v_ready, done(2 * i))
                    nc.tensor.matmul(pj[:, 1 - u, :], w96["L3_k"], ctxT[:, u, :], start=True, stop=True).then_inc(
                        projected, 1)
                    pe.wait_ge(q_ready, done(g))
                    for k in range(GRP):
                        ins = nc.tensor.matmul(pj[:, u, k * P:(k + 1) * P], ctxT[:, u, k * P:(k + 1) * P],
                                               w96["L3_v"], start=True, stop=True)
                    ins.then_inc(projected, 1)
                for s in range(BODY + 4):
                    n = BODY * i + s
                    if s < BODY:
                        u, k = divmod(s, GRP)
                        pe.wait_ge(q_ready, done(2 * i + u))
                        pe.wait_ge(masked, done(n - 2))
                        pe.wait_ge(spread, done(n))
                        nc.tensor.matmul(S[:, s % 2, :], qT[:, u, k * P:(k + 1) * P], kx[:, s % 2, :, :],
                                         start=True, stop=True).then_inc(scored, 1)
                    if 2 <= s < BODY + 2:
                        pe.wait_ge(aT_ready, done(n - 3))
                        pe.wait_ge(weighted, done(n - 2))
                        for h in range(H3):
                            ins = nc.tensor.matmul(tb[:, 0:P], E[:, s % 2, h, :], D[:, s % 2, h, :], start=(h == 0),
                                                   stop=(h == H3 - 1))
                        ins.then_inc(averaged, 1)
                    if 3 <= s < BODY + 3:
                        b = s - 3
                        u, k = divmod(b, GRP)
                        pe.wait_ge(v_ready, done(2 * i + u))
                        pe.wait_ge(ctT_ready, done(n - 4))
                        pe.wait_ge(aT_ready, done(n - 3))
                        nc.tensor.matmul(cb[:, 0:P], V[:, u, k, :], aT[:, b % 2, :], start=True, stop=True).then_inc(
                            ct_done, 1)
                    if 4 <= s:
                        b = s - 4
                        pe.wait_ge(film_read, done(n - 5))
                        pe.wait_ge(ctT_ready, done(n - 4))
                        nc.tensor.matmul(fb[:, 0:2 * P], ctT[:, b // GRP, b % GRP * P:(b % GRP + 1) * P],
                                         x3["film"][:, 0:2 * P], start=True, stop=False)
                        nc.tensor.matmul(fb[:, 0:2 * P], C.ones[0:1, :], C.rows["L3_film"][0:1, 0:2 * P], start=False,
                                         stop=True).then_inc(film_done, 1)



CD = 16
CHUNKS = P // CD
RING = 3


def convolve(nc, C, xin):
    with ExitStack() as ctx:
        a = Alloc(nc, ctx, "conv")
        xr = a.sb("xr", [P, NB * P])
        Tz = a.sb("Tz", [P, RING, CD, P])
        rev = a.ps("rev", [P, 2, 512])
        Y = a.ps("Y", [P, 2, 512])
        fetched = [a.sem(f"fetched{k}") for k in range(RING)]
        reversed_, kept_a, kept_v = a.sem("reversed"), a.sem("kept_a"), a.sem("kept_v")
        summed, y_a, y_v = a.sem("summed"), a.sem("y_a"), a.sem("y_v")
        xr3 = xr[:, :].rearrange("p (b d) -> p b d", b=NB)
        y3 = xin[:, :].rearrange("p (b d) -> p d b", b=NB)
        kpad = C.kpad_dram
        block = ctx.enter_context(nc.Block())

        @block.sync
        def _(sp):
            for c in range(CHUNKS):
                if c >= RING:
                    sp.wait_ge(summed, c - RING + 1)
                src = bass.AP(tensor=kpad.tensor, offset=kpad.offset + c * CD * 2 * P,
                              ap=[[1, P], [2 * P, CD], [1, P]])
                sp.dma_start(Tz[:, c % RING, :, :], src).then_inc(fetched[c % RING], 16)

        @block.tensor
        def _(pe):
            for c in range(8):
                if c >= 2:
                    pe.wait_ge(kept_v if c % 2 else kept_a, c // 2)
                nc.tensor.matmul(rev[:, c % 2, :], C.reverse, xin[:, 512 * c:512 * c + 512],
                                 start=True, stop=True).then_inc(reversed_, 1)
            pe.wait_ge(kept_a, 4)
            pe.wait_ge(kept_v, 4)
            for c in range(CHUNKS):
                pe.wait_ge(fetched[c % RING], 16 * (c // RING + 1))
                if c >= 2:
                    pe.wait_ge(y_v if c % 2 else y_a, c // 2)
                for d in range(CD):
                    ins = nc.tensor.matmul(Y[:, c % 2, d * NB:(d + 1) * NB], Tz[:, c % RING, d, :],
                                           xr3[:, :, c * CD + d], start=True, stop=True)
                ins.then_inc(summed, 1)

        @block.scalar
        def _(act):
            for c in range(0, 8, 2):
                act.wait_ge(reversed_, c + 1)
                nc.scalar.activation(xr[:, 512 * c:512 * c + 512], rev[:, 0, :], ACT.Identity).then_inc(kept_a, 1)
            for c in range(0, CHUNKS, 2):
                act.wait_ge(summed, c + 1)
                nc.scalar.activation(y3[:, c * CD:(c + 1) * CD, :], Y[:, 0, :].rearrange("p (d b) -> p d b", d=CD),
                                     ACT.Identity).then_inc(y_a, 1)

        @block.vector
        def _(v):
            for c in range(1, 8, 2):
                v.wait_ge(reversed_, c + 1)
                nc.vector.tensor_copy(xr[:, 512 * c:512 * c + 512], rev[:, 1, :]).then_inc(kept_v, 1)
            for c in range(1, CHUNKS, 2):
                v.wait_ge(summed, c + 1)
                nc.vector.tensor_copy(y3[:, c * CD:(c + 1) * CD, :],
                                      Y[:, 1, :].rearrange("p (d b) -> p d b", d=CD)).then_inc(y_v, 1)



def film_feed_forward(nc, C, x3, y, tg):
    NC = 4
    with ExitStack() as ctx:
        a = Alloc(nc, ctx, "L3b")
        F = Front(a)
        NF, NO = Norm(a, "nf"), Norm(a, "no")
        ctT = a.sb("ctT", [P, 2, TOK])
        film = a.sb("film", [P, 2, 2 * P])
        y2 = a.sb("y2", [P, 2, P])
        hn = a.sb("hn", [P, 2, GRP, P])
        hT = a.sb("hT", [P, 2, TOK])
        aT = a.sb("aT", [P, 2, NC, TOK])
        fb = a.ps("fb", [P, 2, 512])
        tr = a.ps("tr", [P, 512])
        U = a.ps("U", [P, 3, 512])
        Y = a.ps("Y", [P, 2, 512])
        ct_in = [a.sem(f"ct_in{u}") for u in range(2)]
        film_done = a.sem("film_done")
        film_read = a.sem("film_read")
        hn_ready = a.sem("hn_ready")
        turned = a.sem("turned2")
        hT_ready = a.sem("hT_ready")
        opened = a.sem("opened")
        a_ready = a.sem("a_ready")
        closed = a.sem("closed")
        y_read = a.sem("y_read")
        own = a.sem("own")
        block = ctx.enter_context(nc.Block())
        yt = y[:, :].rearrange("p (i b d) -> p i b d", i=TURNS, b=BODY)

        @block.sync
        def _(sp):
            with sp.Fori(0, TURNS) as i:
                for u in range(2):
                    sp.wait_ge(film_done, done(BODY * (i - 1) + GRP * u + GRP - 1))
                    sp.dma_start(ctT[:, u, :], C.ctT_v[:, bass.ds(i, 1), u, :]).then_inc(ct_in[u], 16)

        @block.gpsimd
        def _(pool):
            for x in (F.N, NF, NO):
                pool.sem_inc(x.root_ready, CREDIT)
            with pool.Fori(0, TURNS) as i:
                for x in (F.N, NF, NO):
                    for u in range(2):
                        x.root(nc, pool, C, i, u)

        @block.vector
        def _(v):
            for x in (F.N.var_ready, NF.var_ready, NO.var_ready, film_read, hn_ready, y_read):
                v.sem_inc(x, CREDIT)
            vec = Steps(own)
            b2_row = C.rows["L3_b2"].unsqueeze(1).to_broadcast([P, GRP, P])
            g_row = C.rows["L3_g_out"].unsqueeze(1).to_broadcast([P, GRP, P])
            b_row = C.rows["L3_b_out"].unsqueeze(1).to_broadcast([P, GRP, P])
            with v.Fori(0, TURNS) as i:
                for u in range(2):
                    F.statistics(nc, v, vec, C, i, u)
                for u in range(2):
                    F.N.affine(nc, v, vec, i, u)
                    for k in range(GRP):
                        F.N.apply(nc, F.st[:, u, k, :], C.Xt[:, bass.ds(i, 1), GRP * u + k, :], u, k).then_inc(vec.done, vec.one())
                for b in range(BODY):
                    u, k = divmod(b, GRP)
                    v.wait_ge(film_done, done(BODY * i + b))
                    nc.vector.tensor_tensor(film[:, b % 2, :], fb[:, b % 2, 0:2 * P], C.rows["L3_film"][:, 2 * P:4 * P],
                                            ALU.add).then_inc(film_read, 1)
                    v.wait_ge(film_read, done(BODY * i + b))
                    nc.vector.tensor_tensor(y2[:, b % 2, :], yt[:, bass.ds(i, 1), b, :], film[:, b % 2, 0:P],
                                                    ALU.mult).then_inc(vec.done, vec.one())
                    nc.vector.wait_ge(vec.done, vec.count)
                    nc.vector.tensor_tensor(y2[:, b % 2, :], y2[:, b % 2, :], film[:, b % 2, P:2 * P], ALU.add).then_inc(vec.done, vec.one())
                    nc.vector.wait_ge(vec.done, vec.count)
                    nc.vector.tensor_tensor(F.st[:, u, k, :], F.st[:, u, k, :], y2[:, b % 2, :], ALU.add).then_inc(vec.done, vec.one())
                nc.vector.wait_ge(vec.done, vec.count)
                for u in range(2):
                    NF.statistics(nc, vec, lambda k: F.st[:, u, k, :], u)
                for u in range(2):
                    NF.affine(nc, v, vec, i, u)
                    v.wait_ge(turned, done(2 * (i - 1) + u))
                    for k in range(GRP):
                        ins = NF.apply(nc, hn[:, u, k, :], F.st[:, u, k, :], u, k)
                    ins.then_inc(hn_ready, 1)
                    v.wait_ge(hn_ready, done(2 * i + u))
                    nc.vector.tensor_tensor(F.st[:, u, :, :], F.st[:, u, :, :], b2_row, ALU.add).then_inc(vec.done, vec.one())
                nc.vector.wait_ge(vec.done, vec.count)
                for u in range(2):
                    v.wait_ge(closed, done(2 * i + u))
                    nc.vector.tensor_tensor(F.st[:, u, :, :], F.st[:, u, :, :],
                                            Y[:, u, :].rearrange("p (k d) -> p k d", k=GRP), ALU.add).then_inc(y_read, 1)
                    v.wait_ge(y_read, done(2 * i + u))
                    nc.vector.memset(C.carrier[:, :], 0.0)
                    NO.statistics(nc, vec, lambda k: F.st[:, u, k, :], u)
                for u in range(2):
                    NO.affine(nc, v, vec, i, u)
                    for k in range(GRP):
                        NO.apply(nc, F.st[:, u, k, :], F.st[:, u, k, :], u, k).then_inc(vec.done, vec.one())
                    nc.vector.wait_ge(vec.done, vec.count)
                    nc.vector.tensor_tensor(F.st[:, u, :, :], F.st[:, u, :, :], g_row, ALU.mult).then_inc(vec.done, vec.one())
                    nc.vector.wait_ge(vec.done, vec.count)
                    nc.vector.tensor_tensor(F.st[:, u, :, :], F.st[:, u, :, :], b_row, ALU.add).then_inc(vec.done, vec.one())
                    nc.vector.wait_ge(vec.done, vec.count)
                    x = C.Xt[:, bass.ds(i, 1), GRP * u:GRP * u + GRP, :].rearrange("p o k d -> p (o k d)")
                    nc.vector.scalar_tensor_tensor(out=x, in0=F.st[:, u, :, :].rearrange("p k d -> p (k d)"),
                                                           scalar=tg, in1=x, op0=ALU.mult, op1=ALU.add).then_inc(vec.done, vec.one())
                v.wait_ge(vec.done, vec.count)
                v.sem_clear(vec.done)
                vec.restart()

        @block.scalar
        def _(act):
            for x in (hT_ready, a_ready):
                act.sem_inc(x, CREDIT)
            with act.Fori(0, TURNS) as i:
                for u in range(2):
                    act.wait_ge(turned, done(2 * i + u))
                    nc.scalar.activation(hT[:, u, :], tr[:, :], ACT.Identity, scale=x3["g_ffn"],
                                         bias=x3["b_ffn"]).then_inc(hT_ready, 1)
                for u in range(2):
                    for c in range(NC):
                        n = NC * (2 * i + u) + c
                        act.wait_ge(opened, done(n))
                        nc.scalar.activation(aT[:, u, c, :], U[:, (NC * u + c) % 2, :], ACT.Gelu,
                                             bias=x3["b1"][:, c:c + 1]).then_inc(a_ready, 1)

        @block.tensor
        def _(pe):
            for x in (film_done, turned, opened, closed):
                pe.sem_inc(x, CREDIT)
            w2 = x3["W2"].rearrange("p (c d) -> p c d", c=NC)
            with pe.Fori(0, TURNS) as i:
                for b in range(BODY):
                    u, k = divmod(b, GRP)
                    if k == 0:
                        pe.wait_ge(ct_in[u], 16 * i + 16)
                    pe.wait_ge(film_read, done(BODY * i + b - 2))
                    nc.tensor.matmul(fb[:, b % 2, 0:2 * P], ctT[:, u, k * P:(k + 1) * P], x3["film"][:, 2 * P:4 * P],
                                     start=True, stop=True).then_inc(film_done, 1)
                for u in range(2):
                    pe.wait_ge(hT_ready, done(2 * i + u - 1))
                    pe.wait_ge(hn_ready, done(2 * i + u))
                    for k in range(GRP):
                        ins = nc.tensor.transpose(tr[:, k * P:(k + 1) * P], hn[:, u, k, :], C.ident)
                    ins.then_inc(turned, 1)
                for u in range(2):
                    pe.wait_ge(hT_ready, done(2 * i + u))
                    for c in range(NC):
                        n = NC * (2 * i + u) + c
                        pe.wait_ge(a_ready, done(n - 2))
                        nc.tensor.matmul(U[:, (NC * u + c) % 2, :], x3["W1"][:, c * P:(c + 1) * P], hT[:, u, :],
                                         start=True, stop=True).then_inc(opened, 1)
                for u in range(2):
                    pe.wait_ge(a_ready, done(NC * (2 * i + u) + NC - 1))
                    pe.wait_ge(y_read, done(2 * (i - 1) + u))
                    for k in range(GRP):
                        for c in range(NC):
                            ins = nc.tensor.matmul(Y[:, u, k * P:(k + 1) * P], aT[:, u, c, k * P:(k + 1) * P], w2[:, c, :],
                                                   start=(c == 0), stop=(c == NC - 1))
                    ins.then_inc(closed, 1)



NTOK = NB * P
EXPERTS = 8
def capacity_experts(nc, C, W, wt, slot, xn, xnT):
    NC = 4
    tiles = [(k, min(P, CAPACITY - k)) for k in range(0, CAPACITY, P)]
    with ExitStack() as ctx:
        a = Alloc(nc, ctx, "L3f")
        aT = a.sb("aT", [P, 2, NC, TOK])
        yb = a.sb("yb", [P, 2, GRP, P])
        xg = a.sb("xg", [P, 3, len(tiles), P])
        xgT = a.sb("xgT", [P, 2, CAPACITY])
        yg = a.sb("yg", [P, 2, len(tiles), P])
        tr = a.ps("tr", [P, 512])
        U = a.ps("U", [P, 4, 512])
        Y = a.ps("Y", [P, 2, 512])
        opened, a_ready, closed, y_read, added = (
            a.sem("opened"), a.sem("a_ready"), a.sem("closed"), a.sem("y_read"), a.sem("added"))
        sent = a.sem("sent")
        fetched = [a.sem(f"fetched{q}") for q in range(3)]
        turned = a.sem("turned")
        xgT_ready = a.sem("xgT_ready")
        e_opened, e_active, e_closed = a.sem("e_opened"), a.sem("e_active"), a.sem("e_closed")
        yg_ready = a.sem("yg_ready")
        put = [a.sem(f"put{q}") for q in range(2)]
        back = [a.sem(f"back{q}") for q in range(NB // BACK)]
        summed = a.sem("summed")
        block = ctx.enter_context(nc.Block())
        units = E8 + 1
        w1 = W["W1"].rearrange("p (e c f) -> p e c f", e=units, c=NC)
        w2 = W["W2"].rearrange("p (e c d) -> p e c d", e=units, c=NC)
        b1 = W["b1"].rearrange("p (e c) -> p e c", e=units)
        b2 = C.rows["L3f_b2"].rearrange("p (e d) -> p e d", e=units)
        wt_t = wt[:, :, :].rearrange("p j (i b) -> p j i b", i=TURNS)
        xnT_t = xnT[:, :].rearrange("p (i u t) -> p i u t", i=TURNS, u=2)
        GROUPS = 2 * TURNS
        full = CAPACITY // P
        rest = CAPACITY - full * P

        def rows(dram, e):
            own = dram[e * CAPACITY:(e + 1) * CAPACITY, :]
            return own[0:full * P, :].rearrange("(k p) d -> p k d", p=P), own[full * P:, :]

        @block.gpsimd
        def _(pool):
            send_rows(nc, slot, xn, C.expert_in, EXPERT_ROWS, sent)
            pool.wait_ge(sent, 16 * 2 * NB)
            pool.wait_ge(closed, done(GROUPS - 1))
            for q in range(2):
                pool.wait_ge(put[q], 32 * (E8 // 2))
            bring_rows(nc, slot, C.expert_out, EXPERT_ROWS, xn, xnT, back)

        @block.sync
        def _(sp):
            def fetch(e):
                if e >= 3:
                    sp.wait_ge(turned, e - 2)
                whole, last = rows(C.expert_in, e)
                sp.dma_start(xg[:, e % 3, 0:full, :], whole).then_inc(fetched[e % 3], 16)
                sp.dma_start(xg[0:rest, e % 3, full, :], last).then_inc(fetched[e % 3], 16)

            sp.wait_ge(sent, 16 * 2 * NB)
            fetch(0)
            fetch(1)
            for e in range(E8):
                if e + 2 < E8:
                    fetch(e + 2)
                sp.wait_ge(yg_ready, e + 1)
                whole, last = rows(C.expert_out, e)
                sp.dma_start(whole, yg[:, e % 2, 0:full, :]).then_inc(put[e % 2], 16)
                sp.dma_start(last, yg[0:rest, e % 2, full, :]).then_inc(put[e % 2], 16)
            for q in range(2):
                sp.wait_ge(put[q], 32 * (E8 // 2))

        @block.vector
        def _(v):
            for x in (y_read, added):
                v.sem_inc(x, CREDIT)
            with v.Fori(0, TURNS) as i:
                for u in range(2):
                    n = 2 * i + u
                    v.wait_ge(closed, done(n))
                    v.wait_ge(added, done(n - 2))
                    nc.vector.tensor_tensor(yb[:, u, :, :], Y[:, u, :].rearrange("p (k d) -> p k d", k=GRP),
                                            b2[:, 0:1, :].to_broadcast([P, GRP, P]), ALU.add).then_inc(y_read, 1)
                    v.wait_ge(y_read, done(n))
                    for k in range(GRP):
                        b = GRP * u + k
                        x = C.Xt[:, bass.ds(i, 1), b, :]
                        ins = nc.vector.scalar_tensor_tensor(out=x, in0=yb[:, u, k, :],
                                                             scalar=wt_t[:, 2, bass.ds(i, 1), b], in1=x,
                                                             op0=ALU.mult, op1=ALU.add)
                    ins.then_inc(added, 1)
            for e in range(E8):
                if e >= 2:
                    v.wait_ge(put[e % 2], 32 * (e // 2))
                v.wait_ge(e_closed, e + 1)
                y = Y[:, e % 2, 0:len(tiles) * P].rearrange("p (k d) -> p k d", d=P)
                nc.vector.tensor_tensor(yg[:, e % 2, 0:full, :], y[:, 0:full, :],
                                        b2[:, e + 1:e + 2, :].to_broadcast([P, full, P]), ALU.add)
                nc.vector.tensor_tensor(yg[0:rest, e % 2, full, :], y[0:rest, full, :], b2[0:rest, e + 1, :],
                                        ALU.add).then_inc(yg_ready, 1)
            v.wait_ge(added, done(GROUPS - 1))
            combine(nc, C, v, wt, xn, xnT, back, summed)

        @block.scalar
        def _(act):
            act.sem_inc(a_ready, CREDIT)
            with act.Fori(0, TURNS) as i:
                for u in range(2):
                    act.wait_ge(closed, done(2 * i + u - 2))
                    for c in range(NC):
                        act.wait_ge(opened, done(NC * (2 * i + u) + c))
                        nc.scalar.activation(aT[:, u, c, :], U[:, c, :], ACT.Gelu,
                                             bias=b1[:, 0, c:c + 1]).then_inc(a_ready, 1)
            act.wait_ge(closed, done(GROUPS - 1))

            def take(e):
                act.wait_ge(turned, e + 1)
                nc.scalar.activation(xgT[:, e % 2, :], tr[:, 0:CAPACITY], ACT.Identity).then_inc(xgT_ready, 1)

            take(0)
            for e in range(E8):
                if e + 1 < E8:
                    if e >= 1:
                        act.wait_ge(e_opened, NC * e)
                    take(e + 1)
                if e >= 2:
                    act.wait_ge(e_closed, e - 1)
                for c in range(NC):
                    act.wait_ge(e_opened, NC * e + c + 1)
                    nc.scalar.activation(aT[:, e % 2, c, 0:CAPACITY], U[:, c, 0:CAPACITY], ACT.Gelu,
                                         bias=b1[:, e + 1, c:c + 1]).then_inc(e_active, 1)

        @block.tensor
        def _(pe):
            for x in (opened, closed):
                pe.sem_inc(x, CREDIT)

            def close(i, t):
                pe.wait_ge(y_read, done(2 * i + t - 2))
                pe.wait_ge(a_ready, done(NC * (2 * i + t) + NC - 1))
                for k in range(GRP):
                    for c in range(NC):
                        ins = nc.tensor.matmul(Y[:, t % 2, k * P:(k + 1) * P], aT[:, t % 2, c, k * P:(k + 1) * P],
                                               w2[:, 0, c, :], start=(c == 0), stop=(c == NC - 1))
                ins.then_inc(closed, 1)

            with pe.Fori(0, TURNS) as i:
                for u in range(2):
                    for c in range(NC):
                        pe.wait_ge(a_ready, done(NC * (2 * i + u - 1) + c))
                        nc.tensor.matmul(U[:, c, :], w1[:, 0, c, :], xnT_t[:, bass.ds(i, 1), u, :], start=True,
                                         stop=True).then_inc(opened, 1)
                    if u:
                        close(i, 0)
                close(i, 1)
            pe.wait_ge(y_read, done(GROUPS - 1))

            def turn(e):
                pe.wait_ge(fetched[e % 3], 32 * (e // 3 + 1))
                if e:
                    pe.wait_ge(xgT_ready, e)
                for k, (at, m) in enumerate(tiles):
                    ins = nc.tensor.transpose(tr[:, at:at + m], xg[0:m, e % 3, k, :], C.ident[0:m, 0:m])
                ins.then_inc(turned, 1)

            turn(0)
            for e in range(E8 + 1):
                if e < E8:
                    pe.wait_ge(xgT_ready, e + 1)
                    for c in range(NC):
                        if e >= 1:
                            pe.wait_ge(e_active, NC * (e - 1) + c + 1)
                        nc.tensor.matmul(U[:, c, 0:CAPACITY], w1[:, e + 1, c, :], xgT[:, e % 2, :], start=True,
                                         stop=True).then_inc(e_opened, 1)
                    if e + 1 < E8:
                        turn(e + 1)
                if e >= 1:
                    if e >= 3:
                        pe.wait_ge(yg_ready, e - 2)
                    pe.wait_ge(e_active, NC * e)
                    for k, (at, m) in enumerate(tiles):
                        for c in range(NC):
                            ins = nc.tensor.matmul(Y[0:m, (e - 1) % 2, k * P:(k + 1) * P],
                                                   aT[:, (e - 1) % 2, c, at:at + m], w2[:, e, c, :],
                                                   start=(c == 0), stop=(c == NC - 1))
                    ins.then_inc(e_closed, 1)



ROWS = [("gates", 8), ("alpha", 4), ("L1_bo", P), ("L1_bv", P), ("L2_bo", P), ("L2f_bg", 4),
        ("mod_gate", 1), ("L3_film", 512), ("L3_g_in", P), ("L3_b_in", P), ("L3_g_out", P), ("L3_b_out", P), ("L3_b2", P),
        ("L3f_b2", 9 * P)]
SECTIONS = {
    "const": [("ident", P), ("mask16", HEADS), ("iota8", 8), ("tile_no", TILES), ("ones8", 8), ("minus_half", 4), ("reverse", P),
              ("head_mask", H3), ("upto", P), ("ones", P)],
    "x0": [("L0_q", P), ("L0_o", P)],
    "x1": [("L1_q", P), ("L1_o", P), ("L1_bq", 1), ("L1_bk", 1)],
    "x2": [("L2_q", INNER), ("L2_o", INNER)],
    "f0": [("L0f_router", 8), ("L0f_sgate", 256), ("L0f_sup", 256), ("L0f_sdown", 256),
           ("L0f_gate", 4096), ("L0f_up", 4096), ("L0f_down", 4096)],
    "f1": [("L1f_router", 8), ("L1f_sgate", 256), ("L1f_sup", 256), ("L1f_sdown", 256),
           ("L1f_gate", 1024), ("L1f_up", 1024), ("L1f_down", 1024)],
}
LATER = {
    "f2": [("Wi", 512), ("Wo", 512), ("Wg", 4)],
    "f3": [("router", 8), ("W1", 9 * 512), ("W2", 9 * 512), ("b1", 9 * 4)],
}
LAST = {
    "x3": [("q", P), ("film", 512), ("g_ffn", 1), ("b_ffn", 1), ("W1", 512), ("b1", 4), ("W2", 512), ("log_dt", 1),
           ("D_skip", 1), ("A_re", NS), ("A_im", NS), ("C_re", NS), ("C_im", NS)],
}
LATE = len(LATER)
SECTION96 = [("L0_k", P), ("L0_v", P), ("L1_k", P), ("L1_v", P),
             ("L2_k", INNER), ("L2_v", INNER), ("L2_ki", INNER), ("L2_vi", INNER), ("L3_k", P), ("L3_v", P)]
SECTION32 = [("q_down", P), ("k_down", KV), ("v_down", KV), ("o_down", INNER),
             ("q_up", INNER), ("k_up", INNER), ("v_up", INNER), ("o_up", P)]
SECTION4 = [("A", 512), ("B", 2048)]
ROW_PLACE, ROW_N = columns(ROWS)
PLACES = {s: columns(parts) for s, parts in SECTIONS.items()}
LATER_PLACES = {s: columns(parts) for s, parts in LATER.items()}
LAST_PLACES = {s: columns(parts) for s, parts in LAST.items()}
PLACE32, N32 = columns(SECTION32)
PLACE4, N4 = columns(SECTION4)
PLACE96, N96 = columns(SECTION96)


def load_later(nc, C, later, dram):
    with nc.Block() as block:
        @block.sync
        def _(sp):
            for s, packed in later.items():
                sp.dma_start(packed.tile, dram[f"sec_{s}"]).then_inc(C.late_landed, 16)


def program(nc, dram, out):
    with ExitStack() as ctx:
        C = Core()
        X = ctx.enter_context(nc.sbuf_tensor("X", [P, NB * P], F32))
        rows = ctx.enter_context(nc.sbuf_tensor("rows", [P, ROW_N], F32))
        w96 = ctx.enter_context(nc.sbuf_tensor("w96", [KV, N96], F32))
        tgs = ctx.enter_context(nc.sbuf_tensor("tgs", [P, 8], F32))
        sec = {}
        for s, (place, n) in PLACES.items():
            sec[s] = Packed(ctx.enter_context(nc.sbuf_tensor(f"sec_{s}", [P, n], F32)), place)
        landed = ctx.enter_context(nc.semaphore("landed"))
        rest_landed = ctx.enter_context(nc.semaphore("rest_landed"))
        C.last_landed = ctx.enter_context(nc.semaphore("last_landed"))
        C.late_landed = ctx.enter_context(nc.semaphore("late_landed"))
        C.v_ipa_dram = nc.dram_tensor("v_ipa", (P, INNER), F32, kind="Internal").ap()
        C.tile_in = nc.dram_tensor("tile_in", ((TILES + AHEAD) * P, P), F32, kind="Internal").ap()
        C.tile_out = nc.dram_tensor("tile_out", (TILES * P, P), F32, kind="Internal").ap()
        C.expert_in = nc.dram_tensor("expert_in", (EXPERT_ROWS, P), F32, kind="Internal").ap()
        C.expert_out = nc.dram_tensor("expert_out", (EXPERT_ROWS, P), F32, kind="Internal").ap()
        C.kpad_dram = nc.dram_tensor("kpad", (P, 2 * P), F32, kind="Internal").ap()
        C.ctT_v = nc.dram_tensor("ctT", (P, NB * P), F32, kind="Internal").ap().rearrange(
            "p (i u t) -> p i u t", i=TURNS, u=2)
        kv_mask = ctx.enter_context(nc.sbuf_tensor("kv_mask", [P, NB * P], U8))
        C.kv_mask_v = kv_mask[:, :].rearrange("p (i b t) -> p i b t", i=TURNS, b=BODY)
        q_mask8 = ctx.enter_context(nc.sbuf_tensor("q_mask8", [P, NB], U8))
        q_mask = ctx.enter_context(nc.sbuf_tensor("q_mask", [P, NB], F32))
        C.q_mask_v = q_mask[:, :].rearrange("p (i b) -> p i b", i=TURNS)
        C.v_ipa_v = C.v_ipa_dram.rearrange("(i u b t) n -> t i u b n", i=TURNS, u=2, b=GRP)
        tanh_done = ctx.enter_context(nc.semaphore("tanh_done"))
        stored = ctx.enter_context(nc.semaphore("stored"))

        C.X = X
        C.carrier = ctx.enter_context(nc.sbuf_tensor("carrier", [P, 1], F32))
        C.Xt = X[:, :].rearrange("p (i b d) -> p i b d", i=TURNS, b=BODY)
        C.ctxT_v = dram["ctxT"].rearrange("c (i u t) -> c i u t", i=TURNS, u=2)
        C.rows = Packed(rows, ROW_PLACE)
        K = sec["const"]
        C.ident, C.mask16, C.iota8, C.tile_no, C.ones8, C.minus_half, C.reverse, C.head_mask, C.upto, C.ones = (
            K[n] for n in ("ident", "mask16", "iota8", "tile_no", "ones8", "minus_half", "reverse", "head_mask", "upto", "ones"))
        W96 = Packed(w96, PLACE96)

        at, later = 0, {}
        for s, (place, n) in LATER_PLACES.items():
            later[s] = Packed(sec["f0"].tile[:, at:at + n], place)
            at += n
        place, n = LAST_PLACES["x3"]
        x3 = Packed(sec["f1"].tile[:, 0:n], place)
        C.f2 = dict(later["f2"].items())
        C.f2["We"] = sec["f0"].tile[:, at:at + 4 * 512]

        first96 = PLACE96["L1_k"][0]
        small = ROW_PLACE["L1_bo"][0]
        rows_in = dram["rows"].partition_broadcast(P)
        first = [(rows[:, 0:small], rows_in[:, 0:small]), (X[:, :], dram["x"]), (w96[:, 0:first96], dram["w96"][:, 0:first96]),
                 (sec["const"].tile[:, :], dram["sec_const"]), (sec["x0"].tile[:, :], dram["sec_x0"])]
        background = [(sec["f0"].tile[:, :], dram["sec_f0"]), (rows[:, small:], rows_in[:, small:]),
                      (w96[:, first96:], dram["w96"][:, first96:]), (sec["x1"].tile[:, :], dram["sec_x1"]),
                      (sec["f1"].tile[:, :], dram["sec_f1"]), (sec["x2"].tile[:, :], dram["sec_x2"]),
                      (kv_mask[:, :], dram["kv_mask"].partition_broadcast(P)), (q_mask8[:, :], dram["q_mask"])]
        with nc.Block() as block:
            @block.sync
            def _(sp):
                for dst, src in first:
                    sp.dma_start(dst, src).then_inc(landed, 16)
                sp.wait_ge(landed, 16 * len(first))

            @block.scalar
            def _(act):
                act.wait_ge(landed, 16 * len(first))
                nc.scalar.activation(tgs[:, :], C.rows["gates"], ACT.Tanh).then_inc(tanh_done, 1)
                act.wait_ge(tanh_done, 1)

        tg = lambda n: tgs[:, n:n + 1]
        if STAGES > 0:
            attention16(nc, C, "L0", sec["x0"], sec["x0"]["L0_q"], W96["L0_k"], W96["L0_v"], sec["x0"]["L0_o"], tg(0), False,
                        background, rest_landed)
            with nc.Block() as block:
                @block.sync
                def _(sp):
                    sp.wait_ge(rest_landed, 16 * len(background))

                @block.scalar
                def _(act):
                    act.wait_ge(rest_landed, 16 * len(background))
                    nc.scalar.activation(q_mask[:, :], q_mask8[:, :], ACT.Identity).then_inc(tanh_done, 1)
                    act.wait_ge(tanh_done, 2)
        if STAGES > 1:
            with (nc.sbuf_tensor("wt0", [P, 2, NB], F32) as wt, nc.sbuf_tensor("slot0", [P, 2, NB], U32) as slot,
                  nc.sbuf_tensor("tile_expert", [P, TILES], U32) as tile_expert,
                  nc.sbuf_tensor("xn0", [P, NB * P], F32) as xn, nc.sbuf_tensor("xnT0", [P, NB * P], F32) as xnT):
                route(nc, C, "rt0", sec["f0"]["L0f_router"], tg(4), wt, slot, xn, xnT, C.tile_in, (TILES + AHEAD) * P,
                      tile_expert)
                tiled_experts(nc, C, "L0f", sec["f0"], tg(4), wt, slot, xn, xnT, tile_expert)
        if STAGES > 2:
            load_later(nc, C, later, dram)
            attention16(nc, C, "L1", sec["x1"], sec["x1"]["L1_q"], W96["L1_k"], W96["L1_v"], sec["x1"]["L1_o"], tg(1), True)
        if STAGES > 3:
            gated_experts(nc, C, "L1f", sec["f1"], 1, tg(5))
        if STAGES > 4:
            merge_lora(nc, C, sec["x2"], W96, x3, dram)
            attention_ipa(nc, C, sec["x2"], W96, tg(2))
        if STAGES > 5:
            shared_experts(nc, C, tg(6))
        if STAGES > 6:
            with nc.sbuf_tensor("xin", [P, NB * P], F32) as xin:
                convolution_kernel(nc, C, x3, C.rows)
                attention_top32(nc, C, x3, W96, xin)
                convolve(nc, C, xin)
                film_feed_forward(nc, C, x3, xin, tg(3))
        if STAGES > 7:
            with (nc.sbuf_tensor("wt", [P, 3, NB], F32) as wt, nc.sbuf_tensor("slot", [P, 2, NB], U32) as slot,
                  nc.sbuf_tensor("xn", [P, NB * P], F32) as xn, nc.sbuf_tensor("xnT", [P, NB * P], F32) as xnT):
                route(nc, C, "rt", later["f3"]["router"], tg(7), wt, slot, xn, xnT, C.expert_in, EXPERT_ROWS)
                capacity_experts(nc, C, later["f3"], wt, slot, xn, xnT)

        with nc.Block() as block:
            @block.sync
            def _(sp):
                sp.dma_start(out, X[:, :]).then_inc(stored, 16)
                sp.wait_ge(stored, 16)


STAGES = 8


def kernel(**inputs):
    import numpy as np
    import concourse.bacc as _bacc
    from concourse.bass_utils import run_bass_kernel_spmd as _run

    I = {k: np.asarray(v) for k, v in inputs.items()}
    f = np.arange(P)

    def chunked(w):
        e = w.reshape(-1, w.shape[-2] // P, P, w.shape[-1])
        return e.transpose(2, 0, 1, 3).reshape(P, -1)

    def stacked(w):
        return w.transpose(1, 0, 2).reshape(w.shape[1], -1)

    part = {
        "ident": np.eye(P, dtype=np.float32),
        "mask16": (f[:, None] // HD == np.arange(HEADS)).astype(np.float32),
        "iota8": np.tile(np.arange(8, dtype=np.float32), (P, 1)),
        "tile_no": np.tile(np.arange(TILES, dtype=np.float32), (P, 1)),
        "ones8": np.ones((P, 8), np.float32),
        "minus_half": np.full((P, 4), -0.5, np.float32),
        "L0_q": I["L0_xattn_Wq"].T, "L0_o": I["L0_xattn_Wo"].T,
        "L0_k": I["L0_xattn_Wk"].T, "L0_v": I["L0_xattn_Wv"].T,
        "L1_q": I["L1_xattn_Wq"], "L1_o": I["L1_xattn_Wo"], "L1_k": I["L1_xattn_Wk"], "L1_v": I["L1_xattn_Wv"],
        "L1_bq": I["L1_xattn_bq"][:, None], "L1_bk": I["L1_xattn_bk"][:, None],
        "L0f_router": I["L0_ffn_gate_w"].T, "L0f_sgate": I["L0_ffn_sh_gate"], "L0f_sup": I["L0_ffn_sh_up"],
        "L0f_sdown": chunked(I["L0_ffn_sh_down"]), "L0f_gate": stacked(I["L0_ffn_gate_k"]),
        "L0f_up": stacked(I["L0_ffn_up_k"]), "L0f_down": chunked(I["L0_ffn_down_k"]),
        "L1f_router": I["L1_ffn_router_w"], "L1f_sgate": I["L1_ffn_shared_gate_w"],
        "L1f_sup": I["L1_ffn_shared_up_w"], "L1f_sdown": chunked(I["L1_ffn_shared_down_w"]),
        "L1f_gate": stacked(I["L1_ffn_gate_w"]), "L1f_up": stacked(I["L1_ffn_up_w"]),
        "L1f_down": chunked(I["L1_ffn_down_w"]),
        "L2_q": I["L2_xattn_Wq"], "L2_o": chunked(I["L2_xattn_Wo"]),
        "L2_k": I["L2_xattn_Wk"], "L2_v": I["L2_xattn_Wv"],
        "L2_ki": I["L2_xattn_Wk_ipa"], "L2_vi": I["L2_xattn_Wv_ipa"],
        "q_down": I["L2_xattn_q_down"].T, "k_down": I["L2_xattn_k_down"].T, "v_down": I["L2_xattn_v_down"].T,
        "o_down": I["L2_xattn_o_down"].T, "q_up": I["L2_xattn_q_up"], "k_up": I["L2_xattn_k_up"],
        "v_up": I["L2_xattn_v_up"], "o_up": I["L2_xattn_o_up"], "L2_bo": I["L2_xattn_bo"],
        "alpha": np.concatenate([I[f"L2_xattn_{n}_alpha"] for n in "qkvo"]),
        "A": I["L2_ffn_A"].transpose(1, 0, 2).reshape(4, 512),
        "B": I["L2_ffn_B"].transpose(2, 0, 1).reshape(4, 2048),
        "Wi": I["L2_ffn_Wi"].T, "Wo": chunked(I["L2_ffn_Wo"].T), "Wg": I["L2_ffn_Wg"].T, "L2f_bg": I["L2_ffn_bg"],
        "reverse": np.ascontiguousarray(np.eye(P, dtype=np.float32)[::-1]),
        "head_mask": (f[:, None] // D3 == np.arange(H3)).astype(np.float32),
        "q": I["L3_xattn_Wq"], "L3_k": I["L3_xattn_Wk"], "L3_v": I["L3_xattn_Wv"],
        "film": np.concatenate([I["L3_xattn_W_film_in"], I["L3_xattn_W_film_out"]], axis=1),
        "g_ffn": I["L3_xattn_g_ffn"][:, None], "b_ffn": I["L3_xattn_b_ffn"][:, None],
        "W1": I["L3_xattn_W1"], "b1": I["L3_xattn_b1"].reshape(4, P).T, "W2": chunked(I["L3_xattn_W2"]),
        "log_dt": I["L3_xattn_log_dt"][:, None], "D_skip": I["L3_xattn_D_skip"][:, None],
        "A_re": I["L3_xattn_A_re"], "A_im": I["L3_xattn_A_im"], "C_re": I["L3_xattn_C_re"], "C_im": I["L3_xattn_C_im"],
        "mod_gate": I["L3_xattn_mod_gate"].reshape(1),
        "L3_film": np.concatenate([I["L3_xattn_b_film_in"], I["L3_xattn_b_film_out"]]),
        "L3_g_in": I["L3_xattn_g_norm_in"], "L3_b_in": I["L3_xattn_b_norm_in"],
        "L3_g_out": I["L3_xattn_g_norm_out"], "L3_b_out": I["L3_xattn_b_norm_out"], "L3_b2": I["L3_xattn_b2"],
        "upto": np.triu(np.ones((P, P), np.float32)), "ones": np.ones((P, P), np.float32),
        "router": I["L3_ffn_Wr"],
        "gates": np.concatenate([I["g_xattn"], I["g_ffn"]]), "L1_bo": I["L1_xattn_bo"], "L1_bv": I["L1_xattn_bv"],
    }

    last = {
        "W1": np.concatenate([I["L3_ffn_fw1"], stacked(I["L3_ffn_W1"])], axis=1),
        "W2": np.concatenate([chunked(I["L3_ffn_fw2"]), chunked(I["L3_ffn_W2"])], axis=1),
        "b1": np.concatenate([I["L3_ffn_fb1"][None], I["L3_ffn_b1"]]).reshape(9, 4, P).transpose(2, 0, 1).reshape(P, 36),
    }
    part["L3f_b2"] = np.concatenate([I["L3_ffn_fb2"], I["L3_ffn_b2"].reshape(-1)])

    def pack(parts, axis, part=part):
        for name, n in parts:
            assert part[name].shape[axis] == n, (name, part[name].shape)
        return np.ascontiguousarray(np.concatenate([part[name] for name, _ in parts], axis=axis))

    arrays = {
        "x": np.ascontiguousarray(I["x"].transpose(1, 0, 2).reshape(P, NB * P)),
        "ctxT": np.ascontiguousarray(I["ctx_768"].transpose(2, 0, 1).reshape(KV, NB * P)),
        "kv_mask": I["mask_BxS2_bf1"].reshape(-1), "q_mask": np.ascontiguousarray(I["mask_BxS_bf1"].T),
        "rows": pack(ROWS, 0), "w96": pack(SECTION96, 1), "w32": pack(SECTION32, 1), "w4": pack(SECTION4, 1),
    }
    for s, parts in {**SECTIONS, **LATER, **LAST}.items():
        arrays[f"sec_{s}"] = pack(parts, 1, {**part, **last} if s == "f3" else part)

    nc = _bacc.Bacc("TRN2", target_bir_lowering=False, num_devices=1)
    dram = {k: nc.dram_tensor(f"in_{k}", v.shape, mybir.dt.from_np(v.dtype), kind="ExternalInput").ap()
            for k, v in arrays.items()}
    out = nc.dram_tensor("out_0", (P, NB * P), F32, kind="ExternalOutput").ap()
    program(nc, dram, out)
    r = _run(nc, [{f"in_{k}": v for k, v in arrays.items()}], core_ids=[0])
    return np.ascontiguousarray(r.results[0]["out_0"].reshape(P, NB, P).transpose(1, 0, 2))
```

```python
from contextlib import ExitStack

import concourse.bass as bass
from concourse import mybir

F32 = mybir.dt.float32
U8 = mybir.dt.uint8
U32 = mybir.dt.uint32
ALU = mybir.AluOpType
ACT = mybir.ActivationFunctionType
AX = mybir.AxisListType

P = 128
NB = 32
KV = 96
BODY = 8
TURNS = NB // BODY
GRP = 4
TOK = GRP * P
EPS = 1e-5


CREDIT = 64


def done(n):
    return n + (CREDIT + 1)


class Steps:

    def __init__(self, sem):
        self.done, self.count = sem, 0

    def one(self):
        self.count += 1
        return 1

    def restart(self):
        self.count = 0


class Alloc:

    def __init__(self, nc, ctx, tag):
        self.nc, self.ctx, self.tag, self.sems = nc, ctx, tag, []
        ctx.callback(self.close)

    def sb(self, name, shape, dt=F32):
        return self.ctx.enter_context(self.nc.sbuf_tensor(f"{self.tag}_{name}", shape, dt))

    def ps(self, name, shape):
        return self.ctx.enter_context(self.nc.psum_tensor(f"{self.tag}_{name}", shape, F32))

    def close(self):
        self.nc.clear_and_free_semaphores(self.sems)
        self.nc.all_engine_barrier()

    def sem(self, name):
        s = self.nc.alloc_semaphore(f"{self.tag}_{name}")
        self.sems.append(s)
        return s


class Core:
    pass


def columns(parts):
    at, out = 0, {}
    for name, n in parts:
        out[name] = (at, n)
        at += n
    return out, at


class Packed:

    def __init__(self, tile, place):
        self.tile, self.place = tile, place

    def __getitem__(self, name):
        at, n = self.place[name]
        return self.tile[:, at:at + n]

    def items(self):
        return [(name, self[name]) for name in self.place]



class Norm:

    def __init__(self, a, tag):
        self.stats = a.sb(f"{tag}_stats", [P, 2, GRP, 6])
        self.mv = a.sb(f"{tag}_mv", [P, 2, GRP, 2])
        self.var = a.sb(f"{tag}_var", [P, 2, GRP])
        self.y0 = a.sb(f"{tag}_y0", [P, 2, GRP])
        self.t = a.sb(f"{tag}_newton", [P, 2, GRP])
        self.rs = a.sb(f"{tag}_rs", [P, 2, GRP])
        self.nm = a.sb(f"{tag}_nm", [P, 2, GRP])
        self.var_ready = a.sem(f"{tag}_var_ready")
        self.root_ready = a.sem(f"{tag}_root_ready")

    def statistics(self, nc, vec, row, u):
        for k in range(GRP):
            nc.vector.bn_stats(self.stats[:, u, k, :], row(k)).then_inc(vec.done, vec.one())
        nc.vector.wait_ge(vec.done, vec.count)
        for k in range(GRP):
            nc.vector.bn_aggr(self.mv[:, u, k, :], self.stats[:, u, k, :]).then_inc(vec.done, vec.one())
        nc.vector.wait_ge(vec.done, vec.count)
        nc.vector.tensor_scalar(self.var[:, u, :], self.mv[:, u, :, 1], EPS, None, ALU.add).then_inc(
            self.var_ready, 1)

    def root(self, nc, pool, C, i, u):
        pool.wait_ge(self.var_ready, done(2 * i + u))
        nc.gpsimd.tensor_tensor(self.y0[:, u, :], self.var[:, u, :], C.minus_half[:, :], ALU.pow).then_inc(
            self.root_ready, 1)

    def affine(self, nc, v, vec, i, u):
        y0, var, t, rs, nm = (x[:, u, :] for x in (self.y0, self.var, self.t, self.rs, self.nm))
        v.wait_ge(self.root_ready, done(2 * i + u))
        nc.vector.tensor_tensor(t, y0, y0, ALU.mult).then_inc(vec.done, vec.one())
        nc.vector.wait_ge(vec.done, vec.count)
        nc.vector.tensor_tensor(t, t, var, ALU.mult).then_inc(vec.done, vec.one())
        nc.vector.wait_ge(vec.done, vec.count)
        nc.vector.tensor_scalar(t, t, -0.5, 1.5, ALU.mult, ALU.add).then_inc(vec.done, vec.one())
        nc.vector.wait_ge(vec.done, vec.count)
        nc.vector.tensor_tensor(rs, t, y0, ALU.mult).then_inc(vec.done, vec.one())
        nc.vector.wait_ge(vec.done, vec.count)
        nc.vector.scalar_tensor_tensor(out=nm, in0=self.mv[:, u, :, 0], scalar=-1.0, in1=rs,
                                               op0=ALU.mult, op1=ALU.mult).then_inc(vec.done, vec.one())
        nc.vector.wait_ge(vec.done, vec.count)

    def apply(self, nc, dst, src, u, k):
        return nc.vector.tensor_scalar(dst, src, self.rs[:, u, k:k + 1], self.nm[:, u, k:k + 1], ALU.mult, ALU.add)


class Front:

    def __init__(self, a):
        self.st = a.sb("st", [P, 2, GRP, P])
        self.xnT = a.sb("xnT", [P, 2, TOK])
        self.N = Norm(a, "x")
        self.root_ready = self.N.root_ready
        self.st_ready = a.sem("st_ready")
        self.turned = a.sem("turned")
        self.xnT_ready = a.sem("xnT_ready")

    def open_vector(self, v):
        v.sem_inc(self.N.var_ready, CREDIT)
        v.sem_inc(self.st_ready, CREDIT)

    def statistics(self, nc, v, vec, C, i, u):
        self.N.statistics(nc, vec, lambda k: C.Xt[:, bass.ds(i, 1), GRP * u + k, :], u)

    def root(self, nc, pool, C, i, u):
        self.N.root(nc, pool, C, i, u)

    def normalise(self, nc, v, vec, C, i, u):
        self.N.affine(nc, v, vec, i, u)
        v.wait_ge(self.turned, done(2 * i + u - 2))
        for k in range(GRP):
            ins = self.N.apply(nc, self.st[:, u, k, :], C.Xt[:, bass.ds(i, 1), GRP * u + k, :], u, k)
        ins.then_inc(self.st_ready, 1)

    def turn(self, nc, pe, C, i, u, bank):
        pe.wait_ge(self.st_ready, done(2 * i + u))
        for k in range(GRP):
            ins = nc.tensor.transpose(bank[:, k * P:(k + 1) * P], self.st[:, u, k, :], C.ident)
        ins.then_inc(self.turned, 1)

    def take(self, nc, act, C, i, u, bank):
        act.wait_ge(self.turned, done(2 * i + u))
        nc.scalar.activation(self.xnT[:, u, :], bank, ACT.Identity).then_inc(self.xnT_ready, 1)



HD = 8
HEADS = 16
QUAD = 4
CLAMP = 10000.0


def of_turn(i, n, count, each):
    m = n // each
    return (i - 1, m + count) if m < 0 else (i, m)


def attention16(nc, C, tag, W, wqT, wkT, wvT, woT, tg, affine, background=(), background_landed=None):
    units = BODY * QUAD
    flip, weigh = 3, 5

    def due(n, first):
        return (n >= 0 or not first) and n < units

    scale = HD ** -0.5
    with ExitStack() as ctx:
        a = Alloc(nc, ctx, tag)
        F = Front(a)
        ctxT = a.sb("ctxT", [KV, 2, TOK])
        qT = a.sb("qT", [P, 2, TOK])
        kT = a.sb("kT", [P, 2, TOK])
        kx = a.sb("kx", [P, 2, HEADS, P])
        V = a.sb("V", [P, 2, GRP * HEADS, HD + 1])
        mx = a.sb("mx", [P, 4, QUAD])
        pr = a.sb("pr", [P, 4, QUAD, P])
        pT = a.sb("pT", [P, 2, QUAD, P])
        rden = a.sb("rden", [P, HEADS])
        on = a.sb("on", [P, 2, P])
        oT = a.sb("oT", [P, 2, P])
        bqs = a.sb("bqs", [P, 1])
        res = a.sb("res", [P, P])
        pj = a.ps("pj", [P, 2, 512])
        S = a.ps("S", [P, 2, 512])
        T = a.ps("T", [P, 2, 512])
        O = a.ps("O", [P, 512])
        tail = a.ps("tail", [P, 512])
        Ov = O[:, 0:HEADS * (HD + 1)].rearrange("p (h e) -> p h e", e=HD + 1)
        oTp, outp = tail[:, 0:P], tail[:, P:2 * P]

        ctx_in = [a.sem(f"ctx_in{u}") for u in range(2)]
        once = a.sem("once")
        projected = a.sem("projected")
        q_ready = a.sem("q_ready")
        k_ready = a.sem("k_ready")
        v_ready = a.sem("v_ready")
        spread = a.sem("spread")
        scored = a.sem("scored")
        clipped = a.sem("clipped")
        maxed = a.sem("maxed")
        shifted = a.sem("shifted")
        exped = a.sem("exped")
        flipped = a.sem("flipped")
        pT_ready = a.sem("pT_ready")
        weighed = a.sem("weighed")
        normed = a.sem("normed")
        oT_done = a.sem("oT_done")
        oT_ready = a.sem("oT_ready")
        out_done = a.sem("out_done")
        added = a.sem("added")
        own = a.sem("own")

        block = ctx.enter_context(nc.Block())

        @block.sync
        def _(sp):
            def context(i, u):
                sp.dma_start(ctxT[:, u, :], C.ctxT_v[:, bass.ds(i, 1), u, :]).then_inc(ctx_in[u], 16)

            for u in range(2):
                context(0, u)
            for dst, src in background:
                sp.dma_start(dst, src).then_inc(background_landed, 16)
            with sp.Fori(1, TURNS) as i:
                for u in range(2):
                    sp.wait_ge(projected, done(6 * i + 3 * u - 4))
                    context(i, u)

        @block.gpsimd
        def _(pool):
            pool.sem_inc(F.root_ready, CREDIT)
            pool.sem_inc(spread, CREDIT)
            if affine:
                pool.sem_inc(shifted, CREDIT)
            nc.gpsimd.memset(V[:, :, :, HD:HD + 1], 1.0).then_inc(once, 1)

            def keys(i, b, half):
                u, k = divmod(b, GRP)
                heads = slice(8 * half, 8 * half + 8)
                pool.wait_ge(k_ready, done(2 * i + u))
                pool.wait_ge(scored, done(units * i + QUAD * (b - 2) + QUAD - 1))
                nc.gpsimd.tensor_tensor(
                    kx[:, b % 2, heads, :], kT[:, u, k * P:(k + 1) * P].unsqueeze(1).to_broadcast([P, 8, P]),
                    C.mask16[:, heads].unsqueeze(2).to_broadcast([P, 8, P]), ALU.mult).then_inc(spread, 1)

            def subtract(i, s):
                pool.wait_ge(maxed, done(units * i + s))
                x = pr[:, s % 4, :, :]
                nc.gpsimd.tensor_tensor(x, x, mx[:, s % 4, :].unsqueeze(2).to_broadcast([P, QUAD, P]),
                                        ALU.subtract).then_inc(shifted, 1)

            def front(i):
                for u in range(2):
                    F.root(nc, pool, C, i, u)

            def turn(i, last):
                for s in range(units):
                    if s == 16 and not last:
                        front(i + 1)
                    if s % 2 == 0 and not (last and s // QUAD + 1 >= BODY):
                        b = s // QUAD + 1
                        keys(i + b // BODY, b % BODY, s % QUAD // 2)
                    if affine:
                        subtract(i, s)

            front(0)
            for half in range(2):
                keys(0, 0, half)
            with pool.Fori(0, TURNS - 1) as i:
                turn(i, False)
            turn(TURNS - 1, True)

        @block.vector
        def _(v):
            F.open_vector(v)
            for x in (clipped, maxed) if affine else (shifted,):
                v.sem_inc(x, CREDIT)
            v.sem_inc(normed, CREDIT)
            v.sem_inc(added, CREDIT)
            vec = Steps(own)
            if affine:
                v.sem_inc(v_ready, CREDIT)
                nc.vector.tensor_scalar(bqs[:, :], W["L1_bq"], scale, None, ALU.mult).then_inc(once, 1)

            def values(i, u):
                v.wait_ge(projected, done(6 * i + 3 * u + 2))
                nc.vector.tensor_tensor(
                    V[:, u, :, 0:HD].rearrange("p (b h) e -> p b h e", b=GRP),
                    pj[:, u, :].rearrange("p (b h e) -> p b h e", b=GRP, e=HD),
                    C.rows["L1_bv"].rearrange("p (h e) -> p h e", e=HD).unsqueeze(1)
                    .to_broadcast([P, GRP, HEADS, HD]), ALU.add).then_inc(v_ready, 1)

            def normalise(i, b):
                v.wait_ge(weighed, done(units * i + QUAD * b + QUAD - 1))
                nc.vector.reciprocal(rden[:, :], Ov[:, :, HD]).then_inc(vec.done, vec.one())
                v.wait_ge(oT_done, done(BODY * i + b - 2))
                nc.vector.wait_ge(vec.done, vec.count)
                nc.vector.tensor_tensor(
                    on[:, b % 2, :].rearrange("p (h e) -> p h e", e=HD), Ov[:, :, 0:HD],
                    rden[:, :].unsqueeze(2).to_broadcast([P, HEADS, HD]), ALU.mult).then_inc(normed, 1)

            def shift(i, s):
                n = units * i + s
                v.wait_ge(flipped, done(n - 4))
                v.wait_ge(scored, done(n))
                bank = S[:, s % 2, :].rearrange("p (j t) -> p j t", j=QUAD)
                if affine:
                    nc.vector.tensor_scalar(pr[:, s % 4, :, :], bank, CLAMP, -CLAMP, ALU.min, ALU.max).then_inc(clipped, 1)
                    v.wait_ge(clipped, done(n))
                    nc.vector.tensor_reduce(mx[:, s % 4, :], pr[:, s % 4, :, :], AX.X, ALU.max).then_inc(maxed, 1)
                else:
                    nc.vector.tensor_reduce(mx[:, s % 4, :], bank, AX.X, ALU.max).then_inc(vec.done, vec.one())
                    nc.vector.wait_ge(vec.done, vec.count)
                    nc.vector.tensor_tensor(pr[:, s % 4, :, :], bank,
                                            mx[:, s % 4, :].unsqueeze(2).to_broadcast([P, QUAD, P]),
                                            ALU.subtract).then_inc(shifted, 1)

            def residual(i, b):
                v.wait_ge(out_done, done(BODY * i + b))
                src = outp
                if affine:
                    nc.vector.tensor_tensor(res[:, :], outp, C.rows["L1_bo"], ALU.add).then_inc(vec.done, vec.one())
                    nc.vector.wait_ge(vec.done, vec.count)
                    src = res[:, :]
                x = C.Xt[:, bass.ds(i, 1), b, :]
                nc.vector.scalar_tensor_tensor(out=x, in0=src, scalar=tg, in1=x, op0=ALU.mult,
                                               op1=ALU.add).then_inc(added, 1)

            def turn(i, first, last):
                if affine:
                    values(i, 0)
                for s in range(units + (10 if last else 0)):
                    if (s - 1) % QUAD == 0 and due(s - 9, first):
                        normalise(*of_turn(i, s - 9, BODY, QUAD))
                    if s == 10 and affine:
                        values(i, 1)
                    if s < units:
                        shift(i, s)
                    if (s - 1) % QUAD == 0 and due(s - 13, first):
                        residual(*of_turn(i, s - 13, BODY, QUAD))
                    if not last and s in (14, 15):
                        F.statistics(nc, v, vec, C, i + 1, s - 14)
                    if not last and s in (18, 19):
                        F.normalise(nc, v, vec, C, i + 1, s - 18)
                v.wait_ge(vec.done, vec.count)
                v.sem_clear(vec.done)
                vec.restart()

            for u in range(2):
                F.statistics(nc, v, vec, C, 0, u)
            for u in range(2):
                F.normalise(nc, v, vec, C, 0, u)
            v.wait_ge(vec.done, vec.count)
            v.sem_clear(vec.done)
            vec.restart()
            turn(0, True, False)
            with v.Fori(1, TURNS - 1) as i:
                turn(i, False, False)
            turn(TURNS - 1, False, True)
            v.wait_ge(added, done(NB - 1))

        @block.scalar
        def _(act):
            act.sem_inc(F.xnT_ready, CREDIT)
            act.sem_inc(q_ready, CREDIT)
            act.sem_inc(k_ready, CREDIT)
            act.sem_inc(exped, CREDIT)
            act.sem_inc(pT_ready, CREDIT)
            act.sem_inc(oT_ready, CREDIT)
            if affine:
                act.wait_ge(once, 2)
            else:
                act.sem_inc(v_ready, CREDIT)
                act.wait_ge(once, 1)

            def project(i, u):
                act.wait_ge(projected, done(6 * i + 3 * u))
                nc.scalar.activation(qT[:, u, :], pj[:, u, :], ACT.Identity, scale=scale,
                                     bias=bqs[:, 0:1] if affine else 0.0).then_inc(q_ready, 1)
                act.wait_ge(spread, done(2 * (BODY * i + GRP * u + 3 - BODY) + 1))
                act.wait_ge(projected, done(6 * i + 3 * u + 1))
                nc.scalar.activation(kT[:, u, :], pj[:, 1 - u, :], ACT.Identity,
                                     bias=W["L1_bk"] if affine else 0.0).then_inc(k_ready, 1)
                if not affine:
                    act.wait_ge(projected, done(6 * i + 3 * u + 2))
                    nc.scalar.activation(V[:, u, :, 0:HD], pj[:, u, :].rearrange("p (n e) -> p n e", e=HD),
                                         ACT.Identity).then_inc(v_ready, 1)

            def front(i):
                for u in range(2):
                    F.take(nc, act, C, i, u, pj[:, u, :])

            def turn(i, first, last):
                for s in range(units + (8 if last else 0)):
                    n = units * i + s
                    if s == 10:
                        project(i, 1)
                    if s == 24 and not last:
                        front(i + 1)
                    if s == 26 and not last:
                        project(i + 1, 0)
                    if s < units:
                        act.wait_ge(shifted, done(n))
                        nc.scalar.activation(pr[:, s % 4, :, :], pr[:, s % 4, :, :], ACT.Exp).then_inc(exped, 1)
                    if due(s - flip, first):
                        m = s - flip
                        act.wait_ge(weighed, done(n - flip - 2))
                        act.wait_ge(flipped, done(n - flip))
                        nc.scalar.activation(pT[:, m % 2, :, :], T[:, m % 2, :].rearrange("p (j t) -> p j t", j=QUAD),
                                             ACT.Identity).then_inc(pT_ready, 1)
                    if (s - 1) % QUAD == 2 and due(s - 11, first):
                        b = (s - 11) // QUAD
                        act.wait_ge(out_done, done(BODY * i + b - 2))
                        act.wait_ge(oT_done, done(BODY * i + b))
                        nc.scalar.activation(oT[:, b % 2, :], oTp, ACT.Identity).then_inc(oT_ready, 1)

            front(0)
            project(0, 0)
            turn(0, True, False)
            with act.Fori(1, TURNS - 1) as i:
                turn(i, False, False)
            turn(TURNS - 1, False, True)

        @block.tensor
        def _(pe):
            pe.sem_inc(F.turned, CREDIT)
            for x in (projected, scored, flipped, weighed, oT_done, out_done):
                pe.sem_inc(x, CREDIT)
            pe.wait_ge(once, 2 if affine else 1)

            def project(i, u):
                g = 2 * i + u
                pe.wait_ge(F.xnT_ready, done(2 * i + 1))
                if u:
                    pe.wait_ge(k_ready, done(2 * i))
                nc.tensor.matmul(pj[:, u, :], wqT, F.xnT[:, u, :], start=True, stop=True).then_inc(projected, 1)
                pe.wait_ge(ctx_in[u], 16 * i + 16)
                if u:
                    pe.wait_ge(v_ready, done(2 * i))
                nc.tensor.matmul(pj[:, 1 - u, :], wkT, ctxT[:, u, :], start=True, stop=True).then_inc(projected, 1)
                pe.wait_ge(q_ready, done(g))
                for k in range(GRP):
                    ins = nc.tensor.matmul(pj[:, u, k * P:(k + 1) * P], ctxT[:, u, k * P:(k + 1) * P], wvT,
                                           start=True, stop=True)
                ins.then_inc(projected, 1)

            def front(i):
                pe.wait_ge(k_ready, done(2 * i - 1))
                F.turn(nc, pe, C, i, 0, pj[:, 0, :])
                pe.wait_ge(v_ready, done(2 * i - 1))
                F.turn(nc, pe, C, i, 1, pj[:, 1, :])

            def turn(i, first, last):
                for s in range(units + (9 if last else 0)):
                    n = units * i + s
                    if s == 10:
                        project(i, 1)
                    if s == 23 and not last:
                        front(i + 1)
                    if s == 26 and not last:
                        project(i + 1, 0)
                    if s < units:
                        b, r = divmod(s, QUAD)
                        u, k = divmod(b, GRP)
                        if r == 0:
                            pe.wait_ge(q_ready, done(2 * i + u))
                        if r % 2 == 0:
                            pe.wait_ge(spread, done(2 * (BODY * i + b) + r // 2))
                        pe.wait_ge(clipped if affine else shifted, done(n - 2))
                        nc.tensor.matmul(S[:, s % 2, :], qT[:, u, k * P:(k + 1) * P],
                                         kx[:, b % 2, QUAD * r:QUAD * r + QUAD, :],
                                         start=True, stop=True).then_inc(scored, 1)
                    if due(s - flip, first):
                        m = s - flip
                        pe.wait_ge(pT_ready, done(n - flip - 2))
                        pe.wait_ge(exped, done(n - flip))
                        for j in range(QUAD):
                            ins = nc.tensor.transpose(T[:, m % 2, j * P:(j + 1) * P], pr[:, m % 4, j, :], C.ident)
                        ins.then_inc(flipped, 1)
                    if due(s - weigh, first):
                        m = s - weigh
                        b, r = divmod(m, QUAD)
                        u, k = divmod(b % BODY, GRP)
                        if r == 0:
                            pe.wait_ge(v_ready, done(2 * i + b // GRP))
                            pe.wait_ge(normed, done(BODY * i + b - 1))
                        pe.wait_ge(pT_ready, done(n - weigh))
                        for j in range(QUAD):
                            h = QUAD * r + j
                            ins = nc.tensor.matmul(Ov[:, h, :], pT[:, m % 2, j, :], V[:, u, k * HEADS + h, :],
                                                   start=True, stop=True)
                        ins.then_inc(weighed, 1)
                    if (s - 1) % QUAD == 1 and due(s - 10, first):
                        b = (s - 10) // QUAD
                        pe.wait_ge(added, done(BODY * i + b - 1))
                        pe.wait_ge(normed, done(BODY * i + b))
                        nc.tensor.transpose(oTp, on[:, b % 2, :], C.ident).then_inc(oT_done, 1)
                    if (s - 1) % QUAD == 3 and due(s - 12, first):
                        b = (s - 12) // QUAD
                        pe.wait_ge(oT_ready, done(BODY * i + b))
                        nc.tensor.matmul(outp, oT[:, b % 2, :], woT, start=True, stop=True).then_inc(out_done, 1)

            front(0)
            project(0, 0)
            turn(0, True, False)
            with pe.Fori(1, TURNS - 1) as i:
                turn(i, False, False)
            turn(TURNS - 1, False, True)



E8 = 8


class Router:

    def __init__(self, a, n):
        self.n = n
        self.lg = a.sb("lg", [P, BODY, E8])
        self.top = a.sb("top", [P, BODY, 8])
        self.idx = a.sb("idx", [P, BODY, 8], U32)
        self.idf = a.sb("idf", [P, BODY, 2])
        self.ex = a.sb("ex", [P, BODY, E8])
        self.m0 = a.sb("m0", [P, BODY, E8])
        self.m1 = a.sb("m1", [P, BODY, E8])
        self.sum = a.sb("sum", [P, BODY])
        self.rcp = a.sb("rcp", [P, BODY])
        self.shift_done = a.sem("rt_shift")
        self.exp_done = a.sem("rt_exp")

    def choose(self, nc, v, vec, C, i):
        for b in range(BODY):
            nc.vector.max(self.top[:, b, :], self.lg[:, b, :]).then_inc(vec.done, vec.one())
        nc.vector.wait_ge(vec.done, vec.count)
        for b in range(BODY):
            nc.vector.max_index(self.idx[:, b, :], self.top[:, b, :], self.lg[:, b, :]).then_inc(vec.done, vec.one())
        nc.vector.tensor_tensor(self.ex[:, :, :], self.lg[:, :, :], self.top[:, :, 0:1].to_broadcast([P, BODY, E8]),
                                ALU.subtract).then_inc(self.shift_done, 1)
        nc.vector.wait_ge(vec.done, vec.count)
        nc.vector.tensor_copy(self.idf[:, :, :], self.idx[:, :, 0:2]).then_inc(vec.done, vec.one())
        nc.vector.wait_ge(vec.done, vec.count)
        for m, j in ((self.m0, 0), (self.m1, 1)):
            nc.vector.tensor_tensor(m[:, :, :], C.iota8.unsqueeze(1).to_broadcast([P, BODY, E8]),
                                            self.idf[:, :, j:j + 1].to_broadcast([P, BODY, E8]), ALU.is_equal).then_inc(vec.done, vec.one())
        nc.vector.wait_ge(vec.done, vec.count)
        nc.vector.tensor_tensor(self.m0[:, :, :], self.m0[:, :, :], self.m1[:, :, :], ALU.add).then_inc(vec.done, vec.one())

    def exponentials(self, nc, act, i):
        act.wait_ge(self.shift_done, done(i))
        nc.scalar.activation(self.ex[:, :, :], self.ex[:, :, :], ACT.Exp).then_inc(self.exp_done, 1)

    def probabilities(self, nc, v, vec, i):
        v.wait_ge(self.exp_done, done(i))
        nc.vector.tensor_reduce(self.sum[:, :], self.ex[:, :, :], AX.X, ALU.add).then_inc(vec.done, vec.one())
        nc.vector.wait_ge(vec.done, vec.count)
        nc.vector.reciprocal(self.rcp[:, :], self.sum[:, :]).then_inc(vec.done, vec.one())
        nc.vector.tensor_tensor(self.m1[:, :, :], self.ex[:, :, :], self.m0[:, :, :], ALU.mult).then_inc(vec.done, vec.one())
        nc.vector.wait_ge(vec.done, vec.count)


def gated_experts(nc, C, tag, W, nf, tg):
    with ExitStack() as ctx:
        a = Alloc(nc, ctx, tag)
        F = Front(a)
        R = Router(a, BODY)
        wt = a.sb("wt", [P, BODY, E8 + 1])
        sg = a.sb("sg", [P, 2, TOK])
        aT = a.sb("aT", [P, 2, max(nf, 2), TOK])
        tr = a.ps("tr", [P, 512])
        lgp = a.ps("lgp", [P, 512])
        G = a.ps("G", [P, 2, 512])
        U = a.ps("U", [P, 2, 512])
        Y = a.ps("Y", [P, 2, 512])
        gate = W[f"{tag}_gate"].rearrange("p (e c f) -> p e c f", e=E8, c=nf)
        up = W[f"{tag}_up"].rearrange("p (e c f) -> p e c f", e=E8, c=nf)
        down = W[f"{tag}_down"].rearrange("p (e c d) -> p e c d", e=E8, c=nf)
        sgate, sup, sdown = (W[f"{tag}_s{x}"].rearrange("p (c f) -> p c f", c=2) for x in ("gate", "up", "down"))
        router = W[f"{tag}_router"]

        chunks = [(0, c) for c in range(2)] + [(e + 1, c) for e in range(E8) for c in range(nf)]
        N = len(chunks)
        last_of = {t: n for n, (t, _) in enumerate(chunks)}
        units = E8 + 1

        logits = a.sem("logits")
        lg_read = a.sem("lg_read")
        opened = a.sem("opened")
        gated = a.sem("gated")
        a_ready = a.sem("a_ready")
        closed = a.sem("closed")
        added = a.sem("added")
        once = a.sem("once")
        own = a.sem("own")
        block = ctx.enter_context(nc.Block())

        @block.gpsimd
        def _(pool):
            pool.sem_inc(F.root_ready, CREDIT)
            with pool.Fori(0, TURNS) as i:
                for u in range(2):
                    F.root(nc, pool, C, i, u)

        @block.vector
        def _(v):
            F.open_vector(v)
            for x in (R.shift_done, lg_read, a_ready, added):
                v.sem_inc(x, CREDIT)
            vec = Steps(own)
            nc.vector.tensor_scalar(wt[:, :, E8], C.ones8, tg, None, ALU.mult).then_inc(once, 1)
            v.wait_ge(once, 1)

            def activate(i, u, n):
                t, c = chunks[n]
                m = N * (2 * i + u) + n
                v.wait_ge(closed, done(units * (2 * i + u) + t - 2))
                v.wait_ge(gated, done(m))
                nc.vector.tensor_tensor(aT[:, (t + u) % 2, c, :], sg[:, n % 2, :], U[:, n % 2, :],
                                        ALU.mult).then_inc(a_ready, 1)

            def add(i, u, t):
                v.wait_ge(closed, done(units * (2 * i + u) + t))
                v.wait_ge(added, done(units * (2 * i + u) + t - 1))
                for k in range(GRP):
                    b = GRP * u + k
                    x = C.Xt[:, bass.ds(i, 1), b, :]
                    ins = nc.vector.scalar_tensor_tensor(
                        out=x, in0=Y[:, (t + u) % 2, k * P:(k + 1) * P], scalar=wt[:, b, (t + E8) % 9:(t + E8) % 9 + 1],
                        in1=x, op0=ALU.mult, op1=ALU.add)
                ins.then_inc(added, 1)

            def turn(i, last):
                for n in range(2):
                    activate(i, 0, n)
                v.wait_ge(logits, done(i))
                nc.vector.tensor_copy(R.lg[:, :, :], lgp[:, 0:BODY * E8].rearrange("p (b e) -> p b e", e=E8)).then_inc(
                    lg_read, 1)
                v.wait_ge(lg_read, done(i))
                nc.vector.memset(C.carrier[:, :], 0.0)
                R.choose(nc, v, vec, C, i)
                R.probabilities(nc, v, vec, i)
                nc.vector.tensor_scalar(R.rcp[:, :], R.rcp[:, :], tg, None, ALU.mult).then_inc(vec.done, vec.one())
                nc.vector.wait_ge(vec.done, vec.count)
                nc.vector.tensor_tensor(wt[:, :, 0:E8], R.m1[:, :, :],
                                                R.rcp[:, :].unsqueeze(2).to_broadcast([P, BODY, E8]), ALU.mult).then_inc(vec.done, vec.one())
                nc.vector.wait_ge(vec.done, vec.count)
                for u in range(2):
                    due = 0
                    for n in range(2 if u == 0 else 0, N):
                        if u == 1 and not last:
                            if n in (N - 7, N - 6):
                                F.statistics(nc, v, vec, C, i + 1, n - N + 7)
                            if n in (N - 4, N - 3):
                                F.normalise(nc, v, vec, C, i + 1, n - N + 4)
                        activate(i, u, n)
                        while due < units and last_of[due] + LAG_ADD <= n:
                            add(i, u, due)
                            due += 1
                    for t in range(due, units):
                        add(i, u, t)
                v.wait_ge(vec.done, vec.count)
                v.sem_clear(vec.done)
                vec.restart()

            for u in range(2):
                F.statistics(nc, v, vec, C, 0, u)
            for u in range(2):
                F.normalise(nc, v, vec, C, 0, u)
            v.wait_ge(vec.done, vec.count)
            v.sem_clear(vec.done)
            vec.restart()
            with v.Fori(0, TURNS - 1) as i:
                turn(i, False)
            turn(TURNS - 1, True)
            v.wait_ge(added, done(units * 2 * TURNS - 1))

        @block.scalar
        def _(act):
            for x in (F.xnT_ready, R.exp_done, gated):
                act.sem_inc(x, CREDIT)

            def silu(i, u, n):
                m = N * (2 * i + u) + n
                act.wait_ge(a_ready, done(m - 2))
                act.wait_ge(opened, done(m))
                nc.scalar.activation(sg[:, n % 2, :], G[:, n % 2, :], ACT.Silu).then_inc(gated, 1)

            def turn(i, last):
                silu(i, 0, 0)
                silu(i, 0, 1)
                R.exponentials(nc, act, i)
                for u in range(2):
                    for n in range(2 if u == 0 else 0, N):
                        silu(i, u, n)
                        if u == 1 and n == N - 2 and not last:
                            F.take(nc, act, C, i + 1, 0, tr[:, :])
                if not last:
                    F.take(nc, act, C, i + 1, 1, tr[:, :])

            for u in range(2):
                F.take(nc, act, C, 0, u, tr[:, :])
            with act.Fori(0, TURNS - 1) as i:
                turn(i, False)
            turn(TURNS - 1, True)

        @block.tensor
        def _(pe):
            for x in (F.turned, logits, opened, closed):
                pe.sem_inc(x, CREDIT)

            def open_chunk(i, u, n):
                t, c = chunks[n]
                m = N * (2 * i + u) + n
                g_w, u_w = (sgate[:, c, :], sup[:, c, :]) if t == 0 else (gate[:, t - 1, c, :], up[:, t - 1, c, :])
                pe.wait_ge(a_ready, done(m - 2))
                nc.tensor.matmul(G[:, n % 2, :], g_w, F.xnT[:, u, :], start=True, stop=True)
                nc.tensor.matmul(U[:, n % 2, :], u_w, F.xnT[:, u, :], start=True, stop=True).then_inc(opened, 1)

            def close(i, u, t):
                pe.wait_ge(a_ready, done(N * (2 * i + u) + last_of[t]))
                pe.wait_ge(added, done(units * (2 * i + u) + t - 2))
                nchunk = 2 if t == 0 else nf
                for k in range(GRP):
                    for c in range(nchunk):
                        d_w = sdown[:, c, :] if t == 0 else down[:, t - 1, c, :]
                        ins = nc.tensor.matmul(Y[:, (t + u) % 2, k * P:(k + 1) * P],
                                               aT[:, (t + u) % 2, c, k * P:(k + 1) * P], d_w,
                                               start=(c == 0), stop=(c == nchunk - 1))
                ins.then_inc(closed, 1)

            def front(i, u):
                pe.wait_ge(F.xnT_ready, done(2 * i + u - 1))
                F.turn(nc, pe, C, i, u, tr)

            def turn(i, last):
                open_chunk(i, 0, 0)
                open_chunk(i, 0, 1)
                pe.wait_ge(F.xnT_ready, done(2 * i + 1))
                pe.wait_ge(lg_read, done(i - 1))
                for b in range(BODY):
                    u, k = divmod(b, GRP)
                    ins = nc.tensor.matmul(lgp[:, b * E8:(b + 1) * E8], F.xnT[:, u, k * P:(k + 1) * P], router,
                                           start=True, stop=True)
                ins.then_inc(logits, 1)
                for u in range(2):
                    due = 0
                    for n in range(2 if u == 0 else 0, N):
                        open_chunk(i, u, n)
                        if u == 1 and n == N - 2 and not last:
                            front(i + 1, 0)
                        if u == 1 and n == N - 1 and not last:
                            front(i + 1, 1)
                        while due < units and last_of[due] + LAG_CLOSE <= n:
                            close(i, u, due)
                            due += 1
                    for t in range(due, units):
                        close(i, u, t)

            front(0, 0)
            front(0, 1)
            with pe.Fori(0, TURNS - 1) as i:
                turn(i, False)
            turn(TURNS - 1, True)


LAG_CLOSE = 2
LAG_ADD = 3



CAPACITY = 320
EXPERT_ROWS = E8 * CAPACITY
NOWHERE = 4095
TILES = 2 * NB + E8
STEP = 4
AHEAD = STEP
BACK = 4


def send_rows(nc, slot, xn, dram, rows, sent):
    for b in range(NB):
        for j in range(2):
            nc.gpsimd.indirect_dma_start(
                dram, bass.IndirectOffsetOnAxis(slot[:, j, b:b + 1], 0), xn[:, b * P:(b + 1) * P], None,
                bounds_check=rows - 1, oob_is_err=False).then_inc(sent, 16)


def bring_rows(nc, slot, dram, rows, first, second, back):
    for b in range(NB):
        for j, dst in ((0, first), (1, second)):
            nc.gpsimd.indirect_dma_start(
                dst[:, b * P:(b + 1) * P], None, dram, bass.IndirectOffsetOnAxis(slot[:, j, b:b + 1], 0),
                bounds_check=rows - 1, oob_is_err=False).then_inc(back[b // BACK], 16)


def combine(nc, C, v, wt, first, second, back, summed):
    for q in range(NB // BACK):
        v.wait_ge(back[q], 16 * 2 * BACK)
        for j, src in ((0, first), (1, second)):
            if j == 1:
                v.wait_ge(summed, 2 * q + 1)
            for b in range(BACK * q, BACK * q + BACK):
                x = C.X[:, b * P:(b + 1) * P]
                ins = nc.vector.scalar_tensor_tensor(out=x, in0=src[:, b * P:(b + 1) * P], scalar=wt[:, j, b:b + 1],
                                                     in1=x, op0=ALU.mult, op1=ALU.add)
            ins.then_inc(summed, 1)
    v.wait_ge(summed, 2 * (NB // BACK))


def route(nc, C, tag, router_w, tg, wt, slot, xn, xnT, dram, dram_rows, tile_expert=None):
    capacity = tile_expert is None
    with ExitStack() as ctx:
        a = Alloc(nc, ctx, tag)
        F = Front(a)
        R = Router(a, BODY)
        share = a.sb("share", [P, NB, E8])
        second = a.sb("second", [P, NB, E8])
        place = a.sb("place", [P, NB, E8])
        picked = a.sb("picked", [P, NB, E8])
        where = a.sb("where", [P, NB])
        zeros = a.sb("zeros", [P, P])
        chosen = a.sb("chosen", [P, NB, E8])
        keep = a.sb("keep", [P, E8, NB])
        free = a.sb("free", [P, NB])
        eligible = a.sb("eligible", [P, NB])
        before = a.sb("before", [P, NB])
        zero = a.sb("zero", [P, NB])
        if not capacity:
            before8 = a.sb("before8", [P, E8, NB])
            full = a.sb("full", [P, E8, NB])
            tokens = a.sb("tokens", [P, E8])
            tiles = a.sb("tiles", [P, E8])
            ends = a.sb("ends", [P, E8])
            ended = a.sb("ended", [P, TILES, E8])
            owner = a.sb("owner", [P, TILES])
        tr = a.ps("tr", [P, 512])
        lgp = a.ps("lgp", [P, 512])
        rank = a.ps("rank", [P, 512])
        logits = a.sem("logits")
        lg_read = a.sem("lg_read")
        xn_kept, xnT_kept = a.sem("xn_kept"), a.sem("xnT_kept")
        zeroed, cleared = a.sem("zeroed"), a.sem("cleared")
        own, counted, offered, settled = a.sem("own"), a.sem("counted"), a.sem("offered"), a.sem("settled")
        block = ctx.enter_context(nc.Block())
        share_t = share[:, :, :].rearrange("p (i b) e -> p i b e", i=TURNS)
        chosen_t = chosen[:, :, :].rearrange("p (i b) e -> p i b e", i=TURNS)

        second_t = second[:, :, :].rearrange("p (i b) e -> p i b e", i=TURNS)
        xn_t = xn[:, :].rearrange("p (i u t) -> p i u t", i=TURNS, u=2)
        xnT_t = xnT[:, :].rearrange("p (i u t) -> p i u t", i=TURNS, u=2)

        @block.sync
        def _(sp):
            sp.wait_ge(zeroed, 1)
            sp.dma_start(dram.rearrange("(k p) d -> p k d", p=P),
                         zeros[:, :].unsqueeze(1).to_broadcast([P, dram_rows // P, P])).then_inc(cleared, 16)
            sp.wait_ge(cleared, 16)

        @block.gpsimd
        def _(pool):
            nc.gpsimd.memset(zeros[:, :], 0.0).then_inc(zeroed, 1)
            pool.sem_inc(F.root_ready, CREDIT)
            with pool.Fori(0, TURNS) as i:
                for u in range(2):
                    F.root(nc, pool, C, i, u)

        @block.vector
        def _(v):
            F.open_vector(v)
            for x in (R.shift_done, lg_read, xn_kept, xnT_kept):
                v.sem_inc(x, CREDIT)
            vec = Steps(own)

            def turn(i, last):
                for u in range(2):
                    v.wait_ge(F.st_ready, done(2 * i + u))
                    nc.vector.tensor_scalar(xn_t[:, bass.ds(i, 1), u, :], F.st[:, u, :, :].rearrange("p k d -> p (k d)"),
                                            1.0, None, ALU.mult).then_inc(xn_kept, 1)
                if not last:
                    v.wait_ge(xn_kept, done(2 * i + 1))
                    nc.vector.memset(C.carrier[:, :], 0.0)
                    for u in range(2):
                        F.statistics(nc, v, vec, C, i + 1, u)
                    for u in range(2):
                        F.normalise(nc, v, vec, C, i + 1, u)
                for u in range(2):
                    v.wait_ge(F.xnT_ready, done(2 * i + u))
                    nc.vector.tensor_scalar(xnT_t[:, bass.ds(i, 1), u, :], F.xnT[:, u, :], 1.0, None,
                                            ALU.mult).then_inc(xnT_kept, 1)
                v.wait_ge(logits, done(i))
                nc.vector.tensor_copy(R.lg[:, :, :], lgp[:, 0:BODY * E8].rearrange("p (b e) -> p b e", e=E8)).then_inc(
                    lg_read, 1)
                v.wait_ge(lg_read, done(i))
                nc.vector.memset(C.carrier[:, :], 0.0)
                R.choose(nc, v, vec, C, i)
                nc.vector.tensor_scalar(second_t[:, bass.ds(i, 1), :, :], R.m1[:, :, :].unsqueeze(1), 1.0, None,
                                        ALU.mult).then_inc(vec.done, vec.one())
                nc.vector.wait_ge(vec.done, vec.count)
                R.probabilities(nc, v, vec, i)
                wide = lambda x: x[:, :].unsqueeze(2).to_broadcast([P, BODY, E8])
                if capacity:
                    nc.vector.tensor_tensor(R.m1[:, :, :], R.m1[:, :, :], wide(R.rcp), ALU.mult).then_inc(
                        vec.done, vec.one())
                if capacity:
                    nc.vector.wait_ge(vec.done, vec.count)
                    nc.vector.tensor_reduce(R.sum[:, :], R.m1[:, :, :], AX.X, ALU.add).then_inc(vec.done, vec.one())
                    nc.vector.wait_ge(vec.done, vec.count)
                    nc.vector.tensor_scalar(R.sum[:, :], R.sum[:, :], 1e-9, None, ALU.max).then_inc(vec.done, vec.one())
                    nc.vector.wait_ge(vec.done, vec.count)
                    nc.vector.reciprocal(R.rcp[:, :], R.sum[:, :]).then_inc(vec.done, vec.one())
                    nc.vector.wait_ge(vec.done, vec.count)
                one_turn = [P, 1, BODY, E8]
                nc.vector.tensor_tensor(share_t[:, bass.ds(i, 1), :, :], R.m1[:, :, :].unsqueeze(1),
                                                R.rcp[:, :].unsqueeze(1).unsqueeze(3).to_broadcast(one_turn), ALU.mult).then_inc(vec.done, vec.one())
                nc.vector.tensor_scalar(chosen_t[:, bass.ds(i, 1), :, :], R.m0[:, :, :].unsqueeze(1), 1.0, None,
                                                ALU.mult).then_inc(vec.done, vec.one())
                v.wait_ge(vec.done, vec.count)
                v.sem_clear(vec.done)
                vec.restart()

            for u in range(2):
                F.statistics(nc, v, vec, C, 0, u)
            for u in range(2):
                F.normalise(nc, v, vec, C, 0, u)
            v.wait_ge(vec.done, vec.count)
            v.sem_clear(vec.done)
            vec.restart()
            with v.Fori(0, TURNS - 1) as i:
                turn(i, False)
            turn(TURNS - 1, True)

            def op(out, x, y, f):
                nc.vector.tensor_tensor(out, x, y, f).then_inc(vec.done, vec.one())
                nc.vector.wait_ge(vec.done, vec.count)

            nc.vector.memset(zero[:, :], 0.0).then_inc(vec.done, vec.one())
            nc.vector.wait_ge(vec.done, vec.count)
            if capacity:
                nc.vector.memset(free[:, :], 1.0).then_inc(vec.done, vec.one())
                nc.vector.wait_ge(vec.done, vec.count)
                for e in range(EXPERTS):
                    op(eligible[:, :], chosen[:, :, e], free[:, :], ALU.mult)
                    nc.vector.tensor_tensor_scan(before[:, :], eligible[:, :], zero[:, :], 0.0, ALU.add, ALU.add).then_inc(vec.done, vec.one())
                    nc.vector.wait_ge(vec.done, vec.count)
                    nc.vector.tensor_tensor(before[:, :], before[:, :], eligible[:, :], ALU.subtract).then_inc(offered, 1)
                    v.wait_ge(counted, e + 1)
                    nc.vector.scalar_tensor_tensor(out=keep[:, e, :], in0=rank[:, 0:NB], scalar=float(CAPACITY),
                                                           in1=eligible[:, :], op0=ALU.is_le, op1=ALU.mult).then_inc(vec.done, vec.one())
                    nc.vector.tensor_scalar(place[:, :, e], rank[:, 0:NB], float(e * CAPACITY - 1 - NOWHERE), None,
                                            ALU.add).then_inc(vec.done, vec.one())
                    nc.vector.wait_ge(vec.done, vec.count)
                    op(eligible[:, :], eligible[:, :], keep[:, e, :], ALU.subtract)
                    op(free[:, :], free[:, :], eligible[:, :], ALU.subtract)
                kept = keep[:, :, :].rearrange("p e b -> p b e")
                op(place[:, :, :], place[:, :, :], kept, ALU.mult)
                op(share[:, :, :], share[:, :, :], kept, ALU.mult)
                op(share[:, :, :], share[:, :, :], free[:, :].unsqueeze(2).to_broadcast([P, NB, E8]), ALU.mult)
            else:
                for e in range(E8):
                    nc.vector.tensor_tensor_scan(before8[:, e, :], chosen[:, :, e], zero[:, :], 0.0, ALU.add,
                                                 ALU.add).then_inc(vec.done, vec.one())
                nc.vector.wait_ge(vec.done, vec.count)
                nc.vector.tensor_scalar(tokens[:, :], before8[:, :, NB - 1], 1.0, None, ALU.mult).then_inc(
                    vec.done, vec.one())
                nc.vector.wait_ge(vec.done, vec.count)
                nc.vector.tensor_tensor(before8[:, :, :], before8[:, :, :], chosen[:, :, :].rearrange("p b e -> p e b"),
                                        ALU.subtract).then_inc(offered, 1)
                v.wait_ge(counted, 1)
                nc.vector.tensor_scalar(tokens[:, :], rank[:, NB * E8:NB * E8 + E8], 1.0 / P, None, ALU.mult).then_inc(
                    vec.done, vec.one())
                nc.vector.wait_ge(vec.done, vec.count)
                op(full[:, :, :], tokens[:, :].unsqueeze(2).to_broadcast([P, E8, NB]),
                   C.tile_no[:, 0:NB].unsqueeze(1).to_broadcast([P, E8, NB]), ALU.is_gt)
                nc.vector.tensor_reduce(tiles[:, :], full[:, :, :], AX.X, ALU.add).then_inc(vec.done, vec.one())
                nc.vector.wait_ge(vec.done, vec.count)
                nc.vector.tensor_tensor_scan(ends[:, :], tiles[:, :], zero[:, 0:E8], 0.0, ALU.add, ALU.add).then_inc(
                    vec.done, vec.one())
                nc.vector.wait_ge(vec.done, vec.count)
                op(tiles[:, :], ends[:, :], tiles[:, :], ALU.subtract)
                nc.vector.tensor_scalar(tiles[:, :], tiles[:, :], float(P), -1.0, ALU.mult, ALU.add).then_inc(
                    vec.done, vec.one())
                nc.vector.wait_ge(vec.done, vec.count)
                nc.vector.tensor_tensor(place[:, :, :], rank[:, 0:NB * E8].rearrange("p (e b) -> p b e", e=E8),
                                        tiles[:, :].unsqueeze(1).to_broadcast([P, NB, E8]), ALU.add).then_inc(
                    vec.done, vec.one())
                nc.vector.tensor_tensor(ended[:, :, :], C.tile_no.unsqueeze(2).to_broadcast([P, TILES, E8]),
                                        ends[:, :].unsqueeze(1).to_broadcast([P, TILES, E8]), ALU.is_ge).then_inc(
                    vec.done, vec.one())
                nc.vector.wait_ge(vec.done, vec.count)
                nc.vector.tensor_reduce(owner[:, :], ended[:, :, :], AX.X, ALU.add).then_inc(vec.done, vec.one())
                nc.vector.wait_ge(vec.done, vec.count)
                nc.vector.tensor_scalar(owner[:, :], owner[:, :], float(E8 - 1), None, ALU.min).then_inc(
                    vec.done, vec.one())
                nc.vector.wait_ge(vec.done, vec.count)
                nc.vector.tensor_copy(tile_expert[:, :], owner[:, :]).then_inc(vec.done, vec.one())
                nc.vector.wait_ge(vec.done, vec.count)
            op(chosen[:, :, :], chosen[:, :, :], second[:, :, :], ALU.subtract)
            for j, choice in ((0, chosen), (1, second)):
                op(picked[:, :, :], place[:, :, :], choice[:, :, :], ALU.mult)
                nc.vector.tensor_reduce(where[:, :], picked[:, :, :], AX.X, ALU.add).then_inc(vec.done, vec.one())
                nc.vector.wait_ge(vec.done, vec.count)
                nc.vector.tensor_scalar(where[:, :], where[:, :], float(NOWHERE) if capacity else 0.0, None, ALU.add).then_inc(
                    vec.done, vec.one())
                nc.vector.wait_ge(vec.done, vec.count)
                nc.vector.tensor_copy(slot[:, j, :], where[:, :]).then_inc(vec.done, vec.one())
                op(picked[:, :, :], share[:, :, :], choice[:, :, :], ALU.mult)
                nc.vector.tensor_reduce(wt[:, j, :], picked[:, :, :], AX.X, ALU.add).then_inc(vec.done, vec.one())
                nc.vector.wait_ge(vec.done, vec.count)
            if capacity:
                nc.vector.tensor_scalar(wt[:, 2, :], free[:, :], -1.0, 1.0, ALU.mult, ALU.add).then_inc(vec.done, vec.one())
                nc.vector.wait_ge(vec.done, vec.count)
            shares = 3 if capacity else 2
            nc.vector.tensor_scalar(wt[:, 0:shares, :], wt[:, 0:shares, :], tg, None, ALU.mult).then_inc(settled, 1)
            v.wait_ge(settled, 1)

        @block.scalar
        def _(act):
            for x in (F.xnT_ready, R.exp_done):
                act.sem_inc(x, CREDIT)

            def front(i):
                for u in range(2):
                    act.wait_ge(xnT_kept, done(2 * i + u - 2))
                    F.take(nc, act, C, i, u, tr[:, :])

            front(0)
            with act.Fori(0, TURNS - 1) as i:
                front(i + 1)
                R.exponentials(nc, act, i)
            R.exponentials(nc, act, TURNS - 1)

        @block.tensor
        def _(pe):
            for x in (F.turned, logits):
                pe.sem_inc(x, CREDIT)

            def front(i):
                for u in range(2):
                    pe.wait_ge(F.xnT_ready, done(2 * i + u - 1))
                    F.turn(nc, pe, C, i, u, tr)

            def turn(i):
                pe.wait_ge(F.xnT_ready, done(2 * i + 1))
                pe.wait_ge(lg_read, done(i - 1))
                for b in range(BODY):
                    u, k = divmod(b, GRP)
                    ins = nc.tensor.matmul(lgp[:, b * E8:(b + 1) * E8], F.xnT[:, u, k * P:(k + 1) * P], router_w,
                                           start=True, stop=True)
                ins.then_inc(logits, 1)

            front(0)
            with pe.Fori(0, TURNS - 1) as i:
                turn(i)
                front(i + 1)
            turn(TURNS - 1)
            if capacity:
                for e in range(EXPERTS):
                    pe.wait_ge(offered, e + 1)
                    nc.tensor.matmul(rank[:, 0:NB], C.upto, eligible[:, :], start=True, stop=False)
                    nc.tensor.matmul(rank[:, 0:NB], C.ones, before[:, :], start=False, stop=True).then_inc(counted, 1)
            else:
                pe.wait_ge(offered, 1)
                nc.tensor.matmul(rank[:, 0:NB * E8], C.upto, chosen[:, :, :].rearrange("p b e -> p e b"), start=True,
                                 stop=False)
                nc.tensor.matmul(rank[:, 0:NB * E8], C.ones, before8[:, :, :], start=False, stop=True)
                nc.tensor.matmul(rank[:, NB * E8:NB * E8 + E8], C.ones, tokens[:, :], start=True, stop=True).then_inc(
                    counted, 1)


def tiled_experts(nc, C, tag, W, tg, wt, slot, xn, xnT, tile_expert):
    NC = 4
    TURNS_T = TILES // STEP
    with ExitStack() as ctx:
        a = Alloc(nc, ctx, tag)
        sg = a.sb("sg", [P, 2, TOK])
        hT = a.sb("hT", [P, 2, 2, TOK])
        xg = a.sb("xg", [P, STEP, P])
        xgT = a.sb("xgT", [P, 2, P])
        h = a.sb("h", [P, 2, TOK])
        aT = a.sb("aT", [P, 2, TOK])
        yg = a.sb("yg", [P, STEP, P])
        tr = a.ps("tr", [P, 512])
        G = a.ps("G", [P, 2, 512])
        U = a.ps("U", [P, 2, 512])
        T = a.ps("T", [P, 2, 512])
        Y = a.ps("Y", [P, 512])
        gate = W[f"{tag}_gate"].rearrange("p (e f) -> p e f", e=E8)
        up = W[f"{tag}_up"].rearrange("p (e f) -> p e f", e=E8)
        down = W[f"{tag}_down"].rearrange("p (e c d) -> p e c d", e=E8, c=NC)
        sgate, sup, sdown = (W[f"{tag}_s{x}"].rearrange("p (c f) -> p c f", c=2) for x in ("gate", "up", "down"))
        s_opened, s_gated, s_active, s_closed, s_added = (
            a.sem("s_opened"), a.sem("s_gated"), a.sem("s_active"), a.sem("s_closed"), a.sem("s_added"))
        sent = a.sem("sent")
        fetched = [a.sem(f"fetched{q}") for q in range(STEP)]
        turned = a.sem("turned")
        xgT_ready = a.sem("xgT_ready")
        opened = a.sem("opened")
        gated = a.sem("gated")
        h_ready = a.sem("h_ready")
        flipped = a.sem("flipped")
        aT_ready = a.sem("aT_ready")
        closed = a.sem("closed")
        yg_ready = a.sem("yg_ready")
        put = [a.sem(f"put{q}") for q in range(STEP)]
        yg_free = a.sem("yg_free")
        back = [a.sem(f"back{q}") for q in range(NB // BACK)]
        summed = a.sem("summed")
        block = ctx.enter_context(nc.Block())
        GROUPS = 2 * TURNS
        xnT_t = xnT[:, :].rearrange("p (i u t) -> p i u t", i=TURNS, u=2)
        X_t = C.X[:, :].rearrange("p (i u t) -> p i u t", i=TURNS, u=2)
        rows_in = C.tile_in.rearrange("(i q p) d -> p i q d", q=STEP, p=P)
        rows_out = C.tile_out.rearrange("(i q p) d -> p i q d", q=STEP, p=P)
        owner = tile_expert[:, :].rearrange("p (i q) -> p i q", q=STEP)

        @block.gpsimd
        def _(pool):
            pool.sem_inc(yg_free, CREDIT)
            send_rows(nc, slot, xn, C.tile_in, TILES * P, sent)
            with pool.Fori(0, TURNS_T) as i:
                for q in range(STEP):
                    pool.wait_ge(put[q], 16 * i + 16)
                    pool.sem_inc(yg_free, 1)
            pool.wait_ge(sent, 16 * 2 * NB)
            pool.wait_ge(s_closed, done(GROUPS - 1))
            bring_rows(nc, slot, C.tile_out, TILES * P, xn, xnT, back)

        @block.sync
        def _(sp):
            sp.wait_ge(sent, 16 * 2 * NB)
            for q in range(STEP):
                sp.dma_start(xg[:, q, :], rows_in[:, 0, q, :]).then_inc(fetched[q], 16)
            with sp.Fori(0, TURNS_T) as i:
                for q in range(STEP):
                    sp.wait_ge(turned, done(STEP * i + q))
                    sp.dma_start(xg[:, q, :], rows_in[:, bass.ds(i + 1, 1), q, :]).then_inc(fetched[q], 16)
                    sp.wait_ge(yg_ready, done(STEP * i + q))
                    sp.dma_start(rows_out[:, bass.ds(i, 1), q, :], yg[:, q, :]).then_inc(put[q], 16)
            for q in range(STEP):
                sp.wait_ge(put[q], 16 * TURNS_T)
                sp.wait_ge(fetched[q], 16 * (TURNS_T + 1))

        @block.vector
        def _(v):
            for x in (s_active, s_added, h_ready, yg_ready):
                v.sem_inc(x, CREDIT)

            def add_shared(i, t):
                v.wait_ge(s_closed, done(2 * i + t))
                x = X_t[:, bass.ds(i, 1), t, :]
                nc.vector.scalar_tensor_tensor(out=x, in0=(Y, tr)[t][:, :], scalar=tg, in1=x, op0=ALU.mult,
                                               op1=ALU.add).then_inc(s_added, 1)

            with v.Fori(0, TURNS) as i:
                for u in range(2):
                    for c in range(2):
                        m = 2 * (2 * i + u) + c
                        v.wait_ge(s_closed, done(2 * i + u - 2))
                        v.wait_ge(s_gated, done(m))
                        nc.vector.tensor_tensor(hT[:, u, c, :], sg[:, c, :], U[:, c, :], ALU.mult).then_inc(s_active, 1)
                    if u:
                        add_shared(i, 0)
                add_shared(i, 1)

            def activate(t, n):
                v.wait_ge(flipped, done(n - 2))
                v.wait_ge(gated, done(n))
                nc.vector.tensor_tensor(h[:, t % 2, :], sg[:, t % 2, :], U[:, t % 2, :], ALU.mult).then_inc(h_ready, 1)

            def keep(t, n):
                v.wait_ge(yg_free, done(n - STEP))
                v.wait_ge(closed, done(n))
                nc.vector.tensor_scalar(yg[:, t % STEP, :], Y[:, 0:P], 1.0, None, ALU.mult).then_inc(yg_ready, 1)

            def turn(i, first):
                for q in range(STEP):
                    n = STEP * i + q
                    activate(q, n)
                    if not first or q >= 2:
                        keep(q - 2, n - 2)

            turn(0, True)
            with v.Fori(1, TURNS_T) as i:
                turn(i, False)
            for t in (TILES - 2, TILES - 1):
                keep(t, t)
            combine(nc, C, v, wt, xn, xnT, back, summed)

        @block.scalar
        def _(act):
            for x in (s_gated, xgT_ready, gated, aT_ready):
                act.sem_inc(x, CREDIT)
            with act.Fori(0, TURNS) as i:
                for u in range(2):
                    for c in range(2):
                        m = 2 * (2 * i + u) + c
                        act.wait_ge(s_active, done(m - 2))
                        act.wait_ge(s_opened, done(m))
                        nc.scalar.activation(sg[:, c, :], G[:, c, :], ACT.Silu).then_inc(s_gated, 1)

            def take(t, n):
                act.wait_ge(opened, done(n - 2))
                act.wait_ge(turned, done(n))
                nc.scalar.activation(xgT[:, t % 2, :], tr[:, 0:P], ACT.Identity).then_inc(xgT_ready, 1)

            def silu(t, n):
                act.wait_ge(h_ready, done(n - 2))
                act.wait_ge(opened, done(n))
                nc.scalar.activation(sg[:, t % 2, :], G[:, t % 2, :], ACT.Silu).then_inc(gated, 1)

            def take_hidden(t, n):
                act.wait_ge(closed, done(n - 2))
                act.wait_ge(flipped, done(n))
                nc.scalar.activation(aT[:, t % 2, :], T[:, t % 2, :], ACT.Identity).then_inc(aT_ready, 1)

            def turn(i, first):
                for q in range(STEP):
                    n = STEP * i + q
                    take(q + 1, n + 1)
                    silu(q, n)
                    if not first or q >= 1:
                        take_hidden(q - 1, n - 1)

            act.wait_ge(s_active, done(2 * GROUPS - 1))
            take(0, 0)
            turn(0, True)
            with act.Fori(1, TURNS_T) as i:
                turn(i, False)
            take_hidden(TILES - 1, TILES - 1)

        @block.tensor
        def _(pe):
            for x in (s_opened, s_closed, turned, opened, flipped, closed):
                pe.sem_inc(x, CREDIT)

            def close_shared(i, t):
                pe.wait_ge(s_active, done(2 * (2 * i + t) + 1))
                pe.wait_ge(s_added, done(2 * i + t - 2))
                for k in range(GRP):
                    for c in range(2):
                        ins = nc.tensor.matmul((Y, tr)[t][:, k * P:(k + 1) * P], hT[:, t, c, k * P:(k + 1) * P],
                                               sdown[:, c, :], start=(c == 0), stop=(c == 1))
                ins.then_inc(s_closed, 1)

            with pe.Fori(0, TURNS) as i:
                for u in range(2):
                    for c in range(2):
                        m = 2 * (2 * i + u) + c
                        x = xnT_t[:, bass.ds(i, 1), u, :]
                        pe.wait_ge(s_active, done(m - 2))
                        nc.tensor.matmul(G[:, c, :], sgate[:, c, :], x, start=True, stop=True)
                        nc.tensor.matmul(U[:, c, :], sup[:, c, :], x, start=True, stop=True).then_inc(s_opened, 1)
                    if u:
                        close_shared(i, 0)
                close_shared(i, 1)
            pe.wait_ge(s_added, done(GROUPS - 1))

            def flip_input(t, n, turns):
                pe.wait_ge(xgT_ready, done(n - 1))
                pe.wait_ge(fetched[t % STEP], 16 * turns)
                nc.tensor.transpose(tr[:, 0:P], xg[:, t % STEP, :], C.ident).then_inc(turned, 1)

            def open_tile(t, n, e):
                pe.wait_ge(h_ready, done(n - 2))
                pe.wait_ge(xgT_ready, done(n))
                nc.tensor.matmul(G[:, t % 2, :], xgT[:, t % 2, :], gate[:, bass.ds(e, 1), :], start=True, stop=True)
                nc.tensor.matmul(U[:, t % 2, :], xgT[:, t % 2, :], up[:, bass.ds(e, 1), :], start=True,
                                 stop=True).then_inc(opened, 1)

            def flip_hidden(t, n):
                pe.wait_ge(aT_ready, done(n - 2))
                pe.wait_ge(h_ready, done(n))
                for c in range(NC):
                    ins = nc.tensor.transpose(T[:, t % 2, c * P:(c + 1) * P], h[:, t % 2, c * P:(c + 1) * P], C.ident)
                ins.then_inc(flipped, 1)

            def close_tile(t, n, e):
                pe.wait_ge(yg_ready, done(n - 1))
                pe.wait_ge(aT_ready, done(n))
                for c in range(NC):
                    ins = nc.tensor.matmul(Y[:, 0:P], aT[:, t % 2, c * P:(c + 1) * P], down[:, bass.ds(e, 1), c, :],
                                           start=(c == 0), stop=(c == NC - 1))
                ins.then_inc(closed, 1)

            def expert_of(i, q):
                return pe.value_load(owner[0:1, bass.ds(i, 1), q], min_val=0, max_val=E8 - 1)

            def turn(i, first):
                experts = {q: expert_of(i, q) for q in range(STEP)}
                if not first:
                    experts.update({q: expert_of(i - 1, q + STEP) for q in (-2, -1)})
                for q in range(STEP):
                    n = STEP * i + q
                    flip_input(q + 1, n + 1, i + 1 + (q + 1) // STEP)
                    open_tile(q, n, experts[q])
                    if not first or q >= 1:
                        flip_hidden(q - 1, n - 1)
                    if not first or q >= 2:
                        close_tile(q - 2, n - 2, experts[q - 2])

            flip_input(0, 0, 1)
            turn(0, True)
            with pe.Fori(1, TURNS_T) as i:
                turn(i, False)
            flip_hidden(TILES - 1, TILES - 1)
            for t in (TILES - 2, TILES - 1):
                close_tile(t, t, expert_of(TURNS_T - 1, t % STEP))



H2, D2 = 16, 64
INNER = H2 * D2
NCH = INNER // P
RANK = 32
IPA = 4
ORG = P - IPA


def merge_lora(nc, C, x2, w96, x3, dram):
    with ExitStack() as ctx:
        a = Alloc(nc, ctx, "merge")
        w32 = Packed(a.sb("w32", [RANK, N32]), PLACE32)
        w4 = Packed(a.sb("w4", [4, N4]), PLACE4)
        ctx_ipa = a.sb("ctx_ipa", [KV, NB, IPA])
        v_ipa = a.sb("v_ipa", [P, INNER])
        al = a.sb("al", [P, 4])
        bank = a.ps("bank", [P, 2, 512])
        loaded, scaled, done = a.sem("loaded"), a.sem("scaled"), a.sem("done")
        product = a.sem("product")
        kept = a.sem("kept")
        pieces = []
        for half in range(2):
            cols = slice(512 * half, 512 * half + 512)
            pieces.append((w32["q_down"], w32["q_up"][:, cols], 512, ("add", x2["L2_q"][:, cols], 0)))
            pieces.append((w32["k_down"], w32["k_up"][:, cols], 512, ("add", w96["L2_k"][:, cols], 1)))
            pieces.append((w32["v_down"], w32["v_up"][:, cols], 512, ("add", w96["L2_v"][:, cols], 2)))
        for half in range(2):
            cols = slice(512 * half, 512 * half + 512)
            pieces.append((ctx_ipa[:, :, :].rearrange("c b t -> c (b t)"), w96["L2_vi"][:, cols], 512,
                           ("copy", v_ipa[:, cols], 0)))
        for c in range(NCH):
            pieces.append((w32["o_down"][:, c * P:(c + 1) * P], w32["o_up"], P,
                           ("add", x2["L2_o"][:, c * P:(c + 1) * P], 3)))
        for e in range(4):
            pieces.append((w4["A"][:, e * P:(e + 1) * P], w4["B"][:, e * 512:(e + 1) * 512], 512,
                           ("lora", C.f2["We"][:, e * 512:(e + 1) * 512], 0)))
        block = ctx.enter_context(nc.Block())

        @block.sync
        def _(sp):
            sp.dma_start(x3.tile, dram["sec_x3"]).then_inc(C.last_landed, 16)
            sp.dma_start(w32.tile[:, :], dram["w32"]).then_inc(loaded, 16)
            sp.dma_start(w4.tile[:, :], dram["w4"]).then_inc(loaded, 16)
            sp.dma_start(ctx_ipa[:, :, :], dram["ctxT"].rearrange("c (b t) -> c b t", b=NB)[:, :, ORG:P]).then_inc(
                loaded, 16)
            sp.wait_ge(loaded, 48)
            sp.wait_ge(done, 1)
            sp.dma_start(C.v_ipa_dram, v_ipa[:, :]).then_inc(kept, 16)
            sp.wait_ge(kept, 16)

        @block.tensor
        def _(pe):
            pe.wait_ge(loaded, 48)
            for n, (lhsT, rhs, w, _) in enumerate(pieces):
                if n >= 2:
                    pe.wait_ge(scaled, n)
                m = lhsT.shape[1]
                nc.tensor.matmul(bank[0:m, n % 2, 0:w], lhsT, rhs, start=True, stop=True).then_inc(product, 1)

        @block.vector
        def _(v):
            nc.vector.tensor_scalar(al[:, :], C.rows["alpha"], 1.0 / RANK, None, ALU.mult).then_inc(scaled, 1)
            v.wait_ge(scaled, 1)
            v.wait_ge(C.late_landed, 16 * LATE)
            for n, (lhsT, _, w, (what, dst, j)) in enumerate(pieces):
                m = lhsT.shape[1]
                v.wait_ge(product, n + 1)
                src = bank[0:m, n % 2, 0:w]
                if what == "copy":
                    ins = nc.vector.tensor_copy(dst, src)
                elif what == "lora":
                    ins = nc.vector.tensor_tensor(dst, src, C.f2["Wi"], ALU.add)
                else:
                    ins = nc.vector.scalar_tensor_tensor(out=dst, in0=src, scalar=al[0:m, j:j + 1], in1=dst,
                                                         op0=ALU.mult, op1=ALU.add)
                ins.then_inc(scaled, 1)
            v.wait_ge(scaled, len(pieces) + 1)
            nc.vector.tensor_scalar(x2["L2_q"], x2["L2_q"], D2 ** -0.5, None, ALU.mult).then_inc(done, 1)


def attention_ipa(nc, C, x2, w96, tg):
    units = BODY * 4
    U = GRP * 4
    NP = 24
    with ExitStack() as ctx:
        a = Alloc(nc, ctx, "L2")
        F = Front(a)
        ctxT = a.sb("ctxT", [KV, TOK])
        qT = a.sb("qT", [P, NCH, TOK])
        kT = a.sb("kT", [P, NCH, TOK])
        V = a.sb("V", [P, GRP, INNER])
        pr = a.sb("pr", [P, 4, 4, P])
        pT = a.sb("pT", [P, 2, 4, P])
        oT = a.sb("oT", [P, NCH, P])
        mx = a.sb("mx", [P, 4, 2, 4])
        sm = a.sb("sm", [P, 4, 2, 4])
        rc = a.sb("rc", [P, 4, 2, 4])
        res = a.sb("res", [P, P])
        pj = a.ps("pj", [P, 2, 512])
        S = a.ps("S", [P, 2, 512])
        T = a.ps("T", [P, 2, 512])
        O = a.ps("O", [P, 2, 512])
        outp = pj[:, 1, 0:P]

        ctx_in = [a.sem(f"ctx_in{u}") for u in range(2)]
        ipa_in = [a.sem(f"ipa_in{u}") for u in range(2)]
        projected = a.sem("projected")
        kept_a = a.sem("kept_a")
        kept_v = a.sem("kept_v")
        scored = a.sem("scored")
        shifted = a.sem("shifted")
        exped = a.sem("exped")
        summed = a.sem("summed")
        scaled = a.sem("scaled")
        flipped = a.sem("flipped")
        pT_ready = a.sem("pT_ready")
        weighed = a.sem("weighed")
        oT_ready = a.sem("oT_ready")
        out_done = a.sem("out_done")
        added = a.sem("added")
        own = a.sem("own")
        block = ctx.enter_context(nc.Block())
        parts = ((0, slice(0, ORG)), (1, slice(ORG, P)))

        @block.sync
        def _(sp):
            with sp.Fori(0, TURNS) as i:
                for u in range(2):
                    g = 2 * i + u
                    sp.wait_ge(projected, done(NP * g - 1))
                    sp.dma_start(ctxT[:, :], C.ctxT_v[:, bass.ds(i, 1), u, :]).then_inc(ctx_in[u], 16)
                    sp.wait_ge(weighed, done(U * g - 1))
                    sp.dma_start(V[ORG:P, :, :], C.v_ipa_v[:, bass.ds(i, 1), u, :, :]).then_inc(ipa_in[u], 16)

        @block.gpsimd
        def _(pool):
            pool.sem_inc(F.root_ready, CREDIT)
            pool.sem_inc(scaled, CREDIT)

            def front(i):
                for u in range(2):
                    F.root(nc, pool, C, i, u)

            def turn(i, last):
                for s in range(units):
                    n = units * i + s
                    pool.wait_ge(summed, done(n))
                    for j, cols in parts:
                        w = cols.stop - cols.start
                        ins = nc.gpsimd.tensor_tensor(pr[:, s % 4, :, cols], pr[:, s % 4, :, cols],
                                                      rc[:, s % 4, j, :].unsqueeze(2).to_broadcast([P, 4, w]), ALU.mult)
                    ins.then_inc(scaled, 1)
                    if s == U + 3 and not last:
                        front(i + 1)

            front(0)
            with pool.Fori(0, TURNS - 1) as i:
                turn(i, False)
            turn(TURNS - 1, True)

        def destination(n):
            if n < 16:
                return (qT if n < 8 else kT)[:, n % 8, :], P
            k, half = divmod(n - 16, 2)
            return V[0:ORG, k, 512 * half:512 * half + 512], ORG

        @block.vector
        def _(v):
            F.open_vector(v)
            for x in (kept_v, shifted, summed, added):
                v.sem_inc(x, CREDIT)
            vec = Steps(own)

            def shift(i, s):
                n = units * i + s
                v.wait_ge(flipped, done(n - 4))
                v.wait_ge(scored, done(n))
                bank = S[:, s % 2, :].rearrange("p (j t) -> p j t", j=4)
                for j, cols in parts:
                    nc.vector.tensor_reduce(mx[:, s % 4, j, :], bank[:, :, cols], AX.X, ALU.max).then_inc(vec.done, vec.one())
                nc.vector.wait_ge(vec.done, vec.count)
                for j, cols in parts:
                    w = cols.stop - cols.start
                    ins = nc.vector.tensor_tensor(pr[:, s % 4, :, cols], bank[:, :, cols],
                                                  mx[:, s % 4, j, :].unsqueeze(2).to_broadcast([P, 4, w]), ALU.subtract)
                ins.then_inc(shifted, 1)

            def total(i, s):
                v.wait_ge(exped, done(units * i + s))
                for j, cols in parts:
                    nc.vector.tensor_reduce(sm[:, s % 4, j, :], pr[:, s % 4, :, cols], AX.X, ALU.add).then_inc(vec.done, vec.one())
                nc.vector.wait_ge(vec.done, vec.count)
                nc.vector.reciprocal(rc[:, s % 4, :, :], sm[:, s % 4, :, :]).then_inc(summed, 1)

            def residual(i, b):
                v.wait_ge(out_done, done(BODY * i + b))
                nc.vector.tensor_tensor(res[:, :], outp, C.rows["L2_bo"], ALU.add).then_inc(vec.done, vec.one())
                nc.vector.wait_ge(vec.done, vec.count)
                x = C.Xt[:, bass.ds(i, 1), b, :]
                nc.vector.scalar_tensor_tensor(out=x, in0=res[:, :], scalar=tg, in1=x, op0=ALU.mult,
                                               op1=ALU.add).then_inc(added, 1)

            def keep(g, n):
                dst, rows = destination(n)
                v.wait_ge(projected, done(NP * g + n))
                nc.vector.tensor_copy(dst, S[0:rows, 1, :]).then_inc(kept_v, 1)

            def turn(i, last):
                for u in range(2):
                    for s in range(U + 8):
                        if u == 1 and not last:
                            if s in (2, 3):
                                F.statistics(nc, v, vec, C, i + 1, s - 2)
                            if s in (5, 6):
                                F.normalise(nc, v, vec, C, i + 1, s - 5)
                        if s >= U and not (last and u == 1):
                            keep(2 * i + u + 1, 2 * (s - U) + 1)
                        if s < U:
                            shift(i, U * u + s)
                        if 1 <= s < U + 1:
                            total(i, U * u + s - 1)
                        if s >= 11 and s % 4 == 3:
                            residual(i, GRP * u + (s - 11) // 4)
                    if not (last and u == 1):
                        for n in range(17, NP, 2):
                            keep(2 * i + u + 1, n)
                v.wait_ge(vec.done, vec.count)
                v.sem_clear(vec.done)
                vec.restart()

            for u in range(2):
                F.statistics(nc, v, vec, C, 0, u)
            for u in range(2):
                F.normalise(nc, v, vec, C, 0, u)
            for n in range(1, NP, 2):
                keep(0, n)
            v.wait_ge(vec.done, vec.count)
            v.sem_clear(vec.done)
            vec.restart()
            with v.Fori(0, TURNS - 1) as i:
                turn(i, False)
            turn(TURNS - 1, True)
            v.wait_ge(added, done(NB - 1))

        @block.scalar
        def _(act):
            for x in (F.xnT_ready, kept_a, exped, pT_ready, oT_ready):
                act.sem_inc(x, CREDIT)

            def keep(g, n):
                dst, rows = destination(n)
                act.wait_ge(projected, done(NP * g + n))
                nc.scalar.activation(dst, S[0:rows, 0, :], ACT.Identity).then_inc(kept_a, 1)

            def turn(i, last):
                for u in range(2):
                    for s in range(U + 8):
                        n = units * i + U * u + s
                        if u == 1 and s in (10, 12) and not last:
                            F.take(nc, act, C, i + 1, s // 2 - 5, pj[:, 0, :])
                        if s >= U and not (last and u == 1):
                            keep(2 * i + u + 1, 2 * (s - U))
                        if s < U:
                            act.wait_ge(shifted, done(n))
                            nc.scalar.activation(pr[:, s % 4, :, :], pr[:, s % 4, :, :], ACT.Exp).then_inc(exped, 1)
                        if 3 <= s < U + 3:
                            m = s - 3
                            act.wait_ge(weighed, done(n - 5))
                            act.wait_ge(flipped, done(n - 3))
                            nc.scalar.activation(pT[:, m % 2, :, :],
                                                 T[:, m % 2, :].rearrange("p (j t) -> p j t", j=4),
                                                 ACT.Identity).then_inc(pT_ready, 1)
                        if s >= 6 and s % 2 == 0:
                            m = s - 5
                            b, half = divmod(m // 2, 2)
                            if b < GRP:
                                act.wait_ge(out_done, done(BODY * i + GRP * u + b - 1))
                                act.wait_ge(weighed, done(units * i + U * u + m))
                                nc.scalar.activation(oT[:, 4 * half:4 * half + 4, :],
                                                     O[:, half, :].rearrange("p (c t) -> p c t", c=4),
                                                     ACT.Identity).then_inc(oT_ready, 1)
                    if not (last and u == 1):
                        for m in range(16, NP, 2):
                            keep(2 * i + u + 1, m)

            for u in range(2):
                F.take(nc, act, C, 0, u, pj[:, 0, :])
            for m in range(0, NP, 2):
                keep(0, m)
            with act.Fori(0, TURNS - 1) as i:
                turn(i, False)
            turn(TURNS - 1, True)

        @block.tensor
        def _(pe):
            for x in (F.turned, projected, scored, flipped, weighed, out_done):
                pe.sem_inc(x, CREDIT)

            def project(i, u, n):
                g = 2 * i + u
                if n < 2:
                    pe.wait_ge(shifted, done(U * g - 1))
                if n == 8:
                    pe.wait_ge(ctx_in[u % 2], 16 * (i + u // 2) + 16)
                if n % 2 == 0:
                    pe.wait_ge(kept_a, done(12 * g + n // 2 - 1))
                else:
                    pe.wait_ge(kept_v, done(12 * g + n // 2 - 1))
                bank = S[:, n % 2, :]
                c = n % 8
                if n < 8:
                    ins = nc.tensor.matmul(bank, x2["L2_q"][:, c * P:(c + 1) * P], F.xnT[:, u % 2, :], start=True, stop=True)
                elif n < 16:
                    bt = bank.rearrange("p (b t) -> p b t", b=GRP)
                    ct = ctxT[:, :].rearrange("c (b t) -> c b t", b=GRP)
                    for w, (_, cols) in (("L2_k", parts[0]), ("L2_ki", parts[1])):
                        ins = nc.tensor.matmul(bt[:, :, cols], w96[w][:, c * P:(c + 1) * P], ct[:, :, cols],
                                               start=True, stop=True)
                else:
                    k, half = divmod(n - 16, 2)
                    ins = nc.tensor.matmul(bank, ctxT[:, k * P:(k + 1) * P],
                                           w96["L2_v"][:, 512 * half:512 * half + 512], start=True, stop=True)
                ins.then_inc(projected, 1)

            def front(i, u):
                pe.wait_ge(F.xnT_ready, done(2 * i + u - 1))
                F.turn(nc, pe, C, i, u, pj[:, 0, :])

            def turn(i, last):
                for u in range(2):
                    pe.wait_ge(kept_a, done(12 * (2 * i + u) + 11))
                    pe.wait_ge(kept_v, done(12 * (2 * i + u) + 11))
                    for s in range(U + 8):
                        n = units * i + U * u + s
                        if u == 1 and s in (9, 11) and not last:
                            front(i + 1, (s - 9) // 2)
                        if s >= U and not (last and u == 1):
                            if s == U and u == 1:
                                pe.wait_ge(F.xnT_ready, done(2 * i + 3))
                            project(i, u + 1, 2 * (s - U))
                            project(i, u + 1, 2 * (s - U) + 1)
                        if s < U:
                            k, q = divmod(s, 4)
                            p, half = q % 2, q // 2
                            rows = slice(64 * p, 64 * p + 64)
                            pe.wait_ge(shifted, done(n - 2))
                            for j in range(4):
                                c = 4 * half + j
                                ins = nc.tensor.matmul(S[:, s % 2, j * P:(j + 1) * P], qT[rows, c, k * P:(k + 1) * P],
                                                       kT[rows, c, k * P:(k + 1) * P], start=True, stop=True)
                            ins.then_inc(scored, 1)
                        if 3 <= s < U + 3:
                            m = s - 3
                            pe.wait_ge(pT_ready, done(n - 5))
                            pe.wait_ge(scaled, done(n - 3))
                            for j in range(4):
                                ins = nc.tensor.transpose(T[:, m % 2, j * P:(j + 1) * P], pr[:, m % 4, j, :], C.ident)
                            ins.then_inc(flipped, 1)
                        if 5 <= s < U + 5:
                            m = s - 5
                            k, q = divmod(m, 4)
                            p, half = q % 2, q // 2
                            if m == 0:
                                pe.wait_ge(ipa_in[u], 16 * i + 16)
                            pe.wait_ge(oT_ready, done(2 * (BODY * i + GRP * u + k - 1) + half))
                            pe.wait_ge(pT_ready, done(n - 5))
                            for j in range(4):
                                h = 8 * half + 2 * j + p
                                ins = nc.tensor.matmul(O[64 * p:64 * p + 64, half, j * P:(j + 1) * P],
                                                       V[:, k, D2 * h:D2 * h + D2], pT[:, m % 2, j, :],
                                                       start=True, stop=True)
                            ins.then_inc(weighed, 1)
                        if s >= 10 and s % 4 == 2:
                            b = (s - 10) // 4
                            pe.wait_ge(added, done(BODY * i + GRP * u + b - 1))
                            pe.wait_ge(oT_ready, done(2 * (BODY * i + GRP * u + b) + 1))
                            for c in range(NCH):
                                ins = nc.tensor.matmul(outp, oT[:, c, :], x2["L2_o"][:, c * P:(c + 1) * P],
                                                       start=(c == 0), stop=(c == NCH - 1))
                            ins.then_inc(out_done, 1)
                    if not (last and u == 1):
                        for m in range(16, NP):
                            project(i, u + 1, m)

            front(0, 0)
            front(0, 1)
            pe.wait_ge(F.xnT_ready, done(1))
            for m in range(NP):
                project(0, 0, m)
            with pe.Fori(0, TURNS - 1) as i:
                turn(i, False)
            turn(TURNS - 1, True)



NS = 64
SC = 16
TWO_PI = (6.28125, 0.0019350051879882812, 3.019915981956753e-07)
ROUND = 1.5 * 2.0 ** 23
HALF_TURN = 3.1415925


class ConvolutionKernel:

    def __init__(self, a, x3):
        self.x3 = x3
        self.dt = a.sb("dt", [P, 1])
        names = "th q f sh cos sin ar er zr zi z2r z2i wr nr ni den cr ci t0 t1".split()
        self.B = {n: a.sb(n, [P, NS])[:, :] for n in names}
        self.Pr = a.sb("Pr", [P, SC, P])
        self.Pi = a.sb("Pi", [P, SC, P // 2])
        self.u0 = a.sb("u0", [P, SC, P // 2])
        self.u1 = a.sb("u1", [P, SC, P // 2])
        self.pad = a.sb("pad", [P, 2 * P])
        self.dt_done, self.angle_ready, self.sines = a.sem("dt_done"), a.sem("angle"), a.sem("sines")
        self.den_ready, self.inverted = a.sem("den_ready"), a.sem("inverted")
        self.own, self.ready, self.stored = a.sem("k_own"), a.sem("k_ready"), a.sem("k_stored")

    def steps(self, act, nc, C):
        act.wait_ge(C.last_landed, 16)
        nc.scalar.activation(self.dt[:, :], self.x3["log_dt"], ACT.Exp).then_inc(self.dt_done, 1)

    def functions(self, act, nc):
        B = self.B
        act.wait_ge(self.angle_ready, 1)
        nc.scalar.activation(B["er"], B["ar"], ACT.Exp).then_inc(self.sines, 1)
        nc.scalar.activation(B["sin"], B["f"], ACT.Sin).then_inc(self.sines, 1)
        nc.scalar.activation(B["sh"], B["f"], ACT.Sin, scale=0.5).then_inc(self.sines, 1)

    def tt(self, nc, out, x, y, op):
        nc.gpsimd.tensor_tensor(out, x, y, op).then_inc(self.pool.done, self.pool.one())
        nc.gpsimd.wait_ge(self.pool.done, self.pool.count)

    def ts(self, nc, out, x, s1, s2, op0, op1=ALU.bypass):
        ins = (nc.gpsimd.tensor_scalar(out, x, s1, s2, op0, op1) if s2 is not None
               else nc.gpsimd.tensor_scalar(out, x, s1, None, op0))
        ins.then_inc(self.pool.done, self.pool.one())
        nc.gpsimd.wait_ge(self.pool.done, self.pool.count)

    def product(self, nc, outr, outi, xr, xi, yr, yi, t0, t1):
        self.tt(nc, t0, xr, yr, ALU.mult)
        self.tt(nc, t1, xi, yi, ALU.mult)
        self.tt(nc, outr, t0, t1, ALU.subtract)
        if outi is not None:
            self.tt(nc, t0, xr, yi, ALU.mult)
            self.tt(nc, t1, xi, yr, ALU.mult)
            self.tt(nc, outi, t0, t1, ALU.add)

    def invert(self, v, nc):
        v.wait_ge(self.den_ready, 1)
        nc.vector.reciprocal(self.B["den"], self.B["den"]).then_inc(self.inverted, 1)

    def angle(self, nc, pool, C):
        B, x3 = self.B, self.x3
        self.pool = Steps(self.own)
        dt = self.dt[:, 0:1].to_broadcast([P, NS])
        pool.wait_ge(C.last_landed, 16)
        self.tt(nc, B["t0"], x3["A_re"], x3["A_re"], ALU.mult)
        self.tt(nc, B["t1"], x3["A_im"], x3["A_im"], ALU.mult)
        nc.gpsimd.tensor_tensor(B["den"], B["t0"], B["t1"], ALU.add).then_inc(self.den_ready, 1)
        pool.wait_ge(self.dt_done, 1)
        self.tt(nc, B["ar"], x3["A_re"], dt, ALU.mult)
        self.tt(nc, B["th"], x3["A_im"], dt, ALU.mult)
        self.ts(nc, B["q"], B["th"], 1.0 / (2.0 * 3.141592653589793), ROUND, ALU.mult, ALU.add)
        self.ts(nc, B["q"], B["q"], ROUND, None, ALU.subtract)
        src = B["th"]
        for part in TWO_PI:
            self.ts(nc, B["t0"], B["q"], -part, None, ALU.mult)
            self.tt(nc, B["f"], B["t0"], src, ALU.add)
            src = B["f"]
        nc.gpsimd.tensor_scalar(B["f"], B["f"], HALF_TURN, -HALF_TURN, ALU.min, ALU.max).then_inc(self.angle_ready, 1)

    def coefficients(self, nc, pool):
        B, x3 = self.B, self.x3
        pool.wait_ge(self.sines, 3)
        pool.wait_ge(self.inverted, 1)
        self.tt(nc, B["cos"], B["sh"], B["sh"], ALU.mult)
        self.ts(nc, B["cos"], B["cos"], -2.0, 1.0, ALU.mult, ALU.add)
        self.tt(nc, B["zr"], B["er"], B["cos"], ALU.mult)
        self.tt(nc, B["zi"], B["er"], B["sin"], ALU.mult)
        self.ts(nc, B["wr"], B["zr"], 1.0, None, ALU.subtract)
        self.product(nc, B["nr"], B["ni"], x3["C_re"], x3["C_im"], B["wr"], B["zi"], B["t0"], B["t1"])
        self.ts(nc, B["z2i"], x3["A_im"], -1.0, None, ALU.mult)
        self.product(nc, B["cr"], B["ci"], B["nr"], B["ni"], x3["A_re"], B["z2i"], B["t0"], B["t1"])
        for x in ("cr", "ci"):
            self.tt(nc, B[x], B[x], B["den"], ALU.mult)
            self.ts(nc, B[x], B[x], 2.0, None, ALU.mult)
        nc.gpsimd.memset(self.pad[:, :], 0.0).then_inc(self.pool.done, self.pool.one())
        nc.gpsimd.wait_ge(self.pool.done, self.pool.count)

    def states(self, nc, part):
        B, Pr, Pi, u0, u1 = self.B, self.Pr, self.Pi, self.u0, self.u1
        n = slice(SC * part, SC * part + SC)
        nc.gpsimd.tensor_copy(Pr[:, :, 0:1], B["cr"][:, n].unsqueeze(2)).then_inc(self.pool.done, self.pool.one())
        nc.gpsimd.tensor_copy(Pi[:, :, 0:1], B["ci"][:, n].unsqueeze(2)).then_inc(self.pool.done, self.pool.one())
        nc.gpsimd.wait_ge(self.pool.done, self.pool.count)
        L, z = 1, ("zr", "zi")
        while L < P:
            wide = lambda x: B[x][:, n].unsqueeze(2).to_broadcast([P, SC, L])
            self.product(nc, Pr[:, :, L:2 * L], Pi[:, :, L:2 * L] if 2 * L < P else None, Pr[:, :, 0:L], Pi[:, :, 0:L],
                         wide(z[0]), wide(z[1]), u0[:, :, 0:L], u1[:, :, 0:L])
            if 2 * L < P:
                new = ("z2r", "z2i") if z[0] in ("zr", "nr") else ("nr", "ni")
                self.product(nc, B[new[0]][:, n], B[new[1]][:, n], B[z[0]][:, n], B[z[1]][:, n],
                             B[z[0]][:, n], B[z[1]][:, n], B["t0"][:, n], B["t1"][:, n])
                z = new
            L *= 2
        m = SC
        while m > 1:
            m //= 2
            self.tt(nc, Pr[:, 0:m, :], Pr[:, 0:m, :], Pr[:, m:2 * m, :], ALU.add)
        K = self.pad[:, P - 1:2 * P - 1]
        self.tt(nc, K, K, Pr[:, 0, :], ALU.add)

    def finish(self, nc, pool, C):
        x3, K0, mg = self.x3, self.pad[:, P - 1:P], C.rows["mod_gate"]
        self.tt(nc, K0, K0, x3["D_skip"], ALU.add)
        self.tt(nc, x3["film"], x3["film"], mg.to_broadcast([P, 512]), ALU.mult)
        self.tt(nc, C.rows["L3_film"], C.rows["L3_film"], mg.to_broadcast([P, 512]), ALU.mult)
        for at in (0, 256):
            fb = C.rows["L3_film"][:, at:at + P]
            self.ts(nc, fb, fb, 1.0, None, ALU.add)
        pool.sem_inc(self.ready, 1)

    def store(self, sp, C):
        sp.wait_ge(self.ready, 1)
        sp.dma_start(C.kpad_dram, self.pad[:, :]).then_inc(self.stored, 16)
        sp.wait_ge(self.stored, 16)



def shared_experts(nc, C, tg, x3):
    with ExitStack() as ctx:
        a = Alloc(nc, ctx, "L2f")
        F = Front(a)
        R = Router(a, BODY)
        wt = a.sb("wt", [P, BODY, E8])
        r = a.sb("r", [P, 2, 4, 512])
        half = a.sb("half", [P, 2, 512])
        c = a.sb("c", [P, 2, 512])
        cT = a.sb("cT", [P, 2, 4, P])
        H = a.ps("H", [P, 4, 512])
        T = a.ps("T", [P, 512])
        Y = a.ps("Y", [P, 512])
        tr = a.ps("tr", [P, 512])
        lgp = a.ps("lgp", [P, 512])
        We, Wo, Wg = C.f2["We"], C.f2["Wo"], C.f2["Wg"]
        logits = a.sem("logits")
        lg_read = a.sem("lg_read")
        weights = a.sem("weights")
        opened = a.sem("opened")
        relued = a.sem("relued")
        summed = a.sem("summed")
        flipped = a.sem("flipped")
        cT_ready = a.sem("cT_ready")
        closed = a.sem("closed")
        added = a.sem("added")
        own = a.sem("own")
        K = ConvolutionKernel(a, x3)
        block = ctx.enter_context(nc.Block())

        @block.gpsimd
        def _(pool):
            pool.sem_inc(F.root_ready, CREDIT)

            def front(i):
                for u in range(2):
                    F.root(nc, pool, C, i, u)

            front(0)
            K.angle(nc, pool, C)
            front(1)
            K.coefficients(nc, pool)
            K.states(nc, 0)
            front(2)
            K.states(nc, 1)
            front(3)
            K.states(nc, 2)
            K.states(nc, 3)
            K.finish(nc, pool, C)

        @block.sync
        def _(sp):
            K.store(sp, C)

        @block.vector
        def _(v):
            F.open_vector(v)
            for x in (R.shift_done, lg_read, weights, summed, added):
                v.sem_inc(x, CREDIT)
            vec = Steps(own)
            nc.vector.memset(R.lg[:, :, :], -1e30).then_inc(vec.done, vec.one())
            v.wait_ge(vec.done, vec.count)
            v.sem_clear(vec.done)
            vec.restart()

            def choose(i):
                v.wait_ge(logits, done(i))
                nc.vector.tensor_tensor(R.lg[:, :, 0:4], lgp[:, 0:BODY * 4].rearrange("p (b e) -> p b e", e=4),
                                        C.rows["L2f_bg"].unsqueeze(1).to_broadcast([P, BODY, 4]),
                                        ALU.add).then_inc(lg_read, 1)
                v.wait_ge(lg_read, done(i))
                nc.vector.memset(C.carrier[:, :], 0.0)
                R.choose(nc, v, vec, C, i)
                R.probabilities(nc, v, vec, i)
                nc.vector.tensor_tensor(wt[:, :, :], R.m1[:, :, :], R.rcp[:, :].unsqueeze(2).to_broadcast([P, BODY, E8]),
                                        ALU.mult).then_inc(weights, 1)

            def turn(i, last):
                for s in range(BODY + 2):
                    if not last:
                        if s in (3, 4):
                            F.statistics(nc, v, vec, C, i + 1, s - 3)
                        if s in (5, 6):
                            F.normalise(nc, v, vec, C, i + 1, s - 5)
                        if s == BODY + 1:
                            choose(i + 1)
                    if s < BODY:
                        n = BODY * i + s
                        v.wait_ge(relued, done(4 * n + 3))
                        v.wait_ge(flipped, done(n - 2))
                        for j, dst in ((0, c), (2, half)):
                            nc.vector.tensor_tensor(dst[:, s % 2, :], r[:, s % 2, j, :], r[:, s % 2, j + 1, :], ALU.add).then_inc(vec.done, vec.one())
                        nc.vector.wait_ge(vec.done, vec.count)
                        nc.vector.tensor_tensor(c[:, s % 2, :], c[:, s % 2, :], half[:, s % 2, :],
                                                ALU.add).then_inc(summed, 1)
                    if s >= 2:
                        b = s - 2
                        v.wait_ge(closed, done(BODY * i + b))
                        x = C.Xt[:, bass.ds(i, 1), b, :]
                        nc.vector.scalar_tensor_tensor(out=x, in0=Y[:, 0:P], scalar=tg, in1=x, op0=ALU.mult,
                                                       op1=ALU.add).then_inc(added, 1)
                v.wait_ge(vec.done, vec.count)
                v.sem_clear(vec.done)
                vec.restart()

            for u in range(2):
                F.statistics(nc, v, vec, C, 0, u)
            for u in range(2):
                F.normalise(nc, v, vec, C, 0, u)
            choose(0)
            K.invert(v, nc)
            v.wait_ge(vec.done, vec.count)
            v.sem_clear(vec.done)
            vec.restart()
            with v.Fori(0, TURNS - 1) as i:
                turn(i, False)
            turn(TURNS - 1, True)
            v.wait_ge(added, done(NB - 1))

        @block.scalar
        def _(act):
            for x in (F.xnT_ready, R.exp_done, relued, cT_ready):
                act.sem_inc(x, CREDIT)
            def turn(i, last):
                act.wait_ge(weights, done(i))
                for s in range(BODY + 1):
                    n = BODY * i + s
                    if s < BODY:
                        act.wait_ge(summed, done(n - 2))
                        for e in range(4):
                            act.wait_ge(opened, done(4 * n + e))
                            nc.scalar.activation(r[:, s % 2, e, :], H[:, e, :], ACT.Relu,
                                                 scale=wt[:, s, e:e + 1]).then_inc(relued, 1)
                    if s >= 1:
                        act.wait_ge(closed, done(n - 3))
                        act.wait_ge(flipped, done(n - 1))
                        nc.scalar.activation(cT[:, (s - 1) % 2, :, :], T[:, :].rearrange("p (c t) -> p c t", c=4),
                                             ACT.Identity).then_inc(cT_ready, 1)
                    if s >= BODY - 1 and not last:
                        F.take(nc, act, C, i + 1, s - BODY + 1, tr[:, :])
                if not last:
                    R.exponentials(nc, act, i + 1)

            for u in range(2):
                F.take(nc, act, C, 0, u, tr[:, :])
            R.exponentials(nc, act, 0)
            K.steps(act, nc, C)
            turn(0, False)
            K.functions(act, nc)
            with act.Fori(1, TURNS - 1) as i:
                turn(i, False)
            turn(TURNS - 1, True)

        @block.tensor
        def _(pe):
            for x in (F.turned, logits, opened, flipped, closed):
                pe.sem_inc(x, CREDIT)

            def front(i, u):
                pe.wait_ge(F.xnT_ready, done(2 * i + u - 1))
                F.turn(nc, pe, C, i, u, tr)

            def route_turn(i):
                pe.wait_ge(F.xnT_ready, done(2 * i + 1))
                pe.wait_ge(lg_read, done(i - 1))
                for b in range(BODY):
                    u, k = divmod(b, GRP)
                    ins = nc.tensor.matmul(lgp[:, b * 4:(b + 1) * 4], F.xnT[:, u, k * P:(k + 1) * P], Wg,
                                           start=True, stop=True)
                ins.then_inc(logits, 1)

            def turn(i, last):
                for s in range(BODY + 2):
                    n = BODY * i + s
                    if s < BODY:
                        u, k = divmod(s, GRP)
                        for e in range(4):
                            pe.wait_ge(relued, done(4 * (n - 1) + e))
                            nc.tensor.matmul(H[:, e, :], F.xnT[:, u, k * P:(k + 1) * P], We[:, 512 * e:512 * e + 512],
                                             start=True, stop=True).then_inc(opened, 1)
                    if s in (BODY - 1, BODY) and not last:
                        front(i + 1, s - BODY + 1)
                    if s == BODY + 1 and not last:
                        route_turn(i + 1)
                    if 1 <= s < BODY + 1:
                        pe.wait_ge(cT_ready, done(n - 2))
                        pe.wait_ge(summed, done(n - 1))
                        for j in range(4):
                            ins = nc.tensor.transpose(T[:, j * P:(j + 1) * P], c[:, (s - 1) % 2, j * P:(j + 1) * P], C.ident)
                        ins.then_inc(flipped, 1)
                    if s >= 2:
                        pe.wait_ge(added, done(n - 3))
                        pe.wait_ge(cT_ready, done(n - 2))
                        for j in range(4):
                            ins = nc.tensor.matmul(Y[:, 0:P], cT[:, s % 2, j, :], Wo[:, j * P:(j + 1) * P],
                                                   start=(j == 0), stop=(j == 3))
                        ins.then_inc(closed, 1)

            front(0, 0)
            front(0, 1)
            route_turn(0)
            with pe.Fori(0, TURNS - 1) as i:
                turn(i, False)
            turn(TURNS - 1, True)



KTOP = 32
H3, D3 = 4, 32
MASKED = -1e30
TAKEN = -3e38


def attention_top32(nc, C, x3, w96, xin):
    with ExitStack() as ctx:
        a = Alloc(nc, ctx, "L3")
        F = Front(a)
        N2 = Norm(a, "n2")
        ctxT = a.sb("ctxT", [KV, 2, TOK])
        qT = a.sb("qT", [P, 2, TOK])
        kT = a.sb("kT", [P, 2, TOK])
        kx = a.sb("kx", [P, 2, H3, P])
        V = a.sb("V", [P, 2, GRP, P])
        x1 = a.sb("x1", [P, 2, GRP, P])
        A = a.sb("A", [P, 2, H3, P])
        Wk = a.sb("Wk", [P, 2, H3, P])
        E = a.sb("E", [P, 2, H3, P])
        D = a.sb("D", [P, 2, H3, P])
        neg = a.sb("neg", [P, P])
        top = a.sb("top", [P, 2, H3, 8])
        top2 = a.sb("top2", [P, H3, 8])
        nmax = a.sb("nmax", [P, 2, H3])
        sm = a.sb("sm", [P, H3])
        rc = a.sb("rc", [P, 2, H3])
        aT = a.sb("aT", [P, 2, P])
        ctT = a.sb("ctT", [P, 2, TOK])
        t = a.sb("t", [P, P])
        pj = a.ps("pj", [P, 2, 512])
        S = a.ps("S", [P, 2, 512])
        tb = a.ps("tb", [P, 512])
        cb = a.ps("cb", [P, 512])
        fb = a.ps("fb", [P, 512])

        ctx_in = [a.sem(f"ctx_in{u}") for u in range(2)]
        ct_out = [a.sem(f"ct_out{u}") for u in range(2)]
        ct_stored = a.sem("ct_stored")
        projected = a.sem("projected")
        q_ready = a.sem("q_ready")
        k_ready = a.sem("k_ready")
        v_ready = a.sem("v_ready")
        spread = a.sem("spread")
        x1_ready = a.sem("x1_ready")
        x1_scaled = a.sem("x1_scaled")
        x1_done = a.sem("x1_done")
        scored = a.sem("scored")
        masked = a.sem("masked")
        chosen = a.sem("chosen")
        exped = a.sem("exped")
        kept = a.sem("kept")
        weights = a.sem("weights")
        weighted = a.sem("weighted")
        averaged = a.sem("averaged")
        aT_ready = a.sem("aT_ready")
        ct_done = a.sem("ct_done")
        ctT_ready = a.sem("ctT_ready")
        film_done = a.sem("film_done")
        film_read = a.sem("film_read")
        own = a.sem("own")
        block = ctx.enter_context(nc.Block())
        xt = xin[:, :].rearrange("p (i b d) -> p i b d", i=TURNS, b=BODY)
        STEPS = BODY + 5

        @block.sync
        def _(sp):
            sp.sem_inc(ct_stored, CREDIT)

            def context(i, u):
                sp.dma_start(ctxT[:, u, :], C.ctxT_v[:, bass.ds(i, 1), u, :]).then_inc(ctx_in[u], 16)

            def turn(i, last):
                if not last:
                    for u in range(2):
                        sp.wait_ge(projected, done(6 * i + 3 * u + 2))
                        context(i + 1, u)
                for u in range(2):
                    sp.wait_ge(ctT_ready, done(BODY * i + GRP * u + GRP - 1))
                    sp.dma_start(C.ctT_v[:, bass.ds(i, 1), u, :], ctT[:, u, :]).then_inc(ct_out[u], 16)
                for u in range(2):
                    sp.wait_ge(ct_out[u], 16 * i + 16)
                    sp.sem_inc(ct_stored, 1)

            for u in range(2):
                context(0, u)
            with sp.Fori(0, TURNS - 1) as i:
                turn(i, False)
            turn(TURNS - 1, True)

        @block.gpsimd
        def _(pool):
            for x in (F.root_ready, N2.root_ready, spread, x1_done, kept, weighted):
                pool.sem_inc(x, CREDIT)

            def front(i):
                for u in range(2):
                    F.root(nc, pool, C, i, u)
                for u in range(2):
                    N2.root(nc, pool, C, i, u)

            def turn(i, last):
                def keys(b):
                    u, k = divmod(b, GRP)
                    pool.wait_ge(k_ready, done(2 * i + u))
                    pool.wait_ge(scored, done(BODY * i + b - 2))
                    nc.gpsimd.tensor_tensor(
                        kx[:, b % 2, :, :], kT[:, u, k * P:(k + 1) * P].unsqueeze(1).to_broadcast([P, H3, P]),
                        C.head_mask.unsqueeze(2).to_broadcast([P, H3, P]), ALU.mult).then_inc(spread, 1)

                keys(0)
                keys(1)
                for u in range(2):
                    pool.wait_ge(x1_ready, done(2 * i + u))
                    g_row = C.rows["L3_g_in"].unsqueeze(1).to_broadcast([P, GRP, P])
                    b_row = C.rows["L3_b_in"].unsqueeze(1).to_broadcast([P, GRP, P])
                    nc.gpsimd.tensor_tensor(x1[:, u, :, :], x1[:, u, :, :], g_row, ALU.mult).then_inc(x1_scaled, 1)
                    pool.wait_ge(x1_scaled, 2 * i + u + 1)
                    nc.gpsimd.tensor_tensor(x1[:, u, :, :], x1[:, u, :, :], b_row, ALU.add).then_inc(x1_done, 1)
                for s in range(BODY + 1):
                    n = BODY * i + s
                    if s < BODY:
                        pool.wait_ge(exped, done(n))
                        nc.gpsimd.tensor_tensor(E[:, s % 2, :, :], E[:, s % 2, :, :], Wk[:, s % 2, :, :],
                                                ALU.subtract).then_inc(kept, 1)
                        if s + 2 < BODY:
                            keys(s + 2)
                    if s >= 1:
                        pool.wait_ge(weights, done(n - 1))
                        pool.wait_ge(averaged, done(n - 3))
                        nc.gpsimd.tensor_tensor(D[:, (s - 1) % 2, :, :], C.ident.unsqueeze(1).to_broadcast([P, H3, P]),
                                                rc[:, (s - 1) % 2, :].unsqueeze(2).to_broadcast([P, H3, P]),
                                                ALU.mult).then_inc(weighted, 1)
                if not last:
                    front(i + 1)

            front(0)
            with pool.Fori(0, TURNS - 1) as i:
                turn(i, False)
            turn(TURNS - 1, True)

        @block.vector
        def _(v):
            F.open_vector(v)
            for x in (N2.var_ready, x1_ready, masked, chosen, weights, film_read):
                v.sem_inc(x, CREDIT)
            vec = Steps(own)

            def choose(i, s):
                n = BODY * i + s
                nc.vector.tensor_scalar(neg[:, :], C.kv_mask_v[:, bass.ds(i, 1), s, :], 1.0, -MASKED,
                                                ALU.subtract, ALU.mult).then_inc(vec.done, vec.one())
                v.wait_ge(exped, done(n - 2))
                v.wait_ge(kept, done(n - 2))
                v.wait_ge(scored, done(n))
                nc.vector.wait_ge(vec.done, vec.count)
                nc.vector.tensor_tensor(A[:, s % 2, :, :], S[:, s % 2, :].rearrange("p (h t) -> p h t", h=H3),
                                        neg[:, :].unsqueeze(1).to_broadcast([P, H3, P]), ALU.add).then_inc(masked, 1)
                v.wait_ge(masked, done(n))
                nc.vector.memset(C.carrier[:, :], 0.0)
                replaced = [vec.count] * H3
                for r in range(KTOP // 8):
                    src = A if r == 0 else Wk
                    t8 = top[:, s % 2, :, :] if r == 0 else top2[:, :, :]
                    found = []
                    for h in range(H3):
                        nc.vector.wait_ge(vec.done, replaced[h])
                        nc.vector.max(t8[:, h, :], src[:, s % 2, h, :]).then_inc(vec.done, vec.one())
                        found.append(vec.count)
                    for h in range(H3):
                        nc.vector.wait_ge(vec.done, found[h])
                        nc.vector.match_replace(Wk[:, s % 2, h, :], t8[:, h, :], src[:, s % 2, h, :],
                                                TAKEN).then_inc(vec.done, vec.one())
                        replaced[h] = vec.count
                nc.vector.wait_ge(vec.done, vec.count)
                nc.vector.tensor_scalar(nmax[:, s % 2, :], top[:, s % 2, :, 0], -1.0, None, ALU.mult).then_inc(chosen, 1)

            def total(i, b):
                v.wait_ge(kept, done(BODY * i + b))
                nc.vector.tensor_reduce(sm[:, :], E[:, b % 2, :, :], AX.X, ALU.add).then_inc(vec.done, vec.one())
                nc.vector.wait_ge(vec.done, vec.count)
                nc.vector.reciprocal(sm[:, :], sm[:, :]).then_inc(vec.done, vec.one())
                nc.vector.wait_ge(vec.done, vec.count)
                nc.vector.tensor_scalar(rc[:, b % 2, :], sm[:, :], C.q_mask_v[:, bass.ds(i, 1), b], 1.0 / H3,
                                        ALU.mult, ALU.mult).then_inc(weights, 1)

            def modulate(i, b):
                u, k = divmod(b, GRP)
                n = BODY * i + b
                v.wait_ge(x1_done, done(2 * i + u))
                v.wait_ge(film_done, done(n))
                nc.vector.wait_ge(vec.done, vec.count)
                nc.vector.tensor_tensor(t[:, :], x1[:, u, k, :], fb[:, 0:P], ALU.mult).then_inc(vec.done, vec.one())
                nc.vector.wait_ge(vec.done, vec.count)
                nc.vector.tensor_tensor(xt[:, bass.ds(i, 1), b, :], t[:, :], fb[:, P:2 * P], ALU.add).then_inc(
                    film_read, 1)

            def second_statistics(i):
                v.wait_ge(F.st_ready, done(2 * i + 1))
                nc.vector.memset(C.carrier[:, :], 0.0)
                for u in range(2):
                    N2.statistics(nc, vec, lambda k: F.st[:, u, k, :], u)

            def second_norm(i, u):
                N2.affine(nc, v, vec, i, u)
                for k in range(GRP):
                    ins = N2.apply(nc, x1[:, u, k, :], F.st[:, u, k, :], u, k)
                ins.then_inc(x1_ready, 1)

            def turn(i, last):
                for s in range(STEPS):
                    if s < BODY:
                        choose(i, s)
                    if 1 <= s < BODY + 1:
                        total(i, s - 1)
                    if not last:
                        if s == BODY:
                            for u in range(2):
                                F.statistics(nc, v, vec, C, i + 1, u)
                        if s == BODY + 1:
                            for u in range(2):
                                F.normalise(nc, v, vec, C, i + 1, u)
                        if s == BODY + 2:
                            second_statistics(i + 1)
                        if s == BODY + 3:
                            second_norm(i + 1, 0)
                    if 5 <= s < BODY + 5:
                        modulate(i, s - 5)
                v.wait_ge(film_read, done(BODY * i + BODY - 1))
                nc.vector.memset(C.carrier[:, :], 0.0)
                if not last:
                    second_norm(i + 1, 1)
                v.wait_ge(vec.done, vec.count)
                v.sem_clear(vec.done)
                vec.restart()

            for u in range(2):
                F.statistics(nc, v, vec, C, 0, u)
            for u in range(2):
                F.normalise(nc, v, vec, C, 0, u)
            second_statistics(0)
            for u in range(2):
                second_norm(0, u)
            v.wait_ge(vec.done, vec.count)
            v.sem_clear(vec.done)
            vec.restart()
            with v.Fori(0, TURNS - 1) as i:
                turn(i, False)
            turn(TURNS - 1, True)

        @block.scalar
        def _(act):
            for x in (F.xnT_ready, q_ready, k_ready, v_ready, exped, aT_ready, ctT_ready):
                act.sem_inc(x, CREDIT)

            def project(i):
                for u in range(2):
                    act.wait_ge(projected, done(6 * i + 3 * u))
                    nc.scalar.activation(qT[:, u, :], pj[:, u, :], ACT.Identity,
                                         scale=D3 ** -0.5).then_inc(q_ready, 1)
                    act.wait_ge(spread, done(BODY * i + GRP * u + 3 - BODY))
                    act.wait_ge(projected, done(6 * i + 3 * u + 1))
                    nc.scalar.activation(kT[:, u, :], pj[:, 1 - u, :], ACT.Identity).then_inc(k_ready, 1)
                    act.wait_ge(projected, done(6 * i + 3 * u + 2))
                    nc.scalar.activation(V[:, u, :, :], pj[:, u, :].rearrange("p (b d) -> p b d", b=GRP),
                                         ACT.Identity).then_inc(v_ready, 1)

            def turn(i, last):
                for s in range(BODY + 4):
                    n = BODY * i + s
                    if 2 <= s < BODY + 2:
                        act.wait_ge(ct_done, done(n - 4))
                        act.wait_ge(averaged, done(n - 2))
                        nc.scalar.activation(aT[:, (s - 2) % 2, :], tb[:, 0:P], ACT.Identity).then_inc(aT_ready, 1)
                    if 3 <= s < BODY + 3:
                        b = s - 3
                        if b % GRP == 0:
                            act.wait_ge(ct_stored, done(2 * (i - 1) + b // GRP))
                        act.wait_ge(ct_done, done(BODY * i + b))
                        nc.scalar.activation(ctT[:, b // GRP, b % GRP * P:(b % GRP + 1) * P], cb[:, 0:P],
                                             ACT.Identity).then_inc(ctT_ready, 1)
                    if s < BODY:
                        act.wait_ge(averaged, done(n - 2))
                        act.wait_ge(chosen, done(n))
                        for x in (E, Wk):
                            src = A if x is E else Wk
                            for h in range(H3):
                                ins = nc.scalar.activation(x[:, s % 2, h, :], src[:, s % 2, h, :], ACT.Exp,
                                                           bias=nmax[:, s % 2, h:h + 1])
                        ins.then_inc(exped, 1)
                    if s >= BODY + 2 and not last:
                        F.take(nc, act, C, i + 1, s - BODY - 2, pj[:, s - BODY - 2, :])
                if not last:
                    project(i + 1)

            for u in range(2):
                F.take(nc, act, C, 0, u, pj[:, u, :])
            project(0)
            with act.Fori(0, TURNS - 1) as i:
                turn(i, False)
            turn(TURNS - 1, True)

        @block.tensor
        def _(pe):
            for x in (F.turned, projected, scored, averaged, ct_done, film_done):
                pe.sem_inc(x, CREDIT)

            def front(i, u):
                pe.wait_ge(v_ready if u else k_ready, done(2 * i - 1))
                F.turn(nc, pe, C, i, u, pj[:, u, :])

            def project(i):
                for u in range(2):
                    g = 2 * i + u
                    pe.wait_ge(F.xnT_ready, done(2 * i + 1))
                    if u:
                        pe.wait_ge(k_ready, done(2 * i))
                    nc.tensor.matmul(pj[:, u, :], x3["q"], F.xnT[:, u, :], start=True, stop=True).then_inc(
                        projected, 1)
                    pe.wait_ge(ctx_in[u], 16 * i + 16)
                    if u:
                        pe.wait_ge(v_ready, done(2 * i))
                    nc.tensor.matmul(pj[:, 1 - u, :], w96["L3_k"], ctxT[:, u, :], start=True, stop=True).then_inc(
                        projected, 1)
                    pe.wait_ge(q_ready, done(g))
                    for k in range(GRP):
                        ins = nc.tensor.matmul(pj[:, u, k * P:(k + 1) * P], ctxT[:, u, k * P:(k + 1) * P],
                                               w96["L3_v"], start=True, stop=True)
                    ins.then_inc(projected, 1)

            def turn(i, last):
                for s in range(BODY + 4):
                    n = BODY * i + s
                    if s < BODY:
                        u, k = divmod(s, GRP)
                        pe.wait_ge(q_ready, done(2 * i + u))
                        pe.wait_ge(masked, done(n - 2))
                        pe.wait_ge(spread, done(n))
                        nc.tensor.matmul(S[:, s % 2, :], qT[:, u, k * P:(k + 1) * P], kx[:, s % 2, :, :],
                                         start=True, stop=True).then_inc(scored, 1)
                    if 2 <= s < BODY + 2:
                        pe.wait_ge(aT_ready, done(n - 3))
                        pe.wait_ge(weighted, done(n - 2))
                        for h in range(H3):
                            ins = nc.tensor.matmul(tb[:, 0:P], E[:, s % 2, h, :], D[:, s % 2, h, :], start=(h == 0),
                                                   stop=(h == H3 - 1))
                        ins.then_inc(averaged, 1)
                    if 3 <= s < BODY + 3:
                        b = s - 3
                        u, k = divmod(b, GRP)
                        pe.wait_ge(v_ready, done(2 * i + u))
                        pe.wait_ge(ctT_ready, done(n - 4))
                        pe.wait_ge(aT_ready, done(n - 3))
                        nc.tensor.matmul(cb[:, 0:P], V[:, u, k, :], aT[:, b % 2, :], start=True, stop=True).then_inc(
                            ct_done, 1)
                    if 4 <= s:
                        b = s - 4
                        pe.wait_ge(film_read, done(n - 5))
                        pe.wait_ge(ctT_ready, done(n - 4))
                        nc.tensor.matmul(fb[:, 0:2 * P], ctT[:, b // GRP, b % GRP * P:(b % GRP + 1) * P],
                                         x3["film"][:, 0:2 * P], start=True, stop=False)
                        nc.tensor.matmul(fb[:, 0:2 * P], C.ones[0:1, :], C.rows["L3_film"][0:1, 0:2 * P], start=False,
                                         stop=True).then_inc(film_done, 1)
                    if s >= BODY + 2 and not last:
                        front(i + 1, s - BODY - 2)
                if not last:
                    project(i + 1)

            front(0, 0)
            front(0, 1)
            project(0)
            with pe.Fori(0, TURNS - 1) as i:
                turn(i, False)
            turn(TURNS - 1, True)



CD = 16
CHUNKS = P // CD
RING = 3


def convolve(nc, C, xin):
    with ExitStack() as ctx:
        a = Alloc(nc, ctx, "conv")
        xr = a.sb("xr", [P, NB * P])
        Tz = a.sb("Tz", [P, RING, CD, P])
        rev = a.ps("rev", [P, 2, 512])
        Y = a.ps("Y", [P, 2, 512])
        fetched = [a.sem(f"fetched{k}") for k in range(RING)]
        reversed_, kept_a, kept_v = a.sem("reversed"), a.sem("kept_a"), a.sem("kept_v")
        summed, y_a, y_v = a.sem("summed"), a.sem("y_a"), a.sem("y_v")
        xr3 = xr[:, :].rearrange("p (b d) -> p b d", b=NB)
        y3 = xin[:, :].rearrange("p (b d) -> p d b", b=NB)
        kpad = C.kpad_dram
        block = ctx.enter_context(nc.Block())

        @block.sync
        def _(sp):
            for c in range(CHUNKS):
                if c >= RING:
                    sp.wait_ge(summed, c - RING + 1)
                src = bass.AP(tensor=kpad.tensor, offset=kpad.offset + c * CD * 2 * P,
                              ap=[[1, P], [2 * P, CD], [1, P]])
                sp.dma_start(Tz[:, c % RING, :, :], src).then_inc(fetched[c % RING], 16)

        @block.tensor
        def _(pe):
            for c in range(8):
                if c >= 2:
                    pe.wait_ge(kept_v if c % 2 else kept_a, c // 2)
                nc.tensor.matmul(rev[:, c % 2, :], C.reverse, xin[:, 512 * c:512 * c + 512],
                                 start=True, stop=True).then_inc(reversed_, 1)
            pe.wait_ge(kept_a, 4)
            pe.wait_ge(kept_v, 4)
            for c in range(CHUNKS):
                pe.wait_ge(fetched[c % RING], 16 * (c // RING + 1))
                if c >= 2:
                    pe.wait_ge(y_v if c % 2 else y_a, c // 2)
                for d in range(CD):
                    ins = nc.tensor.matmul(Y[:, c % 2, d * NB:(d + 1) * NB], Tz[:, c % RING, d, :],
                                           xr3[:, :, c * CD + d], start=True, stop=True)
                ins.then_inc(summed, 1)

        @block.scalar
        def _(act):
            for c in range(0, 8, 2):
                act.wait_ge(reversed_, c + 1)
                nc.scalar.activation(xr[:, 512 * c:512 * c + 512], rev[:, 0, :], ACT.Identity).then_inc(kept_a, 1)
            for c in range(0, CHUNKS, 2):
                act.wait_ge(summed, c + 1)
                nc.scalar.activation(y3[:, c * CD:(c + 1) * CD, :], Y[:, 0, :].rearrange("p (d b) -> p d b", d=CD),
                                     ACT.Identity).then_inc(y_a, 1)

        @block.vector
        def _(v):
            for c in range(1, 8, 2):
                v.wait_ge(reversed_, c + 1)
                nc.vector.tensor_copy(xr[:, 512 * c:512 * c + 512], rev[:, 1, :]).then_inc(kept_v, 1)
            for c in range(1, CHUNKS, 2):
                v.wait_ge(summed, c + 1)
                nc.vector.tensor_copy(y3[:, c * CD:(c + 1) * CD, :],
                                      Y[:, 1, :].rearrange("p (d b) -> p d b", d=CD)).then_inc(y_v, 1)



def film_feed_forward(nc, C, x3, y, tg):
    NC = 4
    with ExitStack() as ctx:
        a = Alloc(nc, ctx, "L3b")
        F = Front(a)
        NF, NO = Norm(a, "nf"), Norm(a, "no")
        ctT = a.sb("ctT", [P, 2, TOK])
        y2 = a.sb("y2", [P, 2, P])
        hn = a.sb("hn", [P, 2, GRP, P])
        hT = a.sb("hT", [P, 2, TOK])
        aT = a.sb("aT", [P, 2, NC, TOK])
        fb = a.ps("fb", [P, 2, 512])
        tr = a.ps("tr", [P, 512])
        U = a.ps("U", [P, 3, 512])
        Y = a.ps("Y", [P, 2, 512])
        ct_in = [a.sem(f"ct_in{u}") for u in range(2)]
        film_done = a.sem("film_done")
        film_read = a.sem("film_read")
        hn_ready = a.sem("hn_ready")
        turned = a.sem("turned2")
        hT_ready = a.sem("hT_ready")
        opened = a.sem("opened")
        a_ready = a.sem("a_ready")
        closed = a.sem("closed")
        y_read = a.sem("y_read")
        own = a.sem("own")
        block = ctx.enter_context(nc.Block())
        yt = y[:, :].rearrange("p (i b d) -> p i b d", i=TURNS, b=BODY)

        @block.sync
        def _(sp):
            with sp.Fori(0, TURNS) as i:
                for u in range(2):
                    sp.wait_ge(film_done, done(BODY * (i - 1) + GRP * u + GRP - 1))
                    sp.dma_start(ctT[:, u, :], C.ctT_v[:, bass.ds(i, 1), u, :]).then_inc(ct_in[u], 16)

        @block.gpsimd
        def _(pool):
            for x in (F.N, NF, NO):
                pool.sem_inc(x.root_ready, CREDIT)

            def turn(i, last):
                NF.root(nc, pool, C, i, 0)
                F.N.root(nc, pool, C, i, 1)
                NF.root(nc, pool, C, i, 1)
                NO.root(nc, pool, C, i, 0)
                if not last:
                    F.N.root(nc, pool, C, i + 1, 0)
                NO.root(nc, pool, C, i, 1)

            F.N.root(nc, pool, C, 0, 0)
            with pool.Fori(0, TURNS - 1) as i:
                turn(i, False)
            turn(TURNS - 1, True)

        @block.vector
        def _(v):
            for x in (F.N.var_ready, NF.var_ready, NO.var_ready, film_read, hn_ready, y_read):
                v.sem_inc(x, CREDIT)
            vec = Steps(own)
            g_row = C.rows["L3_g_out"].unsqueeze(1).to_broadcast([P, GRP, P])
            b_row = C.rows["L3_b_out"].unsqueeze(1).to_broadcast([P, GRP, P])

            def normalise(i, u):
                F.statistics(nc, v, vec, C, i, u)
                F.N.affine(nc, v, vec, i, u)
                for k in range(GRP):
                    F.N.apply(nc, F.st[:, u, k, :], C.Xt[:, bass.ds(i, 1), GRP * u + k, :], u, k).then_inc(
                        vec.done, vec.one())
                nc.vector.wait_ge(vec.done, vec.count)

            def modulate(i, u):
                for k in range(GRP):
                    b = GRP * u + k
                    v.wait_ge(film_done, done(BODY * i + b))
                    nc.vector.tensor_tensor(y2[:, b % 2, :], yt[:, bass.ds(i, 1), b, :], fb[:, b % 2, 0:P],
                                            ALU.mult).then_inc(vec.done, vec.one())
                    nc.vector.wait_ge(vec.done, vec.count)
                    nc.vector.tensor_tensor(y2[:, b % 2, :], y2[:, b % 2, :], fb[:, b % 2, P:2 * P], ALU.add).then_inc(
                        film_read, 1)
                    v.wait_ge(film_read, done(BODY * i + b))
                    nc.vector.tensor_tensor(F.st[:, u, k, :], F.st[:, u, k, :], y2[:, b % 2, :], ALU.add).then_inc(
                        vec.done, vec.one())
                nc.vector.wait_ge(vec.done, vec.count)

            def enter(i, u):
                NF.statistics(nc, vec, lambda k: F.st[:, u, k, :], u)
                NF.affine(nc, v, vec, i, u)
                v.wait_ge(turned, done(2 * (i - 1) + u))
                for k in range(GRP):
                    ins = NF.apply(nc, hn[:, u, k, :], F.st[:, u, k, :], u, k)
                ins.then_inc(hn_ready, 1)

            def leave(i, u):
                v.wait_ge(hn_ready, done(2 * i + u))
                v.wait_ge(closed, done(2 * i + u))
                nc.vector.tensor_tensor(F.st[:, u, :, :], F.st[:, u, :, :],
                                        Y[:, u, :].rearrange("p (k d) -> p k d", k=GRP), ALU.add).then_inc(y_read, 1)
                v.wait_ge(y_read, done(2 * i + u))
                nc.vector.memset(C.carrier[:, :], 0.0)
                NO.statistics(nc, vec, lambda k: F.st[:, u, k, :], u)
                NO.affine(nc, v, vec, i, u)
                for k in range(GRP):
                    NO.apply(nc, F.st[:, u, k, :], F.st[:, u, k, :], u, k).then_inc(vec.done, vec.one())
                nc.vector.wait_ge(vec.done, vec.count)
                nc.vector.tensor_tensor(F.st[:, u, :, :], F.st[:, u, :, :], g_row, ALU.mult).then_inc(vec.done, vec.one())
                nc.vector.wait_ge(vec.done, vec.count)
                nc.vector.tensor_tensor(F.st[:, u, :, :], F.st[:, u, :, :], b_row, ALU.add).then_inc(vec.done, vec.one())
                nc.vector.wait_ge(vec.done, vec.count)
                x = C.Xt[:, bass.ds(i, 1), GRP * u:GRP * u + GRP, :].rearrange("p o k d -> p (o k d)")
                nc.vector.scalar_tensor_tensor(out=x, in0=F.st[:, u, :, :].rearrange("p k d -> p (k d)"), scalar=tg,
                                               in1=x, op0=ALU.mult, op1=ALU.add).then_inc(vec.done, vec.one())
                nc.vector.wait_ge(vec.done, vec.count)

            def turn(i, last):
                modulate(i, 0)
                enter(i, 0)
                normalise(i, 1)
                modulate(i, 1)
                enter(i, 1)
                leave(i, 0)
                if not last:
                    normalise(i + 1, 0)
                leave(i, 1)
                v.wait_ge(vec.done, vec.count)
                v.sem_clear(vec.done)
                vec.restart()

            normalise(0, 0)
            v.wait_ge(vec.done, vec.count)
            v.sem_clear(vec.done)
            vec.restart()
            with v.Fori(0, TURNS - 1) as i:
                turn(i, False)
            turn(TURNS - 1, True)

        @block.scalar
        def _(act):
            for x in (hT_ready, a_ready):
                act.sem_inc(x, CREDIT)
            with act.Fori(0, TURNS) as i:
                for u in range(2):
                    act.wait_ge(turned, done(2 * i + u))
                    nc.scalar.activation(hT[:, u, :], tr[:, :], ACT.Identity, scale=x3["g_ffn"],
                                         bias=x3["b_ffn"]).then_inc(hT_ready, 1)
                    for c in range(NC):
                        n = NC * (2 * i + u) + c
                        act.wait_ge(closed, done(2 * (i - 1) + u))
                        act.wait_ge(opened, done(n))
                        nc.scalar.activation(aT[:, u, c, :], U[:, (NC * u + c) % 2, :], ACT.Gelu,
                                             bias=x3["b1"][:, c:c + 1]).then_inc(a_ready, 1)

        @block.tensor
        def _(pe):
            for x in (film_done, turned, opened, closed):
                pe.sem_inc(x, CREDIT)
            w2 = x3["W2"].rearrange("p (c d) -> p c d", c=NC)

            def film(i, u):
                pe.wait_ge(ct_in[u], 16 * i + 16)
                for k in range(GRP):
                    b = GRP * u + k
                    pe.wait_ge(film_read, done(BODY * i + b - 2))
                    nc.tensor.matmul(fb[:, b % 2, 0:2 * P], ctT[:, u, k * P:(k + 1) * P], x3["film"][:, 2 * P:4 * P],
                                     start=True, stop=False)
                    nc.tensor.matmul(fb[:, b % 2, 0:2 * P], C.ones[0:1, :], C.rows["L3_film"][0:1, 2 * P:4 * P],
                                     start=False, stop=True).then_inc(film_done, 1)

            def open_group(i, u):
                pe.wait_ge(hT_ready, done(2 * i + u - 1))
                pe.wait_ge(hn_ready, done(2 * i + u))
                for k in range(GRP):
                    ins = nc.tensor.transpose(tr[:, k * P:(k + 1) * P], hn[:, u, k, :], C.ident)
                ins.then_inc(turned, 1)
                pe.wait_ge(hT_ready, done(2 * i + u))
                for c in range(NC):
                    n = NC * (2 * i + u) + c
                    pe.wait_ge(a_ready, done(n - 2))
                    nc.tensor.matmul(U[:, (NC * u + c) % 2, :], x3["W1"][:, c * P:(c + 1) * P], hT[:, u, :],
                                     start=True, stop=True).then_inc(opened, 1)

            def close_group(i, u):
                pe.wait_ge(a_ready, done(NC * (2 * i + u) + NC - 1))
                pe.wait_ge(y_read, done(2 * (i - 1) + u))
                for k in range(GRP):
                    for c in range(NC):
                        nc.tensor.matmul(Y[:, u, k * P:(k + 1) * P], aT[:, u, c, k * P:(k + 1) * P], w2[:, c, :],
                                         start=(c == 0), stop=False)
                    ins = nc.tensor.matmul(Y[:, u, k * P:(k + 1) * P], C.ones[0:1, :], C.rows["L3_b2"][0:1, :],
                                           start=False, stop=True)
                ins.then_inc(closed, 1)

            with pe.Fori(0, TURNS) as i:
                film(i, 0)
                open_group(i, 0)
                film(i, 1)
                close_group(i, 0)
                open_group(i, 1)
                close_group(i, 1)



NTOK = NB * P
EXPERTS = 8
def capacity_experts(nc, C, W, wt, slot, xn, xnT):
    NC = 4
    tiles = [(k, min(P, CAPACITY - k)) for k in range(0, CAPACITY, P)]
    with ExitStack() as ctx:
        a = Alloc(nc, ctx, "L3f")
        aT = a.sb("aT", [P, 2, NC, TOK])
        yb = a.sb("yb", [P, 2, GRP, P])
        xg = a.sb("xg", [P, 3, len(tiles), P])
        xgT = a.sb("xgT", [P, 2, CAPACITY])
        yg = a.sb("yg", [P, 2, len(tiles), P])
        tr = a.ps("tr", [P, 512])
        U = a.ps("U", [P, 4, 512])
        Y = a.ps("Y", [P, 2, 512])
        opened, a_ready, closed, y_read, added = (
            a.sem("opened"), a.sem("a_ready"), a.sem("closed"), a.sem("y_read"), a.sem("added"))
        sent = a.sem("sent")
        fetched = [a.sem(f"fetched{q}") for q in range(3)]
        turned = a.sem("turned")
        xgT_ready = a.sem("xgT_ready")
        e_opened, e_active, e_closed = a.sem("e_opened"), a.sem("e_active"), a.sem("e_closed")
        yg_ready = a.sem("yg_ready")
        put = [a.sem(f"put{q}") for q in range(2)]
        back = [a.sem(f"back{q}") for q in range(NB // BACK)]
        summed = a.sem("summed")
        block = ctx.enter_context(nc.Block())
        units = E8 + 1
        w1 = W["W1"].rearrange("p (e c f) -> p e c f", e=units, c=NC)
        w2 = W["W2"].rearrange("p (e c d) -> p e c d", e=units, c=NC)
        b1 = W["b1"].rearrange("p (e c) -> p e c", e=units)
        b2 = C.rows["L3f_b2"].rearrange("p (e d) -> p e d", e=units)
        wt_t = wt[:, :, :].rearrange("p j (i b) -> p j i b", i=TURNS)
        xnT_t = xnT[:, :].rearrange("p (i u t) -> p i u t", i=TURNS, u=2)
        GROUPS = 2 * TURNS
        full = CAPACITY // P
        rest = CAPACITY - full * P

        def rows(dram, e):
            own = dram[e * CAPACITY:(e + 1) * CAPACITY, :]
            return own[0:full * P, :].rearrange("(k p) d -> p k d", p=P), own[full * P:, :]

        @block.gpsimd
        def _(pool):
            send_rows(nc, slot, xn, C.expert_in, EXPERT_ROWS, sent)
            pool.wait_ge(sent, 16 * 2 * NB)
            pool.wait_ge(closed, done(GROUPS - 1))
            for q in range(2):
                pool.wait_ge(put[q], 32 * (E8 // 2))
            bring_rows(nc, slot, C.expert_out, EXPERT_ROWS, xn, xnT, back)

        @block.sync
        def _(sp):
            def fetch(e):
                if e >= 3:
                    sp.wait_ge(turned, e - 2)
                whole, last = rows(C.expert_in, e)
                sp.dma_start(xg[:, e % 3, 0:full, :], whole).then_inc(fetched[e % 3], 16)
                sp.dma_start(xg[0:rest, e % 3, full, :], last).then_inc(fetched[e % 3], 16)

            sp.wait_ge(sent, 16 * 2 * NB)
            fetch(0)
            fetch(1)
            for e in range(E8):
                if e + 2 < E8:
                    fetch(e + 2)
                sp.wait_ge(yg_ready, e + 1)
                whole, last = rows(C.expert_out, e)
                sp.dma_start(whole, yg[:, e % 2, 0:full, :]).then_inc(put[e % 2], 16)
                sp.dma_start(last, yg[0:rest, e % 2, full, :]).then_inc(put[e % 2], 16)
            for q in range(2):
                sp.wait_ge(put[q], 32 * (E8 // 2))

        @block.vector
        def _(v):
            for x in (y_read, added):
                v.sem_inc(x, CREDIT)
            with v.Fori(0, TURNS) as i:
                for u in range(2):
                    n = 2 * i + u
                    v.wait_ge(closed, done(n))
                    v.wait_ge(added, done(n - 2))
                    nc.vector.tensor_tensor(yb[:, u, :, :], Y[:, u, :].rearrange("p (k d) -> p k d", k=GRP),
                                            b2[:, 0:1, :].to_broadcast([P, GRP, P]), ALU.add).then_inc(y_read, 1)
                    v.wait_ge(y_read, done(n))
                    for k in range(GRP):
                        b = GRP * u + k
                        x = C.Xt[:, bass.ds(i, 1), b, :]
                        ins = nc.vector.scalar_tensor_tensor(out=x, in0=yb[:, u, k, :],
                                                             scalar=wt_t[:, 2, bass.ds(i, 1), b], in1=x,
                                                             op0=ALU.mult, op1=ALU.add)
                    ins.then_inc(added, 1)
            for e in range(E8):
                if e >= 2:
                    v.wait_ge(put[e % 2], 32 * (e // 2))
                v.wait_ge(e_closed, e + 1)
                y = Y[:, e % 2, 0:len(tiles) * P].rearrange("p (k d) -> p k d", d=P)
                nc.vector.tensor_tensor(yg[:, e % 2, 0:full, :], y[:, 0:full, :],
                                        b2[:, e + 1:e + 2, :].to_broadcast([P, full, P]), ALU.add)
                nc.vector.tensor_tensor(yg[0:rest, e % 2, full, :], y[0:rest, full, :], b2[0:rest, e + 1, :],
                                        ALU.add).then_inc(yg_ready, 1)
            v.wait_ge(added, done(GROUPS - 1))
            combine(nc, C, v, wt, xn, xnT, back, summed)

        @block.scalar
        def _(act):
            act.sem_inc(a_ready, CREDIT)
            with act.Fori(0, TURNS) as i:
                for u in range(2):
                    act.wait_ge(closed, done(2 * i + u - 2))
                    for c in range(NC):
                        act.wait_ge(opened, done(NC * (2 * i + u) + c))
                        nc.scalar.activation(aT[:, u, c, :], U[:, c, :], ACT.Gelu,
                                             bias=b1[:, 0, c:c + 1]).then_inc(a_ready, 1)
            act.wait_ge(closed, done(GROUPS - 1))

            def take(e):
                act.wait_ge(turned, e + 1)
                nc.scalar.activation(xgT[:, e % 2, :], tr[:, 0:CAPACITY], ACT.Identity).then_inc(xgT_ready, 1)

            take(0)
            for e in range(E8):
                if e + 1 < E8:
                    if e >= 1:
                        act.wait_ge(e_opened, NC * e)
                    take(e + 1)
                if e >= 2:
                    act.wait_ge(e_closed, e - 1)
                for c in range(NC):
                    act.wait_ge(e_opened, NC * e + c + 1)
                    nc.scalar.activation(aT[:, e % 2, c, 0:CAPACITY], U[:, c, 0:CAPACITY], ACT.Gelu,
                                         bias=b1[:, e + 1, c:c + 1]).then_inc(e_active, 1)

        @block.tensor
        def _(pe):
            for x in (opened, closed):
                pe.sem_inc(x, CREDIT)

            def close(i, t):
                pe.wait_ge(y_read, done(2 * i + t - 2))
                pe.wait_ge(a_ready, done(NC * (2 * i + t) + NC - 1))
                for k in range(GRP):
                    for c in range(NC):
                        ins = nc.tensor.matmul(Y[:, t % 2, k * P:(k + 1) * P], aT[:, t % 2, c, k * P:(k + 1) * P],
                                               w2[:, 0, c, :], start=(c == 0), stop=(c == NC - 1))
                ins.then_inc(closed, 1)

            with pe.Fori(0, TURNS) as i:
                for u in range(2):
                    for c in range(NC):
                        pe.wait_ge(a_ready, done(NC * (2 * i + u - 1) + c))
                        nc.tensor.matmul(U[:, c, :], w1[:, 0, c, :], xnT_t[:, bass.ds(i, 1), u, :], start=True,
                                         stop=True).then_inc(opened, 1)
                    if u:
                        close(i, 0)
                close(i, 1)
            pe.wait_ge(y_read, done(GROUPS - 1))

            def turn(e):
                pe.wait_ge(fetched[e % 3], 32 * (e // 3 + 1))
                if e:
                    pe.wait_ge(xgT_ready, e)
                for k, (at, m) in enumerate(tiles):
                    ins = nc.tensor.transpose(tr[:, at:at + m], xg[0:m, e % 3, k, :], C.ident[0:m, 0:m])
                ins.then_inc(turned, 1)

            turn(0)
            for e in range(E8 + 1):
                if e < E8:
                    pe.wait_ge(xgT_ready, e + 1)
                    for c in range(NC):
                        if e >= 1:
                            pe.wait_ge(e_active, NC * (e - 1) + c + 1)
                        nc.tensor.matmul(U[:, c, 0:CAPACITY], w1[:, e + 1, c, :], xgT[:, e % 2, :], start=True,
                                         stop=True).then_inc(e_opened, 1)
                    if e + 1 < E8:
                        turn(e + 1)
                if e >= 1:
                    if e >= 3:
                        pe.wait_ge(yg_ready, e - 2)
                    pe.wait_ge(e_active, NC * e)
                    for k, (at, m) in enumerate(tiles):
                        for c in range(NC):
                            ins = nc.tensor.matmul(Y[0:m, (e - 1) % 2, k * P:(k + 1) * P],
                                                   aT[:, (e - 1) % 2, c, at:at + m], w2[:, e, c, :],
                                                   start=(c == 0), stop=(c == NC - 1))
                    ins.then_inc(e_closed, 1)



ROWS = [("gates", 8), ("alpha", 4), ("L1_bo", P), ("L1_bv", P), ("L2_bo", P), ("L2f_bg", 4),
        ("mod_gate", 1), ("L3_film", 512), ("L3_g_in", P), ("L3_b_in", P), ("L3_g_out", P), ("L3_b_out", P), ("L3_b2", P),
        ("L3f_b2", 9 * P)]
SECTIONS = {
    "const": [("ident", P), ("mask16", HEADS), ("iota8", 8), ("tile_no", TILES), ("ones8", 8), ("minus_half", 4), ("reverse", P),
              ("head_mask", H3), ("upto", P), ("ones", P)],
    "x0": [("L0_q", P), ("L0_o", P)],
    "x1": [("L1_q", P), ("L1_o", P), ("L1_bq", 1), ("L1_bk", 1)],
    "x2": [("L2_q", INNER), ("L2_o", INNER)],
    "f0": [("L0f_router", 8), ("L0f_sgate", 256), ("L0f_sup", 256), ("L0f_sdown", 256),
           ("L0f_gate", 4096), ("L0f_up", 4096), ("L0f_down", 4096)],
    "f1": [("L1f_router", 8), ("L1f_sgate", 256), ("L1f_sup", 256), ("L1f_sdown", 256),
           ("L1f_gate", 1024), ("L1f_up", 1024), ("L1f_down", 1024)],
}
LATER = {
    "f2": [("Wi", 512), ("Wo", 512), ("Wg", 4)],
    "f3": [("router", 8), ("W1", 9 * 512), ("W2", 9 * 512), ("b1", 9 * 4)],
}
LAST = {
    "x3": [("q", P), ("film", 512), ("g_ffn", 1), ("b_ffn", 1), ("W1", 512), ("b1", 4), ("W2", 512), ("log_dt", 1),
           ("D_skip", 1), ("A_re", NS), ("A_im", NS), ("C_re", NS), ("C_im", NS)],
}
LATE = len(LATER)
SECTION96 = [("L0_k", P), ("L0_v", P), ("L1_k", P), ("L1_v", P),
             ("L2_k", INNER), ("L2_v", INNER), ("L2_ki", INNER), ("L2_vi", INNER), ("L3_k", P), ("L3_v", P)]
SECTION32 = [("q_down", P), ("k_down", KV), ("v_down", KV), ("o_down", INNER),
             ("q_up", INNER), ("k_up", INNER), ("v_up", INNER), ("o_up", P)]
SECTION4 = [("A", 512), ("B", 2048)]
ROW_PLACE, ROW_N = columns(ROWS)
PLACES = {s: columns(parts) for s, parts in SECTIONS.items()}
LATER_PLACES = {s: columns(parts) for s, parts in LATER.items()}
LAST_PLACES = {s: columns(parts) for s, parts in LAST.items()}
PLACE32, N32 = columns(SECTION32)
PLACE4, N4 = columns(SECTION4)
PLACE96, N96 = columns(SECTION96)


def load_later(nc, C, later, dram):
    with nc.Block() as block:
        @block.sync
        def _(sp):
            for s, packed in later.items():
                sp.dma_start(packed.tile, dram[f"sec_{s}"]).then_inc(C.late_landed, 16)


def program(nc, dram, out):
    with ExitStack() as ctx:
        C = Core()
        X = ctx.enter_context(nc.sbuf_tensor("X", [P, NB * P], F32))
        rows = ctx.enter_context(nc.sbuf_tensor("rows", [P, ROW_N], F32))
        w96 = ctx.enter_context(nc.sbuf_tensor("w96", [KV, N96], F32))
        tgs = ctx.enter_context(nc.sbuf_tensor("tgs", [P, 8], F32))
        sec = {}
        for s, (place, n) in PLACES.items():
            sec[s] = Packed(ctx.enter_context(nc.sbuf_tensor(f"sec_{s}", [P, n], F32)), place)
        landed = ctx.enter_context(nc.semaphore("landed"))
        rest_landed = ctx.enter_context(nc.semaphore("rest_landed"))
        C.last_landed = ctx.enter_context(nc.semaphore("last_landed"))
        C.late_landed = ctx.enter_context(nc.semaphore("late_landed"))
        C.v_ipa_dram = nc.dram_tensor("v_ipa", (P, INNER), F32, kind="Internal").ap()
        C.tile_in = nc.dram_tensor("tile_in", ((TILES + AHEAD) * P, P), F32, kind="Internal").ap()
        C.tile_out = nc.dram_tensor("tile_out", (TILES * P, P), F32, kind="Internal").ap()
        C.expert_in = nc.dram_tensor("expert_in", (EXPERT_ROWS, P), F32, kind="Internal").ap()
        C.expert_out = nc.dram_tensor("expert_out", (EXPERT_ROWS, P), F32, kind="Internal").ap()
        C.kpad_dram = nc.dram_tensor("kpad", (P, 2 * P), F32, kind="Internal").ap()
        C.ctT_v = nc.dram_tensor("ctT", (P, NB * P), F32, kind="Internal").ap().rearrange(
            "p (i u t) -> p i u t", i=TURNS, u=2)
        kv_mask = ctx.enter_context(nc.sbuf_tensor("kv_mask", [P, NB * P], U8))
        C.kv_mask_v = kv_mask[:, :].rearrange("p (i b t) -> p i b t", i=TURNS, b=BODY)
        q_mask8 = ctx.enter_context(nc.sbuf_tensor("q_mask8", [P, NB], U8))
        q_mask = ctx.enter_context(nc.sbuf_tensor("q_mask", [P, NB], F32))
        C.q_mask_v = q_mask[:, :].rearrange("p (i b) -> p i b", i=TURNS)
        C.v_ipa_v = C.v_ipa_dram.rearrange("(i u b t) n -> t i u b n", i=TURNS, u=2, b=GRP)
        tanh_done = ctx.enter_context(nc.semaphore("tanh_done"))
        stored = ctx.enter_context(nc.semaphore("stored"))

        C.X = X
        C.carrier = ctx.enter_context(nc.sbuf_tensor("carrier", [P, 1], F32))
        C.Xt = X[:, :].rearrange("p (i b d) -> p i b d", i=TURNS, b=BODY)
        C.ctxT_v = dram["ctxT"].rearrange("c (i u t) -> c i u t", i=TURNS, u=2)
        C.rows = Packed(rows, ROW_PLACE)
        K = sec["const"]
        C.ident, C.mask16, C.iota8, C.tile_no, C.ones8, C.minus_half, C.reverse, C.head_mask, C.upto, C.ones = (
            K[n] for n in ("ident", "mask16", "iota8", "tile_no", "ones8", "minus_half", "reverse", "head_mask", "upto", "ones"))
        W96 = Packed(w96, PLACE96)

        at, later = 0, {}
        for s, (place, n) in LATER_PLACES.items():
            later[s] = Packed(sec["f0"].tile[:, at:at + n], place)
            at += n
        place, n = LAST_PLACES["x3"]
        x3 = Packed(sec["f1"].tile[:, 0:n], place)
        C.f2 = dict(later["f2"].items())
        C.f2["We"] = sec["f0"].tile[:, at:at + 4 * 512]

        first96 = PLACE96["L1_k"][0]
        small = ROW_PLACE["L1_bo"][0]
        rows_in = dram["rows"].partition_broadcast(P)
        first = [(rows[:, 0:small], rows_in[:, 0:small]), (X[:, :], dram["x"]), (w96[:, 0:first96], dram["w96"][:, 0:first96]),
                 (sec["const"].tile[:, :], dram["sec_const"]), (sec["x0"].tile[:, :], dram["sec_x0"])]
        background = [(sec["f0"].tile[:, :], dram["sec_f0"]), (rows[:, small:], rows_in[:, small:]),
                      (w96[:, first96:], dram["w96"][:, first96:]), (sec["x1"].tile[:, :], dram["sec_x1"]),
                      (sec["f1"].tile[:, :], dram["sec_f1"]), (sec["x2"].tile[:, :], dram["sec_x2"]),
                      (kv_mask[:, :], dram["kv_mask"].partition_broadcast(P)), (q_mask8[:, :], dram["q_mask"])]
        with nc.Block() as block:
            @block.sync
            def _(sp):
                for dst, src in first:
                    sp.dma_start(dst, src).then_inc(landed, 16)
                sp.wait_ge(landed, 16 * len(first))

            @block.scalar
            def _(act):
                act.wait_ge(landed, 16 * len(first))
                nc.scalar.activation(tgs[:, :], C.rows["gates"], ACT.Tanh).then_inc(tanh_done, 1)
                act.wait_ge(tanh_done, 1)

        tg = lambda n: tgs[:, n:n + 1]
        attention16(nc, C, "L0", sec["x0"], sec["x0"]["L0_q"], W96["L0_k"], W96["L0_v"], sec["x0"]["L0_o"], tg(0), False,
                    background, rest_landed)
        with nc.Block() as block:
            @block.sync
            def _(sp):
                sp.wait_ge(rest_landed, 16 * len(background))

            @block.scalar
            def _(act):
                act.wait_ge(rest_landed, 16 * len(background))
                nc.scalar.activation(q_mask[:, :], q_mask8[:, :], ACT.Identity).then_inc(tanh_done, 1)
                act.wait_ge(tanh_done, 2)
        with (nc.sbuf_tensor("wt0", [P, 2, NB], F32) as wt, nc.sbuf_tensor("slot0", [P, 2, NB], U32) as slot,
              nc.sbuf_tensor("tile_expert", [P, TILES], U32) as tile_expert,
              nc.sbuf_tensor("xn0", [P, NB * P], F32) as xn, nc.sbuf_tensor("xnT0", [P, NB * P], F32) as xnT):
            route(nc, C, "rt0", sec["f0"]["L0f_router"], tg(4), wt, slot, xn, xnT, C.tile_in, (TILES + AHEAD) * P,
                  tile_expert)
            tiled_experts(nc, C, "L0f", sec["f0"], tg(4), wt, slot, xn, xnT, tile_expert)
        load_later(nc, C, later, dram)
        attention16(nc, C, "L1", sec["x1"], sec["x1"]["L1_q"], W96["L1_k"], W96["L1_v"], sec["x1"]["L1_o"], tg(1), True)
        gated_experts(nc, C, "L1f", sec["f1"], 1, tg(5))
        merge_lora(nc, C, sec["x2"], W96, x3, dram)
        attention_ipa(nc, C, sec["x2"], W96, tg(2))
        shared_experts(nc, C, tg(6), x3)
        with nc.sbuf_tensor("xin", [P, NB * P], F32) as xin:
            attention_top32(nc, C, x3, W96, xin)
            convolve(nc, C, xin)
            film_feed_forward(nc, C, x3, xin, tg(3))
        with (nc.sbuf_tensor("wt", [P, 3, NB], F32) as wt, nc.sbuf_tensor("slot", [P, 2, NB], U32) as slot,
              nc.sbuf_tensor("xn", [P, NB * P], F32) as xn, nc.sbuf_tensor("xnT", [P, NB * P], F32) as xnT):
            route(nc, C, "rt", later["f3"]["router"], tg(7), wt, slot, xn, xnT, C.expert_in, EXPERT_ROWS)
            capacity_experts(nc, C, later["f3"], wt, slot, xn, xnT)

        with nc.Block() as block:
            @block.sync
            def _(sp):
                sp.dma_start(out, X[:, :]).then_inc(stored, 16)
                sp.wait_ge(stored, 16)


def kernel(**inputs):
    import numpy as np
    import concourse.bacc as _bacc
    from concourse.bass_utils import run_bass_kernel_spmd as _run

    I = {k: np.asarray(v) for k, v in inputs.items()}
    f = np.arange(P)

    def chunked(w):
        e = w.reshape(-1, w.shape[-2] // P, P, w.shape[-1])
        return e.transpose(2, 0, 1, 3).reshape(P, -1)

    def stacked(w):
        return w.transpose(1, 0, 2).reshape(w.shape[1], -1)

    part = {
        "ident": np.eye(P, dtype=np.float32),
        "mask16": (f[:, None] // HD == np.arange(HEADS)).astype(np.float32),
        "iota8": np.tile(np.arange(8, dtype=np.float32), (P, 1)),
        "tile_no": np.tile(np.arange(TILES, dtype=np.float32), (P, 1)),
        "ones8": np.ones((P, 8), np.float32),
        "minus_half": np.full((P, 4), -0.5, np.float32),
        "L0_q": I["L0_xattn_Wq"].T, "L0_o": I["L0_xattn_Wo"].T,
        "L0_k": I["L0_xattn_Wk"].T, "L0_v": I["L0_xattn_Wv"].T,
        "L1_q": I["L1_xattn_Wq"], "L1_o": I["L1_xattn_Wo"], "L1_k": I["L1_xattn_Wk"], "L1_v": I["L1_xattn_Wv"],
        "L1_bq": I["L1_xattn_bq"][:, None], "L1_bk": I["L1_xattn_bk"][:, None],
        "L0f_router": I["L0_ffn_gate_w"].T, "L0f_sgate": I["L0_ffn_sh_gate"], "L0f_sup": I["L0_ffn_sh_up"],
        "L0f_sdown": chunked(I["L0_ffn_sh_down"]), "L0f_gate": stacked(I["L0_ffn_gate_k"]),
        "L0f_up": stacked(I["L0_ffn_up_k"]), "L0f_down": chunked(I["L0_ffn_down_k"]),
        "L1f_router": I["L1_ffn_router_w"], "L1f_sgate": I["L1_ffn_shared_gate_w"],
        "L1f_sup": I["L1_ffn_shared_up_w"], "L1f_sdown": chunked(I["L1_ffn_shared_down_w"]),
        "L1f_gate": stacked(I["L1_ffn_gate_w"]), "L1f_up": stacked(I["L1_ffn_up_w"]),
        "L1f_down": chunked(I["L1_ffn_down_w"]),
        "L2_q": I["L2_xattn_Wq"], "L2_o": chunked(I["L2_xattn_Wo"]),
        "L2_k": I["L2_xattn_Wk"], "L2_v": I["L2_xattn_Wv"],
        "L2_ki": I["L2_xattn_Wk_ipa"], "L2_vi": I["L2_xattn_Wv_ipa"],
        "q_down": I["L2_xattn_q_down"].T, "k_down": I["L2_xattn_k_down"].T, "v_down": I["L2_xattn_v_down"].T,
        "o_down": I["L2_xattn_o_down"].T, "q_up": I["L2_xattn_q_up"], "k_up": I["L2_xattn_k_up"],
        "v_up": I["L2_xattn_v_up"], "o_up": I["L2_xattn_o_up"], "L2_bo": I["L2_xattn_bo"],
        "alpha": np.concatenate([I[f"L2_xattn_{n}_alpha"] for n in "qkvo"]),
        "A": I["L2_ffn_A"].transpose(1, 0, 2).reshape(4, 512),
        "B": I["L2_ffn_B"].transpose(2, 0, 1).reshape(4, 2048),
        "Wi": I["L2_ffn_Wi"].T, "Wo": chunked(I["L2_ffn_Wo"].T), "Wg": I["L2_ffn_Wg"].T, "L2f_bg": I["L2_ffn_bg"],
        "reverse": np.ascontiguousarray(np.eye(P, dtype=np.float32)[::-1]),
        "head_mask": (f[:, None] // D3 == np.arange(H3)).astype(np.float32),
        "q": I["L3_xattn_Wq"], "L3_k": I["L3_xattn_Wk"], "L3_v": I["L3_xattn_Wv"],
        "film": np.concatenate([I["L3_xattn_W_film_in"], I["L3_xattn_W_film_out"]], axis=1),
        "g_ffn": I["L3_xattn_g_ffn"][:, None], "b_ffn": I["L3_xattn_b_ffn"][:, None],
        "W1": I["L3_xattn_W1"], "b1": I["L3_xattn_b1"].reshape(4, P).T, "W2": chunked(I["L3_xattn_W2"]),
        "log_dt": I["L3_xattn_log_dt"][:, None], "D_skip": I["L3_xattn_D_skip"][:, None],
        "A_re": I["L3_xattn_A_re"], "A_im": I["L3_xattn_A_im"], "C_re": I["L3_xattn_C_re"], "C_im": I["L3_xattn_C_im"],
        "mod_gate": I["L3_xattn_mod_gate"].reshape(1),
        "L3_film": np.concatenate([I["L3_xattn_b_film_in"], I["L3_xattn_b_film_out"]]),
        "L3_g_in": I["L3_xattn_g_norm_in"], "L3_b_in": I["L3_xattn_b_norm_in"],
        "L3_g_out": I["L3_xattn_g_norm_out"], "L3_b_out": I["L3_xattn_b_norm_out"], "L3_b2": I["L3_xattn_b2"],
        "upto": np.triu(np.ones((P, P), np.float32)), "ones": np.ones((P, P), np.float32),
        "router": I["L3_ffn_Wr"],
        "gates": np.concatenate([I["g_xattn"], I["g_ffn"]]), "L1_bo": I["L1_xattn_bo"], "L1_bv": I["L1_xattn_bv"],
    }

    last = {
        "W1": np.concatenate([I["L3_ffn_fw1"], stacked(I["L3_ffn_W1"])], axis=1),
        "W2": np.concatenate([chunked(I["L3_ffn_fw2"]), chunked(I["L3_ffn_W2"])], axis=1),
        "b1": np.concatenate([I["L3_ffn_fb1"][None], I["L3_ffn_b1"]]).reshape(9, 4, P).transpose(2, 0, 1).reshape(P, 36),
    }
    part["L3f_b2"] = np.concatenate([I["L3_ffn_fb2"], I["L3_ffn_b2"].reshape(-1)])

    def pack(parts, axis, part=part):
        for name, n in parts:
            assert part[name].shape[axis] == n, (name, part[name].shape)
        return np.ascontiguousarray(np.concatenate([part[name] for name, _ in parts], axis=axis))

    arrays = {
        "x": np.ascontiguousarray(I["x"].transpose(1, 0, 2).reshape(P, NB * P)),
        "ctxT": np.ascontiguousarray(I["ctx_768"].transpose(2, 0, 1).reshape(KV, NB * P)),
        "kv_mask": I["mask_BxS2_bf1"].reshape(-1), "q_mask": np.ascontiguousarray(I["mask_BxS_bf1"].T),
        "rows": pack(ROWS, 0), "w96": pack(SECTION96, 1), "w32": pack(SECTION32, 1), "w4": pack(SECTION4, 1),
    }
    for s, parts in {**SECTIONS, **LATER, **LAST}.items():
        arrays[f"sec_{s}"] = pack(parts, 1, {**part, **last} if s == "f3" else part)

    nc = _bacc.Bacc("TRN2", target_bir_lowering=False, num_devices=1)
    dram = {k: nc.dram_tensor(f"in_{k}", v.shape, mybir.dt.from_np(v.dtype), kind="ExternalInput").ap()
            for k, v in arrays.items()}
    out = nc.dram_tensor("out_0", (P, NB * P), F32, kind="ExternalOutput").ap()
    program(nc, dram, out)
    r = _run(nc, [{f"in_{k}": v for k, v in arrays.items()}], core_ids=[0])
    return np.ascontiguousarray(r.results[0]["out_0"].reshape(P, NB, P).transpose(1, 0, 2))
```
